# Optimizing a Trainium2 kernel written in Bass

```python
import numpy as np
import jax
import jax.numpy as jnp

def _softmax(x, axis=-1):
    return jax.nn.softmax(x, axis=axis)

def _gelu(x):
    return jax.nn.gelu(x, approximate=True)

def _silu(x):
    return jax.nn.silu(x)

def _sigmoid(x):
    return jax.nn.sigmoid(x)

def _layernorm(x, axis=-1, eps=1e-05):
    m = jnp.mean(x, axis=axis, keepdims=True)
    v = jnp.var(x, axis=axis, keepdims=True)
    return (x - m) / jnp.sqrt(v + eps)

def _scatter_add(tgt, idx, src, axis=0):
    return tgt.at[idx].add(src)

def _segment_sum(src, seg, n):
    return jax.ops.segment_sum(src, seg, n)
kernel_name = 'mk_perceiver_d4_seqx_r8_fe7f30'

def setup_inputs(seed: int=0):
    np.random.seed(seed)
    _w = jnp.asarray

    def _rec_inputs():
        import jax
        import jax.numpy as jnp
        _rk = jax.random.key(seed)
        x = -0.0002928 + 1 * jax.random.normal(jax.random.fold_in(_rk, 1), (128, 32, 128), jnp.float32)
        _lenS = 32 - jax.random.randint(jax.random.fold_in(_rk, 7), (128,), 0, max(1, 32 // 4) + 1, jnp.int32)
        _lenS2 = 257 - jax.random.randint(jax.random.fold_in(_rk, 8), (128,), 0, max(1, 257 // 4) + 1, jnp.int32)
        _ctx_1024P = jax.random.normal(jax.random.fold_in(_rk, 11), (128, 16, 128), jnp.float32)
        _ctx_1024c = jax.random.dirichlet(jax.random.fold_in(_rk, 511), 0.3 * jnp.ones((16,), jnp.float32), (128, 257))
        _ctx_1024t = jnp.einsum('bsk,bkd->bsd', _ctx_1024c, _ctx_1024P)
        _ctx_1024t = _ctx_1024t * jax.lax.rsqrt(jnp.mean(jnp.square(_ctx_1024t)) + 1e-12) * 0.953939
        ctx_1024 = -1.39393e-06 + 0.999914 * (_ctx_1024t + 0.3 * jax.random.normal(jax.random.fold_in(_rk, 611), (128, 257, 128), jnp.float32))
        _validS = jnp.arange(32)[None, :] < _lenS[:, None]
        _validS2 = jnp.arange(257)[None, :] < _lenS2[:, None]
        _causal = jnp.tril(jnp.ones((32, 32), dtype=bool))
        mask_BxS2_if1 = jnp.where(jnp.ones((128, 257), dtype=bool), 1, 0).astype(jnp.int32)
        mask_1x1xSxS2_ik0 = jnp.where(jnp.broadcast_to(_validS2[0:1, None, None, :], (1, 1, 32, 257)), 0, 1).astype(jnp.int32)
        return (x, ctx_1024, mask_BxS2_if1, mask_1x1xSxS2_ik0)
    x, ctx_1024, mask_BxS2_if1, mask_1x1xSxS2_ik0 = _rec_inputs()

    def _L0_xattn_setup():
        import jax, jax.numpy as jnp
        import numpy as np
        D_MODEL = 128
        NUM_HEADS = 16
        D_K = D_MODEL // NUM_HEADS
        NEG = -1000000000.0

        def _split_heads(x, B):
            return x.reshape(B, -1, NUM_HEADS, D_K).transpose(0, 2, 1, 3)
        key = jax.random.key(seed)
        ks = jax.random.split(key, 7)
        B, S = (2, 256)
        q = jax.random.normal(ks[0], (B, S, D_MODEL), dtype=jnp.float32)
        k = jax.random.normal(ks[1], (B, S, D_MODEL), dtype=jnp.float32)
        v = jax.random.normal(ks[2], (B, S, D_MODEL), dtype=jnp.float32)
        mask = jnp.ones((B, S), dtype=jnp.int32)
        scale = 1.0 / np.sqrt(D_MODEL)
        Wq = jax.random.normal(ks[3], (D_MODEL, D_MODEL), dtype=jnp.float32) * scale
        Wk = jax.random.normal(ks[4], (D_MODEL, D_MODEL), dtype=jnp.float32) * scale
        Wv = jax.random.normal(ks[5], (D_MODEL, D_MODEL), dtype=jnp.float32) * scale
        Wo = jax.random.normal(ks[6], (D_MODEL, D_MODEL), dtype=jnp.float32) * scale
        return {'q': q, 'k': k, 'v': v, 'mask': mask, 'Wq': Wq, 'Wk': Wk, 'Wv': Wv, 'Wo': Wo}
    _L0_xattn_all = _L0_xattn_setup()
    _L0_xattn_in = {k: v for k, v in _L0_xattn_all.items() if k in ('Wq', 'Wk', 'Wv', 'Wo')}
    del _L0_xattn_all

    def _L0_attn_setup():
        import jax, jax.numpy as jnp
        import numpy as np
        DIM = 128
        DIM_HEAD = 64
        HEADS = 8
        INNER = DIM_HEAD * HEADS
        SCALE = DIM_HEAD ** (-0.5)
        COS_SCALE = 1.0

        def layer_norm(x, w, b, eps=1e-05):
            mu = jnp.mean(x, axis=-1, keepdims=True)
            var = jnp.var(x, axis=-1, keepdims=True)
            return (x - mu) * jax.lax.rsqrt(var + eps) * w + b
        key = jax.random.key(seed)
        ks = jax.random.split(key, 6)
        x = jax.random.normal(ks[0], (4, 256, DIM), dtype=jnp.float32)
        Wq = jax.random.normal(ks[1], (DIM, INNER), dtype=jnp.float32) * DIM ** (-0.5)
        Wkv = jax.random.normal(ks[2], (DIM, 2 * DIM_HEAD), dtype=jnp.float32) * DIM ** (-0.5)
        Wo = jax.random.normal(ks[3], (INNER, DIM), dtype=jnp.float32) * INNER ** (-0.5)
        norm_w = jnp.ones((DIM,), jnp.float32)
        norm_b = jnp.zeros((DIM,), jnp.float32)
        out_norm_w = jnp.ones((DIM,), jnp.float32)
        out_norm_b = jnp.zeros((DIM,), jnp.float32)
        return {'x': x, 'Wq': Wq, 'Wkv': Wkv, 'Wo': Wo, 'norm_w': norm_w, 'norm_b': norm_b, 'out_norm_w': out_norm_w, 'out_norm_b': out_norm_b}
    _L0_attn_all = _L0_attn_setup()
    _L0_attn_in = {k: v for k, v in _L0_attn_all.items() if k in ('Wq', 'Wkv', 'Wo', 'norm_w', 'norm_b', 'out_norm_w', 'out_norm_b')}
    del _L0_attn_all

    def _L0_ffn_setup():
        import jax, jax.numpy as jnp
        import numpy as np
        B, S, H, E = (4, 256, 128, 8)
        key = jax.random.key(seed)
        k1, k2, k3 = jax.random.split(key, 3)
        scale_w = 1.0 / np.sqrt(H)
        return {'x': jax.random.normal(k1, (B, S, H), dtype=jnp.float32), 'router_w': jax.random.normal(k2, (H, E), dtype=jnp.float32) * scale_w, 'router_b': jnp.zeros((E,), dtype=jnp.float32), 'expert_w': jax.random.normal(k3, (E, H, H), dtype=jnp.float32) * scale_w, 'expert_b': jnp.zeros((E, H), dtype=jnp.float32)}
    _L0_ffn_all = _L0_ffn_setup()
    _L0_ffn_in = {k: v for k, v in _L0_ffn_all.items() if k in ('router_w', 'router_b', 'expert_w', 'expert_b')}
    del _L0_ffn_all

    def _L1_xattn_setup():
        import jax, jax.numpy as jnp
        import numpy as np
        NUM_HEADS = 16
        D_MODEL = 128
        HEAD_DIM = D_MODEL // NUM_HEADS
        SCALE = 8.0 / HEAD_DIM
        LN_EPS = 1e-05

        def _layernorm(x, g, b):
            mu = jnp.mean(x, axis=-1, keepdims=True)
            var = jnp.mean(jnp.square(x - mu), axis=-1, keepdims=True)
            return (x - mu) * jax.lax.rsqrt(var + LN_EPS) * g + b
        key = jax.random.key(seed)
        ks = jax.random.split(key, 8)
        B, N, M = (2, 256, 256)
        std = 1.0 / np.sqrt(D_MODEL)
        return {'x1': jax.random.normal(ks[0], (B, N, D_MODEL), jnp.float32), 'x2': jax.random.normal(ks[1], (B, M, D_MODEL), jnp.float32), 'Wq': jax.random.normal(ks[2], (D_MODEL, D_MODEL), jnp.float32) * std, 'Wk': jax.random.normal(ks[3], (D_MODEL, D_MODEL), jnp.float32) * std, 'Wv': jax.random.normal(ks[4], (D_MODEL, D_MODEL), jnp.float32) * std, 'Wp': jax.random.normal(ks[5], (D_MODEL, D_MODEL), jnp.float32) * std, 'bp': jnp.zeros((D_MODEL,), jnp.float32), 'ln_g': jnp.ones((HEAD_DIM,), jnp.float32), 'ln_b': jnp.zeros((HEAD_DIM,), jnp.float32)}
    _L1_xattn_all = _L1_xattn_setup()
    _L1_xattn_in = {k: v for k, v in _L1_xattn_all.items() if k in ('Wq', 'Wk', 'Wv', 'Wp', 'bp', 'ln_g', 'ln_b')}
    del _L1_xattn_all

    def _L1_attn_setup():
        import math
        import jax, jax.numpy as jnp
        import numpy as np
        D_MODEL = 128
        N_HEADS = 16
        D_HEAD = D_MODEL // N_HEADS
        SEQ = 512
        BATCH = 1
        BASE = 10000.0
        EPS = 1e-05

        def _layernorm(x, g, b):
            mu = jnp.mean(x, axis=-1, keepdims=True)
            var = jnp.mean(jnp.square(x - mu), axis=-1, keepdims=True)
            return (x - mu) * jax.lax.rsqrt(var + EPS) * g + b

        def _rotate(x, cos, sin):
            b, H, n, dh = x.shape
            xr = x.reshape(b, H, n, dh // 2, 2)
            x1, x2 = (xr[..., 0], xr[..., 1])
            r1 = x1 * cos - x2 * sin
            r2 = x1 * sin + x2 * cos
            return jnp.stack([r1, r2], axis=-1).reshape(b, H, n, dh)

        def _block(x, ln1_g, ln1_b, ln2_g, ln2_b, Wqkv, Wo, W1, b1, W2, b2):
            b, n, d = x.shape
            H, dh = (N_HEADS, D_HEAD)
            h = _layernorm(x, ln1_g, ln1_b)
            qkv = (h @ Wqkv).reshape(b, n, 3, H, dh)
            q = jnp.transpose(qkv[:, :, 0], (0, 2, 1, 3))
            k = jnp.transpose(qkv[:, :, 1], (0, 2, 1, 3))
            v = jnp.transpose(qkv[:, :, 2], (0, 2, 1, 3))
            inv_freq = BASE ** (-(jnp.arange(0, dh, 2, dtype=jnp.float32) / dh))
            theta = jnp.arange(n, dtype=jnp.float32)[:, None] * inv_freq[None, :]
            cos, sin = (jnp.cos(theta), jnp.sin(theta))
            q = _rotate(q, cos, sin)
            k = _rotate(k, cos, sin)
            s = jnp.einsum('bhqd,bhkd->bhqk', q, k) / math.sqrt(dh)
            causal = jnp.tril(jnp.ones((n, n), dtype=bool))
            s = jnp.where(causal, s, -jnp.inf)
            a = jax.nn.softmax(s, axis=-1)
            o = jnp.einsum('bhqk,bhkd->bqhd', a, v).reshape(b, n, d)
            x = x + o @ Wo
            h2 = _layernorm(x, ln2_g, ln2_b)
            f = jax.nn.gelu(h2 @ W1 + b1, approximate=False) @ W2 + b2
            return x + f
        key = jax.random.key(seed)
        ks = jax.random.split(key, 8)
        d, h = (D_MODEL, 4 * D_MODEL)
        s = 0.02
        return {'x': jax.random.normal(ks[0], (BATCH, SEQ, d), jnp.float32), 'ln1_g': jnp.ones((d,), jnp.float32), 'ln1_b': jnp.zeros((d,), jnp.float32), 'ln2_g': jnp.ones((d,), jnp.float32), 'ln2_b': jnp.zeros((d,), jnp.float32), 'Wqkv': jax.random.normal(ks[1], (d, 3 * d), jnp.float32) * s, 'Wo': jax.random.normal(ks[2], (d, d), jnp.float32) * s, 'W1': jax.random.normal(ks[3], (d, h), jnp.float32) * s, 'b1': jnp.zeros((h,), jnp.float32), 'W2': jax.random.normal(ks[4], (h, d), jnp.float32) * s, 'b2': jnp.zeros((d,), jnp.float32)}
    _L1_attn_all = _L1_attn_setup()
    _L1_attn_in = {k: v for k, v in _L1_attn_all.items() if k in ('ln1_g', 'ln1_b', 'ln2_g', 'ln2_b', 'Wqkv', 'Wo', 'W1', 'b1', 'W2', 'b2')}
    del _L1_attn_all

    def _L1_ffn_setup():
        import jax, jax.numpy as jnp
        import numpy as np
        DIM = 128
        NUM_EXPERTS = 8
        EXPERT_DIM = 384
        B, S = (1, 256)
        key = jax.random.key(seed)
        ks = jax.random.split(key, 7)
        sd = 0.02
        x = jax.random.normal(ks[0], (B, S, DIM), dtype=jnp.float32)
        Wr = jax.random.normal(ks[1], (DIM, NUM_EXPERTS), dtype=jnp.float32) * sd
        br = jnp.zeros((NUM_EXPERTS,), dtype=jnp.float32)
        W1 = jax.random.normal(ks[2], (NUM_EXPERTS, DIM, EXPERT_DIM), dtype=jnp.float32) * sd
        b1 = jnp.zeros((NUM_EXPERTS, EXPERT_DIM), dtype=jnp.float32)
        W2 = jax.random.normal(ks[3], (NUM_EXPERTS, EXPERT_DIM, DIM), dtype=jnp.float32) * sd
        b2 = jnp.zeros((NUM_EXPERTS, DIM), dtype=jnp.float32)
        return {'x': x, 'Wr': Wr, 'br': br, 'W1': W1, 'b1': b1, 'W2': W2, 'b2': b2}
    _L1_ffn_all = _L1_ffn_setup()
    _L1_ffn_in = {k: v for k, v in _L1_ffn_all.items() if k in ('Wr', 'br', 'W1', 'b1', 'W2', 'b2')}
    del _L1_ffn_all

    def _L2_xattn_setup():
        import jax, jax.numpy as jnp
        import numpy as np
        B, S, D, H = (2, 256, 128, 16)
        DK = D // H
        key = jax.random.key(seed)
        ks = jax.random.split(key, 12)
        std = 1.0 / np.sqrt(D)
        inp = {'query': jax.random.normal(ks[0], (B, S, D), jnp.float32), 'key': jax.random.normal(ks[1], (B, S, D), jnp.float32), 'value': jax.random.normal(ks[2], (B, S, D), jnp.float32), 'mask': jnp.tril(jnp.ones((S, S), jnp.int32))[None, None, :, :], 'Wq': jax.random.normal(ks[3], (D, D), jnp.float32) * std, 'bq': jax.random.normal(ks[4], (D,), jnp.float32) * std, 'Wk': jax.random.normal(ks[5], (D, D), jnp.float32) * std, 'bk': jax.random.normal(ks[6], (D,), jnp.float32) * std, 'Wv': jax.random.normal(ks[7], (D, D), jnp.float32) * std, 'bv': jax.random.normal(ks[8], (D,), jnp.float32) * std, 'Wo': jax.random.normal(ks[9], (D, D), jnp.float32) * std, 'bo': jax.random.normal(ks[10], (D,), jnp.float32) * std}
        return inp
    _L2_xattn_all = _L2_xattn_setup()
    _L2_xattn_in = {k: v for k, v in _L2_xattn_all.items() if k in ('Wq', 'bq', 'Wk', 'bk', 'Wv', 'bv', 'Wo', 'bo')}
    del _L2_xattn_all

    def _L2_attn_setup():
        import jax, jax.numpy as jnp
        import numpy as np
        BATCH, SEQ = (2, 256)
        D_MODEL, D_STATE, D_CONV, EXPAND = (128, 16, 4, 2)
        D_INNER = EXPAND * D_MODEL

        def _selective_scan(xc, delta, A, Bm, Cm):
            dA = jnp.exp(delta[..., None] * A)
            dBx = delta[..., None] * Bm[:, :, None, :] * xc[..., None]
            h0 = jnp.zeros((xc.shape[0], xc.shape[2], A.shape[1]), xc.dtype)

            def step(h, inp):
                dA_t, dBx_t, c_t = inp
                h = dA_t * h + dBx_t
                y = jnp.einsum('bdn,bn->bd', h, c_t)
                return (h, y)
            _, ys = jax.lax.scan(step, h0, (dA.swapaxes(0, 1), dBx.swapaxes(0, 1), Cm.swapaxes(0, 1)))
            return ys.swapaxes(0, 1)

        def _forward(x, W_in, conv_w, conv_b, W_xproj, w_dt, b_dt, A_log, D_param, W_out):
            xz = x @ W_in
            x_inner, z = jnp.split(xz, 2, axis=-1)
            xc = jax.lax.conv_general_dilated(x_inner.swapaxes(1, 2), conv_w, window_strides=(1,), padding=[(D_CONV - 1, 0)], dimension_numbers=('NCH', 'OIH', 'NCH'), feature_group_count=D_INNER) + conv_b[None, :, None]
            xc = jax.nn.silu(xc.swapaxes(1, 2))
            x_ssm = xc @ W_xproj
            delta_raw = x_ssm[..., :1]
            Bm = x_ssm[..., 1:1 + D_STATE]
            Cm = x_ssm[..., 1 + D_STATE:]
            delta = jax.nn.softplus(delta_raw * w_dt + b_dt)
            A = -jnp.exp(A_log)
            y = _selective_scan(xc, delta, A, Bm, Cm)
            y = y + xc * D_param
            y = y * jax.nn.silu(z)
            return y @ W_out
        key = jax.random.key(seed)
        ks = jax.random.split(key, 8)
        x = jax.random.normal(ks[0], (BATCH, SEQ, D_MODEL), jnp.float32)
        W_in = jax.random.normal(ks[1], (D_MODEL, 2 * D_INNER), jnp.float32) * D_MODEL ** (-0.5)
        conv_w = jax.random.normal(ks[2], (D_INNER, 1, D_CONV), jnp.float32) * D_CONV ** (-0.5)
        conv_b = jnp.zeros((D_INNER,), jnp.float32)
        W_xproj = jax.random.normal(ks[3], (D_INNER, 2 * D_STATE + 1), jnp.float32) * D_INNER ** (-0.5)
        w_dt = jax.random.normal(ks[4], (D_INNER,), jnp.float32)
        b_dt = jnp.zeros((D_INNER,), jnp.float32)
        A_log = jnp.log(jnp.tile(jnp.arange(1, D_STATE + 1, dtype=jnp.float32), (D_INNER, 1)))
        D_param = jnp.ones((D_INNER,), jnp.float32)
        W_out = jax.random.normal(ks[5], (D_INNER, D_MODEL), jnp.float32) * D_INNER ** (-0.5)
        return dict(x=x, W_in=W_in, conv_w=conv_w, conv_b=conv_b, W_xproj=W_xproj, w_dt=w_dt, b_dt=b_dt, A_log=A_log, D_param=D_param, W_out=W_out)
    _L2_attn_all = _L2_attn_setup()
    _L2_attn_in = {k: v for k, v in _L2_attn_all.items() if k in ('W_in', 'conv_w', 'conv_b', 'W_xproj', 'w_dt', 'b_dt', 'A_log', 'D_param', 'W_out')}
    del _L2_attn_all

    def _L2_ffn_setup():
        import jax, jax.numpy as jnp
        import numpy as np
        B, S, H, FF, E = (4, 512, 128, 512, 8)
        EPS = 1e-05
        key = jax.random.key(seed)
        ks = jax.random.split(key, 8)
        std = 0.02
        return {'x': jax.random.normal(ks[0], (B, S, H), jnp.float32), 'norm_weight': jnp.ones((H,), jnp.float32), 'router_w': jax.random.normal(ks[1], (E, H), jnp.float32) * std, 'router_b': jnp.zeros((E,), jnp.float32), 'fc1_w': jax.random.normal(ks[2], (E, FF, H), jnp.float32) * std, 'fc1_b': jnp.zeros((E, FF), jnp.float32), 'fc2_w': jax.random.normal(ks[3], (E, H, FF), jnp.float32) * std, 'fc2_b': jnp.zeros((E, H), jnp.float32)}
    _L2_ffn_all = _L2_ffn_setup()
    _L2_ffn_in = {k: v for k, v in _L2_ffn_all.items() if k in ('norm_weight', 'router_w', 'router_b', 'fc1_w', 'fc1_b', 'fc2_w', 'fc2_b')}
    del _L2_ffn_all

    def _L3_xattn_setup():
        import jax, jax.numpy as jnp
        import numpy as np
        H = 128
        B = 8
        L_CHAR = 256
        L_SUB = 128

        def _linear(x, W, b):
            return jnp.einsum('blh,oh->blo', x, W) + b

        def _interp_linear(x, out_len):
            L_in = x.shape[1]
            pos = (jnp.arange(out_len, dtype=x.dtype) + 0.5) * (L_in / out_len) - 0.5
            pos = jnp.clip(pos, 0.0, L_in - 1)
            lo = jnp.floor(pos).astype(jnp.int32)
            hi = jnp.minimum(lo + 1, L_in - 1)
            w = (pos - lo.astype(x.dtype))[None, :, None]
            return x[:, lo] * (1 - w) + x[:, hi] * w
        key = jax.random.key(seed)
        ks = jax.random.split(key, 18)
        s = 0.02
        inp = {'char_emb': jax.random.normal(ks[0], (B, L_CHAR, H), jnp.float32), 'subword_emb': jax.random.normal(ks[1], (B, L_SUB, H), jnp.float32)}
        names = ['Wq_c', 'Wk_s', 'Wv_s', 'Wq_s', 'Wk_c', 'Wv_c']
        for i, n in enumerate(names):
            inp[n] = jax.random.normal(ks[2 + 2 * i], (H, H), jnp.float32) * s
            inp['b' + n[1:]] = jax.random.normal(ks[3 + 2 * i], (H,), jnp.float32) * s
        inp['Wg'] = jax.random.normal(ks[14], (H, 2 * H), jnp.float32) * s
        inp['bg'] = jax.random.normal(ks[15], (H,), jnp.float32) * s
        return inp
    _L3_xattn_all = _L3_xattn_setup()
    _L3_xattn_in = {k: v for k, v in _L3_xattn_all.items() if k in ('Wq_c', 'bq_c', 'Wk_s', 'bk_s', 'Wv_s', 'bv_s', 'Wq_s', 'bq_s', 'Wk_c', 'bk_c', 'Wv_c', 'bv_c', 'Wg', 'bg')}
    del _L3_xattn_all

    def _L3_attn_setup():
        import jax, jax.numpy as jnp
        import numpy as np
        import math
        DIM = 128
        NUM_HEADS = 16
        HEAD_DIM = DIM // NUM_HEADS
        LOGIT_SCALE_MAX = math.log(1.0 / 0.01)
        EPS = 1e-12

        def _l2_normalize(t):
            n = jnp.sqrt(jnp.sum(t * t, axis=-1, keepdims=True))
            return t / jnp.maximum(n, EPS)
        key = jax.random.key(seed)
        ks = jax.random.split(key, 4)
        L, N, C = (128, 8, DIM)
        scale = HEAD_DIM ** (-0.5)
        x = jax.random.normal(ks[0], (L, N, C), dtype=jnp.float32)
        in_proj_weight = jax.random.normal(ks[1], (3 * C, C), dtype=jnp.float32) * scale
        in_proj_bias = jnp.zeros((3 * C,), dtype=jnp.float32)
        logit_scale = jnp.full((NUM_HEADS, 1, 1), math.log(10.0), dtype=jnp.float32)
        head_scale = jnp.ones((NUM_HEADS, 1, 1), dtype=jnp.float32)
        out_w = jax.random.normal(ks[2], (C, C), dtype=jnp.float32) * C ** (-0.5)
        out_b = jax.random.normal(ks[3], (C,), dtype=jnp.float32) * 0.01
        return {'x': x, 'in_proj_weight': in_proj_weight, 'in_proj_bias': in_proj_bias, 'logit_scale': logit_scale, 'head_scale': head_scale, 'out_w': out_w, 'out_b': out_b}
    _L3_attn_all = _L3_attn_setup()
    _L3_attn_in = {k: v for k, v in _L3_attn_all.items() if k in ('in_proj_weight', 'in_proj_bias', 'logit_scale', 'head_scale', 'out_w', 'out_b')}
    del _L3_attn_all

    def _L3_ffn_setup():
        import jax, jax.numpy as jnp
        import numpy as np
        TOP_K = 2
        key = jax.random.key(seed)
        ks = jax.random.split(key, 6)
        B, S, D, BN, E = (32, 256, 128, 64, 8)
        return {'x': jax.random.normal(ks[0], (B, S, D), dtype=jnp.float32), 'gate_w': jax.random.normal(ks[1], (E, D), dtype=jnp.float32) * 0.02, 'down_w': jax.random.normal(ks[2], (E, BN, D), dtype=jnp.float32) * 0.02, 'down_b': jax.random.normal(ks[3], (E, BN), dtype=jnp.float32) * 0.02, 'up_w': jax.random.normal(ks[4], (E, D, BN), dtype=jnp.float32) * 0.02, 'up_b': jax.random.normal(ks[5], (E, D), dtype=jnp.float32) * 0.02}
    _L3_ffn_all = _L3_ffn_setup()
    _L3_ffn_in = {k: v for k, v in _L3_ffn_all.items() if k in ('gate_w', 'down_w', 'down_b', 'up_w', 'up_b')}
    del _L3_ffn_all
    return {'x': x, 'ctx_1024': ctx_1024, 'mask_BxS2_if1': mask_BxS2_if1, 'mask_1x1xSxS2_ik0': mask_1x1xSxS2_ik0, 'L0_xattn_Wq': _L0_xattn_in['Wq'], 'L0_xattn_Wk': _L0_xattn_in['Wk'], 'L0_xattn_Wv': _L0_xattn_in['Wv'], 'L0_xattn_Wo': _L0_xattn_in['Wo'], 'L0_attn_Wq': _L0_attn_in['Wq'], 'L0_attn_Wkv': _L0_attn_in['Wkv'], 'L0_attn_Wo': _L0_attn_in['Wo'], 'L0_attn_norm_w': _L0_attn_in['norm_w'], 'L0_attn_norm_b': _L0_attn_in['norm_b'], 'L0_attn_out_norm_w': _L0_attn_in['out_norm_w'], 'L0_attn_out_norm_b': _L0_attn_in['out_norm_b'], 'L0_ffn_router_w': _L0_ffn_in['router_w'], 'L0_ffn_router_b': _L0_ffn_in['router_b'], 'L0_ffn_expert_w': _L0_ffn_in['expert_w'], 'L0_ffn_expert_b': _L0_ffn_in['expert_b'], 'L1_xattn_Wq': _L1_xattn_in['Wq'], 'L1_xattn_Wk': _L1_xattn_in['Wk'], 'L1_xattn_Wv': _L1_xattn_in['Wv'], 'L1_xattn_Wp': _L1_xattn_in['Wp'], 'L1_xattn_bp': _L1_xattn_in['bp'], 'L1_xattn_ln_g': _L1_xattn_in['ln_g'], 'L1_xattn_ln_b': _L1_xattn_in['ln_b'], 'L1_attn_ln1_g': _L1_attn_in['ln1_g'], 'L1_attn_ln1_b': _L1_attn_in['ln1_b'], 'L1_attn_ln2_g': _L1_attn_in['ln2_g'], 'L1_attn_ln2_b': _L1_attn_in['ln2_b'], 'L1_attn_Wqkv': _L1_attn_in['Wqkv'], 'L1_attn_Wo': _L1_attn_in['Wo'], 'L1_attn_W1': _L1_attn_in['W1'], 'L1_attn_b1': _L1_attn_in['b1'], 'L1_attn_W2': _L1_attn_in['W2'], 'L1_attn_b2': _L1_attn_in['b2'], 'L1_ffn_Wr': _L1_ffn_in['Wr'], 'L1_ffn_br': _L1_ffn_in['br'], 'L1_ffn_W1': _L1_ffn_in['W1'], 'L1_ffn_b1': _L1_ffn_in['b1'], 'L1_ffn_W2': _L1_ffn_in['W2'], 'L1_ffn_b2': _L1_ffn_in['b2'], 'L2_xattn_Wq': _L2_xattn_in['Wq'], 'L2_xattn_bq': _L2_xattn_in['bq'], 'L2_xattn_Wk': _L2_xattn_in['Wk'], 'L2_xattn_bk': _L2_xattn_in['bk'], 'L2_xattn_Wv': _L2_xattn_in['Wv'], 'L2_xattn_bv': _L2_xattn_in['bv'], 'L2_xattn_Wo': _L2_xattn_in['Wo'], 'L2_xattn_bo': _L2_xattn_in['bo'], 'L2_attn_W_in': _L2_attn_in['W_in'], 'L2_attn_conv_w': _L2_attn_in['conv_w'], 'L2_attn_conv_b': _L2_attn_in['conv_b'], 'L2_attn_W_xproj': _L2_attn_in['W_xproj'], 'L2_attn_w_dt': _L2_attn_in['w_dt'], 'L2_attn_b_dt': _L2_attn_in['b_dt'], 'L2_attn_A_log': _L2_attn_in['A_log'], 'L2_attn_D_param': _L2_attn_in['D_param'], 'L2_attn_W_out': _L2_attn_in['W_out'], 'L2_ffn_norm_weight': _L2_ffn_in['norm_weight'], 'L2_ffn_router_w': _L2_ffn_in['router_w'], 'L2_ffn_router_b': _L2_ffn_in['router_b'], 'L2_ffn_fc1_w': _L2_ffn_in['fc1_w'], 'L2_ffn_fc1_b': _L2_ffn_in['fc1_b'], 'L2_ffn_fc2_w': _L2_ffn_in['fc2_w'], 'L2_ffn_fc2_b': _L2_ffn_in['fc2_b'], 'L3_xattn_Wq_c': _L3_xattn_in['Wq_c'], 'L3_xattn_bq_c': _L3_xattn_in['bq_c'], 'L3_xattn_Wk_s': _L3_xattn_in['Wk_s'], 'L3_xattn_bk_s': _L3_xattn_in['bk_s'], 'L3_xattn_Wv_s': _L3_xattn_in['Wv_s'], 'L3_xattn_bv_s': _L3_xattn_in['bv_s'], 'L3_xattn_Wq_s': _L3_xattn_in['Wq_s'], 'L3_xattn_bq_s': _L3_xattn_in['bq_s'], 'L3_xattn_Wk_c': _L3_xattn_in['Wk_c'], 'L3_xattn_bk_c': _L3_xattn_in['bk_c'], 'L3_xattn_Wv_c': _L3_xattn_in['Wv_c'], 'L3_xattn_bv_c': _L3_xattn_in['bv_c'], 'L3_xattn_Wg': _L3_xattn_in['Wg'], 'L3_xattn_bg': _L3_xattn_in['bg'], 'L3_attn_in_proj_weight': _L3_attn_in['in_proj_weight'], 'L3_attn_in_proj_bias': _L3_attn_in['in_proj_bias'], 'L3_attn_logit_scale': _L3_attn_in['logit_scale'], 'L3_attn_head_scale': _L3_attn_in['head_scale'], 'L3_attn_out_w': _L3_attn_in['out_w'], 'L3_attn_out_b': _L3_attn_in['out_b'], 'L3_ffn_gate_w': _L3_ffn_in['gate_w'], 'L3_ffn_down_w': _L3_ffn_in['down_w'], 'L3_ffn_down_b': _L3_ffn_in['down_b'], 'L3_ffn_up_w': _L3_ffn_in['up_w'], 'L3_ffn_up_b': _L3_ffn_in['up_b']}

def reference(x, ctx_1024, mask_BxS2_if1, mask_1x1xSxS2_ik0, L0_xattn_Wq, L0_xattn_Wk, L0_xattn_Wv, L0_xattn_Wo, L0_attn_Wq, L0_attn_Wkv, L0_attn_Wo, L0_attn_norm_w, L0_attn_norm_b, L0_attn_out_norm_w, L0_attn_out_norm_b, L0_ffn_router_w, L0_ffn_router_b, L0_ffn_expert_w, L0_ffn_expert_b, L1_xattn_Wq, L1_xattn_Wk, L1_xattn_Wv, L1_xattn_Wp, L1_xattn_bp, L1_xattn_ln_g, L1_xattn_ln_b, L1_attn_ln1_g, L1_attn_ln1_b, L1_attn_ln2_g, L1_attn_ln2_b, L1_attn_Wqkv, L1_attn_Wo, L1_attn_W1, L1_attn_b1, L1_attn_W2, L1_attn_b2, L1_ffn_Wr, L1_ffn_br, L1_ffn_W1, L1_ffn_b1, L1_ffn_W2, L1_ffn_b2, L2_xattn_Wq, L2_xattn_bq, L2_xattn_Wk, L2_xattn_bk, L2_xattn_Wv, L2_xattn_bv, L2_xattn_Wo, L2_xattn_bo, L2_attn_W_in, L2_attn_conv_w, L2_attn_conv_b, L2_attn_W_xproj, L2_attn_w_dt, L2_attn_b_dt, L2_attn_A_log, L2_attn_D_param, L2_attn_W_out, L2_ffn_norm_weight, L2_ffn_router_w, L2_ffn_router_b, L2_ffn_fc1_w, L2_ffn_fc1_b, L2_ffn_fc2_w, L2_ffn_fc2_b, L3_xattn_Wq_c, L3_xattn_bq_c, L3_xattn_Wk_s, L3_xattn_bk_s, L3_xattn_Wv_s, L3_xattn_bv_s, L3_xattn_Wq_s, L3_xattn_bq_s, L3_xattn_Wk_c, L3_xattn_bk_c, L3_xattn_Wv_c, L3_xattn_bv_c, L3_xattn_Wg, L3_xattn_bg, L3_attn_in_proj_weight, L3_attn_in_proj_bias, L3_attn_logit_scale, L3_attn_head_scale, L3_attn_out_w, L3_attn_out_b, L3_ffn_gate_w, L3_ffn_down_w, L3_ffn_down_b, L3_ffn_up_w, L3_ffn_up_b):
    import jax
    import jax.numpy as jnp

    def _L0_xattn_ref(q, k, v, mask, Wq, Wk, Wv, Wo):
        import jax, jax.numpy as jnp
        import numpy as np
        D_MODEL = 128
        NUM_HEADS = 16
        D_K = D_MODEL // NUM_HEADS
        NEG = -1000000000.0

        def _split_heads(x, B):
            return x.reshape(B, -1, NUM_HEADS, D_K).transpose(0, 2, 1, 3)
        B = q.shape[0]
        qh = _split_heads(q @ Wq.T, B)
        kh = _split_heads(k @ Wk.T, B)
        vh = _split_heads(v @ Wv.T, B)
        scores = jnp.einsum('bhqd,bhkd->bhqk', qh, kh) / jnp.sqrt(jnp.float32(D_K))
        Sq, Sk = (scores.shape[-2], scores.shape[-1])
        causal = jnp.triu(jnp.ones((Sq, Sk), dtype=bool), k=1)
        scores = jnp.where(causal[None, None], NEG, scores)
        pad = mask[:, None, None, :] == 0
        scores = jnp.where(pad, NEG, scores)
        weights = jax.nn.softmax(scores, axis=-1)
        out = jnp.einsum('bhqk,bhkd->bhqd', weights, vh)
        out = out.transpose(0, 2, 1, 3).reshape(B, -1, D_MODEL)
        return out @ Wo.T

    def _L0_attn_ref(x, Wq, Wkv, Wo, norm_w, norm_b, out_norm_w, out_norm_b):
        import jax, jax.numpy as jnp
        import numpy as np
        DIM = 128
        DIM_HEAD = 64
        HEADS = 8
        INNER = DIM_HEAD * HEADS
        SCALE = DIM_HEAD ** (-0.5)
        COS_SCALE = 1.0

        def layer_norm(x, w, b, eps=1e-05):
            mu = jnp.mean(x, axis=-1, keepdims=True)
            var = jnp.var(x, axis=-1, keepdims=True)
            return (x - mu) * jax.lax.rsqrt(var + eps) * w + b
        b, n, _ = x.shape
        xn = layer_norm(x, norm_w, norm_b)
        q = xn @ Wq
        kv = xn @ Wkv
        k, v = (kv[..., :DIM_HEAD], kv[..., DIM_HEAD:])
        q = q.reshape(b, n, HEADS, DIM_HEAD).transpose(0, 2, 1, 3) * SCALE
        sim = jnp.einsum('bhid,bjd->bhij', q, k) * COS_SCALE
        attn = jax.nn.softmax(sim.astype(jnp.float32), axis=-1).astype(sim.dtype)
        out = jnp.einsum('bhij,bjd->bhid', attn, v)
        out = out.transpose(0, 2, 1, 3).reshape(b, n, INNER)
        out = out @ Wo
        return layer_norm(out, out_norm_w, out_norm_b)

    def _L0_ffn_ref(x, router_w, router_b, expert_w, expert_b):
        import jax, jax.numpy as jnp
        import numpy as np
        B, S, H, E = (4, 256, 128, 8)
        b, s, h = x.shape
        xt = x.reshape(b * s, h)
        logits = xt @ router_w + router_b
        probs = jax.nn.softmax(logits, axis=-1)
        gate = jnp.max(probs, axis=-1)
        idx = jnp.argmax(probs, axis=-1)
        out_all = jnp.einsum('th,ehd->ted', xt, expert_w) + expert_b[None, :, :]
        e_out = jnp.take_along_axis(out_all, idx[:, None, None], axis=1)[:, 0, :]
        y = gate[:, None] * e_out
        return y.reshape(b, s, h)

    def _L1_xattn_ref(x1, x2, Wq, Wk, Wv, Wp, bp, ln_g, ln_b):
        import jax, jax.numpy as jnp
        import numpy as np
        NUM_HEADS = 16
        D_MODEL = 128
        HEAD_DIM = D_MODEL // NUM_HEADS
        SCALE = 8.0 / HEAD_DIM
        LN_EPS = 1e-05

        def _layernorm(x, g, b):
            mu = jnp.mean(x, axis=-1, keepdims=True)
            var = jnp.mean(jnp.square(x - mu), axis=-1, keepdims=True)
            return (x - mu) * jax.lax.rsqrt(var + LN_EPS) * g + b
        B, N, C = x1.shape
        M = x2.shape[1]
        H, D = (NUM_HEADS, HEAD_DIM)
        q = (x1 @ Wq.T).reshape(B, N, H, D).transpose(0, 2, 1, 3)
        k = (x2 @ Wk.T).reshape(B, M, H, D).transpose(0, 2, 1, 3)
        v = (x2 @ Wv.T).reshape(B, M, H, D).transpose(0, 2, 1, 3)
        q = _layernorm(q, ln_g, ln_b)
        k = _layernorm(k, ln_g, ln_b)
        q = q * SCALE
        attn = jnp.einsum('bhnd,bhmd->bhnm', q, k)
        attn = jax.nn.softmax(attn, axis=-1)
        out = jnp.einsum('bhnm,bhmd->bhnd', attn, v)
        out = out.transpose(0, 2, 1, 3).reshape(B, N, C)
        return out @ Wp.T + bp

    def _L1_attn_ref(x, ln1_g, ln1_b, ln2_g, ln2_b, Wqkv, Wo, W1, b1, W2, b2):
        import math
        import jax, jax.numpy as jnp
        import numpy as np
        D_MODEL = 128
        N_HEADS = 16
        D_HEAD = D_MODEL // N_HEADS
        SEQ = 512
        BATCH = 1
        BASE = 10000.0
        EPS = 1e-05

        def _layernorm(x, g, b):
            mu = jnp.mean(x, axis=-1, keepdims=True)
            var = jnp.mean(jnp.square(x - mu), axis=-1, keepdims=True)
            return (x - mu) * jax.lax.rsqrt(var + EPS) * g + b

        def _rotate(x, cos, sin):
            b, H, n, dh = x.shape
            xr = x.reshape(b, H, n, dh // 2, 2)
            x1, x2 = (xr[..., 0], xr[..., 1])
            r1 = x1 * cos - x2 * sin
            r2 = x1 * sin + x2 * cos
            return jnp.stack([r1, r2], axis=-1).reshape(b, H, n, dh)

        def _block(x, ln1_g, ln1_b, ln2_g, ln2_b, Wqkv, Wo, W1, b1, W2, b2):
            b, n, d = x.shape
            H, dh = (N_HEADS, D_HEAD)
            h = _layernorm(x, ln1_g, ln1_b)
            qkv = (h @ Wqkv).reshape(b, n, 3, H, dh)
            q = jnp.transpose(qkv[:, :, 0], (0, 2, 1, 3))
            k = jnp.transpose(qkv[:, :, 1], (0, 2, 1, 3))
            v = jnp.transpose(qkv[:, :, 2], (0, 2, 1, 3))
            inv_freq = BASE ** (-(jnp.arange(0, dh, 2, dtype=jnp.float32) / dh))
            theta = jnp.arange(n, dtype=jnp.float32)[:, None] * inv_freq[None, :]
            cos, sin = (jnp.cos(theta), jnp.sin(theta))
            q = _rotate(q, cos, sin)
            k = _rotate(k, cos, sin)
            s = jnp.einsum('bhqd,bhkd->bhqk', q, k) / math.sqrt(dh)
            causal = jnp.tril(jnp.ones((n, n), dtype=bool))
            s = jnp.where(causal, s, -jnp.inf)
            a = jax.nn.softmax(s, axis=-1)
            o = jnp.einsum('bhqk,bhkd->bqhd', a, v).reshape(b, n, d)
            x = x + o @ Wo
            h2 = _layernorm(x, ln2_g, ln2_b)
            f = jax.nn.gelu(h2 @ W1 + b1, approximate=False) @ W2 + b2
            return x + f
        return _block(x, ln1_g, ln1_b, ln2_g, ln2_b, Wqkv, Wo, W1, b1, W2, b2)

    def _L1_ffn_ref(x, Wr, br, W1, b1, W2, b2):
        import jax, jax.numpy as jnp
        import numpy as np
        DIM = 128
        NUM_EXPERTS = 8
        EXPERT_DIM = 384
        B, S = (1, 256)
        router_logits = x @ Wr + br
        expert_idx = jnp.argmax(router_logits, axis=-1)
        onehot = jax.nn.one_hot(expert_idx, NUM_EXPERTS, dtype=x.dtype)
        h = jax.nn.gelu(jnp.einsum('bsd,edh->bseh', x, W1) + b1, approximate=False)
        y = jnp.einsum('bseh,ehd->bsed', h, W2) + b2
        out = jnp.einsum('bsed,bse->bsd', y, onehot)
        return out

    def _L2_xattn_ref(query, key, value, mask, Wq, bq, Wk, bk, Wv, bv, Wo, bo):
        import jax, jax.numpy as jnp
        import numpy as np
        B, S, D, H = (2, 256, 128, 16)
        DK = D // H
        b = query.shape[0]
        Q = query @ Wq.T + bq
        K = key @ Wk.T + bk
        V = value @ Wv.T + bv
        Q = Q.reshape(b, -1, H, DK).transpose(0, 2, 1, 3)
        K = K.reshape(b, -1, H, DK).transpose(0, 2, 1, 3)
        V = V.reshape(b, -1, H, DK).transpose(0, 2, 1, 3)
        scores = jnp.einsum('bhqd,bhkd->bhqk', Q, K) / jnp.sqrt(jnp.float32(DK))
        scores = jnp.where(mask == 0, -jnp.inf, scores)
        weights = jax.nn.softmax(scores, axis=-1)
        attn = jnp.einsum('bhqk,bhkd->bhqd', weights, V)
        attn = attn.transpose(0, 2, 1, 3).reshape(b, -1, D)
        return attn @ Wo.T + bo

    def _L2_attn_ref(x, W_in, conv_w, conv_b, W_xproj, w_dt, b_dt, A_log, D_param, W_out):
        import jax, jax.numpy as jnp
        import numpy as np
        BATCH, SEQ = (2, 256)
        D_MODEL, D_STATE, D_CONV, EXPAND = (128, 16, 4, 2)
        D_INNER = EXPAND * D_MODEL

        def _selective_scan(xc, delta, A, Bm, Cm):
            dA = jnp.exp(delta[..., None] * A)
            dBx = delta[..., None] * Bm[:, :, None, :] * xc[..., None]
            h0 = jnp.zeros((xc.shape[0], xc.shape[2], A.shape[1]), xc.dtype)

            def step(h, inp):
                dA_t, dBx_t, c_t = inp
                h = dA_t * h + dBx_t
                y = jnp.einsum('bdn,bn->bd', h, c_t)
                return (h, y)
            _, ys = jax.lax.scan(step, h0, (dA.swapaxes(0, 1), dBx.swapaxes(0, 1), Cm.swapaxes(0, 1)))
            return ys.swapaxes(0, 1)

        def _forward(x, W_in, conv_w, conv_b, W_xproj, w_dt, b_dt, A_log, D_param, W_out):
            xz = x @ W_in
            x_inner, z = jnp.split(xz, 2, axis=-1)
            xc = jax.lax.conv_general_dilated(x_inner.swapaxes(1, 2), conv_w, window_strides=(1,), padding=[(D_CONV - 1, 0)], dimension_numbers=('NCH', 'OIH', 'NCH'), feature_group_count=D_INNER) + conv_b[None, :, None]
            xc = jax.nn.silu(xc.swapaxes(1, 2))
            x_ssm = xc @ W_xproj
            delta_raw = x_ssm[..., :1]
            Bm = x_ssm[..., 1:1 + D_STATE]
            Cm = x_ssm[..., 1 + D_STATE:]
            delta = jax.nn.softplus(delta_raw * w_dt + b_dt)
            A = -jnp.exp(A_log)
            y = _selective_scan(xc, delta, A, Bm, Cm)
            y = y + xc * D_param
            y = y * jax.nn.silu(z)
            return y @ W_out
        return _forward(x, W_in, conv_w, conv_b, W_xproj, w_dt, b_dt, A_log, D_param, W_out)

    def _L2_ffn_ref(x, norm_weight, router_w, router_b, fc1_w, fc1_b, fc2_w, fc2_b):
        import jax, jax.numpy as jnp
        import numpy as np
        B, S, H, FF, E = (4, 512, 128, 512, 8)
        EPS = 1e-05
        b, s, h = x.shape
        T = b * s
        e = router_w.shape[0]
        cap = T // e
        x_flat = x.reshape(T, h)
        xn = x_flat * jax.lax.rsqrt(jnp.mean(x_flat * x_flat, axis=-1, keepdims=True) + EPS) * norm_weight
        logits = xn @ router_w.T + router_b
        probs = jax.nn.softmax(logits, axis=-1)
        gates, idx = jax.lax.top_k(probs.T, cap)
        xe = xn[idx]
        hmid = jnp.einsum('ech,efh->ecf', xe, fc1_w) + fc1_b[:, None, :]
        hmid = jax.nn.gelu(hmid, approximate=False)
        ye = jnp.einsum('ecf,ehf->ech', hmid, fc2_w) + fc2_b[:, None, :]
        flat_idx = idx.reshape(-1)
        weighted = (ye * gates[..., None]).reshape(-1, h)
        out = jnp.zeros((T, h), x.dtype).at[flat_idx].add(weighted)
        gate_sums = jnp.zeros((T, 1), x.dtype).at[flat_idx].add(gates.reshape(-1, 1))
        out = out / jnp.maximum(gate_sums, 1e-09)
        return out.reshape(b, s, h)

    def _L3_xattn_ref(char_emb, subword_emb, Wq_c, bq_c, Wk_s, bk_s, Wv_s, bv_s, Wq_s, bq_s, Wk_c, bk_c, Wv_c, bv_c, Wg, bg):
        import jax, jax.numpy as jnp
        import numpy as np
        H = 128
        B = 8
        L_CHAR = 256
        L_SUB = 128

        def _linear(x, W, b):
            return jnp.einsum('blh,oh->blo', x, W) + b

        def _interp_linear(x, out_len):
            L_in = x.shape[1]
            pos = (jnp.arange(out_len, dtype=x.dtype) + 0.5) * (L_in / out_len) - 0.5
            pos = jnp.clip(pos, 0.0, L_in - 1)
            lo = jnp.floor(pos).astype(jnp.int32)
            hi = jnp.minimum(lo + 1, L_in - 1)
            w = (pos - lo.astype(x.dtype))[None, :, None]
            return x[:, lo] * (1 - w) + x[:, hi] * w
        h = char_emb.shape[-1]
        scale = 1.0 / jnp.sqrt(jnp.asarray(h, char_emb.dtype))
        Q_char = _linear(char_emb, Wq_c, bq_c)
        K_sub = _linear(subword_emb, Wk_s, bk_s)
        V_sub = _linear(subword_emb, Wv_s, bv_s)
        scores = jnp.einsum('bqh,bkh->bqk', Q_char, K_sub) * scale
        char2sub = jnp.einsum('bqk,bkh->bqh', jax.nn.softmax(scores, axis=-1), V_sub)
        Q_sub = _linear(subword_emb, Wq_s, bq_s)
        K_char = _linear(char_emb, Wk_c, bk_c)
        V_char = _linear(char_emb, Wv_c, bv_c)
        scores2 = jnp.einsum('bqh,bkh->bqk', Q_sub, K_char) * scale
        sub2char = jnp.einsum('bqk,bkh->bqh', jax.nn.softmax(scores2, axis=-1), V_char)
        L_char = char_emb.shape[1]
        if sub2char.shape[1] != L_char:
            sub2char = _interp_linear(sub2char, L_char)
        gate_in = jnp.concatenate([char2sub, sub2char], axis=-1)
        gate = jax.nn.sigmoid(jnp.einsum('blh,oh->blo', gate_in, Wg) + bg)
        return gate * char2sub + (1 - gate) * sub2char

    def _L3_attn_ref(x, in_proj_weight, in_proj_bias, logit_scale, head_scale, out_w, out_b):
        import jax, jax.numpy as jnp
        import numpy as np
        import math
        DIM = 128
        NUM_HEADS = 16
        HEAD_DIM = DIM // NUM_HEADS
        LOGIT_SCALE_MAX = math.log(1.0 / 0.01)
        EPS = 1e-12

        def _l2_normalize(t):
            n = jnp.sqrt(jnp.sum(t * t, axis=-1, keepdims=True))
            return t / jnp.maximum(n, EPS)
        L, N, C = x.shape
        H, hd = (NUM_HEADS, HEAD_DIM)
        qkv = x @ in_proj_weight.T + in_proj_bias
        q, k, v = jnp.split(qkv, 3, axis=-1)

        def to_heads(t):
            return t.reshape(L, N, H, hd).transpose(1, 2, 0, 3)
        q, k, v = (to_heads(q), to_heads(k), to_heads(v))
        ls = jnp.exp(jnp.minimum(logit_scale, LOGIT_SCALE_MAX))
        attn = jnp.einsum('nhld,nhmd->nhlm', _l2_normalize(q), _l2_normalize(k)) * ls
        attn = jax.nn.softmax(attn, axis=-1)
        o = jnp.einsum('nhlm,nhmd->nhld', attn, v)
        o = o * head_scale
        o = o.transpose(2, 0, 1, 3).reshape(L, N, C)
        return o @ out_w.T + out_b

    def _L3_ffn_ref(x, gate_w, down_w, down_b, up_w, up_b):
        import jax, jax.numpy as jnp
        import numpy as np
        TOP_K = 2
        pooled = x.mean(axis=1)
        gate = jax.nn.softmax(pooled @ gate_w.T, axis=-1)
        top_w, top_i = jax.lax.top_k(gate, TOP_K)
        top_w = top_w / (top_w.sum(axis=-1, keepdims=True) + 1e-08)
        Wd = down_w[top_i]
        bd = down_b[top_i]
        Wu = up_w[top_i]
        bu = up_b[top_i]
        h = jax.nn.gelu(jnp.einsum('bsd,bkcd->bksc', x, Wd) + bd[:, :, None, :], approximate=False)
        h = h * top_w[:, :, None, None]
        out = jnp.einsum('bksc,bkdc->bsd', h, Wu)
        out = out + (top_w[:, :, None] * bu).sum(axis=1)[:, None, :]
        return out
    x = x + _L0_xattn_ref(_layernorm(x, axis=-1), ctx_1024, ctx_1024, mask_BxS2_if1, L0_xattn_Wq, L0_xattn_Wk, L0_xattn_Wv, L0_xattn_Wo)
    x = x + _L0_attn_ref(_layernorm(x, axis=-1), L0_attn_Wq, L0_attn_Wkv, L0_attn_Wo, L0_attn_norm_w, L0_attn_norm_b, L0_attn_out_norm_w, L0_attn_out_norm_b)
    x = x + _L0_ffn_ref(_layernorm(x, axis=-1), L0_ffn_router_w, L0_ffn_router_b, L0_ffn_expert_w, L0_ffn_expert_b)
    x = x + _L1_xattn_ref(_layernorm(x, axis=-1), ctx_1024, L1_xattn_Wq, L1_xattn_Wk, L1_xattn_Wv, L1_xattn_Wp, L1_xattn_bp, L1_xattn_ln_g, L1_xattn_ln_b)
    x = x + _L1_attn_ref(_layernorm(x, axis=-1), L1_attn_ln1_g, L1_attn_ln1_b, L1_attn_ln2_g, L1_attn_ln2_b, L1_attn_Wqkv, L1_attn_Wo, L1_attn_W1, L1_attn_b1, L1_attn_W2, L1_attn_b2)
    x = x + _L1_ffn_ref(_layernorm(x, axis=-1), L1_ffn_Wr, L1_ffn_br, L1_ffn_W1, L1_ffn_b1, L1_ffn_W2, L1_ffn_b2)
    x = x + _L2_xattn_ref(_layernorm(x, axis=-1), ctx_1024, ctx_1024, mask_1x1xSxS2_ik0, L2_xattn_Wq, L2_xattn_bq, L2_xattn_Wk, L2_xattn_bk, L2_xattn_Wv, L2_xattn_bv, L2_xattn_Wo, L2_xattn_bo)
    x = x + _L2_attn_ref(_layernorm(x, axis=-1), L2_attn_W_in, L2_attn_conv_w, L2_attn_conv_b, L2_attn_W_xproj, L2_attn_w_dt, L2_attn_b_dt, L2_attn_A_log, L2_attn_D_param, L2_attn_W_out)
    x = x + _L2_ffn_ref(_layernorm(x, axis=-1), L2_ffn_norm_weight, L2_ffn_router_w, L2_ffn_router_b, L2_ffn_fc1_w, L2_ffn_fc1_b, L2_ffn_fc2_w, L2_ffn_fc2_b)
    x = x + _L3_xattn_ref(_layernorm(x, axis=-1), ctx_1024, L3_xattn_Wq_c, L3_xattn_bq_c, L3_xattn_Wk_s, L3_xattn_bk_s, L3_xattn_Wv_s, L3_xattn_bv_s, L3_xattn_Wq_s, L3_xattn_bq_s, L3_xattn_Wk_c, L3_xattn_bk_c, L3_xattn_Wv_c, L3_xattn_bv_c, L3_xattn_Wg, L3_xattn_bg)
    x = x + _L3_attn_ref(_layernorm(x, axis=-1), L3_attn_in_proj_weight, L3_attn_in_proj_bias, L3_attn_logit_scale, L3_attn_head_scale, L3_attn_out_w, L3_attn_out_b)
    x = x + _L3_ffn_ref(_layernorm(x, axis=-1), L3_ffn_gate_w, L3_ffn_down_w, L3_ffn_down_b, L3_ffn_up_w, L3_ffn_up_b)
    return x

_drawn_inputs = setup_inputs


def setup_inputs(seed=0):
    import zlib

    import numpy as np

    out = dict(_drawn_inputs(seed))
    spreads = {'L0_attn_norm_w': (1.0, 0.2),
     'L0_attn_norm_b': (0.0, 0.1),
     'L0_attn_out_norm_w': (1.0, 0.2),
     'L0_attn_out_norm_b': (0.0, 0.1),
     'L0_ffn_router_b': (0.0, 0.1),
     'L0_ffn_expert_b': (0.0, 0.1),
     'L1_xattn_bp': (0.0, 0.1),
     'L1_xattn_ln_g': (1.0, 0.2),
     'L1_xattn_ln_b': (0.0, 0.1),
     'L1_attn_ln1_g': (1.0, 0.6),
     'L1_attn_ln1_b': (0.0, 0.8),
     'L1_attn_ln2_g': (1.0, 0.6),
     'L1_attn_ln2_b': (0.0, 0.8),
     'L1_attn_b1': (0.0, 0.301),
     'L1_attn_b2': (0.0, 0.1),
     'L1_ffn_br': (0.0, 0.1),
     'L1_ffn_b1': (0.0, 0.381),
     'L1_ffn_b2': (0.0, 0.1),
     'L2_attn_conv_b': (0.0, 0.1),
     'L2_attn_b_dt': (0.0, 0.395),
     'L2_attn_D_param': (1.0, 0.2),
     'L2_ffn_norm_weight': (1.0, 0.2),
     'L2_ffn_router_b': (0.0, 0.664),
     'L2_ffn_fc1_b': (0.0, 0.502),
     'L2_ffn_fc2_b': (0.0, 0.1),
     'L3_attn_in_proj_bias': (0.0, 0.1),
     'L3_attn_logit_scale': (2.3025851249694824, 0.2),
     'L3_attn_head_scale': (1.0, 0.2)}
    factors = {'L2_xattn_bk': 200.0,
     'L3_xattn_Wq_c': 8.0,
     'L3_xattn_bq_c': 22.394,
     'L3_xattn_Wk_s': 8.0,
     'L3_xattn_bk_s': 200.0,
     'L3_xattn_bv_s': 6.258,
     'L3_xattn_Wq_s': 8.0,
     'L3_xattn_bq_s': 64.0,
     'L3_xattn_Wk_c': 8.0,
     'L3_xattn_bk_c': 200.0,
     'L3_xattn_bv_c': 7.168,
     'L3_xattn_Wg': 8.0,
     'L3_xattn_bg': 21.896,
     'L3_attn_out_b': 8.0,
     'L3_ffn_gate_w': 8.0,
     'L3_ffn_down_w': 8.0,
     'L3_ffn_down_b': 8.0,
     'L3_ffn_up_w': 8.0,
     'L3_ffn_up_b': 8.0}
    for name, (base, spread) in spreads.items():
        noise = np.random.default_rng([zlib.crc32(name.encode()), seed]).standard_normal(out[name].shape)
        drawn = base * np.exp(spread * noise) if base else spread * noise
        out[name] = jnp.asarray(drawn.astype(out[name].dtype))
    for name, factor in factors.items():
        out[name] = (out[name] * factor).astype(out[name].dtype)
    return out
```

```python
from contextlib import ExitStack, contextmanager

import numpy as np
import concourse.bass as bass
from concourse import mybir

P = 128
B, S, D = 128, 32, 128
T = B * S
TILES = T // P
BT = P // S
GROUPS = T // 512
TG = 512 // P
KEYS = 257
CH = 86
KPAD = 3 * CH
HEADS, HD = 16, 8
EXPERTS = 8
CAP = T // EXPERTS
BIG = 1.0e30
NEG = -1.0e9
EPS = 1e-5

F32 = mybir.dt.float32
BF16 = mybir.dt.bfloat16
I32 = mybir.dt.int32
ALU = mybir.AluOpType
ACT = mybir.ActivationFunctionType
AX = mybir.AxisListType


def made(n):
    return n + 2


def before(n):
    return n + 1


def previous(sems, s, i):
    return (sems[0], made(i)) if s else (sems[1], before(i))


class Names(dict):

    __getattr__ = dict.__getitem__


@contextmanager
def stage(nc, title):
    with ExitStack() as ctx:
        sems, primed = [], []
        opened = ctx.enter_context(nc.semaphore(f"{title}_opened"))
        sems.append(opened)

        def sem(name):
            sems.append(ctx.enter_context(nc.semaphore(f"{title}_{name}")))
            return sems[-1]

        def loop_sem(name):
            primed.append(sem(name))
            return primed[-1]

        yield Names(
            sb=lambda name, shape, dt=F32: ctx.enter_context(nc.sbuf_tensor(f"{title}_{name}", shape, dt)),
            ps=lambda name, shape, dt=F32: ctx.enter_context(nc.psum_tensor(f"{title}_{name}", shape, dt)),
            sem=sem,
            loop_sem=loop_sem,
            pair=lambda name: [loop_sem(f"{name}_a"), loop_sem(f"{name}_b")],
            open=lambda pool: [pool.sem_inc(s, 1) for s in primed + [opened]],
            opened=opened,
        )
        with nc.Block() as block:
            @block.gpsimd
            def _(pool):
                for s in sems:
                    pool.sem_clear(s)


def bc(ap, axis, n):
    a = ap.unsqueeze(axis)
    shape = list(a.shape)
    shape[axis] = n
    return a.to_broadcast(shape)


def normalise(nc, env, title, src, dst_t=None, dst=None, gain=None, shift=None, rms=False):
    with stage(nc, title) as st:
        stats = st.sb("stats", [P, TILES, 6])
        mv = st.sb("mv", [P, TILES, 2])
        var = st.sb("var", [P, TILES])
        std = st.sb("std", [P, TILES])
        rstd = st.sb("rstd", [P, TILES])
        stg = st.sb("stg", [P, 2, TG, D])
        pst = [st.ps(f"pst{s}", [P, 512]) for s in range(2)]
        stats_done, mv_done, var_done = st.sem("stats_done"), st.sem("mv_done"), st.sem("var_done")
        std_done, rstd_done = st.sem("std_done"), st.sem("rstd_done")
        norm_done, turned, copied, kept = st.pair("norm_done"), st.pair("turned"), st.pair("copied"), st.pair("kept")

        with nc.Block() as block:
            @block.gpsimd
            def _(pool):
                st.open(pool)

            @block.vector
            def _(dve):
                with dve.Fori(0, GROUPS) as g:
                    for t in range(TG):
                        last = dve.bn_stats(stats[:, g * TG + t, :], src[:, g * TG + t, :])
                    last.then_inc(stats_done, 1)
                dve.wait_ge(stats_done, GROUPS)
                for n in range(TILES):
                    last = dve.bn_aggr(mv[:, n, :], stats[:, n, :])
                last.then_inc(mv_done, GROUPS)
                dve.wait_ge(mv_done, GROUPS)
                if rms:
                    dve.tensor_tensor(std[:, :], mv[:, :, 0], mv[:, :, 0], ALU.mult).then_inc(mv_done, 1)
                    dve.wait_ge(mv_done, GROUPS + 1)
                    dve.scalar_tensor_tensor(out=var[:, :], in0=mv[:, :, 1], scalar=EPS, in1=std[:, :],
                                             op0=ALU.add, op1=ALU.add).then_inc(var_done, 1)
                else:
                    dve.tensor_scalar(var[:, :], mv[:, :, 1], EPS, None, ALU.add).then_inc(var_done, 1)
                dve.wait_ge(std_done, 1)
                dve.reciprocal(rstd[:, :], std[:, :]).then_inc(rstd_done, 1)
                dve.wait_ge(rstd_done, 1)
                with dve.Fori(0, GROUPS // 2) as i:
                    for s in range(2):
                        if dst_t is not None:
                            dve.wait_ge(turned[s], before(i))
                        if dst is not None:
                            dve.wait_ge(kept[s], before(i))
                        for t in range(TG):
                            n = (2 * i + s) * TG + t
                            if rms:
                                last = dve.tensor_scalar(stg[:, s, t, :], src[:, n, :], rstd[:, bass.ds(n, 1)], None,
                                                         ALU.mult)
                            else:
                                last = dve.tensor_scalar(stg[:, s, t, :], src[:, n, :], mv[:, n, 0:1],
                                                         rstd[:, bass.ds(n, 1)], ALU.subtract, ALU.mult)
                        last.then_inc(norm_done[s], 1)

            @block.tensor
            def _(pe):
                if dst_t is None:
                    return
                with pe.Fori(0, GROUPS // 2) as i:
                    for s in range(2):
                        pe.wait_ge(norm_done[s], made(i))
                        pe.wait_ge(copied[s], before(i))
                        for t in range(TG):
                            last = pe.transpose(pst[s][:, t * P:(t + 1) * P], stg[:, s, t, :], env.ident[:, :])
                        last.then_inc(turned[s], 1)

            @block.scalar
            def _(act):
                act.wait_ge(var_done, 1)
                act.activation(std[:, :], var[:, :], ACT.Sqrt).then_inc(std_done, 1)
                with act.Fori(0, GROUPS // 2) as i:
                    for s in range(2):
                        g = 2 * i + s
                        if dst is not None:
                            act.wait_ge(norm_done[s], made(i))
                            act.activation(dst[:, bass.ds(g * TG, TG), :], stg[:, s], ACT.Copy).then_inc(kept[s], 1)
                        if dst_t is not None:
                            act.wait_ge(turned[s], made(i))
                            out = dst_t[:, bass.ds(g * 512, 512)]
                            if gain is not None and shift is not None:
                                act.activation(out, pst[s][:, :], ACT.Identity, bias=shift, scale=gain
                                               ).then_inc(copied[s], 1)
                            elif gain is not None:
                                act.activation(out, pst[s][:, :], ACT.Copy, scale=gain).then_inc(copied[s], 1)
                            else:
                                act.activation(out, pst[s][:, :], ACT.Copy).then_inc(copied[s], 1)


def load_all(st, block_sync, pairs, sem):
    for dst, src in pairs:
        block_sync.dma_start(dst, src).then_inc(sem, 16)
    return 16 * len(pairs)


def route(nc, env, title, names, W, WT, kind):
    rw_d, rb_d = names
    with stage(nc, title) as st:
        rw = st.sb("rw", [P, EXPERTS])
        rb = st.sb("rb", [1, EXPERTS])
        xs = st.sb("xs", [P, 2, 512])
        LG = st.sb("LG", [P, TILES, EXPERTS])
        m = st.sb("m", [P, TILES])
        l0 = st.sb("l0", [P, TILES, EXPERTS])
        pr = st.sb("pr", [P, TILES, EXPERTS])
        sm = st.sb("sm", [P, TILES])
        rs = st.sb("rs", [P, TILES])
        pl = [st.ps(f"pl{s}", [P, 512]) for s in range(2)]
        loaded, xs_ready, logits, kept = st.sem("loaded"), st.pair("xs_ready"), st.pair("logits"), st.pair("kept")
        dve_step, exp_done, w_ready, w_turned, w_kept = (st.sem(n) for n in
                                                         ("dve_step", "exp_done", "w_ready", "w_turned", "w_kept"))
        with nc.Block() as block:
            @block.gpsimd
            def _(pool):
                st.open(pool)

            @block.sync
            def _(sp):
                sp.dma_start(rw[:, :], rw_d).then_inc(loaded, 16)
                sp.dma_start(rb[:, :], rb_d).then_inc(loaded, 16)

            @block.scalar
            def _(act):
                with act.Fori(0, GROUPS // 2) as i:
                    for s in range(2):
                        act.wait_ge(logits[s], before(i))
                        act.activation(xs[:, s, :], env.XNT[:, bass.ds((2 * i + s) * 512, 512)], ACT.Copy
                                       ).then_inc(xs_ready[s], 1)
                if kind != "one":
                    act.wait_ge(dve_step, 2)
                    act.activation(l0[:, :, :], l0[:, :, :], ACT.Exp).then_inc(exp_done, 1)
                for g in range(GROUPS):
                    act.wait_ge(w_turned, g + 1)
                    act.activation(WT[:, g * 512:(g + 1) * 512], pl[g % 2][0:EXPERTS, :], ACT.Copy).then_inc(w_kept, 1)

            @block.tensor
            def _(pe):
                pe.wait_ge(loaded, 32)
                with pe.Fori(0, GROUPS // 2) as i:
                    for s in range(2):
                        pe.wait_ge(xs_ready[s], made(i))
                        pe.wait_ge(kept[s], before(i))
                        for t in range(TG):
                            o = pl[s][:, t * EXPERTS:(t + 1) * EXPERTS]
                            pe.matmul(o, xs[:, s, t * P:(t + 1) * P], rw[:, :], start=True, stop=False)
                            last = pe.matmul(o, env.ones[0:1, 0:P], rb[:, :], start=False, stop=True)
                        last.then_inc(logits[s], 1)
                pe.wait_ge(w_ready, 1)
                for g in range(GROUPS):
                    if g >= 2:
                        pe.wait_ge(w_kept, g - 1)
                    for t in range(TG):
                        last = pe.transpose(pl[g % 2][0:EXPERTS, t * P:(t + 1) * P], W[:, g * TG + t, :],
                                            env.ident[:, :])
                    last.then_inc(w_turned, 1)

            @block.vector
            def _(dve):
                with dve.Fori(0, GROUPS // 2) as i:
                    for s in range(2):
                        dve.wait_ge(logits[s], made(i))
                        dve.tensor_copy(LG[:, bass.ds((2 * i + s) * TG, TG), :],
                                        pl[s][:, 0:TG * EXPERTS].rearrange("p (t e) -> p t e", e=EXPERTS)
                                        ).then_inc(kept[s], 1)
                dve.wait_ge(kept[0], before(GROUPS // 2))
                dve.wait_ge(kept[1], before(GROUPS // 2))
                step = [0]

                def done(ins):
                    step[0] += 1
                    ins.then_inc(dve_step, 1)
                    dve.wait_ge(dve_step, step[0])

                done(dve.tensor_reduce(m[:, :], LG[:, :, :], AX.X, ALU.max))
                if kind != "one":
                    done(dve.tensor_tensor(l0[:, :, :], LG[:, :, :], bc(m[:, :], 2, EXPERTS), ALU.subtract))
                    dve.wait_ge(exp_done, 1)
                    done(dve.tensor_reduce(sm[:, :], l0[:, :, :], AX.X, ALU.add))
                    done(dve.reciprocal(rs[:, :], sm[:, :]))
                    done(dve.tensor_tensor(pr[:, :, :], l0[:, :, :], bc(rs[:, :], 2, EXPERTS), ALU.mult))
                    done(dve.tensor_reduce(m[:, :], pr[:, :, :], AX.X, ALU.max))
                    src = pr
                else:
                    src = LG
                if kind == "choice":
                    done(dve.tensor_copy(W[:, :, :], pr[:, :, :]))
                else:
                    first_of_max(dve, done, env, src, m, l0, rs, W)
                if kind == "max":
                    done(dve.tensor_tensor(W[:, :, :], W[:, :, :], bc(m[:, :], 2, EXPERTS), ALU.mult))
                dve.wait_ge(dve_step, step[0])
                dve.sem_inc(w_ready, 1)


def first_of_max(dve, done, env, src, m, tmp, top, hot):
    n = src.shape[1]
    done(dve.tensor_tensor(tmp[:, 0:n, :], src[:, 0:n, :], bc(m[:, 0:n], 2, EXPERTS), ALU.is_equal))
    done(dve.tensor_tensor(tmp[:, 0:n, :], tmp[:, 0:n, :], bc(env.countdown[:, :], 1, n), ALU.mult))
    done(dve.tensor_reduce(top[:, 0:n], tmp[:, 0:n, :], AX.X, ALU.max))
    done(dve.tensor_tensor(hot[:, 0:n, :], tmp[:, 0:n, :], bc(top[:, 0:n], 2, EXPERTS), ALU.is_equal))


def linear_experts(nc, env, title, w_d, b_d, W, WT):
    with stage(nc, title) as st:
        we = st.sb("we", [P, EXPERTS * D])
        be = st.sb("be", [EXPERTS, D])
        xs = st.sb("xs", [P, 2, P])
        ws = st.sb("ws", [EXPERTS, 2, P])
        py = [st.ps(f"py{s}", [P, EXPERTS * D]) for s in range(2)]
        pb = [st.ps(f"pb{s}", [P, 512]) for s in range(2)]
        loaded = st.sem("loaded")
        staged, y_ready, y_used, added = st.pair("staged"), st.pair("y_ready"), st.pair("y_used"), st.sem("added")
        with nc.Block() as block:
            @block.gpsimd
            def _(pool):
                st.open(pool)

            @block.sync
            def _(sp):
                sp.dma_start(we[:, :], w_d).then_inc(loaded, 16)
                sp.dma_start(be[:, :], b_d).then_inc(loaded, 16)

            @block.scalar
            def _(act):
                with act.Fori(0, TILES // 2) as i:
                    for s in range(2):
                        n = 2 * i + s
                        act.wait_ge(y_ready[s], before(i))
                        act.activation(xs[:, s, :], env.XNT[:, bass.ds(n * P, P)], ACT.Copy)
                        act.activation(ws[:, s, :], WT[:, bass.ds(n * P, P)], ACT.Copy).then_inc(staged[s], 1)

            @block.tensor
            def _(pe):
                pe.wait_ge(loaded, 32)
                with pe.Fori(0, TILES // 2) as i:
                    for s in range(2):
                        pe.wait_ge(staged[s], made(i))
                        pe.wait_ge(y_used[s], before(i))
                        for h in range(2):
                            pe.matmul(py[s][:, h * 512:(h + 1) * 512], xs[:, s, :], we[:, h * 512:(h + 1) * 512])
                        pe.matmul(pb[s][:, 0:D], ws[:, s, :], be[:, :]).then_inc(y_ready[s], 1)

            @block.vector
            def _(dve):
                with dve.Fori(0, TILES // 2) as i:
                    for s in range(2):
                        n = 2 * i + s
                        dve.wait_ge(y_ready[s], made(i))
                        x = env.X[:, n, :]
                        dve.tensor_tensor(x, x, pb[s][:, 0:D], ALU.add).then_inc(added, 1)
                        for e in range(EXPERTS):
                            dve.wait_ge(added, n * (EXPERTS + 1) + e + 1)
                            dve.scalar_tensor_tensor(out=x, in0=py[s][:, e * D:(e + 1) * D],
                                                     scalar=W[:, n, e:e + 1], in1=x,
                                                     op0=ALU.mult, op1=ALU.add).then_inc(added, 1)
                        dve.wait_ge(added, (n + 1) * (EXPERTS + 1))
                        dve.sem_inc(y_used[s], 1)


def l0_ffn(nc, env, a):
    normalise(nc, env, "l0f_ln", env.X, dst_t=env.XNT)
    with stage(nc, "l0f") as st:
        W = st.sb("W", [P, TILES, EXPERTS])
        WT = st.sb("WT", [EXPERTS, T])
        route(nc, env, "l0f_route", (a.L0_ffn_router_w, a.L0_ffn_router_b), W, WT, "max")
        linear_experts(nc, env, "l0f_exp", a.L0_ffn_expert_w, a.L0_ffn_expert_b, W, WT)


def gelu_experts(nc, env, title, w, experts, chunks, W=None, WT=None, hidden_scale=None, extra=None):
    EC = experts * chunks
    with stage(nc, title) as st:
        w1, w2 = st.sb("w1", [P, EC * P]), st.sb("w2", [P, EC * D])
        b1 = st.sb("b1", [P, EC])
        b2 = st.sb("b2", [EXPERTS if WT is not None else 1, D])
        hid = st.sb("hid", [P, 2, chunks, 512])
        if WT is not None:
            ws = st.sb("ws", [EXPERTS, 512])
        if hidden_scale is not None:
            raw = st.sb("raw", [P, 4, 512])
        pH = [st.ps(f"pH{j}", [P, 512]) for j in range(4)]
        pY = [st.ps(f"pY{j}", [P, 512]) for j in range(2)]
        pB = st.ps("pB", [P, 512])
        loaded = st.sem("loaded")
        h_made, h_kept, h_ready, y_made, y_used, staged, b_made, b_used = (
            st.loop_sem(n) for n in ("h_made", "h_kept", "h_ready", "y_made", "y_used", "staged", "b_made", "b_used"))
        scaled = hidden_scale is not None
        ready = h_ready if scaled else h_kept
        with nc.Block() as block:
            @block.gpsimd
            def _(pool):
                st.open(pool)

            @block.sync
            def _(sp):
                for d, s_ in ((w1[:, :], w.w1), (b1[:, :], w.b1), (w2[:, :], w.w2), (b2[:, :], w.b2)):
                    sp.dma_start(d, s_).then_inc(loaded, 16)

            @block.tensor
            def _(pe):
                pe.wait_ge(loaded, 64)
                with pe.Fori(0, GROUPS) as g:
                    if WT is not None:
                        pe.wait_ge(staged, made(g))
                    pe.wait_ge(b_used, before(g))
                    for t in range(TG):
                        rows = ws[:, t * P:(t + 1) * P] if WT is not None else env.ones[0:1, 0:P]
                        last = pe.matmul(pB[:, t * D:(t + 1) * D], rows, b2[:, :])
                    last.then_inc(b_made, 1)
                    for e in range(experts + 1):
                        if e < experts:
                            for c in range(chunks):
                                k = e * chunks + c
                                pe.wait_ge(h_kept, before(g * EC + max(k - 3, 0)))
                                pe.matmul(pH[k % 4][:, :], w1[:, k * P:(k + 1) * P],
                                          env.XNT[:, bass.ds(g * 512, 512)]).then_inc(h_made, 1)
                        if e >= 1:
                            y = e - 1
                            pe.wait_ge(ready, made(g * EC + y * chunks + chunks - 1))
                            pe.wait_ge(y_used, before(g * experts + max(y - 1, 0)))
                            for t in range(TG):
                                for c in range(chunks):
                                    k = y * chunks + c
                                    last = pe.matmul(pY[y % 2][:, t * D:(t + 1) * D],
                                                     hid[:, y % 2, c, t * P:(t + 1) * P],
                                                     w2[:, k * D:(k + 1) * D], start=c == 0, stop=c == chunks - 1)
                            last.then_inc(y_made, 1)

            @block.scalar
            def _(act):
                act.wait_ge(loaded, 64)
                with act.Fori(0, GROUPS) as g:
                    if WT is not None:
                        act.wait_ge(b_made, before(g))
                        act.activation(ws[:, :], WT[:, bass.ds(g * 512, 512)], ACT.Copy).then_inc(staged, 1)
                    for k in range(EC):
                        e, c = divmod(k, chunks)
                        act.wait_ge(h_made, made(g * EC + k))
                        if scaled:
                            act.wait_ge(h_ready, before(g * EC))
                            out = raw[:, k % 4, :]
                        else:
                            act.wait_ge(y_made, before(g * experts + max(e - 1, 0)))
                            out = hid[:, e % 2, c, :]
                        act.activation(out, pH[k % 4][:, :], ACT.Gelu, bias=b1[:, k:k + 1]).then_inc(h_kept, 1)

            @block.vector
            def _(dve):
                with dve.Fori(0, GROUPS) as g:
                    xg = env.X[:, bass.ds(g * TG, TG), :]
                    tok = lambda ap: ap.rearrange("p (t d) -> p t d", d=D)
                    dve.wait_ge(b_made, made(g))
                    dve.tensor_tensor(xg, xg, tok(pB[:, :]), ALU.add).then_inc(b_used, 1)
                    dve.wait_ge(b_used, made(g))
                    if scaled:
                        dve.wait_ge(y_made, before(g * experts))
                        for c in range(chunks):
                            dve.wait_ge(h_kept, made(g * EC + c))
                            dve.tensor_tensor(hid[:, 0, c, :].rearrange("p (b s) -> p b s", s=S),
                                              raw[:, c % 4, :].rearrange("p (b s) -> p b s", s=S),
                                              bc(hidden_scale[:, c, bass.ds(g * 16, 16)], 2, S), ALU.mult
                                              ).then_inc(h_ready, 1)
                    for e in range(experts):
                        dve.wait_ge(y_made, made(g * experts + e))
                        dve.wait_ge(y_used, before(g * experts + e))
                        if W is None:
                            last = dve.tensor_tensor(xg, xg, tok(pY[e % 2][:, :]), ALU.add)
                        else:
                            for t in range(TG):
                                x = env.X[:, g * TG + t, :]
                                last = dve.scalar_tensor_tensor(
                                    out=x, in0=pY[e % 2][:, t * D:(t + 1) * D], scalar=W[:, g * TG + t, e:e + 1],
                                    in1=x, op0=ALU.mult, op1=ALU.add)
                        last.then_inc(y_used, 1)
                if extra is not None:
                    dve.wait_ge(y_used, before(GROUPS * experts))
                    dve.tensor_tensor(env.X[:, :, :], env.X[:, :, :], extra[:, :, :], ALU.add)


def weights_by_token(nc, env, title, W, WT, normalised):
    with stage(nc, title) as st:
        sm = st.sb("sm", [P, TILES])
        pw = st.ps("pw", [P, 512])
        turned, kept = st.sem("turned"), st.sem("kept")
        with nc.Block() as block:
            @block.tensor
            def _(pe):
                for n in range(TILES):
                    last = pe.transpose(pw[:, n * EXPERTS:(n + 1) * EXPERTS], WT[:, n * P:(n + 1) * P],
                                        env.ident[0:EXPERTS, 0:EXPERTS])
                last.then_inc(turned, 1)

            @block.vector
            def _(dve):
                dve.wait_ge(turned, 1)
                dve.tensor_copy(W[:, :, :], pw[:, 0:TILES * EXPERTS].rearrange("p (n e) -> p n e", e=EXPERTS)
                                ).then_inc(kept, 1)
                if normalised:
                    dve.wait_ge(kept, 1)
                    dve.tensor_reduce(sm[:, :], W[:, :, :], AX.X, ALU.add).then_inc(kept, 1)
                    dve.wait_ge(kept, 2)
                    dve.tensor_scalar(sm[:, :], sm[:, :], 1e-9, None, ALU.max).then_inc(kept, 1)
                    dve.wait_ge(kept, 3)
                    dve.reciprocal(sm[:, :], sm[:, :]).then_inc(kept, 1)
                    dve.wait_ge(kept, 4)
                    dve.tensor_tensor(W[:, :, :], W[:, :, :], bc(sm[:, :], 2, EXPERTS), ALU.mult)


def weights_by_expert(nc, env, title, W, WT):
    with stage(nc, title) as st:
        pw = [st.ps(f"pw{j}", [EXPERTS, 512]) for j in range(2)]
        turned, kept = st.sem("turned"), st.sem("kept")
        with nc.Block() as block:
            @block.tensor
            def _(pe):
                for g in range(GROUPS):
                    if g >= 2:
                        pe.wait_ge(kept, g - 1)
                    for t in range(TG):
                        last = pe.transpose(pw[g % 2][:, t * P:(t + 1) * P], W[:, g * TG + t, :], env.ident[:, :])
                    last.then_inc(turned, 1)

            @block.scalar
            def _(act):
                for g in range(GROUPS):
                    act.wait_ge(turned, g + 1)
                    act.activation(WT[:, g * 512:(g + 1) * 512], pw[g % 2][:, :], ACT.Copy).then_inc(kept, 1)


def choose_tokens(nc, env, title, WT):
    C = P // EXPERTS
    W_ = T // C
    BITS = 30
    scratch = nc.dram_tensor(f"{title}_scratch", (EXPERTS, T), F32).ap()
    scratch2 = nc.dram_tensor(f"{title}_scratch2", (EXPERTS, T), F32).ap()
    rows = lambda s: s.rearrange("e (c t) -> (e c) t", c=C)
    with stage(nc, title) as st:
        pc, gt, rank = (st.sb(n, [P, W_]) for n in ("pc", "gt", "rank"))
        ones, eq = st.sb("ones", [P, W_]), st.sb("eq", [P, W_])
        same, lower = st.sb("same", [P, P]), st.sb("lower", [P, P])
        bits = st.sb("bits", [P, BITS], I32)
        thr, cand, keep, cnt, need = (st.sb(n, [P, 1]) for n in ("thr", "cand", "keep", "cnt", "need"))
        ps = st.ps("ps", [P, 512])
        moved, landed, written = st.sem("moved"), st.sem("landed"), st.sem("written")
        step, counted, summed = st.loop_sem("step"), st.loop_sem("counted"), st.loop_sem("summed")
        ready, zeroed = st.sem("ready"), st.sem("zeroed")
        with nc.Block() as block:
            @block.gpsimd
            def _(pool):
                st.open(pool)

            @block.sync
            def _(sp):
                sp.dma_start(scratch, WT[:, :]).then_inc(moved, 16)
                sp.wait_ge(moved, 16)
                sp.dma_start(pc[:, :], rows(scratch)).then_inc(landed, 16)
                sp.dma_start(same[:, :], env.a.c_same_expert).then_inc(landed, 16)
                sp.dma_start(lower[:, :], env.a.c_lower_chunk).then_inc(landed, 16)
                sp.dma_start(bits[:, :], env.a.bits).then_inc(landed, 16)
                sp.wait_ge(ready, 1)
                sp.dma_start(rows(scratch2), pc[:, :]).then_inc(written, 16)
                sp.wait_ge(written, 16)
                sp.dma_start(WT[:, :], scratch2).then_inc(written, 16)
                sp.wait_ge(written, 32)

            @block.tensor
            def _(pe):
                pe.wait_ge(st.opened, 1)
                pe.wait_ge(landed, 64)
                with pe.Fori(0, BITS) as k:
                    pe.wait_ge(counted, made(k))
                    pe.matmul(ps[:, 0:1], same[:, :], cnt[:, :]).then_inc(summed, 1)
                pe.wait_ge(counted, made(BITS))
                pe.matmul(ps[:, 0:1], same[:, :], cnt[:, :]).then_inc(summed, 1)
                pe.wait_ge(counted, made(BITS + 1))
                pe.matmul(ps[:, 0:1], lower[:, :], cnt[:, :]).then_inc(summed, 1)

            @block.vector
            def _(dve):
                dve.wait_ge(st.opened, 1)
                dve.memset(thr[:, :], 0.0)
                dve.memset(ones[:, :], 1.0).then_inc(zeroed, 1)
                dve.wait_ge(zeroed, 1)
                dve.wait_ge(landed, 64)
                with dve.Fori(0, BITS) as k:
                    dve.wait_ge(step, 4 * k + 1)
                    dve.tensor_tensor(cand[:, :].bitcast(I32), thr[:, :].bitcast(I32), bits[:, bass.ds(k, 1)],
                                      ALU.bitwise_or).then_inc(step, 1)
                    dve.wait_ge(step, 4 * k + 2)
                    dve.tensor_scalar(gt[:, :], pc[:, :], cand[:, 0:1], None, ALU.is_ge).then_inc(step, 1)
                    dve.wait_ge(step, 4 * k + 3)
                    dve.tensor_reduce(cnt[:, :], gt[:, :], AX.X, ALU.add).then_inc(counted, 1)
                    dve.wait_ge(summed, made(k))
                    dve.tensor_scalar(keep[:, :], ps[:, 0:1], float(CAP), None, ALU.is_ge).then_inc(step, 1)
                    dve.wait_ge(step, 4 * k + 4)
                    dve.scalar_tensor_tensor(out=thr[:, :], in0=cand[:, :], scalar=keep[:, 0:1], in1=thr[:, :],
                                             op0=ALU.mult, op1=ALU.max).then_inc(step, 1)
                dve.wait_ge(step, 4 * BITS + 1)
                dve.tensor_scalar(gt[:, :], pc[:, :], thr[:, 0:1], None, ALU.is_gt).then_inc(step, 1)
                dve.wait_ge(step, 4 * BITS + 2)
                dve.tensor_reduce(cnt[:, :], gt[:, :], AX.X, ALU.add).then_inc(counted, 1)
                dve.wait_ge(summed, made(BITS))
                dve.tensor_scalar(need[:, :], ps[:, 0:1], -1.0, float(CAP), ALU.mult, ALU.add).then_inc(step, 1)
                dve.wait_ge(step, 4 * BITS + 3)
                dve.tensor_scalar(eq[:, :], pc[:, :], thr[:, 0:1], None, ALU.is_equal).then_inc(step, 1)
                dve.wait_ge(step, 4 * BITS + 4)
                dve.tensor_tensor_scan(rank[:, :], ones[:, :], eq[:, :], 0.0, ALU.mult, ALU.add).then_inc(step, 1)
                dve.wait_ge(step, 4 * BITS + 5)
                dve.tensor_copy(cnt[:, :], rank[:, W_ - 1:W_]).then_inc(counted, 1)
                dve.wait_ge(summed, made(BITS + 1))
                dve.tensor_scalar(rank[:, :], rank[:, :], ps[:, 0:1], None, ALU.add).then_inc(step, 1)
                dve.wait_ge(step, 4 * BITS + 6)
                dve.tensor_scalar(rank[:, :], rank[:, :], need[:, 0:1], None, ALU.is_le).then_inc(step, 1)
                dve.wait_ge(step, 4 * BITS + 7)
                dve.tensor_tensor(rank[:, :], rank[:, :], eq[:, :], ALU.mult).then_inc(step, 1)
                dve.wait_ge(step, 4 * BITS + 8)
                dve.tensor_tensor(rank[:, :], rank[:, :], gt[:, :], ALU.add).then_inc(step, 1)
                dve.wait_ge(step, 4 * BITS + 9)
                dve.tensor_tensor(pc[:, :], pc[:, :], rank[:, :], ALU.mult).then_inc(ready, 1)


def l1_attn(nc, env, a):
    with stage(nc, "l1a") as st:
        XN = st.sb("XN", [P, TILES, D])
        ln = st.sb("ln", [P, 4])
        landed = st.sem("landed")
        with nc.Block() as block:
            @block.sync
            def _(sp):
                sp.dma_start(ln[:, :], a.L1_attn_ln).then_inc(landed, 16)
                sp.wait_ge(landed, 16)
        normalise(nc, env, "l1a_ln0", env.X, dst=XN)
        normalise(nc, env, "l1a_ln1", XN, dst_t=env.XNT, gain=ln[:, 0:1], shift=ln[:, 1:2])
        w = Names(wq=a.L1_attn_wq, wk=a.L1_attn_wk, wv=a.L1_attn_wv, wo=a.L1_attn_Wo, wq2=a.L1_attn_wq2,
                            wk2=a.L1_attn_wk2, cos=a.c_rope_cos.rearrange("p (a t) -> p a t", a=2),
                            sin=a.c_rope_sin.rearrange("p (a t) -> p a t", a=2), mask=a.c_causal_add)
        tile_attention(nc, env, "l1a_att", "rope", w, XN)
        normalise(nc, env, "l1a_ln2", XN, dst_t=env.XNT, gain=ln[:, 2:3], shift=ln[:, 3:4])
        w = Names(w1=a.L1_attn_W1, b1=a.L1_attn_b1, w2=a.L1_attn_W2, b2=a.L1_attn_b2)
        gelu_experts(nc, env, "l1a_mlp", w, 1, 4, extra=XN)


def l1_ffn(nc, env, a):
    normalise(nc, env, "l1f_ln", env.X, dst_t=env.XNT)
    with stage(nc, "l1f") as st:
        W = st.sb("W", [P, TILES, EXPERTS])
        WT = st.sb("WT", [EXPERTS, T])
        route(nc, env, "l1f_route", (a.L1_ffn_Wr, a.L1_ffn_br), W, WT, "one")
        w = Names(w1=a.L1_ffn_W1, b1=a.L1_ffn_b1, w2=a.L1_ffn_W2, b2=a.L1_ffn_b2)
        gelu_experts(nc, env, "l1f_exp", w, EXPERTS, 3, W=W, WT=WT)


def l2_ffn(nc, env, a):
    with stage(nc, "l2f") as st:
        W = st.sb("W", [P, TILES, EXPERTS])
        WT = st.sb("WT", [EXPERTS, T])
        with stage(nc, "l2f_norm") as st2:
            XN = st2.sb("XN", [P, TILES, D])
            gain = st2.sb("gain", [P, 1])
            landed = st2.sem("landed")
            with nc.Block() as block:
                @block.sync
                def _(sp):
                    sp.dma_start(gain[:, :], a.L2_ffn_norm_weight).then_inc(landed, 16)
                    sp.wait_ge(landed, 16)
            normalise(nc, env, "l2f_ln", env.X, dst=XN)
            normalise(nc, env, "l2f_rms", XN, dst_t=env.XNT, gain=gain[:, 0:1], rms=True)
        route(nc, env, "l2f_route", (a.L2_ffn_router_w, a.L2_ffn_router_b), W, WT, "choice")
        choose_tokens(nc, env, "l2f_choose", WT)
        weights_by_token(nc, env, "l2f_byt", W, WT, normalised=True)
        weights_by_expert(nc, env, "l2f_bye", W, WT)
        w = Names(w1=a.L2_ffn_fc1_w, b1=a.L2_ffn_fc1_b, w2=a.L2_ffn_fc2_w, b2=a.L2_ffn_fc2_b)
        gelu_experts(nc, env, "l2f_exp", w, EXPERTS, 4, W=W, WT=WT)


def pooled_gate(nc, env, title, gate_d, WT, wx):
    with stage(nc, title) as st:
        gw, spread = st.sb("gw", [P, EXPERTS]), st.sb("spread", [EXPERTS, 512])
        pooled = st.sb("pooled", [P, B])
        lg, ex, pr, tmp, hot1, hot2, W = (st.sb(n, [P, 1, EXPERTS])
                                          for n in ("lg", "ex", "pr", "tmp", "hot1", "hot2", "W"))
        m, sm, top, g1, g2 = (st.sb(n, [P, 1]) for n in ("m", "sm", "top", "g1", "g2"))
        wT = st.sb("wT", [EXPERTS, P])
        ps = st.ps("ps", [P, 512])
        loaded, dve_step, lg_made, exp_done, w_done, w_turned, wx_made = (
            st.sem(n) for n in ("loaded", "dve_step", "lg_made", "exp_done", "w_done", "w_turned", "wx_made"))
        with nc.Block() as block:
            @block.sync
            def _(sp):
                sp.dma_start(gw[:, :], gate_d).then_inc(loaded, 16)
                sp.dma_start(spread[:, :], env.a.c_spread).then_inc(loaded, 16)

            @block.tensor
            def _(pe):
                pe.wait_ge(loaded, 32)
                pe.wait_ge(dve_step, 2)
                pe.matmul(ps[:, 0:EXPERTS], pooled[:, :], gw[:, :]).then_inc(lg_made, 1)
                pe.wait_ge(w_done, 1)
                pe.transpose(ps[0:EXPERTS, 0:P], W[:, 0, :], env.ident[:, :]).then_inc(w_turned, 1)
                pe.wait_ge(w_done, 3)
                for c in range(4):
                    last = pe.matmul(ps[:, c * P:(c + 1) * P], spread[:, c * P:(c + 1) * P], wT[:, :])
                last.then_inc(wx_made, 1)

            @block.scalar
            def _(act):
                act.wait_ge(dve_step, 5)
                act.activation(ex[:, :, :], lg[:, :, :], ACT.Exp).then_inc(exp_done, 1)

            @block.vector
            def _(dve):
                step = [0]

                def done(ins):
                    step[0] += 1
                    ins.then_inc(dve_step, 1)
                    dve.wait_ge(dve_step, step[0])

                done(dve.tensor_reduce(pooled[:, :], env.XNT[:, :].rearrange("p (b s) -> p b s", s=S), AX.X, ALU.add))
                done(dve.tensor_scalar(pooled[:, :], pooled[:, :], 1.0 / S, None, ALU.mult))
                dve.wait_ge(lg_made, 1)
                done(dve.tensor_copy(lg[:, 0, :], ps[:, 0:EXPERTS]))
                done(dve.tensor_reduce(m[:, :], lg[:, :, :], AX.X, ALU.max))
                done(dve.tensor_scalar(lg[:, 0, :], lg[:, 0, :], m[:, 0:1], None, ALU.subtract))
                dve.wait_ge(exp_done, 1)
                done(dve.tensor_reduce(sm[:, :], ex[:, :, :], AX.X, ALU.add))
                done(dve.reciprocal(sm[:, :], sm[:, :]))
                done(dve.tensor_scalar(pr[:, 0, :], ex[:, 0, :], sm[:, 0:1], None, ALU.mult))
                done(dve.tensor_reduce(g1[:, :], pr[:, :, :], AX.X, ALU.max))
                first_of_max(dve, done, env, pr, g1, tmp, top, hot1)
                done(dve.scalar_tensor_tensor(out=pr[:, 0, :], in0=hot1[:, 0, :], scalar=-2.0, in1=pr[:, 0, :],
                                              op0=ALU.mult, op1=ALU.add))
                done(dve.tensor_reduce(g2[:, :], pr[:, :, :], AX.X, ALU.max))
                first_of_max(dve, done, env, pr, g2, tmp, top, hot2)
                done(dve.scalar_tensor_tensor(out=sm[:, :], in0=g1[:, :], scalar=1e-8, in1=g2[:, :],
                                              op0=ALU.add, op1=ALU.add))
                done(dve.reciprocal(sm[:, :], sm[:, :]))
                done(dve.tensor_scalar(hot1[:, 0, :], hot1[:, 0, :], g1[:, 0:1], None, ALU.mult))
                done(dve.scalar_tensor_tensor(out=hot1[:, 0, :], in0=hot2[:, 0, :], scalar=g2[:, 0:1],
                                              in1=hot1[:, 0, :], op0=ALU.mult, op1=ALU.add))
                dve.tensor_scalar(W[:, 0, :], hot1[:, 0, :], sm[:, 0:1], None, ALU.mult).then_inc(w_done, 1)
                dve.wait_ge(w_turned, 1)
                dve.tensor_copy(wT[:, :], ps[0:EXPERTS, 0:P]).then_inc(w_done, 1)
                dve.wait_ge(w_done, 2)
                dve.tensor_copy(WT[:, :].rearrange("e (b s) -> e b s", s=S), bc(wT[:, :], 2, S)).then_inc(w_done, 1)
                dve.wait_ge(wx_made, 1)
                dve.tensor_copy(wx[:, :, :], ps[:, :].rearrange("p (c b) -> p c b", b=B))


def l3_ffn(nc, env, a):
    normalise(nc, env, "l3f_ln", env.X, dst_t=env.XNT)
    with stage(nc, "l3f") as st:
        WT = st.sb("WT", [EXPERTS, T])
        wx = st.sb("wx", [P, 4, B])
        pooled_gate(nc, env, "l3f_gate", a.L3_ffn_gate_w, WT, wx)
        w = Names(w1=a.L3_ffn_down_w, b1=a.L3_ffn_down_b, w2=a.L3_ffn_up_w, b2=a.L3_ffn_up_b)
        gelu_experts(nc, env, "l3f_exp", w, 1, 4, WT=WT, hidden_scale=wx)


def tile_attention(nc, env, title, mode, w, res, QA=None, KA=None, csum=None):
    cross, rope, cosine = mode == "cross", mode == "rope", mode == "cosine"
    with stage(nc, title) as st:
        wq, wk, wv, wo = (st.sb(n, [P, D]) for n in ("wq", "wk", "wv", "wo"))
        xs = st.sb("xs", [P, 2, P])
        qT = st.sb("qT", [P, 2, P])
        kb = st.sb("kb", [P, 2, 4, P])
        v = st.sb("v", [P, 2, P])
        prob = st.sb("prob", [P, 2, HEADS, P])
        probT = st.sb("probT", [P, 2, HEADS, P])
        mx = st.sb("mx", [P, 2, HEADS])
        nmx = st.sb("nmx", [P, 2, HEADS])
        sums = st.sb("sums", [P, 2, HEADS])
        rs = st.sb("rs", [P, 2, HEADS])
        os_ = st.sb("os", [P, 2, D])
        oT = st.sb("oT", [P, 2, P])
        mask = st.sb("mask", [P, P])
        loads = [(wv[:, :], w.wv), (wo[:, :], w.wo)]
        if not cosine:
            loads += [(wq[:, :], w.wq), (wk[:, :], w.wk), (mask[:, :], w.mask)]
        if cross:
            kvs = st.sb("kvs", [P, 2, BT, S])
            cs = st.sb("cs", [P, 2, BT, S])
            keep_i = st.sb("keep_i", [P, 2, BT, S], I32)
            keep = st.sb("keep", [P, 2, P])
            fill = st.sb("fill", [P, 2, P])
            off = st.sb("off", [P, P])
            vsum = st.sb("vsum", [P, 2, D])
            e33 = st.sb("e33", [P, 2, HEADS])
            loads += [(off[:, :], w.off)]
        if rope:
            wq2, wk2 = st.sb("wq2", [P, D]), st.sb("wk2", [P, D])
            cos, sin = st.sb("cos", [P, 2, P]), st.sb("sin", [P, 2, P])
            t1, t2 = st.sb("t1", [P, 2, 2, P]), st.sb("t2", [P, 2, 2, P])
            loads += [(wq2[:, :], w.wq2), (wk2[:, :], w.wk2), (cos[:, :, :], w.cos), (sin[:, :, :], w.sin)]
        if cosine:
            bv, bo, hs = st.sb("bv", [1, D]), st.sb("bo", [P, 1]), st.sb("hs", [P, 1])
            loads += [(bv[:, :], w.bv), (bo[:, :], w.bo), (hs[:, :], w.hs)]
        pS = st.ps("pS", [P, HEADS * P])
        pA = st.ps("pA", [P, 512])
        pT = [st.ps(f"pT{j}", [P, 512]) for j in range(2)]
        pO = st.ps("pO", [P, 512])
        O, OT, OUT = (pO[:, n * P:(n + 1) * P] for n in range(3))
        V = (pO if rope else pA)[:, 3 * P:4 * P]
        names = ("kv_landed", "xs_ready", "qkv_ready", "q_kept", "k_kept", "v_kept", "s_ready", "masked", "m_ready",
                 "nm_ready", "p_ready", "o_ready", "rs_ready", "o_kept", "ot_ready", "ot_kept", "out_ready", "finished",
                 "k_built")
        (kv_landed, xs_ready, qkv_ready, q_kept, k_kept, v_kept, s_ready, masked, m_ready, nm_ready, p_ready, o_ready,
         rs_ready, o_kept, ot_ready, ot_kept, out_ready, finished, k_built) = (st.pair(n) for n in names)
        filled = st.pair("filled")
        turned, kept = st.pair("turned"), st.pair("kept")
        loaded = st.sem("loaded")
        units = TILES // 2
        with nc.Block() as block:
            @block.gpsimd
            def _(pool):
                st.open(pool)

            @block.sync
            def _(sp):
                for dst, src in loads:
                    sp.dma_start(dst, src).then_inc(loaded, 16)
                if cross:
                    with sp.Fori(0, units) as i:
                        for s in range(2):
                            n = 2 * i + s
                            sp.wait_ge(finished[s], before(i))
                            sp.dma_start(kvs[:, s], env.a.ctx_t.rearrange("d (b k) -> d b k", k=KEYS)[
                                :, bass.ds(n * BT, BT), 0:S]).then_inc(kv_landed[s], 16)
                            sp.dma_start(keep_i[:, s], env.a.mask_pad[bass.ds(n * BT, BT), 0:S].unsqueeze(0)
                                         .to_broadcast([P, BT, S])).then_inc(kv_landed[s], 16)

            @block.scalar
            def _(act):
                if cosine:
                    act.wait_ge(loaded, 16 * len(loads))
                with act.Fori(0, units) as i:
                    for s in range(2):
                        n = 2 * i + s
                        act.wait_ge(qkv_ready[s], before(i))
                        if cross:
                            act.activation(cs[:, s], bc(csum[:, bass.ds(n * BT, BT)], 2, S), ACT.Copy)
                        if cosine:
                            act.wait_ge(s_ready[s], before(i))
                            act.activation(qT[:, s, :], QA[:, bass.ds(n, P, step=S)], ACT.Copy).then_inc(q_kept[s], 1)
                            act.activation(xs[:, s, :], env.XNT[:, bass.ds(n, P, step=S)], ACT.Copy
                                           ).then_inc(xs_ready[s], 1)
                        else:
                            act.activation(xs[:, s, :], env.XNT[:, bass.ds(n * P, P)], ACT.Copy
                                           ).then_inc(xs_ready[s], 1)
                    for s in range(2):
                        act.wait_ge(qkv_ready[s], made(i))
                        act.wait_ge(o_ready[s], before(i))
                        act.activation(v[:, s, :], V, ACT.Copy).then_inc(v_kept[s], 1)
                        if cross:
                            act.activation(qT[:, s, :], pA[:, 0:P], ACT.Copy, scale=HD ** -0.5).then_inc(q_kept[s], 1)
                            act.wait_ge(finished[s], before(i))
                            act.activation(vsum[:, s, :], pA[:, 2 * P:3 * P], ACT.Copy).then_inc(v_kept[s], 1)
                    for s in range(2):
                        act.wait_ge(nm_ready[s], made(i))
                        act.wait_ge(finished[s], before(i))
                        for h in range(HEADS):
                            e = act.activation(prob[:, s, h, :], pS[:, h * P:(h + 1) * P], ACT.Exp,
                                               bias=nmx[:, s, h:h + 1], accum_out=sums[:, s, h:h + 1])
                            if h % 4 == 3:
                                e.then_inc(p_ready[s], 1)
                        if cross:
                            act.activation(e33[:, s, :], nmx[:, s, :], ACT.Exp, bias=env.neg[:, 0:1]
                                           ).then_inc(p_ready[s], 1)
                    for s in range(2):
                        n = 2 * i + s
                        for j in (1, 3):
                            act.wait_ge(turned[1], made(2 * n + j // 2))
                            act.activation(probT[:, s, 4 * j:4 * j + 4, :], pT[1][:, :].rearrange(
                                "p (h q) -> p h q", q=P), ACT.Copy).then_inc(kept[1], 1)
                    for s in range(2):
                        act.wait_ge(ot_ready[s], made(i))
                        if cosine:
                            act.activation(oT[:, s, :], OT, ACT.Copy, scale=hs[:, 0:1]).then_inc(ot_kept[s], 1)
                        else:
                            act.activation(oT[:, s, :], OT, ACT.Copy).then_inc(ot_kept[s], 1)

            @block.tensor
            def _(pe):
                pe.wait_ge(loaded, 16 * len(loads))
                with pe.Fori(0, units) as i:
                    for s in range(2):
                        pe.wait_ge(xs_ready[s], made(i))
                        sem, value = previous(v_kept, s, i)
                        if cross:
                            pe.wait_ge(sem, 2 * value - 1)
                            pe.wait_ge(kv_landed[s], 32 * i + 33)
                        else:
                            pe.wait_ge(sem, value)
                        if not cosine:
                            pe.wait_ge(*previous(q_kept, s, i))
                            pe.wait_ge(*previous(k_kept, s, i))
                        if rope and not s:
                            pe.wait_ge(finished[1], before(i))
                        x = xs[:, s, :]
                        kv = kvs[:, s].rearrange("p b k -> p (b k)") if cross else x
                        if not cosine:
                            pe.matmul(pA[:, 0:P], wq[:, :], x)
                            pe.matmul(pA[:, P:2 * P], wk[:, :], kv)
                        if rope:
                            pe.matmul(pA[:, 2 * P:3 * P], wq2[:, :], x)
                            pe.matmul(pA[:, 3 * P:4 * P], wk2[:, :], kv)
                        if cross:
                            pe.matmul(pA[:, 2 * P:3 * P], cs[:, s].rearrange("p b k -> p (b k)"), wv[:, :])
                        if cosine:
                            pe.matmul(V, x, wv[:, :], start=True, stop=False)
                            pe.matmul(V, env.ones[0:1, 0:P], bv[:, :], start=False, stop=True
                                      ).then_inc(qkv_ready[s], 1)
                        else:
                            pe.matmul(V, kv, wv[:, :]).then_inc(qkv_ready[s], 1)
                    for s in range(2):
                        pe.wait_ge(q_kept[s], made(i))
                        pe.wait_ge(k_built[s], made(i))
                        sem, value = previous(p_ready, s, i)
                        per = 5 if cross else 4
                        pe.wait_ge(sem, per * value - per + 1)
                        for j in range(4):
                            last = pe.matmul(pS[:, j * 512:(j + 1) * 512], qT[32 * j:32 * j + 32, s, :],
                                             kb[32 * j:32 * j + 32, s].rearrange("p h k -> p (h k)"))
                        last.then_inc(s_ready[s], 1)
                    for s in range(2):
                        n = 2 * i + s
                        for j in range(4):
                            pe.wait_ge(p_ready[s], per * i + j + 2)
                            pe.wait_ge(kept[j % 2], before(2 * n + j // 2))
                            for h in range(4):
                                last = pe.transpose(pT[j % 2][:, h * P:(h + 1) * P], prob[:, s, 4 * j + h, :],
                                                    env.ident[:, :])
                            last.then_inc(turned[j % 2], 1)
                        pe.wait_ge(v_kept[s], 2 * i + 2 if cross else made(i))
                        if s:
                            pe.wait_ge(o_kept[0], made(i))
                        elif rope:
                            pe.wait_ge(v_kept[1], made(i))
                        else:
                            pe.wait_ge(finished[1], before(i))
                        for j in range(4):
                            pe.wait_ge(kept[j % 2], made(2 * n + j // 2))
                            for h in range(4 * j, 4 * j + 4):
                                last = pe.matmul(O[:, h * HD:(h + 1) * HD], probT[:, s, h, :],
                                                 v[:, s, h * HD:(h + 1) * HD])
                        last.then_inc(o_ready[s], 1)
                    for s in range(2):
                        pe.wait_ge(o_kept[s], made(i))
                        if s:
                            pe.wait_ge(finished[0], made(i))
                        else:
                            pe.wait_ge(o_kept[1], made(i))
                        pe.transpose(OT, os_[:, s, :], env.ident[:, :]).then_inc(ot_ready[s], 1)
                        pe.wait_ge(ot_kept[s], made(i))
                        if cosine:
                            pe.matmul(OUT, wo[:, :], oT[:, s, :]).then_inc(out_ready[s], 1)
                        else:
                            pe.matmul(OUT, oT[:, s, :], wo[:, :]).then_inc(out_ready[s], 1)

            @block.vector
            def _(dve):
                dve.wait_ge(loaded, 16 * len(loads))
                heads = bc(env.m4[:, :], 2, P)
                with dve.Fori(0, units) as i:
                    for s in range(2):
                        n = 2 * i + s
                        if cross:
                            dve.wait_ge(v_kept[s], 2 * i + 3)
                            dve.wait_ge(q_kept[s], made(i))
                            dve.wait_ge(s_ready[s], before(i))
                            dve.tensor_tensor(kb[:, s], bc(pA[:, P:2 * P], 1, 4), heads, ALU.mult
                                              ).then_inc(k_kept[s], 1)
                            dve.wait_ge(kv_landed[s], 32 * i + 33)
                            dve.tensor_copy(keep[:, s, :], keep_i[:, s].rearrange("p b k -> p (b k)")
                                            ).then_inc(masked[s], 1)
                            dve.wait_ge(masked[s], 5 * i + 2)
                            dve.tensor_scalar(keep[:, s, :], keep[:, s, :], 0.0, None, ALU.not_equal
                                              ).then_inc(masked[s], 1)
                            dve.wait_ge(masked[s], 5 * i + 3)
                            dve.tensor_tensor(keep[:, s, :], keep[:, s, :], mask[:, :], ALU.mult
                                              ).then_inc(masked[s], 1)
                            dve.wait_ge(masked[s], 5 * i + 4)
                            dve.tensor_scalar(fill[:, s, :], keep[:, s, :], -NEG, NEG, ALU.mult, ALU.add
                                              ).then_inc(masked[s], 1)
                            dve.wait_ge(masked[s], 5 * i + 5)
                            dve.tensor_tensor(fill[:, s, :], fill[:, s, :], off[:, :], ALU.add
                                              ).then_inc(k_built[s], 1)
                        elif rope:
                            dve.wait_ge(qkv_ready[s], made(i))
                            dve.wait_ge(s_ready[s], before(i))
                            ab = lambda o: pA[:, o:o + 2 * P].rearrange("p (a t) -> p a t", t=P)
                            dve.tensor_tensor(t1[:, s], ab(0), cos[:, :, :], ALU.mult)
                            dve.tensor_tensor(t2[:, s], ab(2 * P), sin[:, :, :], ALU.mult).then_inc(k_kept[s], 1)
                            dve.wait_ge(k_kept[s], made(i))
                            dve.tensor_tensor(qT[:, s, :], t1[:, s, 0, :], t2[:, s, 0, :], ALU.add
                                              ).then_inc(q_kept[s], 1)
                            dve.tensor_tensor(t1[:, s, 1, :], t1[:, s, 1, :], t2[:, s, 1, :], ALU.add
                                              ).then_inc(masked[s], 1)
                            dve.wait_ge(masked[s], 2 * i + 2)
                            dve.tensor_tensor(kb[:, s], bc(t1[:, s, 1, :], 1, 4), heads, ALU.mult
                                              ).then_inc(k_built[s], 1)
                        else:
                            dve.wait_ge(s_ready[s], before(i))
                            dve.tensor_tensor(kb[:, s], bc(KA[:, bass.ds(n, P, step=S)], 1, 4), heads, ALU.mult
                                              ).then_inc(k_built[s], 1)
                    for s in range(2):
                        dve.wait_ge(s_ready[s], made(i))
                        sc = pS[:, :].rearrange("p (h k) -> p h k", k=P)
                        if rope:
                            dve.tensor_tensor(sc, sc, bc(mask[:, :], 1, HEADS), ALU.add).then_inc(masked[s], 1)
                            dve.wait_ge(masked[s], 2 * i + 3)
                        if cross:
                            dve.wait_ge(k_built[s], made(i))
                            dve.tensor_tensor(sc, sc, bc(keep[:, s, :], 1, HEADS), ALU.mult).then_inc(masked[s], 1)
                            dve.wait_ge(masked[s], 5 * i + 6)
                            dve.tensor_tensor(sc, sc, bc(fill[:, s, :], 1, HEADS), ALU.add).then_inc(filled[s], 1)
                            dve.wait_ge(filled[s], made(i))
                        dve.tensor_reduce(mx[:, s, :], sc, AX.X, ALU.max).then_inc(m_ready[s], 1)
                        dve.wait_ge(m_ready[s], made(i))
                        if cross:
                            dve.tensor_scalar(nmx[:, s, :], mx[:, s, :], NEG, -1.0, ALU.max, ALU.mult
                                              ).then_inc(nm_ready[s], 1)
                        else:
                            dve.tensor_scalar(nmx[:, s, :], mx[:, s, :], -1.0, None, ALU.mult).then_inc(nm_ready[s], 1)
                    for s in range(2):
                        n = 2 * i + s
                        for j in (0, 2):
                            dve.wait_ge(turned[0], made(2 * n + j // 2))
                            dve.tensor_copy(probT[:, s, 4 * j:4 * j + 4, :], pT[0][:, :].rearrange(
                                "p (h q) -> p h q", q=P)).then_inc(kept[0], 1)
                        if cross:
                            dve.wait_ge(p_ready[s], 5 * i + 6)
                            dve.scalar_tensor_tensor(out=sums[:, s, :], in0=e33[:, s, :], scalar=float(KEYS - S),
                                                     in1=sums[:, s, :], op0=ALU.mult, op1=ALU.add
                                                     ).then_inc(rs_ready[s], 1)
                            dve.wait_ge(rs_ready[s], 3 * i + 2)
                            dve.reciprocal(rs[:, s, :], sums[:, s, :])
                            dve.wait_ge(v_kept[s], 2 * i + 3)
                            dve.tensor_tensor(vsum[:, s, :].rearrange("p (h d) -> p h d", d=HD),
                                              vsum[:, s, :].rearrange("p (h d) -> p h d", d=HD),
                                              bc(e33[:, s, :], 2, HD), ALU.mult).then_inc(rs_ready[s], 1)
                            dve.wait_ge(o_ready[s], made(i))
                            dve.wait_ge(rs_ready[s], 3 * i + 3)
                            dve.tensor_tensor(os_[:, s, :], O, vsum[:, s, :], ALU.add).then_inc(rs_ready[s], 1)
                            dve.wait_ge(rs_ready[s], 3 * i + 4)
                            dve.tensor_tensor(os_[:, s, :].rearrange("p (h d) -> p h d", d=HD),
                                              os_[:, s, :].rearrange("p (h d) -> p h d", d=HD),
                                              bc(rs[:, s, :], 2, HD), ALU.mult).then_inc(o_kept[s], 1)
                        else:
                            dve.wait_ge(p_ready[s], 4 * i + 5)
                            dve.reciprocal(rs[:, s, :], sums[:, s, :]).then_inc(rs_ready[s], 1)
                            dve.wait_ge(o_ready[s], made(i))
                            dve.wait_ge(rs_ready[s], made(i))
                            dve.tensor_tensor(os_[:, s, :].rearrange("p (h d) -> p h d", d=HD),
                                              O.rearrange("p (h d) -> p h d", d=HD),
                                              bc(rs[:, s, :], 2, HD), ALU.mult).then_inc(o_kept[s], 1)
                    for s in range(2):
                        n = 2 * i + s
                        dve.wait_ge(out_ready[s], made(i))
                        if cosine:
                            dve.tensor_scalar(env.XNT[:, bass.ds(n, P, step=S)], OUT, bo[:, 0:1], None, ALU.add
                                              ).then_inc(finished[s], 1)
                        else:
                            dve.tensor_tensor(res[:, n, :], res[:, n, :], OUT, ALU.add).then_inc(finished[s], 1)


def context_tail_sum(nc, env, title, csum):
    with stage(nc, title) as st:
        ctx = st.sb("ctx", [P, 2, 8, KEYS])
        landed, summed = st.pair("landed"), st.pair("summed")
        with nc.Block() as block:
            @block.gpsimd
            def _(pool):
                st.open(pool)

            @block.sync
            def _(sp):
                with sp.Fori(0, B // 16) as i:
                    for s in range(2):
                        sp.wait_ge(summed[s], before(i))
                        sp.dma_start(ctx[:, s].rearrange("p b k -> p (b k)"), env.a.ctx_t[
                            :, bass.ds((2 * i + s) * 8 * KEYS, 8 * KEYS)]).then_inc(landed[s], 16)

            @block.vector
            def _(dve):
                with dve.Fori(0, B // 16) as i:
                    for s in range(2):
                        dve.wait_ge(landed[s], 16 * i + 17)
                        dve.tensor_reduce(csum[:, bass.ds((2 * i + s) * 8, 8)], ctx[:, s, :, S:KEYS], AX.X, ALU.add
                                          ).then_inc(summed[s], 1)


def add_transposed(nc, env, title, src, res):
    with stage(nc, title) as st:
        stg = st.sb("stg", [P, 2, 512])
        pt = [st.ps(f"pt{s}", [P, 512]) for s in range(2)]
        staged, turned, added = st.pair("staged"), st.pair("turned"), st.pair("added")
        with nc.Block() as block:
            @block.gpsimd
            def _(pool):
                st.open(pool)

            @block.scalar
            def _(act):
                with act.Fori(0, GROUPS // 2) as i:
                    for s in range(2):
                        act.wait_ge(turned[s], before(i))
                        act.activation(stg[:, s, :], src[:, bass.ds((2 * i + s) * 512, 512)], ACT.Copy
                                       ).then_inc(staged[s], 1)

            @block.tensor
            def _(pe):
                with pe.Fori(0, GROUPS // 2) as i:
                    for s in range(2):
                        pe.wait_ge(staged[s], made(i))
                        pe.wait_ge(added[s], before(i))
                        for t in range(TG):
                            last = pe.transpose(pt[s][:, t * P:(t + 1) * P], stg[:, s, t * P:(t + 1) * P],
                                                env.ident[:, :])
                        last.then_inc(turned[s], 1)

            @block.vector
            def _(dve):
                with dve.Fori(0, GROUPS // 2) as i:
                    for s in range(2):
                        dve.wait_ge(turned[s], made(i))
                        x = res[:, bass.ds((2 * i + s) * TG, TG), :]
                        dve.tensor_tensor(x, x, pt[s][:, :].rearrange("p (t d) -> p t d", d=D), ALU.add
                                          ).then_inc(added[s], 1)


def l0_xattn(nc, env, a):
    with stage(nc, "l0x") as st:
        csum = st.sb("csum", [P, B])
        context_tail_sum(nc, env, "l0x_sum", csum)
        normalise(nc, env, "l0x_ln", env.X, dst_t=env.XNT)
        w = Names(wq=a.L0_xattn_Wq, wk=a.L0_xattn_Wk, wv=a.L0_xattn_Wv, wo=a.L0_xattn_Wo,
                            mask=a.c_causal01, off=a.c_other_batch)
        tile_attention(nc, env, "l0x_att", "cross", w, env.X, csum=csum)


def head_projection(nc, env, title, mode, w_d, src, dst, units, width, ctx=False, bias_d=None, gain_d=None,
                    scale=1.0, logit_d=None):
    ln, l2 = mode == "ln", mode == "l2"
    with stage(nc, title) as st:
        w = st.sb("w", [P, D])
        cols = st.sb("cols", [P, 4])
        y = st.sb("y", [P, 2, width])
        y2 = st.sb("y2", [P, 2, width])
        sd = st.sb("sd", [P, 2, width])
        if ctx:
            xin = st.sb("xin", [P, 2, width])
        raw, centre = (st.sb("raw", [P, D]), st.sb("centre", [P, P])) if ln else (None, None)
        blk = st.sb("blk", [P, P])
        pY = [st.ps(f"pY{s}", [P, 512]) for s in range(2)]
        pV = [st.ps(f"pV{s}", [P, 512]) for s in range(2)]
        loaded, w_made, w_kept, logit = (st.sem(n) for n in ("loaded", "w_made", "w_kept", "logit"))
        landed, y_made, y_kept, sq_made, var_made, sd_made, rs_made, n_made, done = (
            st.pair(n) for n in ("landed", "y_made", "y_kept", "sq_made", "var_made", "sd_made", "rs_made", "n_made",
                                 "done"))
        loads = [(w[:, :], w_d)] if not ln else [(raw[:, :], w_d), (centre[:, :], env.a.c_centre)]
        loads += [(blk[:, :], env.a.c_head_mean if ln else env.a.c_head_sum)]
        if bias_d is not None:
            loads += [(cols[:, 0:1], bias_d)]
        if gain_d is not None:
            loads += [(cols[:, 1:2], gain_d)]
        if logit_d is not None:
            loads += [(cols[:, 2:3], logit_d)]
        with nc.Block() as block:
            @block.gpsimd
            def _(pool):
                st.open(pool)

            @block.sync
            def _(sp):
                for d, s_ in loads:
                    sp.dma_start(d, s_).then_inc(loaded, 16)
                if ctx:
                    with sp.Fori(0, units // 2) as i:
                        for s in range(2):
                            sp.wait_ge(y_made[s], before(i))
                            sp.dma_start(xin[:, s, :], src[:, bass.ds((2 * i + s) * width, width)]
                                         ).then_inc(landed[s], 16)

            @block.tensor
            def _(pe):
                pe.wait_ge(loaded, 16 * len(loads))
                if ln:
                    pe.matmul(pY[0][:, 0:D], raw[:, :], centre[:, :]).then_inc(w_made, 1)
                    pe.wait_ge(w_kept, 1)
                with pe.Fori(0, units // 2) as i:
                    for s in range(2):
                        if ctx:
                            pe.wait_ge(landed[s], 16 * i + 17)
                            x = xin[:, s, :]
                        else:
                            x = src[:, bass.ds((2 * i + s) * width, width)]
                        pe.wait_ge(y_kept[s], before(i))
                        pe.matmul(pY[s][:, 0:width], w[:, :], x).then_inc(y_made[s], 1)
                    for s in range(2):
                        if mode != "plain":
                            pe.wait_ge(sq_made[s], made(i))
                            pe.wait_ge(sd_made[s], before(i))
                            pe.matmul(pV[s][:, 0:width], blk[:, :], y2[:, s, :]).then_inc(var_made[s], 1)

            @block.scalar
            def _(act):
                act.wait_ge(loaded, 16 * len(loads))
                if ln:
                    act.wait_ge(w_made, 1)
                    act.activation(w[:, :], pY[0][:, 0:D], ACT.Copy).then_inc(w_kept, 1)
                if logit_d is not None:
                    act.wait_ge(logit, 1)
                    act.activation(cols[:, 3:4], cols[:, 2:3], ACT.Exp).then_inc(logit, 1)
                with act.Fori(0, units // 2) as i:
                    for s in range(2):
                        act.wait_ge(y_made[s], made(i))
                        if mode == "plain":
                            out = dst[:, bass.ds((2 * i + s) * width, width)]
                            if bias_d is None:
                                act.activation(out, pY[s][:, 0:width], ACT.Copy, scale=scale).then_inc(y_kept[s], 1)
                            elif scale == 1.0:
                                act.activation(out, pY[s][:, 0:width], ACT.Identity, bias=cols[:, 0:1]
                                               ).then_inc(y_kept[s], 1)
                            else:
                                act.activation(y[:, s, :], pY[s][:, 0:width], ACT.Identity, bias=cols[:, 0:1]
                                               ).then_inc(y_kept[s], 1)
                                act.wait_ge(y_kept[s], made(i))
                                act.activation(out, y[:, s, :], ACT.Copy, scale=scale).then_inc(done[s], 1)
                            continue
                        act.wait_ge(n_made[s], before(i))
                        if l2:
                            act.activation(y[:, s, :], pY[s][:, 0:width], ACT.Identity, bias=cols[:, 0:1]
                                           ).then_inc(y_kept[s], 1)
                        else:
                            act.activation(y[:, s, :], pY[s][:, 0:width], ACT.Copy).then_inc(y_kept[s], 1)
                        act.wait_ge(y_kept[s], made(i))
                        act.wait_ge(var_made[s], before(i))
                        act.activation(y2[:, s, :], y[:, s, :], ACT.Square).then_inc(sq_made[s], 1)
                    if mode != "plain":
                        for s in range(2):
                            act.wait_ge(var_made[s], made(i))
                            act.wait_ge(n_made[s], before(i))
                            if ln:
                                act.activation(sd[:, s, :], pV[s][:, 0:width], ACT.Sqrt, bias=env.eps[:, 0:1]
                                               ).then_inc(sd_made[s], 1)
                            else:
                                act.activation(sd[:, s, :], pV[s][:, 0:width], ACT.Sqrt).then_inc(sd_made[s], 1)

            @block.vector
            def _(dve):
                dve.wait_ge(loaded, 16 * len(loads))
                if logit_d is not None:
                    dve.tensor_scalar(cols[:, 2:3], cols[:, 2:3], float(np.log(100.0)), None, ALU.min
                                      ).then_inc(logit, 1)
                    dve.wait_ge(logit, 2)
                if mode == "plain":
                    return
                with dve.Fori(0, units // 2) as i:
                    for s in range(2):
                        out = dst[:, bass.ds((2 * i + s) * width, width)]
                        dve.wait_ge(sd_made[s], made(i))
                        if l2:
                            dve.tensor_scalar(sd[:, s, :], sd[:, s, :], 1e-12, None, ALU.max).then_inc(rs_made[s], 1)
                            dve.wait_ge(rs_made[s], 2 * i + 2)
                        dve.reciprocal(sd[:, s, :], sd[:, s, :]).then_inc(rs_made[s], 1)
                        dve.wait_ge(rs_made[s], 2 * i + 3 if l2 else made(i))
                        if ln:
                            dve.tensor_tensor(sd[:, s, :], y[:, s, :], sd[:, s, :], ALU.mult).then_inc(done[s], 1)
                            dve.wait_ge(done[s], made(i))
                            dve.tensor_scalar(out, sd[:, s, :], cols[:, 1:2], cols[:, 0:1], ALU.mult, ALU.add
                                              ).then_inc(n_made[s], 1)
                        elif logit_d is not None:
                            dve.scalar_tensor_tensor(out=out, in0=y[:, s, :], scalar=cols[:, 3:4], in1=sd[:, s, :],
                                                     op0=ALU.mult, op1=ALU.mult).then_inc(n_made[s], 1)
                        else:
                            dve.tensor_tensor(out, y[:, s, :], sd[:, s, :], ALU.mult).then_inc(n_made[s], 1)


def cross_attention(nc, env, title, w, QT, KA=None, masked=False):
    with stage(nc, title) as st:
        wk, wv = st.sb("wk", [P, D]), st.sb("wv", [P, D])
        cols = st.sb("cols", [P, 2])
        m4q, selq = st.sb("m4q", [P, 4]), st.sb("selq", [P, S])
        ctx = st.sb("ctx", [P, 2, KPAD])
        kT = st.sb("kT", [P, 2, KPAD])
        qb = st.sb("qb", [P, 2, 4, S])
        v = st.sb("v", [CH, 2, 3, D])
        prob = st.sb("prob", [P, 2, 4, KPAD])
        probT = st.sb("probT", [CH, 2, 4, 3 * P])
        nmx, sums, rs = (st.sb(n, [P, 2, 4]) for n in ("nmx", "sums", "rs"))
        rm = st.sb("rm", [P, 2, 4, 4])
        rx = st.sb("rx", [P, 2, D])
        own = st.sb("own", [P, 4, S])
        ou, on = st.sb("ou", [P, S]), st.sb("on", [P, 2, S])
        loads = [(wv[:, :], w.wv), (m4q[:, :], env.a.c_m4q), (selq[:, :], env.a.c_selq)]
        if KA is None:
            loads += [(wk[:, :], w.wk), (cols[:, 0:1], w.bk), (cols[:, 1:2], w.bv)]
        if masked:
            mask_i, mask = st.sb("mask_i", [P, KEYS], I32), st.sb("mask", [P, KEYS])
            loads += [(mask_i[:, :], w.mask)]
        pS = [st.ps(f"pS{j}", [P, 512]) for j in range(4)]
        pT = [st.ps(f"pT{j}", [P, 512]) for j in range(2)]
        pKV = st.ps("pKV", [P, 512])
        pO = st.ps("pO", [P, 512])
        O, R = pO[:, 0:P], pKV[:, 448:448 + S]
        loaded, mask_made, padded, rs_step = (st.sem(n) for n in ("loaded", "mask_made", "padded", "rs_step"))
        landed = st.pair("landed")
        (q_made, k_made, v_made, k_kept, v_kept, s_made, m_made, p_made, o_made, rs_made, rm_made, rx_made, own_made,
         ou_made, r_made, on_made, done) = (st.loop_sem(n) for n in (
             "q_made", "k_made", "v_made", "k_kept", "v_kept", "s_made", "m_made", "p_made", "o_made", "rs_made",
             "rm_made", "rx_made", "own_made", "ou_made", "r_made", "on_made", "done"))
        turned, kept = st.pair("turned"), st.pair("kept")
        masked_step = st.loop_sem("masked_step")

        def slots(eng, slot):
            slot(0, 0)
            with eng.Fori(0, (B - 4) // 2) as i:
                slot(2 * i + 1, 1)
                slot(2 * i + 2, 0)
            for n in range(B - 3, B):
                slot(n, n % 2)

        def inside(n, ahead=0):
            return not isinstance(n, int) or 0 <= n + ahead < B

        with nc.Block() as block:
            @block.gpsimd
            def _(pool):
                st.open(pool)
                pool.memset(ctx[:, :, KEYS:KPAD], 0.0)
                pool.memset(kT[:, :, KEYS:KPAD], 0.0)
                pool.memset(prob[:, :, :, KEYS:KPAD], 0.0).then_inc(padded, 1)

            @block.sync
            def _(sp):
                for d, s_ in loads:
                    sp.dma_start(d, s_).then_inc(loaded, 16)

                def load(n, s):
                    sp.dma_start(ctx[:, s, 0:KEYS], env.a.ctx_t[:, bass.ds(n * KEYS, KEYS)]).then_inc(landed[s], 16)

                load(0, 0)
                load(1, 1)
                with sp.Fori(0, B // 2 - 1) as i:
                    for s in range(2):
                        sp.wait_ge(v_made, made(2 * i + s))
                        load(2 * i + s + 2, s)

            @block.tensor
            def _(pe):
                pe.wait_ge(loaded, 16 * len(loads))
                pe.wait_ge(padded, 1)

                def landed_count(n, s):
                    return 16 * ((n - s) // 2) + 17 if isinstance(n, int) else 8 * (n - s) + 17

                def keys(n, s):
                    pe.wait_ge(landed[s], landed_count(n, s))
                    pe.wait_ge(v_kept, before(n))
                    if KA is None:
                        pe.matmul(pKV[:, 0:KEYS], wk[:, :], ctx[:, s, 0:KEYS]).then_inc(k_made, 1)

                def values(n, s):
                    if KA is None:
                        pe.wait_ge(k_kept, made(n))
                    if not isinstance(n, int) or n >= 3:
                        pe.wait_ge(on_made, made(n - 3))
                    for c in range(3):
                        last = pe.matmul(pKV[0:CH, c * D:(c + 1) * D], ctx[:, s, c * CH:(c + 1) * CH], wv[:, :])
                    last.then_inc(v_made, 1)

                def scores(n, s, j):
                    if j == 0:
                        pe.wait_ge(q_made, made(n))
                        pe.wait_ge(k_kept, made(n))
                    if not isinstance(n, int) or n:
                        pe.wait_ge(p_made, made(4 * n + j - 4))
                    pe.matmul(pS[j][:, 0:KEYS], qb[32 * j:32 * j + 32, s].rearrange("p h q -> p (h q)"),
                              kT[32 * j:32 * j + 32, s, 0:KEYS]).then_inc(s_made, 1)

                def turn(n, s, j):
                    pe.wait_ge(p_made, made(4 * n + j))
                    pe.wait_ge(kept[j % 2], before(2 * n + j // 2))
                    for c in range(3):
                        last = pe.transpose(pT[j % 2][0:CH, c * P:(c + 1) * P], prob[:, s, j, c * CH:(c + 1) * CH],
                                            env.ident[:, :])
                    last.then_inc(turned[j % 2], 1)

                def attend(n, s, j):
                    if j == 0:
                        pe.wait_ge(v_kept, made(n))
                        pe.wait_ge(own_made, before(n))
                    pe.wait_ge(kept[j % 2], made(2 * n + j // 2))
                    for c in range(3):
                        last = pe.matmul(O[j * 32:j * 32 + 32, :], v[:, s, c, j * 32:j * 32 + 32],
                                         probT[:, s, j, c * P:(c + 1) * P], start=c == 0, stop=c == 2)
                    if j == 3:
                        last.then_inc(o_made, 1)

                def normaliser(n, s):
                    pe.wait_ge(rx_made, made(n))
                    if inside(n, 3):
                        pe.wait_ge(k_kept, made(n + 3))
                    pe.wait_ge(v_kept, made(min(n + 2, B - 1) if isinstance(n, int) else n + 2))
                    pe.matmul(R, rx[:, s, :], selq[:, :]).then_inc(r_made, 1)

                for n in range(2):
                    keys(n, n)
                    values(n, n)
                for j in range(4):
                    scores(0, 0, j)

                def slot(n, s):
                    if inside(n, 2):
                        keys(n + 2, s)
                    for j in range(4):
                        if inside(n, 1):
                            scores(n + 1, 1 - s, j)
                        turn(n, s, j)
                        if j == 0 and inside(n, -1):
                            normaliser(n - 1, 1 - s)
                        if j >= 1:
                            attend(n, s, j - 1)
                    if inside(n, 2):
                        values(n + 2, s)
                    attend(n, s, 3)

                slots(pe, slot)
                normaliser(B - 1, 1)

            @block.scalar
            def _(act):
                act.wait_ge(loaded, 16 * len(loads))
                act.wait_ge(padded, 1)

                def keys(n, s):
                    if KA is not None:
                        if not isinstance(n, int) or n >= 2:
                            act.wait_ge(s_made, made(4 * n - 5))
                        act.activation(kT[:, s, 0:KEYS], KA[:, bass.ds(n * KEYS, KEYS)], ACT.Copy
                                       ).then_inc(k_kept, 1)
                    else:
                        act.wait_ge(k_made, made(n))
                        act.activation(kT[:, s, 0:KEYS], pKV[:, 0:KEYS], ACT.Identity, bias=cols[:, 0:1]
                                       ).then_inc(k_kept, 1)

                def values(n, s):
                    act.wait_ge(v_made, made(n))
                    if not isinstance(n, int) or n >= 2:
                        act.wait_ge(o_made, made(n - 2))
                    act.activation(v[:, s].rearrange("p c d -> p (c d)"), pKV[0:CH, 0:3 * D], ACT.Copy
                                   ).then_inc(v_kept, 1)

                def exponentials(n, s, j):
                    act.wait_ge(m_made, made(4 * n + j))
                    if j == 0 and (not isinstance(n, int) or n >= 2):
                        act.wait_ge(turned[1], made(2 * n - 3))
                        act.wait_ge(rs_made, made(n - 2))
                    act.activation(prob[:, s, j, 0:KEYS], pS[j][:, 0:KEYS], ACT.Exp, bias=nmx[:, s, j:j + 1],
                                   accum_out=sums[:, s, j:j + 1]).then_inc(p_made, 1)

                def keep_turned(n, s, j):
                    act.wait_ge(turned[1], made(2 * n + j // 2))
                    act.activation(probT[:, s, j, :], pT[1][0:CH, 0:3 * P], ACT.Copy).then_inc(kept[1], 1)

                def output(n, s):
                    act.wait_ge(on_made, made(n))
                    out = QT[:, bass.ds(n * S, S)]
                    if KA is None:
                        act.activation(out, on[:, s, :], ACT.Identity, bias=cols[:, 1:2]).then_inc(done, 1)
                    else:
                        act.activation(out, on[:, s, :], ACT.Copy).then_inc(done, 1)

                for n in range(2):
                    keys(n, n)
                    values(n, n)
                for j in range(4):
                    exponentials(0, 0, j)

                def slot(n, s):
                    if inside(n, 2):
                        keys(n + 2, s)
                    for j in range(4):
                        if inside(n, 1):
                            exponentials(n + 1, 1 - s, j)
                        if j == 2 and inside(n, -1):
                            output(n - 1, 1 - s)
                        if j % 2:
                            keep_turned(n, s, j)
                    if inside(n, 2):
                        values(n + 2, s)

                slots(act, slot)
                output(B - 1, 1)

            @block.vector
            def _(dve):
                dve.wait_ge(loaded, 16 * len(loads))
                dve.wait_ge(st.opened, 1)
                if masked:
                    dve.tensor_copy(mask[:, :], mask_i[:, :]).then_inc(mask_made, 1)
                    dve.wait_ge(mask_made, 1)
                    dve.tensor_scalar(mask[:, :], mask[:, :], 0.0, -BIG, ALU.is_equal, ALU.mult
                                      ).then_inc(mask_made, 1)
                    dve.wait_ge(mask_made, 2)

                def queries(n, s):
                    dve.tensor_tensor(qb[:, s], bc(QT[:, bass.ds(n * S, S)], 1, 4), bc(env.m4[:, :], 2, S),
                                      ALU.mult).then_inc(q_made, 1)

                def maxima(n, s, j):
                    dve.wait_ge(s_made, made(4 * n + j))
                    sc = pS[j][:, 0:KEYS]
                    if masked:
                        dve.tensor_tensor(sc, sc, mask[:, :], ALU.add).then_inc(masked_step, 1)
                        dve.wait_ge(masked_step, made(4 * n + j))
                    dve.tensor_reduce(nmx[:, s, j:j + 1], sc, AX.X, ALU.max, negate=True).then_inc(m_made, 1)

                def keep_turned(n, s, j):
                    dve.wait_ge(turned[0], made(2 * n + j // 2))
                    dve.tensor_copy(probT[:, s, j, :], pT[0][0:CH, 0:3 * P]).then_inc(kept[0], 1)

                def factors(n, s):
                    dve.wait_ge(p_made, made(4 * n + 3))
                    dve.reciprocal(rs[:, s, :], sums[:, s, :]).then_inc(rs_made, 1)
                    dve.wait_ge(rs_made, made(n))
                    dve.tensor_tensor(rm[:, s], bc(rs[:, s, :], 2, 4), bc(m4q[:, :], 1, 4), ALU.mult
                                      ).then_inc(rm_made, 1)
                    dve.wait_ge(rm_made, made(n))
                    dve.tensor_copy(rx[:, s, :].rearrange("p (g d) -> p g d", d=HD),
                                    bc(rm[:, s].rearrange("p j h -> p (j h)"), 2, HD)).then_inc(rx_made, 1)

                def own_head(n, s):
                    dve.wait_ge(o_made, made(n))
                    dve.tensor_tensor(own[:, :, :], O.rearrange("p (h q) -> p h q", q=S), bc(env.m4[:, :], 2, S),
                                      ALU.mult).then_inc(own_made, 1)
                    dve.wait_ge(own_made, made(n))
                    dve.tensor_reduce(ou[:, :], own[:, :, :].rearrange("p h q -> p q h"), AX.X, ALU.add
                                      ).then_inc(ou_made, 1)

                def outputs(n, s):
                    dve.wait_ge(ou_made, made(n))
                    dve.wait_ge(r_made, made(n))
                    if not isinstance(n, int) or n >= 2:
                        dve.wait_ge(done, made(n - 2))
                    dve.tensor_tensor(on[:, s, :], R, ou[:, :], ALU.mult).then_inc(on_made, 1)

                queries(0, 0)
                queries(1, 1)
                for j in range(4):
                    maxima(0, 0, j)

                def slot(n, s):
                    if inside(n, -1):
                        own_head(n - 1, 1 - s)
                    if inside(n, 2):
                        queries(n + 2, s)
                    for j in range(4):
                        if inside(n, 1):
                            maxima(n + 1, 1 - s, j)
                        if j % 2 == 0:
                            keep_turned(n, s, j)
                        if j == 0 and inside(n, -1):
                            outputs(n - 1, 1 - s)
                    factors(n, s)

                slots(dve, slot)
                own_head(B - 1, 1)
                outputs(B - 1, 1)


def project_out(nc, env, title, w_d, b_d, src, res):
    with stage(nc, title) as st:
        w, b = st.sb("w", [P, D]), st.sb("b", [1, D])
        stg = st.sb("stg", [P, 2, 512])
        py = [st.ps(f"py{s}", [P, 512]) for s in range(2)]
        loaded = st.sem("loaded")
        staged, y_made, added = st.pair("staged"), st.pair("y_made"), st.pair("added")
        with nc.Block() as block:
            @block.gpsimd
            def _(pool):
                st.open(pool)

            @block.sync
            def _(sp):
                sp.dma_start(w[:, :], w_d).then_inc(loaded, 16)
                sp.dma_start(b[:, :], b_d).then_inc(loaded, 16)

            @block.scalar
            def _(act):
                with act.Fori(0, GROUPS // 2) as i:
                    for s in range(2):
                        act.wait_ge(y_made[s], before(i))
                        act.activation(stg[:, s, :], src[:, bass.ds((2 * i + s) * 512, 512)], ACT.Copy
                                       ).then_inc(staged[s], 1)

            @block.tensor
            def _(pe):
                pe.wait_ge(loaded, 32)
                with pe.Fori(0, GROUPS // 2) as i:
                    for s in range(2):
                        pe.wait_ge(staged[s], made(i))
                        pe.wait_ge(added[s], before(i))
                        for t in range(TG):
                            o = py[s][:, t * D:(t + 1) * D]
                            pe.matmul(o, stg[:, s, t * P:(t + 1) * P], w[:, :], start=True, stop=False)
                            last = pe.matmul(o, env.ones[0:1, 0:P], b[:, :], start=False, stop=True)
                        last.then_inc(y_made[s], 1)

            @block.vector
            def _(dve):
                with dve.Fori(0, GROUPS // 2) as i:
                    for s in range(2):
                        dve.wait_ge(y_made[s], made(i))
                        x = res[:, bass.ds((2 * i + s) * TG, TG), :]
                        dve.tensor_tensor(x, x, py[s][:, :].rearrange("p (t d) -> p t d", d=D), ALU.add
                                          ).then_inc(added[s], 1)


def l1_xattn(nc, env, a):
    normalise(nc, env, "l1x_ln", env.X, dst_t=env.XNT)
    with stage(nc, "l1x") as st:
        KA = st.sb("KA", [P, B * KEYS])
        head_projection(nc, env, "l1x_q", "ln", a.L1_xattn_Wq, env.XNT, env.XNT, GROUPS, 512,
                        bias_d=a.L1_xattn_ln_b, gain_d=a.L1_xattn_ln_g)
        head_projection(nc, env, "l1x_k", "ln", a.L1_xattn_Wk, a.ctx_t, KA, B, KEYS, ctx=True,
                        bias_d=a.L1_xattn_ln_b, gain_d=a.L1_xattn_ln_g)
        w = Names(wv=a.L1_xattn_Wv)
        cross_attention(nc, env, "l1x_att", w, env.XNT, KA=KA)
    project_out(nc, env, "l1x_out", a.L1_xattn_Wp, a.L1_xattn_bp, env.XNT, env.X)


def l2_xattn(nc, env, a):
    normalise(nc, env, "l2x_ln", env.X, dst_t=env.XNT)
    head_projection(nc, env, "l2x_q", "plain", a.L2_xattn_Wq, env.XNT, env.XNT, GROUPS, 512,
                    bias_d=a.L2_xattn_bq, scale=HD ** -0.5)
    w = Names(wk=a.L2_xattn_Wk, bk=a.L2_xattn_bk, wv=a.L2_xattn_Wv, bv=a.L2_xattn_bv, mask=a.mask_if)
    cross_attention(nc, env, "l2x_att", w, env.XNT, masked=True)
    project_out(nc, env, "l2x_out", a.L2_xattn_Wo, a.L2_xattn_bo, env.XNT, env.X)


def l3_attn(nc, env, a):
    normalise(nc, env, "l3a_ln", env.X, dst_t=env.XNT)
    with stage(nc, "l3a") as st:
        QA, KA = st.sb("QA", [P, T]), st.sb("KA", [P, T])
        head_projection(nc, env, "l3a_q", "l2", a.L3_attn_wq, env.XNT, QA, GROUPS, 512, bias_d=a.L3_attn_bq,
                        logit_d=a.L3_attn_logit)
        head_projection(nc, env, "l3a_k", "l2", a.L3_attn_wk, env.XNT, KA, GROUPS, 512, bias_d=a.L3_attn_bk)
        w = Names(wv=a.L3_attn_wv, wo=a.L3_attn_out_w, bv=a.L3_attn_bv, bo=a.L3_attn_out_b,
                            hs=a.L3_attn_head)
        tile_attention(nc, env, "l3a_att", "cosine", w, None, QA=QA, KA=KA)
    add_transposed(nc, env, "l3a_add", env.XNT, env.X)


def multi_query_attention(nc, env, title, w, Y):
    NH, DH = 8, 64
    with stage(nc, title) as st:
        wq, wk, wv, wo = (st.sb(n, [P, k]) for n, k in (("wq", 512), ("wk", D), ("wv", DH), ("wo", 512)))
        off = st.sb("off", [P, P])
        xs = st.sb("xs", [P, 2, P])
        qT = st.sb("qT", [P, 2, 4, P])
        kT = st.sb("kT", [P, 2, P])
        v = st.sb("v", [P, 2, DH])
        prob, probT = st.sb("prob", [P, 2, NH, P]), st.sb("probT", [P, 2, NH, P])
        mx, nmx, sums, rs = (st.sb(n, [P, 2, NH]) for n in ("mx", "nmx", "sums", "rs"))
        os_ = st.sb("os", [P, 2, 4, 2, DH])
        oT = st.sb("oT", [P, 2, 4, P])
        pQ, pK, pO, pX = (st.ps(n, [P, 512]) for n in ("pQ", "pK", "pO", "pX"))
        pS = st.ps("pS", [P, 2, 4, P])
        pT = [st.ps(f"pT{r}", [P, 512]) for r in range(2)]
        loads = [(wq[:, :], w.wq), (wk[:, :], w.wk), (wv[:, :], w.wv), (wo[:, :], w.wo), (off[:, :], w.off)]
        loaded = st.sem("loaded")
        (xs_ready, qkv_made, qkv_kept, s_made, masked, m_made, nm_made, p_made, o_made, rs_made, o_kept, ot_made,
         ot_kept, out_made, finished, turned, kept) = (st.pair(n) for n in (
             "xs_ready", "qkv_made", "qkv_kept", "s_made", "masked", "m_made", "nm_made", "p_made", "o_made",
             "rs_made", "o_kept", "ot_made", "ot_kept", "out_made", "finished", "turned", "kept"))
        with nc.Block() as block:
            @block.gpsimd
            def _(pool):
                st.open(pool)

            @block.sync
            def _(sp):
                for d, s_ in loads:
                    sp.dma_start(d, s_).then_inc(loaded, 16)

            @block.scalar
            def _(act):
                with act.Fori(0, TILES // 2) as i:
                    for s in range(2):
                        act.wait_ge(qkv_made[s], before(i))
                        act.activation(xs[:, s, :], env.XNT[:, bass.ds((2 * i + s) * P, P)], ACT.Copy
                                       ).then_inc(xs_ready[s], 1)
                    for s in range(2):
                        act.wait_ge(qkv_made[s], made(i))
                        act.wait_ge(o_made[s], before(i))
                        act.activation(qT[:, s].rearrange("p c t -> p (c t)"), pQ[:, :], ACT.Copy, scale=DH ** -0.5)
                        act.activation(kT[:, s, :], pK[:, 0:P], ACT.Copy)
                        act.activation(v[:, s, :], pK[:, P:P + DH], ACT.Copy).then_inc(qkv_kept[s], 1)
                    for s in range(2):
                        act.wait_ge(nm_made[s], made(i))
                        act.wait_ge(o_kept[s], before(i))
                        for u in range(NH):
                            e = act.activation(prob[:, s, u, :], pS[:, u // 4, u % 4, :], ACT.Exp,
                                               bias=nmx[:, s, u:u + 1], accum_out=sums[:, s, u:u + 1])
                            if u % 4 == 3:
                                e.then_inc(p_made[s], 1)
                    for s in range(2):
                        act.wait_ge(turned[1], made(2 * i + s))
                        act.activation(probT[:, s, 4:8, :], pT[1][:, :].rearrange("p (h q) -> p h q", q=P), ACT.Copy
                                       ).then_inc(kept[1], 1)
                    for s in range(2):
                        act.wait_ge(ot_made[s], made(i))
                        act.activation(oT[:, s].rearrange("p c t -> p (c t)"), pQ[:, :], ACT.Copy
                                       ).then_inc(ot_kept[s], 1)

            @block.tensor
            def _(pe):
                pe.wait_ge(loaded, 16 * len(loads))
                with pe.Fori(0, TILES // 2) as i:
                    for s in range(2):
                        pe.wait_ge(xs_ready[s], made(i))
                        pe.wait_ge(*((qkv_kept[0], made(i)) if s else (ot_kept[1], before(i))))
                        for c in range(4):
                            pe.matmul(pQ[:, c * P:(c + 1) * P], wq[:, c * P:(c + 1) * P], xs[:, s, :])
                        pe.matmul(pK[:, 0:P], wk[:, :], xs[:, s, :])
                        pe.matmul(pK[:, P:P + DH], xs[:, s, :], wv[:, :]).then_inc(qkv_made[s], 1)
                    for s in range(2):
                        pe.wait_ge(qkv_kept[s], made(i))
                        sem, value = previous(p_made, s, i)
                        pe.wait_ge(sem, 2 * value - 1)
                        for h in range(NH):
                            r = slice(DH * (h % 2), DH * (h % 2) + DH)
                            last = pe.matmul(pS[:, h % 2, h // 2, :], qT[r, s, h // 2, :], kT[r, s, :])
                        last.then_inc(s_made[s], 1)
                    for s in range(2):
                        n = 2 * i + s
                        for r in range(2):
                            pe.wait_ge(p_made[s], 2 * i + r + 2)
                            pe.wait_ge(kept[r], before(n))
                            for u in range(4):
                                last = pe.transpose(pT[r][:, u * P:(u + 1) * P], prob[:, s, 4 * r + u, :],
                                                    env.ident[:, :])
                            last.then_inc(turned[r], 1)
                        pe.wait_ge(*previous(o_kept, s, i))
                        for r in range(2):
                            pe.wait_ge(kept[r], made(n))
                            for u in range(4):
                                h = 2 * u + r
                                last = pe.matmul(pO[:, h * DH:(h + 1) * DH], probT[:, s, 4 * r + u, :], v[:, s, :])
                        last.then_inc(o_made[s], 1)
                    for s in range(2):
                        pe.wait_ge(o_kept[s], made(i))
                        pe.wait_ge(*((ot_kept[0], made(i)) if s else (qkv_kept[1], made(i))))
                        for c in range(4):
                            last = pe.transpose(pQ[:, c * P:(c + 1) * P],
                                                os_[:, s, c].rearrange("p r d -> p (r d)"), env.ident[:, :])
                        last.then_inc(ot_made[s], 1)
                        pe.wait_ge(ot_kept[s], made(i))
                        pe.wait_ge(*previous(finished, s, i))
                        for c in range(4):
                            last = pe.matmul(pX[:, 0:D], oT[:, s, c, :], wo[:, c * D:(c + 1) * D], start=c == 0,
                                             stop=c == 3)
                        last.then_inc(out_made[s], 1)

            @block.vector
            def _(dve):
                dve.wait_ge(loaded, 16 * len(loads))
                with dve.Fori(0, TILES // 2) as i:
                    for s in range(2):
                        dve.wait_ge(s_made[s], made(i))
                        sc = pS[:, :, :, :].rearrange("p r h k -> p (r h) k")
                        dve.tensor_tensor(sc, sc, bc(off[:, :], 1, NH), ALU.add).then_inc(masked[s], 1)
                        dve.wait_ge(masked[s], made(i))
                        dve.tensor_reduce(mx[:, s, :], sc, AX.X, ALU.max).then_inc(m_made[s], 1)
                        dve.wait_ge(m_made[s], made(i))
                        dve.tensor_scalar(nmx[:, s, :], mx[:, s, :], -1.0, None, ALU.mult).then_inc(nm_made[s], 1)
                    for s in range(2):
                        dve.wait_ge(turned[0], made(2 * i + s))
                        dve.tensor_copy(probT[:, s, 0:4, :], pT[0][:, :].rearrange("p (h q) -> p h q", q=P)
                                        ).then_inc(kept[0], 1)
                        dve.wait_ge(p_made[s], 2 * i + 3)
                        dve.reciprocal(rs[:, s, :], sums[:, s, :]).then_inc(rs_made[s], 1)
                        dve.wait_ge(rs_made[s], made(i))
                        dve.wait_ge(o_made[s], made(i))
                        o = pO[:, :].rearrange("p (c r d) -> p c r d", r=2, d=DH)
                        for r in range(2):
                            last = dve.tensor_tensor(os_[:, s, :, r, :], o[:, :, r, :],
                                                     bc(rs[:, s, 4 * r:4 * r + 4], 2, DH), ALU.mult)
                        last.then_inc(o_kept[s], 1)
                    for s in range(2):
                        dve.wait_ge(out_made[s], made(i))
                        dve.tensor_copy(Y[:, 2 * i + s, :], pX[:, 0:D]).then_inc(finished[s], 1)


def l0_attn(nc, env, a):
    with stage(nc, "l0a") as st:
        Y, YN = st.sb("Y", [P, TILES, D]), st.sb("YN", [P, TILES, D])
        ln = st.sb("ln", [P, 2])
        gain, shift = st.sb("gain", [P, D]), st.sb("shift", [P, D])
        landed, step = st.sem("landed"), st.sem("step")
        with nc.Block() as block:
            @block.sync
            def _(sp):
                sp.dma_start(ln[:, :], a.L0_attn_ln).then_inc(landed, 16)
                sp.dma_start(gain[:, :], a.L0_attn_out_norm_w.to_broadcast([P, D])).then_inc(landed, 16)
                sp.dma_start(shift[:, :], a.L0_attn_out_norm_b.to_broadcast([P, D])).then_inc(landed, 16)
                sp.wait_ge(landed, 48)
        normalise(nc, env, "l0a_ln0", env.X, dst=YN)
        normalise(nc, env, "l0a_ln1", YN, dst_t=env.XNT, gain=ln[:, 0:1], shift=ln[:, 1:2])
        w = Names(wq=a.L0_attn_Wq, wk=a.L0_attn_wk2, wv=a.L0_attn_wv, wo=a.L0_attn_Wo, off=a.c_other_batch)
        multi_query_attention(nc, env, "l0a_att", w, Y)
        normalise(nc, env, "l0a_ln2", Y, dst=YN)
        with nc.Block() as block:
            @block.vector
            def _(dve):
                dve.tensor_tensor(YN[:, :, :], YN[:, :, :], bc(gain[:, :], 1, TILES), ALU.mult)
                dve.tensor_tensor(env.X[:, :, :], env.X[:, :, :], bc(shift[:, :], 1, TILES), ALU.add
                                  ).then_inc(step, 1)
                dve.wait_ge(step, 1)
                dve.tensor_tensor(env.X[:, :, :], env.X[:, :, :], YN[:, :, :], ALU.add)


def selective_scan(nc, env, title, a):
    NC, NS = 2, 16
    BG = 512 // S
    with stage(nc, title) as st:
        w_in = st.sb("w_in", [P, 4 * P])
        w_dt_raw, w_bc = st.sb("w_dt_raw", [P, NC, P]), st.sb("w_bc", [P, NC, 96])
        w_out = st.sb("w_out", [P, NC, D])
        conv_w, cols, A = st.sb("conv_w", [P, NC, 4]), st.sb("cols", [P, NC, 4]), st.sb("A", [P, NC, NS])
        sel_f, sel = st.sb("sel_f", [96, 2 * NS]), st.sb("sel", [96, 2 * NS, P], BF16)
        xi, acc, th, xc, sz = (st.sb(n, [P, NC, 512]) for n in ("xi", "acc", "th", "xc", "sz"))
        ab, lg, dl, dx = (st.sb(n, [P, NC, 512]) for n in ("ab", "lg", "dl", "dx"))
        r1, stk = st.sb("r1", [96, 512]), st.sb("stk", [96, 512], BF16)
        dA, dbu, hh, hc = (st.sb(n, [P, NC, 512]) for n in ("dA", "dbu", "hh", "hc"))
        pX = [st.ps(f"pX{c}", [P, 512]) for c in range(2)]
        pZ = [st.ps(f"pZ{c}", [P, 512]) for c in range(2)]
        pBn = [st.ps(f"pBn{c}", [P, 512]) for c in range(2)]
        pCn = [st.ps(f"pCn{c}", [P, 512]) for c in range(2)]
        loads = [(w_in[:, :], a.L2_attn_W_in), (w_dt_raw[:, :, :], a.L2_attn_wx0.rearrange("p (c m) -> p c m", c=NC)),
                 (w_bc[:, :, :], a.L2_attn_wbc.rearrange("p (c m) -> p c m", c=NC)),
                 (w_out[:, :, :], a.L2_attn_W_out.rearrange("p (c m) -> p c m", c=NC)),
                 (conv_w[:, :, :], a.L2_attn_conv_w.rearrange("p (c m) -> p c m", c=NC)),
                 (cols[:, :, :], a.L2_attn_cols.rearrange("p (c m) -> p c m", c=NC)),
                 (A[:, :, :], a.L2_attn_A_log.rearrange("p (c m) -> p c m", c=NC)),
                 (sel_f[:, 0:2 * NS], env.a.c_pick)]
        loaded, prep = st.sem("loaded"), st.sem("prep")
        xz_made, xi_kept, z_act, conv, xc_act, xc_made, sz_made, dbc_made, dl_abs, dl_log, dl_made, split, stk_made = (
            st.loop_sem(n) for n in ("xz_made", "xi_kept", "z_act", "conv", "xc_act", "xc_made", "sz_made",
                                     "dbc_made", "dl_abs", "dl_log", "dl_made", "split", "stk_made"))
        bc_made, da_made, dbu_made, h_made, hc_made, y_added, y_made, y_step, y_ready, out_made, added = (
            st.loop_sem(n) for n in ("bc_made", "da_made", "dbu_made", "h_made", "hc_made", "y_added", "y_made",
                                     "y_step", "y_ready", "out_made", "added"))
        xc_act2, sz_half, dstep = (st.loop_sem(n) for n in ("xc_act2", "sz_half", "dstep"))
        CB, WDT, BDT, DP = range(4)
        by_batch = lambda ap: ap.rearrange("p (b t) -> p b t", t=S)
        with nc.Block() as block:
            @block.gpsimd
            def _(pool):
                st.open(pool)

            @block.sync
            def _(sp):
                for d, s_ in loads:
                    sp.dma_start(d, s_).then_inc(loaded, 16)

            @block.tensor
            def _(pe):
                pe.wait_ge(st.opened, 1)
                pe.wait_ge(loaded, 16 * len(loads))
                pe.wait_ge(prep, 3)
                with pe.Fori(0, GROUPS) as g:
                    pe.wait_ge(added, before(g))
                    x = env.XNT[:, bass.ds(g * 512, 512)]
                    for c in range(NC):
                        pe.matmul(pX[c][:, :], w_in[:, c * P:(c + 1) * P], x)
                        last = pe.matmul(pZ[c][:, :], w_in[:, (2 + c) * P:(3 + c) * P], x)
                    last.then_inc(xz_made, 1)
                    pe.wait_ge(xc_made, made(2 * g + 1))
                    for c in range(NC):
                        pe.matmul(pX[0][:, :], w_dt_raw[:, c, :], xc[:, c, :], start=c == 0, stop=c == 1)
                    for c in range(NC):
                        last = pe.matmul(pX[1][0:96, :], w_bc[:, c, :], xc[:, c, :], start=c == 0, stop=c == 1)
                    last.then_inc(dbc_made, 1)
                    pe.wait_ge(stk_made, made(g))
                    pe.wait_ge(sz_made, made(2 * g + 1))
                    for n in range(NS + 1):
                        if n < NS:
                            pe.wait_ge(hc_made, before(g * NS * NC + max(n - 1, 0) * NC))
                            pe.matmul(pBn[n % 2][:, :], sel[:, n, :], stk[:, :])
                            pe.matmul(pCn[n % 2][:, :], sel[:, NS + n, :], stk[:, :]).then_inc(bc_made, 1)
                        if n >= 1:
                            for c in range(NC):
                                k = (n - 1) * NC + c
                                pe.wait_ge(hc_made, made(g * NS * NC + k))
                                last = pe.matmul(pZ[c][:, :], env.ident[:, :], hc[:, c, :], start=n == 1,
                                                 stop=n == NS).then_inc(y_added, 1)
                    pe.wait_ge(y_ready, made(g))
                    for t in range(TG):
                        for c in range(NC):
                            last = pe.matmul(pX[0][:, t * D:(t + 1) * D], dx[:, c, t * P:(t + 1) * P],
                                             w_out[:, c, :], start=c == 0, stop=c == 1)
                    last.then_inc(out_made, 1)

            @block.scalar
            def _(act):
                act.wait_ge(st.opened, 1)
                act.wait_ge(loaded, 16 * len(loads))
                act.activation(A[:, :, :], A[:, :, :], ACT.Exp).then_inc(prep, 1)
                act.wait_ge(prep, 3)
                with act.Fori(0, GROUPS) as g:
                    act.wait_ge(xz_made, made(g))
                    for c in range(NC):
                        act.activation(xi[:, c, :], pX[c][:, :], ACT.Copy).then_inc(xi_kept, 1)
                    for c in range(NC):
                        act.activation(sz[:, c, :], pZ[c][:, :], ACT.Tanh, scale=0.5).then_inc(z_act, 1)
                    for c in range(NC):
                        act.wait_ge(conv, 5 * (2 * g + c) + 6)
                        act.activation(th[:, c, :], acc[:, c, :], ACT.Tanh, scale=0.5).then_inc(xc_act, 1)
                    act.wait_ge(dbc_made, made(g))
                    for c in range(NC):
                        act.activation(ab[:, c, :], pX[0][:, :], ACT.Abs, scale=cols[:, c, WDT:WDT + 1],
                                       bias=cols[:, c, BDT:BDT + 1]).then_inc(dl_abs, 1)
                        act.wait_ge(dl_abs, 4 * g + 2 * c + 2)
                        act.activation(ab[:, c, :], ab[:, c, :], ACT.Exp, scale=-1.0).then_inc(dl_abs, 1)
                    act.wait_ge(dl_abs, 4 * g + 5)
                    for c in range(NC):
                        act.activation(lg[:, c, :], ab[:, c, :], ACT.Ln, bias=env.ones[:, 0:1]).then_inc(dl_log, 1)
                    act.wait_ge(dl_made, made(g))
                    for n in range(NS):
                        for c in range(NC):
                            k = n * NC + c
                            act.wait_ge(h_made, before(g * NS * NC + max(k - 1, 0)))
                            act.activation(dA[:, c, :], dl[:, c, :], ACT.Exp, scale=A[:, c, n:n + 1]
                                           ).then_inc(da_made, 1)

            @block.vector
            def _(dve):
                dve.wait_ge(st.opened, 1)
                dve.wait_ge(loaded, 16 * len(loads))
                dve.tensor_copy(sel[:, :, :], bc(sel_f[:, 0:2 * NS], 2, P)).then_inc(prep, 1)
                dve.wait_ge(prep, 2)
                dve.tensor_scalar(A[:, :, :], A[:, :, :], -1.0, None, ALU.mult).then_inc(prep, 1)
                with dve.Fori(0, GROUPS) as g:
                    for c in range(NC):
                        dve.wait_ge(xi_kept, made(2 * g + c))
                        dve.tensor_scalar(acc[:, c, :], xi[:, c, :], conv_w[:, c, 3:4], cols[:, c, CB:CB + 1],
                                          ALU.mult, ALU.add).then_inc(conv, 1)
                        for s in range(1, 4):
                            dve.wait_ge(conv, 5 * (2 * g + c) + 1 + s)
                            dve.scalar_tensor_tensor(
                                out=by_batch(acc[:, c, :])[:, :, s:S], in0=by_batch(xi[:, c, :])[:, :, 0:S - s],
                                scalar=conv_w[:, c, 3 - s:4 - s], in1=by_batch(acc[:, c, :])[:, :, s:S],
                                op0=ALU.mult, op1=ALU.add).then_inc(conv, 1)
                        dve.wait_ge(conv, 5 * (2 * g + c) + 5)
                        dve.sem_inc(conv, 1)
                    for c in range(NC):
                        dve.wait_ge(xc_act, made(2 * g + c))
                        dve.tensor_scalar(th[:, c, :], th[:, c, :], 0.5, 0.5, ALU.mult, ALU.add).then_inc(xc_act2, 1)
                        dve.wait_ge(xc_act2, made(2 * g + c))
                        dve.tensor_tensor(xc[:, c, :], acc[:, c, :], th[:, c, :], ALU.mult).then_inc(xc_made, 1)
                    for c in range(NC):
                        dve.wait_ge(z_act, made(2 * g + 1))
                        dve.tensor_scalar(sz[:, c, :], sz[:, c, :], 0.5, 0.5, ALU.mult, ALU.add).then_inc(sz_half, 1)
                        dve.wait_ge(sz_half, made(2 * g + c))
                        dve.tensor_tensor(sz[:, c, :], pZ[c][:, :], sz[:, c, :], ALU.mult).then_inc(sz_made, 1)
                    dve.wait_ge(dbc_made, made(g))
                    src = pX[1]
                    for r, parts in ((0, 1), (32, 2), (64, 3)):
                        rows = slice(r, r + 32)
                        dve.tensor_copy(stk[rows, :], src[rows, :]).then_inc(split, 1)
                        base = 9 * g + {0: 0, 32: 1, 64: 4}[r]
                        for q in range(1, parts):
                            dve.wait_ge(split, base + 2 * (q - 1) + 2)
                            if q == 1:
                                dve.tensor_tensor(r1[rows, :], src[rows, :], stk[rows, :], ALU.subtract
                                                  ).then_inc(split, 1)
                            else:
                                dve.tensor_tensor(r1[rows, :], r1[rows, :], stk[rows, :], ALU.subtract
                                                  ).then_inc(split, 1)
                            dve.wait_ge(split, base + 2 * (q - 1) + 3)
                            dve.tensor_copy(stk[rows, :], r1[rows, :]).then_inc(split, 1)
                    dve.wait_ge(split, 9 * g + 10)
                    dve.sem_inc(stk_made, 1)
                    dve.wait_ge(dl_log, made(2 * g + 1))
                    for c in range(NC):
                        dve.tensor_scalar(dl[:, c, :], pX[0][:, :], cols[:, c, WDT:WDT + 1], cols[:, c, BDT:BDT + 1],
                                          ALU.mult, ALU.add).then_inc(dstep, 1)
                    for c in range(NC):
                        dve.wait_ge(dstep, 8 * g + c + 2)
                        dve.tensor_scalar(dl[:, c, :], dl[:, c, :], 0.0, None, ALU.max).then_inc(dstep, 1)
                    for c in range(NC):
                        dve.wait_ge(dstep, 8 * g + c + 4)
                        dve.tensor_tensor(dl[:, c, :], dl[:, c, :], lg[:, c, :], ALU.add).then_inc(dstep, 1)
                    for c in range(NC):
                        dve.wait_ge(dstep, 8 * g + c + 6)
                        dve.tensor_tensor(dx[:, c, :], dl[:, c, :], xc[:, c, :], ALU.mult).then_inc(dstep, 1)
                    dve.wait_ge(dstep, 8 * g + 9)
                    dve.memset(dl[:, :, :].rearrange("p c (b t) -> p (c b) t", t=S)[:, :, 0:1], BIG
                               ).then_inc(dl_made, 1)
                    for n in range(NS):
                        dve.wait_ge(bc_made, made(g * NS + n))
                        for c in range(NC):
                            k = g * NS * NC + n * NC + c
                            dve.tensor_tensor(dbu[:, c, :], dx[:, c, :], pBn[n % 2][:, :], ALU.mult
                                              ).then_inc(dbu_made, 1)
                        for c in range(NC):
                            k = g * NS * NC + n * NC + c
                            dve.wait_ge(dbu_made, made(k))
                            dve.wait_ge(da_made, made(k))
                            dve.tensor_tensor_scan(hh[:, c, :], dA[:, c, :], dbu[:, c, :], 0.0, ALU.mult, ALU.add
                                                   ).then_inc(h_made, 1)
                        for c in range(NC):
                            k = g * NS * NC + n * NC + c
                            dve.wait_ge(h_made, made(k))
                            dve.wait_ge(y_added, before(g * NS * NC + max(n * NC + c - 1, 0)))
                            dve.tensor_tensor(hc[:, c, :], hh[:, c, :], pCn[n % 2][:, :], ALU.mult
                                              ).then_inc(hc_made, 1)
                    for c in range(NC):
                        dve.wait_ge(y_added, made((g + 1) * NS * NC - 2 + c))
                        dve.scalar_tensor_tensor(out=xc[:, c, :], in0=xc[:, c, :], scalar=cols[:, c, DP:DP + 1],
                                                 in1=pZ[c][:, :], op0=ALU.mult, op1=ALU.add).then_inc(y_step, 1)
                    for c in range(NC):
                        dve.wait_ge(y_step, made(2 * g + c))
                        last = dve.tensor_tensor(dx[:, c, :], xc[:, c, :], sz[:, c, :], ALU.mult)
                    last.then_inc(y_ready, 1)
                    dve.wait_ge(out_made, made(g))
                    x = env.X[:, bass.ds(g * TG, TG), :]
                    dve.tensor_tensor(x, x, pX[0][:, :].rearrange("p (t d) -> p t d", d=D), ALU.add
                                      ).then_inc(added, 1)


def l2_attn(nc, env, a):
    normalise(nc, env, "l2a_ln", env.X, dst_t=env.XNT)
    selective_scan(nc, env, "l2a", a)


def two_way_cross(nc, env, title, a, QC, QP, KC):
    SUB = 2 * S
    SC = D ** -0.5
    with stage(nc, title) as st:
        wqs, wvs, wvc, wg = st.sb("wqs", [P, D]), st.sb("wvs", [P, D]), st.sb("wvc", [P, D]), st.sb("wg", [P, 2 * D])
        cols = st.sb("cols", [P, 5])
        interp, m4q, m2 = st.sb("interp", [P, S]), st.sb("m4q", [P, 4]), st.sb("m2", [P, 2, 4])
        xs, qc, qp, kc = (st.sb(n, [P, 2, P]) for n in ("xs", "qc", "qp", "kc"))
        ctx = st.sb("ctx", [P, 2, BT, KEYS])
        ctn = st.sb("ctn", [CH, 2, BT, 3, D])
        sub = st.sb("sub", [P, 2, BT * SUB])
        qs = st.sb("qs", [P, 2, BT * SUB])
        v = st.sb("v", [P, 2, D])
        qbk = st.sb("qbk", [P, 2, 1])
        p1 = st.sb("p1", [P, 2, KPAD])
        p1T = st.sb("p1T", [CH, 2, 3, P])
        m1, n1, s1, r1 = (st.sb(n, [P, 2, 1]) for n in ("m1", "n1", "s1", "r1"))
        p2 = st.sb("p2", [P, 2, 2, S])
        mx2, nmx2, sm2, rs2 = (st.sb(n, [P, 2, 2]) for n in ("mx2", "nmx2", "sm2", "rs2"))
        rm2 = st.sb("rm2", [P, 2, 2, 4])
        p2m = st.sb("p2m", [P, 2, 2, 4, S])
        pib = st.sb("pib", [P, 2, 4, S])
        cn, cT, c2s, s2c, gt, o = (st.sb(n, [P, 2, P]) for n in ("cn", "cT", "c2s", "s2c", "gt", "o"))
        pA, pS, pS2, pT, pC, pX, pG = (st.ps(n, [P, 512]) for n in ("pA", "pS", "pS2", "pT", "pC", "pX", "pG"))
        BQS, BKS, BVS, BVC, BG_ = range(5)
        loads = [(wqs[:, :], a.L3_xattn_Wq_s), (wvs[:, :], a.L3_xattn_Wv_s), (wvc[:, :], a.L3_xattn_Wv_c),
                 (wg[:, :], a.L3_xattn_Wg), (cols[:, :], a.L3_xattn_cols), (interp[:, :], a.c_interp),
                 (m4q[:, :], a.c_m4q), (m2[:, :, :], a.c_pair.rearrange("p (a b) -> p a b", a=2))]
        loaded, prep = st.sem("loaded"), st.sem("prep")
        names = ("landed", "tokens", "proj", "q_kept", "kept", "s_made", "shifted", "m_made", "n_made", "p_made",
                 "s2_made", "m2_made", "n2_made", "p2_made", "turned", "t_kept", "c_made", "r_made", "c_kept",
                 "ct_made", "ct_kept", "c2s_made", "c2s_kept", "r2_made", "rm_made", "p2m_made", "pi_made", "pib_made",
                 "s2c_made", "s2c_kept", "g_made", "g_kept", "mix", "o_made", "finished")
        q = Names(**{n: st.pair(n) for n in names})
        with nc.Block() as block:
            @block.gpsimd
            def _(pool):
                st.open(pool)
                pool.memset(ctn[:, :, :, 2, :], 0.0)
                pool.memset(p1[:, :, KEYS:KPAD], 0.0).then_inc(prep, 1)

            @block.sync
            def _(sp):
                for d, s_ in loads:
                    sp.dma_start(d, s_).then_inc(loaded, 16)
                sp.wait_ge(prep, 1)
                with sp.Fori(0, TILES // 2) as i:
                    for s in range(2):
                        n = 2 * i + s
                        sp.wait_ge(q.c_made[s], before(i))
                        sp.dma_start(ctx[:, s].rearrange("p b k -> p (b k)"),
                                     a.ctx_t[:, bass.ds(n * BT * KEYS, BT * KEYS)]).then_inc(q.landed[s], 16)
                        sp.dma_start(sub[:, s, :], a.ctx_sub[:, bass.ds(n * BT * SUB, BT * SUB)]
                                     ).then_inc(q.landed[s], 16)
                        rows = a.ctx_n[bass.ds(n * BT, BT)]
                        for c, k in ((0, CH), (1, CH), (2, KEYS - 2 * CH)):
                            sp.dma_start(ctn[0:k, s, :, c, :],
                                         rows[:, c * CH:c * CH + k, :].rearrange("b k d -> k b d")
                                         ).then_inc(q.landed[s], 16)

            @block.scalar
            def _(act):
                act.wait_ge(loaded, 16 * len(loads))
                act.wait_ge(prep, 2)
                with act.Fori(0, TILES // 2) as i:
                    for s in range(2):
                        n = 2 * i + s
                        act.wait_ge(q.s2_made[s], before(i))
                        act.activation(xs[:, s, :], env.XNT[:, bass.ds(n * P, P)], ACT.Copy)
                        act.activation(qc[:, s, :], QC[:, bass.ds(n * P, P)], ACT.Copy)
                        act.activation(qp[:, s, :], QP[:, bass.ds(n * P, P)], ACT.Copy)
                        act.activation(kc[:, s, :], KC[:, bass.ds(n * P, P)], ACT.Copy).then_inc(q.tokens[s], 1)
                    for s in range(2):
                        act.wait_ge(q.proj[s], made(i))
                        act.activation(qs[:, s, :], pA[:, 0:BT * SUB], ACT.Identity, bias=cols[:, BQS:BQS + 1]
                                       ).then_inc(q.q_kept[s], 1)
                        act.wait_ge(q.finished[s], before(i))
                        act.activation(qbk[:, s, :], pA[:, 256:257], ACT.Copy, scale=SC)
                        act.activation(v[:, s, :], pA[:, 260:260 + D], ACT.Copy).then_inc(q.kept[s], 1)
                    for s in range(2):
                        act.wait_ge(q.n_made[s], made(i))
                        act.activation(p1[:, s, 0:KEYS], pS[:, 0:KEYS], ACT.Exp, bias=n1[:, s, :],
                                       accum_out=s1[:, s, :]).then_inc(q.p_made[s], 1)
                        act.wait_ge(q.n2_made[s], made(i))
                        for r in range(2):
                            last = act.activation(p2[:, s, r, :], pS2[:, r * S:(r + 1) * S], ACT.Exp, scale=SC,
                                                  bias=nmx2[:, s, r:r + 1], accum_out=sm2[:, s, r:r + 1])
                        last.then_inc(q.p2_made[s], 1)
                    for s in range(2):
                        act.wait_ge(q.turned[s], made(i))
                        act.activation(p1T[:, s].rearrange("p c q -> p (c q)"), pT[0:CH, 0:3 * P], ACT.Copy
                                       ).then_inc(q.t_kept[s], 1)
                    for s in range(2):
                        act.wait_ge(q.ct_made[s], made(i))
                        act.activation(cT[:, s, :], pC[:, P:2 * P], ACT.Copy).then_inc(q.ct_kept[s], 1)
                        act.wait_ge(q.c2s_made[s], made(i))
                        act.activation(c2s[:, s, :], pX[:, 0:P], ACT.Identity, bias=cols[:, BVS:BVS + 1]
                                       ).then_inc(q.c2s_kept[s], 1)
                        act.wait_ge(q.s2c_made[s], made(i))
                        act.activation(s2c[:, s, :], pX[:, P:2 * P], ACT.Identity, bias=cols[:, BVC:BVC + 1]
                                       ).then_inc(q.s2c_kept[s], 1)
                    for s in range(2):
                        act.wait_ge(q.g_made[s], made(i))
                        act.activation(gt[:, s, :], pG[:, 0:P], ACT.Tanh, scale=0.5, bias=cols[:, BG_:BG_ + 1]
                                       ).then_inc(q.g_kept[s], 1)

            @block.tensor
            def _(pe):
                pe.wait_ge(loaded, 16 * len(loads))
                with pe.Fori(0, TILES // 2) as i:
                    for s in range(2):
                        pe.wait_ge(q.tokens[s], made(i))
                        pe.wait_ge(q.landed[s], 80 * i + 81)
                        pe.wait_ge(*previous(q.kept, s, i))
                        pe.matmul(pA[:, 0:BT * SUB], wqs[:, :], sub[:, s, :])
                        pe.matmul(pA[:, 256:257], qc[:, s, :], cols[:, BKS:BKS + 1])
                        pe.matmul(pA[:, 260:260 + D], xs[:, s, :], wvc[:, :]).then_inc(q.proj[s], 1)
                    for s in range(2):
                        pe.wait_ge(*previous(q.p_made, s, i))
                        for b in range(BT):
                            last = pe.matmul(pS[b * S:(b + 1) * S, 0:KEYS], qp[:, s, b * S:(b + 1) * S],
                                             ctx[:, s, b, :])
                        last.then_inc(q.s_made[s], 1)
                        pe.wait_ge(q.q_kept[s], made(i))
                        pe.wait_ge(*previous(q.p2_made, s, i))
                        if not s:
                            pe.wait_ge(q.pib_made[1], before(i))
                        for b in range(BT):
                            h = (b % 2) * SUB
                            last = pe.matmul(pS2[h:h + SUB, (b // 2) * S:(b // 2 + 1) * S],
                                             qs[:, s, b * SUB:(b + 1) * SUB], kc[:, s, b * S:(b + 1) * S])
                        last.then_inc(q.s2_made[s], 1)
                    for s in range(2):
                        pe.wait_ge(q.p_made[s], made(i))
                        pe.wait_ge(*previous(q.t_kept, s, i))
                        for c in range(3):
                            last = pe.transpose(pT[0:CH, c * P:(c + 1) * P], p1[:, s, c * CH:(c + 1) * CH],
                                                env.ident[:, :])
                        last.then_inc(q.turned[s], 1)
                        pe.wait_ge(q.t_kept[s], made(i))
                        pe.wait_ge(*((q.c_kept[0], made(i)) if s else (q.ct_kept[1], before(i))))
                        for b in range(BT):
                            for c in range(3):
                                last = pe.matmul(pC[b * S:(b + 1) * S, 0:D], p1T[:, s, c, b * S:(b + 1) * S],
                                                 ctn[:, s, b, c, :], start=c == 0, stop=c == 2)
                        last.then_inc(q.c_made[s], 1)
                    for s in range(2):
                        pe.wait_ge(q.p2m_made[s], made(i))
                        pe.wait_ge(*((q.pib_made[0], made(i)) if s else (q.p2_made[1], made(i))))
                        for r in range(2):
                            last = pe.matmul(pS2[:, 64:64 + S], p2m[:, s, r].rearrange("p b k -> p (b k)"),
                                             interp[:, :], start=r == 0, stop=r == 1)
                        last.then_inc(q.pi_made[s], 1)
                    for s in range(2):
                        pe.wait_ge(q.c_kept[s], made(i))
                        pe.wait_ge(*((q.ct_kept[0], made(i)) if s else (q.c_kept[1], made(i))))
                        pe.transpose(pC[:, P:2 * P], cn[:, s, :], env.ident[:, :]).then_inc(q.ct_made[s], 1)
                        pe.wait_ge(q.ct_kept[s], made(i))
                        pe.wait_ge(*previous(q.s2c_kept, s, i))
                        pe.matmul(pX[:, 0:P], wvs[:, :], cT[:, s, :]).then_inc(q.c2s_made[s], 1)
                        pe.wait_ge(q.pib_made[s], made(i))
                        pe.wait_ge(q.kept[s], made(i))
                        pe.wait_ge(q.c2s_kept[s], made(i))
                        pe.matmul(pX[:, P:2 * P], v[:, s, :], pib[:, s].rearrange("p b k -> p (b k)")
                                  ).then_inc(q.s2c_made[s], 1)
                    for s in range(2):
                        pe.wait_ge(q.s2c_kept[s], made(i))
                        pe.wait_ge(*((q.g_kept[0], made(i)) if s else (q.finished[1], before(i))))
                        pe.matmul(pG[:, 0:P], wg[:, 0:D], c2s[:, s, :], start=True, stop=False)
                        pe.matmul(pG[:, 0:P], wg[:, D:2 * D], s2c[:, s, :], start=False, stop=True
                                  ).then_inc(q.g_made[s], 1)
                    for s in range(2):
                        pe.wait_ge(q.mix[s], 4 * i + 5)
                        pe.wait_ge(*((q.finished[0], made(i)) if s else (q.g_kept[1], made(i))))
                        pe.transpose(pG[:, P:2 * P], o[:, s, :], env.ident[:, :]).then_inc(q.o_made[s], 1)

            @block.vector
            def _(dve):
                dve.wait_ge(loaded, 16 * len(loads))
                dve.wait_ge(prep, 1)
                dve.tensor_scalar(cols[:, BG_:BG_ + 1], cols[:, BG_:BG_ + 1], 0.5, None, ALU.mult).then_inc(prep, 1)
                with dve.Fori(0, TILES // 2) as i:
                    for s in range(2):
                        dve.wait_ge(q.s_made[s], made(i))
                        dve.wait_ge(q.kept[s], made(i))
                        dve.tensor_scalar(pS[:, 0:KEYS], pS[:, 0:KEYS], qbk[:, s, :], None, ALU.add
                                          ).then_inc(q.shifted[s], 1)
                        dve.wait_ge(q.shifted[s], made(i))
                        dve.tensor_reduce(m1[:, s, :], pS[:, 0:KEYS], AX.X, ALU.max).then_inc(q.m_made[s], 1)
                        dve.wait_ge(q.m_made[s], made(i))
                        dve.tensor_scalar(n1[:, s, :], m1[:, s, :], -1.0, None, ALU.mult).then_inc(q.n_made[s], 1)
                        dve.wait_ge(q.s2_made[s], made(i))
                        dve.tensor_reduce(mx2[:, s, :], pS2[:, 0:2 * S].rearrange("p (r k) -> p r k", k=S), AX.X,
                                          ALU.max).then_inc(q.m2_made[s], 1)
                        dve.wait_ge(q.m2_made[s], made(i))
                        dve.tensor_scalar(nmx2[:, s, :], mx2[:, s, :], -SC, None, ALU.mult).then_inc(q.n2_made[s], 1)
                    for s in range(2):
                        dve.wait_ge(q.p2_made[s], made(i))
                        dve.reciprocal(r1[:, s, :], s1[:, s, :])
                        dve.reciprocal(rs2[:, s, :], sm2[:, s, :]).then_inc(q.r2_made[s], 1)
                        dve.wait_ge(q.r2_made[s], made(i))
                        dve.tensor_tensor(rm2[:, s], m2[:, :, :], bc(rs2[:, s, :], 2, 4), ALU.mult
                                          ).then_inc(q.rm_made[s], 1)
                        dve.wait_ge(q.rm_made[s], made(i))
                        dve.tensor_tensor(p2m[:, s], bc(p2[:, s], 2, 4), bc(rm2[:, s], 3, S), ALU.mult
                                          ).then_inc(q.p2m_made[s], 1)
                    for s in range(2):
                        dve.wait_ge(q.c_made[s], made(i))
                        dve.tensor_scalar(cn[:, s, :], pC[:, 0:D], r1[:, s, :], None, ALU.mult).then_inc(q.c_kept[s], 1)
                    for s in range(2):
                        dve.wait_ge(q.pi_made[s], made(i))
                        dve.tensor_tensor(pib[:, s], bc(pS2[:, 64:64 + S], 1, 4), bc(m4q[:, :], 2, S), ALU.mult
                                          ).then_inc(q.pib_made[s], 1)
                    for s in range(2):
                        dve.wait_ge(q.g_kept[s], made(i))
                        dve.tensor_scalar(gt[:, s, :], gt[:, s, :], 0.5, 0.5, ALU.mult, ALU.add).then_inc(q.mix[s], 1)
                        dve.tensor_tensor(c2s[:, s, :], c2s[:, s, :], s2c[:, s, :], ALU.subtract).then_inc(q.mix[s], 1)
                        dve.wait_ge(q.mix[s], 4 * i + 3)
                        dve.tensor_tensor(o[:, s, :], c2s[:, s, :], gt[:, s, :], ALU.mult).then_inc(q.mix[s], 1)
                        dve.wait_ge(q.mix[s], 4 * i + 4)
                        dve.tensor_tensor(o[:, s, :], o[:, s, :], s2c[:, s, :], ALU.add).then_inc(q.mix[s], 1)
                    for s in range(2):
                        dve.wait_ge(q.o_made[s], made(i))
                        x = env.X[:, 2 * i + s, :]
                        dve.tensor_tensor(x, x, pG[:, P:2 * P], ALU.add).then_inc(q.finished[s], 1)


def l3_xattn(nc, env, a):
    normalise(nc, env, "l3x_ln", env.X, dst_t=env.XNT)
    with stage(nc, "l3x") as st:
        QC, QP, KC = (st.sb(n, [P, T]) for n in ("QC", "QP", "KC"))
        head_projection(nc, env, "l3x_q", "plain", a.L3_xattn_Wq_c, env.XNT, QC, GROUPS, 512,
                        bias_d=a.L3_xattn_bq_c)
        head_projection(nc, env, "l3x_p", "plain", a.L3_xattn_Wk_s, QC, QP, GROUPS, 512, scale=D ** -0.5)
        head_projection(nc, env, "l3x_k", "plain", a.L3_xattn_Wk_c, env.XNT, KC, GROUPS, 512,
                        bias_d=a.L3_xattn_bk_c)
        two_way_cross(nc, env, "l3x_att", a, QC, QP, KC)


def layouts(v):
    o = {}
    o["x"] = v["x"].reshape(T, D)
    row = lambda n: v[n].reshape(1, -1)
    col = lambda n: v[n].reshape(-1, 1)
    for n in ("L0_ffn_router_w",):
        o[n] = v[n]
    o["L0_ffn_router_b"] = row("L0_ffn_router_b")
    o["L0_ffn_expert_w"] = v["L0_ffn_expert_w"].transpose(1, 0, 2).reshape(D, EXPERTS * D)
    o["L0_ffn_expert_b"] = v["L0_ffn_expert_b"]
    o["ctx_t"] = v["ctx_1024"].transpose(2, 0, 1).reshape(D, B * KEYS)
    o["mask_pad"] = v["mask_BxS2_if1"]
    for n in ("Wq", "Wk", "Wv", "Wo"):
        o["L0_xattn_" + n] = v["L0_xattn_" + n].T
    o["L1_xattn_Wq"], o["L1_xattn_Wk"] = v["L1_xattn_Wq"], v["L1_xattn_Wk"]
    o["L1_xattn_Wv"], o["L1_xattn_Wp"] = v["L1_xattn_Wv"].T, v["L1_xattn_Wp"].T
    o["L1_xattn_bp"] = row("L1_xattn_bp")
    for n in ("L1_xattn_ln_g", "L1_xattn_ln_b"):
        o[n] = np.tile(v[n], HEADS).reshape(D, 1)
    for n in ("Wq", "Wk", "Wv", "Wo"):
        o["L2_xattn_" + n] = v["L2_xattn_" + n].T
    for n in ("bq", "bk", "bv"):
        o["L2_xattn_" + n] = col("L2_xattn_" + n)
    o["L2_xattn_bo"] = row("L2_xattn_bo")
    o["mask_if"] = np.tile(v["mask_1x1xSxS2_ik0"][0, 0], (BT, 1))
    w, b = v["L3_attn_in_proj_weight"], v["L3_attn_in_proj_bias"]
    for n, k in enumerate("qkv"):
        o["L3_attn_w" + k] = w[n * D:(n + 1) * D].T
        o["L3_attn_b" + k] = b[n * D:(n + 1) * D].reshape((1, D) if k == "v" else (D, 1))
    o["L3_attn_logit"] = np.repeat(v["L3_attn_logit_scale"].reshape(HEADS, 1), HD, axis=0)
    o["L3_attn_head"] = np.repeat(v["L3_attn_head_scale"].reshape(HEADS, 1), HD, axis=0)
    o["L3_attn_out_w"], o["L3_attn_out_b"] = v["L3_attn_out_w"].T, col("L3_attn_out_b")
    wqkv = v["L1_attn_Wqkv"]
    swap = np.arange(D) ^ 1
    for n, k in enumerate("qkv"):
        o["L1_attn_w" + k] = wqkv[:, n * D:(n + 1) * D]
    o["L1_attn_wq2"], o["L1_attn_wk2"] = o["L1_attn_wq"][:, swap], o["L1_attn_wk"][:, swap]
    o["L1_attn_Wo"] = v["L1_attn_Wo"]
    o["L1_attn_ln"] = np.stack([v["L1_attn_" + n] for n in ("ln1_g", "ln1_b", "ln2_g", "ln2_b")], axis=1)
    def mlp(w1, b1, w2):
        w1, b1, w2 = (x if x.ndim == 1 + k else x[None] for x, k in ((w1, 2), (b1, 1), (w2, 2)))
        e, _, h = w1.shape
        return (w1.transpose(1, 0, 2).reshape(D, e * h), b1.reshape(e * h // P, P).T,
                w2.reshape(e, h // P, P, D).transpose(2, 0, 1, 3).reshape(P, e * h // P * D))
    o["L1_attn_W1"], o["L1_attn_b1"], o["L1_attn_W2"] = mlp(v["L1_attn_W1"], v["L1_attn_b1"], v["L1_attn_W2"])
    o["L1_attn_b2"] = row("L1_attn_b2")
    o["L1_ffn_Wr"], o["L1_ffn_br"], o["L1_ffn_b2"] = v["L1_ffn_Wr"], row("L1_ffn_br"), v["L1_ffn_b2"]
    o["L1_ffn_W1"], o["L1_ffn_b1"], o["L1_ffn_W2"] = mlp(v["L1_ffn_W1"], v["L1_ffn_b1"], v["L1_ffn_W2"])
    o["L2_ffn_norm_weight"] = col("L2_ffn_norm_weight")
    o["L2_ffn_router_w"], o["L2_ffn_router_b"] = v["L2_ffn_router_w"].T, row("L2_ffn_router_b")
    o["L2_ffn_fc1_w"], o["L2_ffn_fc1_b"], o["L2_ffn_fc2_w"] = mlp(
        v["L2_ffn_fc1_w"].transpose(0, 2, 1), v["L2_ffn_fc1_b"], v["L2_ffn_fc2_w"].transpose(0, 2, 1))
    o["L2_ffn_fc2_b"] = v["L2_ffn_fc2_b"]
    o["L3_ffn_gate_w"] = v["L3_ffn_gate_w"].T
    o["L3_ffn_down_w"], o["L3_ffn_down_b"], o["L3_ffn_up_w"] = mlp(
        v["L3_ffn_down_w"].reshape(512, D).T, v["L3_ffn_down_b"].reshape(512),
        v["L3_ffn_up_w"].transpose(0, 2, 1).reshape(512, D))
    o["L3_ffn_up_b"] = v["L3_ffn_up_b"]
    o["bits"] = np.tile((1 << np.arange(29, -1, -1)).astype(np.int32), (P, 1))
    o["L0_attn_Wq"] = v["L0_attn_Wq"]
    wkv = v["L0_attn_Wkv"]
    o["L0_attn_wk2"], o["L0_attn_wv"] = np.concatenate([wkv[:, :64], wkv[:, :64]], axis=1), wkv[:, 64:]
    o["L0_attn_Wo"] = v["L0_attn_Wo"].reshape(4, P, D).transpose(1, 0, 2).reshape(P, 4 * D)
    o["L0_attn_ln"] = np.stack([v["L0_attn_norm_w"], v["L0_attn_norm_b"]], axis=1)
    o["L0_attn_out_norm_w"], o["L0_attn_out_norm_b"] = row("L0_attn_out_norm_w"), row("L0_attn_out_norm_b")
    o["L2_attn_W_in"] = v["L2_attn_W_in"]
    chunked = lambda m: m.reshape(2, P, -1).transpose(1, 0, 2).reshape(P, -1)
    wx = v["L2_attn_W_xproj"]
    o["L2_attn_wx0"] = chunked(np.repeat(wx[:, 0:1], P, axis=1))
    o["L2_attn_wbc"] = chunked(np.concatenate([wx[:, 1:33]] * 3, axis=1))
    o["L2_attn_W_out"] = chunked(v["L2_attn_W_out"])
    o["L2_attn_conv_w"] = chunked(v["L2_attn_conv_w"][:, 0, :])
    o["L2_attn_cols"] = chunked(np.stack([v["L2_attn_" + n] for n in ("conv_b", "w_dt", "b_dt", "D_param")], axis=1))
    o["L2_attn_A_log"] = chunked(v["L2_attn_A_log"])
    for n in ("Wq_c", "Wk_c", "Wq_s", "Wv_s", "Wv_c"):
        o["L3_xattn_" + n] = v["L3_xattn_" + n].T
    o["L3_xattn_Wk_s"] = v["L3_xattn_Wk_s"]
    o["L3_xattn_bq_c"], o["L3_xattn_bk_c"] = col("L3_xattn_bq_c"), col("L3_xattn_bk_c")
    o["L3_xattn_Wg"] = v["L3_xattn_Wg"].reshape(D, 2, D).transpose(2, 1, 0).reshape(D, 2 * D)
    o["L3_xattn_cols"] = np.stack([v["L3_xattn_" + n] for n in ("bq_s", "bk_s", "bv_s", "bv_c", "bg")], axis=1)
    o["ctx_n"] = v["ctx_1024"]
    lo, hi, _ = interpolation()
    o["ctx_sub"] = v["ctx_1024"][:, np.concatenate([lo, hi])].transpose(2, 0, 1).reshape(D, B * 2 * S)
    return o


def interpolation():
    pos = (np.arange(S, dtype=np.float32) + np.float32(0.5)) * np.float32(KEYS / S) - np.float32(0.5)
    pos = np.clip(pos, 0.0, KEYS - 1)
    lo = np.floor(pos).astype(np.int32)
    return lo, np.minimum(lo + 1, KEYS - 1), pos - lo


def more_constants(c):
    tok = np.arange(P)
    same = tok[:, None] // S == tok[None, :] // S
    causal = same & (tok[:, None] % S >= tok[None, :] % S)
    c["causal01"] = causal
    c["other_batch"] = np.where(same, 0.0, -BIG)
    c["m4"] = np.equal.outer(tok % 32 // HD, np.arange(4))
    c["m4q"] = np.equal.outer(tok // S, np.arange(4))
    c["selq"] = np.equal.outer(tok % S, np.arange(S))
    head = np.equal.outer(tok // HD, tok // HD)
    c["head_sum"] = head
    c["head_mean"] = head / HD
    c["centre"] = np.eye(P) - head / HD
    c["eps"] = np.full((P, 1), EPS)
    c["causal_add"] = np.where(causal, 0.0, -BIG)
    freq = 10000.0 ** (-(np.arange(0, HD, 2, dtype=np.float32) / np.float32(HD)))
    theta = np.arange(S, dtype=np.float32)[None, :] * freq[tok % HD // 2][:, None].astype(np.float32)
    theta = theta[:, tok % S]
    sign = np.where(tok % 2 == 0, -1.0, 1.0)[:, None]
    c["rope_cos"] = np.concatenate([np.cos(theta) * HD ** -0.5, np.cos(theta)], axis=1)
    c["rope_sin"] = np.concatenate([np.sin(theta) * sign * HD ** -0.5, np.sin(theta) * sign], axis=1)
    chunk = P // EXPERTS
    expert_of = tok // chunk
    c["same_expert"] = np.equal.outer(expert_of, expert_of)
    c["lower_chunk"] = c["same_expert"] & (tok[:, None] < tok[None, :])
    c["spread"] = np.equal.outer(np.arange(EXPERTS), np.arange(512) // 64)
    c["pick"] = np.equal.outer(np.arange(96) % 32, np.arange(32))
    weight = interpolation()[2]
    both = np.concatenate([np.diag(1 - weight), np.diag(weight)])
    c["interp"] = np.tile(both, (2, 1))
    c["pair"] = np.concatenate([np.equal.outer(tok // (2 * S) + 2 * r, np.arange(BT)) for r in range(2)], axis=1)
    c["neg"] = np.full((P, 1), NEG)


def build(nc, a, out):
    with ExitStack() as ctx:
        def sb(name, shape, dt=F32):
            return ctx.enter_context(nc.sbuf_tensor(name, shape, dt))

        env = Names(
            X=sb("X", [P, TILES, D]),
            XNT=sb("XNT", [P, T]),
            ident=sb("ident", [P, P]),
            ones=sb("ones", [P, 512]),
            countdown=sb("countdown", [P, EXPERTS]),
            m4=sb("m4", [P, 4]),
            neg=sb("neg", [P, 1]),
            eps=sb("eps", [P, 1]),
            a=a,
        )
        with stage(nc, "load") as st:
            loaded = st.sem("loaded")
            with nc.Block() as block:
                @block.sync
                def _(sp):
                    sp.dma_start(env.X[:, :, :], a.x.rearrange("(i p) d -> p i d", p=P)).then_inc(loaded, 16)
                    for name in ("ident", "ones", "countdown", "m4", "neg", "eps"):
                        sp.dma_start(env[name][:, :], a["c_" + name]).then_inc(loaded, 16)
                    sp.wait_ge(loaded, 112)
        for layer in LAYERS:
            layer(nc, env, a)
        with stage(nc, "store") as st:
            stored = st.sem("stored")
            with nc.Block() as block:
                @block.sync
                def _(sp):
                    sp.dma_start(out.rearrange("(i p) d -> p i d", p=P), env.X[:, :, :]).then_inc(stored, 16)
                    sp.wait_ge(stored, 16)


LAYERS = [l0_xattn, l0_attn, l0_ffn, l1_xattn, l1_attn, l1_ffn, l2_xattn, l2_attn, l2_ffn, l3_xattn, l3_attn, l3_ffn]


def constants():
    c = {}
    c["ident"] = np.eye(P)
    c["ones"] = np.ones((P, 512))
    c["countdown"] = np.tile(EXPERTS - np.arange(EXPERTS), (P, 1))
    more_constants(c)
    return {"c_" + n: np.ascontiguousarray(v, dtype=np.float32) for n, v in c.items()}


def kernel(**inputs):
    import concourse.bacc as bacc
    from concourse.bass_utils import run_bass_kernel_spmd as run

    arrays = {n: np.ascontiguousarray(v) for n, v in layouts({n: np.asarray(v) for n, v in inputs.items()}).items()}
    arrays.update(constants())
    nc = bacc.Bacc("TRN2", target_bir_lowering=False, num_devices=1)
    a = Names(**{n: nc.dram_tensor(n, v.shape, mybir.dt.from_np(v.dtype), kind="ExternalInput").ap()
                           for n, v in arrays.items()})
    out = nc.dram_tensor("out", (T, D), F32, kind="ExternalOutput").ap()
    build(nc, a, out)
    r = run(nc, [arrays], core_ids=[0])
    return r.results[0]["out"].reshape(B, S, D)
```

```python
from contextlib import ExitStack, contextmanager

import numpy as np
import concourse.bass as bass
from concourse import mybir

P = 128
B, S, D = 128, 32, 128
T = B * S
TILES = T // P
BT = P // S
GROUPS = T // 512
TG = 512 // P
KEYS = 257
CH = 86
KPAD = 3 * CH
HEADS, HD = 16, 8
EXPERTS = 8
CAP = T // EXPERTS
BIG = 1.0e30
NEG = -1.0e9
EPS = 1e-5

F32 = mybir.dt.float32
BF16 = mybir.dt.bfloat16
I32 = mybir.dt.int32
ALU = mybir.AluOpType
ACT = mybir.ActivationFunctionType
AX = mybir.AxisListType


def made(n):
    return n + 2


def before(n):
    return n + 1


def previous(sems, s, i):
    return (sems[0], made(i)) if s else (sems[1], before(i))


class Names(dict):

    __getattr__ = dict.__getitem__


@contextmanager
def stage(nc, title):
    with ExitStack() as ctx:
        sems, primed = [], []
        opened = ctx.enter_context(nc.semaphore(f"{title}_opened"))
        sems.append(opened)

        def sem(name):
            sems.append(ctx.enter_context(nc.semaphore(f"{title}_{name}")))
            return sems[-1]

        def loop_sem(name):
            primed.append(sem(name))
            return primed[-1]

        yield Names(
            sb=lambda name, shape, dt=F32: ctx.enter_context(nc.sbuf_tensor(f"{title}_{name}", shape, dt)),
            ps=lambda name, shape, dt=F32: ctx.enter_context(nc.psum_tensor(f"{title}_{name}", shape, dt)),
            sem=sem,
            loop_sem=loop_sem,
            pair=lambda name: [loop_sem(f"{name}_a"), loop_sem(f"{name}_b")],
            open=lambda pool: [pool.sem_inc(s, 1) for s in primed + [opened]],
            opened=opened,
        )
        with nc.Block() as block:
            @block.gpsimd
            def _(pool):
                for s in sems:
                    pool.sem_clear(s)


def bc(ap, axis, n):
    a = ap.unsqueeze(axis)
    shape = list(a.shape)
    shape[axis] = n
    return a.to_broadcast(shape)


def normalise(nc, env, title, src, dst_t=None, dst=None, gain=None, shift=None, rms=False):
    with stage(nc, title) as st:
        stats = st.sb("stats", [P, TILES, 6])
        mv = st.sb("mv", [P, TILES, 2])
        var = st.sb("var", [P, TILES])
        std = st.sb("std", [P, TILES])
        rstd = st.sb("rstd", [P, TILES])
        stg = st.sb("stg", [P, 2, TG, D])
        pst = [st.ps(f"pst{s}", [P, 512]) for s in range(2)]
        stats_done, mv_done, var_done = st.sem("stats_done"), st.sem("mv_done"), st.sem("var_done")
        std_done, rstd_done = st.sem("std_done"), st.sem("rstd_done")
        norm_done, turned, copied, kept = st.pair("norm_done"), st.pair("turned"), st.pair("copied"), st.pair("kept")

        with nc.Block() as block:
            @block.gpsimd
            def _(pool):
                st.open(pool)

            @block.vector
            def _(dve):
                with dve.Fori(0, GROUPS) as g:
                    for t in range(TG):
                        last = dve.bn_stats(stats[:, g * TG + t, :], src[:, g * TG + t, :])
                    last.then_inc(stats_done, 1)
                dve.wait_ge(stats_done, GROUPS)
                for n in range(TILES):
                    last = dve.bn_aggr(mv[:, n, :], stats[:, n, :])
                last.then_inc(mv_done, GROUPS)
                dve.wait_ge(mv_done, GROUPS)
                if rms:
                    dve.tensor_tensor(std[:, :], mv[:, :, 0], mv[:, :, 0], ALU.mult).then_inc(mv_done, 1)
                    dve.wait_ge(mv_done, GROUPS + 1)
                    dve.scalar_tensor_tensor(out=var[:, :], in0=mv[:, :, 1], scalar=EPS, in1=std[:, :],
                                             op0=ALU.add, op1=ALU.add).then_inc(var_done, 1)
                else:
                    dve.tensor_scalar(var[:, :], mv[:, :, 1], EPS, None, ALU.add).then_inc(var_done, 1)
                dve.wait_ge(std_done, 1)
                dve.reciprocal(rstd[:, :], std[:, :]).then_inc(rstd_done, 1)
                dve.wait_ge(rstd_done, 1)
                with dve.Fori(0, GROUPS // 2) as i:
                    for s in range(2):
                        if dst_t is not None:
                            dve.wait_ge(turned[s], before(i))
                        if dst is not None:
                            dve.wait_ge(kept[s], before(i))
                        for t in range(TG):
                            n = (2 * i + s) * TG + t
                            if rms:
                                last = dve.tensor_scalar(stg[:, s, t, :], src[:, n, :], rstd[:, bass.ds(n, 1)], None,
                                                         ALU.mult)
                            else:
                                last = dve.tensor_scalar(stg[:, s, t, :], src[:, n, :], mv[:, n, 0:1],
                                                         rstd[:, bass.ds(n, 1)], ALU.subtract, ALU.mult)
                        last.then_inc(norm_done[s], 1)

            @block.tensor
            def _(pe):
                if dst_t is None:
                    return
                with pe.Fori(0, GROUPS // 2) as i:
                    for s in range(2):
                        pe.wait_ge(norm_done[s], made(i))
                        pe.wait_ge(copied[s], before(i))
                        for t in range(TG):
                            last = pe.transpose(pst[s][:, t * P:(t + 1) * P], stg[:, s, t, :], env.ident[:, :])
                        last.then_inc(turned[s], 1)

            @block.scalar
            def _(act):
                act.wait_ge(var_done, 1)
                act.activation(std[:, :], var[:, :], ACT.Sqrt).then_inc(std_done, 1)
                with act.Fori(0, GROUPS // 2) as i:
                    for s in range(2):
                        g = 2 * i + s
                        if dst is not None:
                            act.wait_ge(norm_done[s], made(i))
                            act.activation(dst[:, bass.ds(g * TG, TG), :], stg[:, s], ACT.Copy).then_inc(kept[s], 1)
                        if dst_t is not None:
                            act.wait_ge(turned[s], made(i))
                            out = dst_t[:, bass.ds(g * 512, 512)]
                            if gain is not None and shift is not None:
                                act.activation(out, pst[s][:, :], ACT.Identity, bias=shift, scale=gain
                                               ).then_inc(copied[s], 1)
                            elif gain is not None:
                                act.activation(out, pst[s][:, :], ACT.Copy, scale=gain).then_inc(copied[s], 1)
                            else:
                                act.activation(out, pst[s][:, :], ACT.Copy).then_inc(copied[s], 1)


def load_all(st, block_sync, pairs, sem):
    for dst, src in pairs:
        block_sync.dma_start(dst, src).then_inc(sem, 16)
    return 16 * len(pairs)


def route(nc, env, title, names, W, WT, kind):
    rw_d, rb_d = names
    with stage(nc, title) as st:
        rw = st.sb("rw", [P, EXPERTS])
        rb = st.sb("rb", [1, EXPERTS])
        xs = st.sb("xs", [P, 2, 512])
        LG = st.sb("LG", [P, TILES, EXPERTS])
        m = st.sb("m", [P, TILES])
        l0 = st.sb("l0", [P, TILES, EXPERTS])
        pr = st.sb("pr", [P, TILES, EXPERTS])
        sm = st.sb("sm", [P, TILES])
        rs = st.sb("rs", [P, TILES])
        pl = [st.ps(f"pl{s}", [P, 512]) for s in range(2)]
        loaded, xs_ready, logits, kept = st.sem("loaded"), st.pair("xs_ready"), st.pair("logits"), st.pair("kept")
        dve_step, exp_done, w_ready, w_turned, w_kept = (st.sem(n) for n in
                                                         ("dve_step", "exp_done", "w_ready", "w_turned", "w_kept"))
        with nc.Block() as block:
            @block.gpsimd
            def _(pool):
                st.open(pool)

            @block.sync
            def _(sp):
                sp.dma_start(rw[:, :], rw_d).then_inc(loaded, 16)
                sp.dma_start(rb[:, :], rb_d).then_inc(loaded, 16)

            @block.scalar
            def _(act):
                with act.Fori(0, GROUPS // 2) as i:
                    for s in range(2):
                        act.wait_ge(logits[s], before(i))
                        act.activation(xs[:, s, :], env.XNT[:, bass.ds((2 * i + s) * 512, 512)], ACT.Copy
                                       ).then_inc(xs_ready[s], 1)
                if kind != "one":
                    act.wait_ge(dve_step, 2)
                    act.activation(l0[:, :, :], l0[:, :, :], ACT.Exp).then_inc(exp_done, 1)
                for g in range(GROUPS):
                    act.wait_ge(w_turned, g + 1)
                    act.activation(WT[:, g * 512:(g + 1) * 512], pl[g % 2][0:EXPERTS, :], ACT.Copy).then_inc(w_kept, 1)

            @block.tensor
            def _(pe):
                pe.wait_ge(loaded, 32)
                with pe.Fori(0, GROUPS // 2) as i:
                    for s in range(2):
                        pe.wait_ge(xs_ready[s], made(i))
                        pe.wait_ge(kept[s], before(i))
                        for t in range(TG):
                            o = pl[s][:, t * EXPERTS:(t + 1) * EXPERTS]
                            pe.matmul(o, xs[:, s, t * P:(t + 1) * P], rw[:, :], start=True, stop=False)
                            last = pe.matmul(o, env.ones[0:1, 0:P], rb[:, :], start=False, stop=True)
                        last.then_inc(logits[s], 1)
                pe.wait_ge(w_ready, 1)
                for g in range(GROUPS):
                    if g >= 2:
                        pe.wait_ge(w_kept, g - 1)
                    for t in range(TG):
                        last = pe.transpose(pl[g % 2][0:EXPERTS, t * P:(t + 1) * P], W[:, g * TG + t, :],
                                            env.ident[:, :])
                    last.then_inc(w_turned, 1)

            @block.vector
            def _(dve):
                with dve.Fori(0, GROUPS // 2) as i:
                    for s in range(2):
                        dve.wait_ge(logits[s], made(i))
                        dve.tensor_copy(LG[:, bass.ds((2 * i + s) * TG, TG), :],
                                        pl[s][:, 0:TG * EXPERTS].rearrange("p (t e) -> p t e", e=EXPERTS)
                                        ).then_inc(kept[s], 1)
                dve.wait_ge(kept[0], before(GROUPS // 2))
                dve.wait_ge(kept[1], before(GROUPS // 2))
                step = [0]

                def done(ins):
                    step[0] += 1
                    ins.then_inc(dve_step, 1)
                    dve.wait_ge(dve_step, step[0])

                done(dve.tensor_reduce(m[:, :], LG[:, :, :], AX.X, ALU.max))
                if kind != "one":
                    done(dve.tensor_tensor(l0[:, :, :], LG[:, :, :], bc(m[:, :], 2, EXPERTS), ALU.subtract))
                    dve.wait_ge(exp_done, 1)
                    done(dve.tensor_reduce(sm[:, :], l0[:, :, :], AX.X, ALU.add))
                    done(dve.reciprocal(rs[:, :], sm[:, :]))
                    done(dve.tensor_tensor(pr[:, :, :], l0[:, :, :], bc(rs[:, :], 2, EXPERTS), ALU.mult))
                    done(dve.tensor_reduce(m[:, :], pr[:, :, :], AX.X, ALU.max))
                    src = pr
                else:
                    src = LG
                if kind == "choice":
                    done(dve.tensor_copy(W[:, :, :], pr[:, :, :]))
                else:
                    first_of_max(dve, done, env, src, m, l0, rs, W)
                if kind == "max":
                    done(dve.tensor_tensor(W[:, :, :], W[:, :, :], bc(m[:, :], 2, EXPERTS), ALU.mult))
                dve.wait_ge(dve_step, step[0])
                dve.sem_inc(w_ready, 1)


def first_of_max(dve, done, env, src, m, tmp, top, hot):
    n = src.shape[1]
    done(dve.tensor_tensor(tmp[:, 0:n, :], src[:, 0:n, :], bc(m[:, 0:n], 2, EXPERTS), ALU.is_equal))
    done(dve.tensor_tensor(tmp[:, 0:n, :], tmp[:, 0:n, :], bc(env.countdown[:, :], 1, n), ALU.mult))
    done(dve.tensor_reduce(top[:, 0:n], tmp[:, 0:n, :], AX.X, ALU.max))
    done(dve.tensor_tensor(hot[:, 0:n, :], tmp[:, 0:n, :], bc(top[:, 0:n], 2, EXPERTS), ALU.is_equal))


def linear_experts(nc, env, title, w_d, b_d, W, WT):
    with stage(nc, title) as st:
        we = st.sb("we", [P, EXPERTS * D])
        be = st.sb("be", [EXPERTS, D])
        xs = st.sb("xs", [P, 2, P])
        ws = st.sb("ws", [EXPERTS, 2, P])
        py = [st.ps(f"py{s}", [P, EXPERTS * D]) for s in range(2)]
        pb = [st.ps(f"pb{s}", [P, 512]) for s in range(2)]
        loaded = st.sem("loaded")
        staged, y_ready, y_used, added = st.pair("staged"), st.pair("y_ready"), st.pair("y_used"), st.sem("added")
        with nc.Block() as block:
            @block.gpsimd
            def _(pool):
                st.open(pool)

            @block.sync
            def _(sp):
                sp.dma_start(we[:, :], w_d).then_inc(loaded, 16)
                sp.dma_start(be[:, :], b_d).then_inc(loaded, 16)

            @block.scalar
            def _(act):
                with act.Fori(0, TILES // 2) as i:
                    for s in range(2):
                        n = 2 * i + s
                        act.wait_ge(y_ready[s], before(i))
                        act.activation(xs[:, s, :], env.XNT[:, bass.ds(n * P, P)], ACT.Copy)
                        act.activation(ws[:, s, :], WT[:, bass.ds(n * P, P)], ACT.Copy).then_inc(staged[s], 1)

            @block.tensor
            def _(pe):
                pe.wait_ge(loaded, 32)
                with pe.Fori(0, TILES // 2) as i:
                    for s in range(2):
                        pe.wait_ge(staged[s], made(i))
                        pe.wait_ge(y_used[s], before(i))
                        for h in range(2):
                            pe.matmul(py[s][:, h * 512:(h + 1) * 512], xs[:, s, :], we[:, h * 512:(h + 1) * 512])
                        pe.matmul(pb[s][:, 0:D], ws[:, s, :], be[:, :]).then_inc(y_ready[s], 1)

            @block.vector
            def _(dve):
                with dve.Fori(0, TILES // 2) as i:
                    for s in range(2):
                        n = 2 * i + s
                        dve.wait_ge(y_ready[s], made(i))
                        x = env.X[:, n, :]
                        dve.tensor_tensor(x, x, pb[s][:, 0:D], ALU.add).then_inc(added, 1)
                        for e in range(EXPERTS):
                            dve.wait_ge(added, n * (EXPERTS + 1) + e + 1)
                            dve.scalar_tensor_tensor(out=x, in0=py[s][:, e * D:(e + 1) * D],
                                                     scalar=W[:, n, e:e + 1], in1=x,
                                                     op0=ALU.mult, op1=ALU.add).then_inc(added, 1)
                        dve.wait_ge(added, (n + 1) * (EXPERTS + 1))
                        dve.sem_inc(y_used[s], 1)


def l0_ffn(nc, env, a):
    normalise(nc, env, "l0f_ln", env.X, dst_t=env.XNT)
    with stage(nc, "l0f") as st:
        W = st.sb("W", [P, TILES, EXPERTS])
        WT = st.sb("WT", [EXPERTS, T])
        route(nc, env, "l0f_route", (a.L0_ffn_router_w, a.L0_ffn_router_b), W, WT, "max")
        linear_experts(nc, env, "l0f_exp", a.L0_ffn_expert_w, a.L0_ffn_expert_b, W, WT)


def gelu_experts(nc, env, title, w, experts, chunks, W=None, WT=None, hidden_scale=None, extra=None):
    EC = experts * chunks
    with stage(nc, title) as st:
        w1, w2 = st.sb("w1", [P, EC * P]), st.sb("w2", [P, EC * D])
        b1 = st.sb("b1", [P, EC])
        b2 = st.sb("b2", [EXPERTS if WT is not None else 1, D])
        hid = st.sb("hid", [P, 2, chunks, 512])
        if WT is not None:
            ws = st.sb("ws", [EXPERTS, 512])
        if hidden_scale is not None:
            raw = st.sb("raw", [P, 4, 512])
        pH = [st.ps(f"pH{j}", [P, 512]) for j in range(4)]
        pY = [st.ps(f"pY{j}", [P, 512]) for j in range(2)]
        pB = st.ps("pB", [P, 512])
        loaded = st.sem("loaded")
        h_made, h_kept, h_ready, y_made, y_used, staged, b_made, b_used = (
            st.loop_sem(n) for n in ("h_made", "h_kept", "h_ready", "y_made", "y_used", "staged", "b_made", "b_used"))
        scaled = hidden_scale is not None
        ready = h_ready if scaled else h_kept
        with nc.Block() as block:
            @block.gpsimd
            def _(pool):
                st.open(pool)

            @block.sync
            def _(sp):
                for d, s_ in ((w1[:, :], w.w1), (b1[:, :], w.b1), (w2[:, :], w.w2), (b2[:, :], w.b2)):
                    sp.dma_start(d, s_).then_inc(loaded, 16)

            @block.tensor
            def _(pe):
                pe.wait_ge(loaded, 64)
                with pe.Fori(0, GROUPS) as g:
                    if WT is not None:
                        pe.wait_ge(staged, made(g))
                    pe.wait_ge(b_used, before(g))
                    for t in range(TG):
                        rows = ws[:, t * P:(t + 1) * P] if WT is not None else env.ones[0:1, 0:P]
                        last = pe.matmul(pB[:, t * D:(t + 1) * D], rows, b2[:, :])
                    last.then_inc(b_made, 1)
                    for e in range(experts + 1):
                        if e < experts:
                            for c in range(chunks):
                                k = e * chunks + c
                                pe.wait_ge(h_kept, before(g * EC + max(k - 3, 0)))
                                pe.matmul(pH[k % 4][:, :], w1[:, k * P:(k + 1) * P],
                                          env.XNT[:, bass.ds(g * 512, 512)]).then_inc(h_made, 1)
                        if e >= 1:
                            y = e - 1
                            pe.wait_ge(ready, made(g * EC + y * chunks + chunks - 1))
                            pe.wait_ge(y_used, before(g * experts + max(y - 1, 0)))
                            for t in range(TG):
                                for c in range(chunks):
                                    k = y * chunks + c
                                    last = pe.matmul(pY[y % 2][:, t * D:(t + 1) * D],
                                                     hid[:, y % 2, c, t * P:(t + 1) * P],
                                                     w2[:, k * D:(k + 1) * D], start=c == 0, stop=c == chunks - 1)
                            last.then_inc(y_made, 1)

            @block.scalar
            def _(act):
                act.wait_ge(loaded, 64)
                with act.Fori(0, GROUPS) as g:
                    if WT is not None:
                        act.wait_ge(b_made, before(g))
                        act.activation(ws[:, :], WT[:, bass.ds(g * 512, 512)], ACT.Copy).then_inc(staged, 1)
                    for k in range(EC):
                        e, c = divmod(k, chunks)
                        act.wait_ge(h_made, made(g * EC + k))
                        if scaled:
                            act.wait_ge(h_ready, before(g * EC))
                            out = raw[:, k % 4, :]
                        else:
                            act.wait_ge(y_made, before(g * experts + max(e - 1, 0)))
                            out = hid[:, e % 2, c, :]
                        act.activation(out, pH[k % 4][:, :], ACT.Gelu, bias=b1[:, k:k + 1]).then_inc(h_kept, 1)

            @block.vector
            def _(dve):
                with dve.Fori(0, GROUPS) as g:
                    xg = env.X[:, bass.ds(g * TG, TG), :]
                    tok = lambda ap: ap.rearrange("p (t d) -> p t d", d=D)
                    dve.wait_ge(b_made, made(g))
                    dve.tensor_tensor(xg, xg, tok(pB[:, :]), ALU.add).then_inc(b_used, 1)
                    dve.wait_ge(b_used, made(g))
                    if scaled:
                        dve.wait_ge(y_made, before(g * experts))
                        for c in range(chunks):
                            dve.wait_ge(h_kept, made(g * EC + c))
                            dve.tensor_tensor(hid[:, 0, c, :].rearrange("p (b s) -> p b s", s=S),
                                              raw[:, c % 4, :].rearrange("p (b s) -> p b s", s=S),
                                              bc(hidden_scale[:, c, bass.ds(g * 16, 16)], 2, S), ALU.mult
                                              ).then_inc(h_ready, 1)
                    for e in range(experts):
                        dve.wait_ge(y_made, made(g * experts + e))
                        dve.wait_ge(y_used, before(g * experts + e))
                        if W is None:
                            last = dve.tensor_tensor(xg, xg, tok(pY[e % 2][:, :]), ALU.add)
                        else:
                            for t in range(TG):
                                x = env.X[:, g * TG + t, :]
                                last = dve.scalar_tensor_tensor(
                                    out=x, in0=pY[e % 2][:, t * D:(t + 1) * D], scalar=W[:, g * TG + t, e:e + 1],
                                    in1=x, op0=ALU.mult, op1=ALU.add)
                        last.then_inc(y_used, 1)
                if extra is not None:
                    dve.wait_ge(y_used, before(GROUPS * experts))
                    dve.tensor_tensor(env.X[:, :, :], env.X[:, :, :], extra[:, :, :], ALU.add)


def weights_by_token(nc, env, title, W, WT, normalised):
    with stage(nc, title) as st:
        sm = st.sb("sm", [P, TILES])
        pw = st.ps("pw", [P, 512])
        turned, kept = st.sem("turned"), st.sem("kept")
        with nc.Block() as block:
            @block.tensor
            def _(pe):
                for n in range(TILES):
                    last = pe.transpose(pw[:, n * EXPERTS:(n + 1) * EXPERTS], WT[:, n * P:(n + 1) * P],
                                        env.ident[0:EXPERTS, 0:EXPERTS])
                last.then_inc(turned, 1)

            @block.vector
            def _(dve):
                dve.wait_ge(turned, 1)
                dve.tensor_copy(W[:, :, :], pw[:, 0:TILES * EXPERTS].rearrange("p (n e) -> p n e", e=EXPERTS)
                                ).then_inc(kept, 1)
                if normalised:
                    dve.wait_ge(kept, 1)
                    dve.tensor_reduce(sm[:, :], W[:, :, :], AX.X, ALU.add).then_inc(kept, 1)
                    dve.wait_ge(kept, 2)
                    dve.tensor_scalar(sm[:, :], sm[:, :], 1e-9, None, ALU.max).then_inc(kept, 1)
                    dve.wait_ge(kept, 3)
                    dve.reciprocal(sm[:, :], sm[:, :]).then_inc(kept, 1)
                    dve.wait_ge(kept, 4)
                    dve.tensor_tensor(W[:, :, :], W[:, :, :], bc(sm[:, :], 2, EXPERTS), ALU.mult)


def weights_by_expert(nc, env, title, W, WT):
    with stage(nc, title) as st:
        pw = [st.ps(f"pw{j}", [EXPERTS, 512]) for j in range(2)]
        turned, kept = st.sem("turned"), st.sem("kept")
        with nc.Block() as block:
            @block.tensor
            def _(pe):
                for g in range(GROUPS):
                    if g >= 2:
                        pe.wait_ge(kept, g - 1)
                    for t in range(TG):
                        last = pe.transpose(pw[g % 2][:, t * P:(t + 1) * P], W[:, g * TG + t, :], env.ident[:, :])
                    last.then_inc(turned, 1)

            @block.scalar
            def _(act):
                for g in range(GROUPS):
                    act.wait_ge(turned, g + 1)
                    act.activation(WT[:, g * 512:(g + 1) * 512], pw[g % 2][:, :], ACT.Copy).then_inc(kept, 1)


def choose_tokens(nc, env, title, WT):
    C = P // EXPERTS
    W_ = T // C
    BITS = 30
    scratch = nc.dram_tensor(f"{title}_scratch", (EXPERTS, T), F32).ap()
    scratch2 = nc.dram_tensor(f"{title}_scratch2", (EXPERTS, T), F32).ap()
    rows = lambda s: s.rearrange("e (c t) -> (e c) t", c=C)
    with stage(nc, title) as st:
        pc, gt, rank = (st.sb(n, [P, W_]) for n in ("pc", "gt", "rank"))
        ones, eq = st.sb("ones", [P, W_]), st.sb("eq", [P, W_])
        same, lower = st.sb("same", [P, P]), st.sb("lower", [P, P])
        bits = st.sb("bits", [P, BITS], I32)
        thr, cand, keep, cnt, need = (st.sb(n, [P, 1]) for n in ("thr", "cand", "keep", "cnt", "need"))
        ps = st.ps("ps", [P, 512])
        moved, landed, written = st.sem("moved"), st.sem("landed"), st.sem("written")
        step, counted, summed = st.loop_sem("step"), st.loop_sem("counted"), st.loop_sem("summed")
        ready, zeroed = st.sem("ready"), st.sem("zeroed")
        with nc.Block() as block:
            @block.gpsimd
            def _(pool):
                st.open(pool)

            @block.sync
            def _(sp):
                sp.dma_start(scratch, WT[:, :]).then_inc(moved, 16)
                sp.wait_ge(moved, 16)
                sp.dma_start(pc[:, :], rows(scratch)).then_inc(landed, 16)
                sp.dma_start(same[:, :], env.a.c_same_expert).then_inc(landed, 16)
                sp.dma_start(lower[:, :], env.a.c_lower_chunk).then_inc(landed, 16)
                sp.dma_start(bits[:, :], env.a.bits).then_inc(landed, 16)
                sp.wait_ge(ready, 1)
                sp.dma_start(rows(scratch2), pc[:, :]).then_inc(written, 16)
                sp.wait_ge(written, 16)
                sp.dma_start(WT[:, :], scratch2).then_inc(written, 16)
                sp.wait_ge(written, 32)

            @block.tensor
            def _(pe):
                pe.wait_ge(st.opened, 1)
                pe.wait_ge(landed, 64)
                with pe.Fori(0, BITS) as k:
                    pe.wait_ge(counted, made(k))
                    pe.matmul(ps[:, 0:1], same[:, :], cnt[:, :]).then_inc(summed, 1)
                pe.wait_ge(counted, made(BITS))
                pe.matmul(ps[:, 0:1], same[:, :], cnt[:, :]).then_inc(summed, 1)
                pe.wait_ge(counted, made(BITS + 1))
                pe.matmul(ps[:, 0:1], lower[:, :], cnt[:, :]).then_inc(summed, 1)

            @block.vector
            def _(dve):
                dve.wait_ge(st.opened, 1)
                dve.memset(thr[:, :], 0.0)
                dve.memset(ones[:, :], 1.0).then_inc(zeroed, 1)
                dve.wait_ge(zeroed, 1)
                dve.wait_ge(landed, 64)
                with dve.Fori(0, BITS) as k:
                    dve.wait_ge(step, 4 * k + 1)
                    dve.tensor_tensor(cand[:, :].bitcast(I32), thr[:, :].bitcast(I32), bits[:, bass.ds(k, 1)],
                                      ALU.bitwise_or).then_inc(step, 1)
                    dve.wait_ge(step, 4 * k + 2)
                    dve.tensor_scalar(gt[:, :], pc[:, :], cand[:, 0:1], None, ALU.is_ge).then_inc(step, 1)
                    dve.wait_ge(step, 4 * k + 3)
                    dve.tensor_reduce(cnt[:, :], gt[:, :], AX.X, ALU.add).then_inc(counted, 1)
                    dve.wait_ge(summed, made(k))
                    dve.tensor_scalar(keep[:, :], ps[:, 0:1], float(CAP), None, ALU.is_ge).then_inc(step, 1)
                    dve.wait_ge(step, 4 * k + 4)
                    dve.scalar_tensor_tensor(out=thr[:, :], in0=cand[:, :], scalar=keep[:, 0:1], in1=thr[:, :],
                                             op0=ALU.mult, op1=ALU.max).then_inc(step, 1)
                dve.wait_ge(step, 4 * BITS + 1)
                dve.tensor_scalar(gt[:, :], pc[:, :], thr[:, 0:1], None, ALU.is_gt).then_inc(step, 1)
                dve.wait_ge(step, 4 * BITS + 2)
                dve.tensor_reduce(cnt[:, :], gt[:, :], AX.X, ALU.add).then_inc(counted, 1)
                dve.wait_ge(summed, made(BITS))
                dve.tensor_scalar(need[:, :], ps[:, 0:1], -1.0, float(CAP), ALU.mult, ALU.add).then_inc(step, 1)
                dve.wait_ge(step, 4 * BITS + 3)
                dve.tensor_scalar(eq[:, :], pc[:, :], thr[:, 0:1], None, ALU.is_equal).then_inc(step, 1)
                dve.wait_ge(step, 4 * BITS + 4)
                dve.tensor_tensor_scan(rank[:, :], ones[:, :], eq[:, :], 0.0, ALU.mult, ALU.add).then_inc(step, 1)
                dve.wait_ge(step, 4 * BITS + 5)
                dve.tensor_copy(cnt[:, :], rank[:, W_ - 1:W_]).then_inc(counted, 1)
                dve.wait_ge(summed, made(BITS + 1))
                dve.tensor_scalar(rank[:, :], rank[:, :], ps[:, 0:1], None, ALU.add).then_inc(step, 1)
                dve.wait_ge(step, 4 * BITS + 6)
                dve.tensor_scalar(rank[:, :], rank[:, :], need[:, 0:1], None, ALU.is_le).then_inc(step, 1)
                dve.wait_ge(step, 4 * BITS + 7)
                dve.tensor_tensor(rank[:, :], rank[:, :], eq[:, :], ALU.mult).then_inc(step, 1)
                dve.wait_ge(step, 4 * BITS + 8)
                dve.tensor_tensor(rank[:, :], rank[:, :], gt[:, :], ALU.add).then_inc(step, 1)
                dve.wait_ge(step, 4 * BITS + 9)
                dve.tensor_tensor(pc[:, :], pc[:, :], rank[:, :], ALU.mult).then_inc(ready, 1)


def l1_attn(nc, env, a):
    with stage(nc, "l1a") as st:
        XN = st.sb("XN", [P, TILES, D])
        ln = st.sb("ln", [P, 4])
        landed = st.sem("landed")
        with nc.Block() as block:
            @block.sync
            def _(sp):
                sp.dma_start(ln[:, :], a.L1_attn_ln).then_inc(landed, 16)
                sp.wait_ge(landed, 16)
        normalise(nc, env, "l1a_ln0", env.X, dst=XN)
        normalise(nc, env, "l1a_ln1", XN, dst_t=env.XNT, gain=ln[:, 0:1], shift=ln[:, 1:2])
        w = Names(wq=a.L1_attn_wq, wk=a.L1_attn_wk, wv=a.L1_attn_wv, wo=a.L1_attn_Wo, wq2=a.L1_attn_wq2,
                            wk2=a.L1_attn_wk2, cos=a.c_rope_cos.rearrange("p (a t) -> p a t", a=2),
                            sin=a.c_rope_sin.rearrange("p (a t) -> p a t", a=2))
        block_attention(nc, env, "l1a_att", w, XN)
        normalise(nc, env, "l1a_ln2", XN, dst_t=env.XNT, gain=ln[:, 2:3], shift=ln[:, 3:4])
        w = Names(w1=a.L1_attn_W1, b1=a.L1_attn_b1, w2=a.L1_attn_W2, b2=a.L1_attn_b2)
        gelu_experts(nc, env, "l1a_mlp", w, 1, 4, extra=XN)


def l1_ffn(nc, env, a):
    normalise(nc, env, "l1f_ln", env.X, dst_t=env.XNT)
    with stage(nc, "l1f") as st:
        W = st.sb("W", [P, TILES, EXPERTS])
        WT = st.sb("WT", [EXPERTS, T])
        route(nc, env, "l1f_route", (a.L1_ffn_Wr, a.L1_ffn_br), W, WT, "one")
        w = Names(w1=a.L1_ffn_W1, b1=a.L1_ffn_b1, w2=a.L1_ffn_W2, b2=a.L1_ffn_b2)
        gelu_experts(nc, env, "l1f_exp", w, EXPERTS, 3, W=W, WT=WT)


def l2_ffn(nc, env, a):
    with stage(nc, "l2f") as st:
        W = st.sb("W", [P, TILES, EXPERTS])
        WT = st.sb("WT", [EXPERTS, T])
        with stage(nc, "l2f_norm") as st2:
            XN = st2.sb("XN", [P, TILES, D])
            gain = st2.sb("gain", [P, 1])
            landed = st2.sem("landed")
            with nc.Block() as block:
                @block.sync
                def _(sp):
                    sp.dma_start(gain[:, :], a.L2_ffn_norm_weight).then_inc(landed, 16)
                    sp.wait_ge(landed, 16)
            normalise(nc, env, "l2f_ln", env.X, dst=XN)
            normalise(nc, env, "l2f_rms", XN, dst_t=env.XNT, gain=gain[:, 0:1], rms=True)
        route(nc, env, "l2f_route", (a.L2_ffn_router_w, a.L2_ffn_router_b), W, WT, "choice")
        choose_tokens(nc, env, "l2f_choose", WT)
        weights_by_token(nc, env, "l2f_byt", W, WT, normalised=True)
        weights_by_expert(nc, env, "l2f_bye", W, WT)
        w = Names(w1=a.L2_ffn_fc1_w, b1=a.L2_ffn_fc1_b, w2=a.L2_ffn_fc2_w, b2=a.L2_ffn_fc2_b)
        gelu_experts(nc, env, "l2f_exp", w, EXPERTS, 4, W=W, WT=WT)


def pooled_gate(nc, env, title, gate_d, WT, wx):
    with stage(nc, title) as st:
        gw, spread = st.sb("gw", [P, EXPERTS]), st.sb("spread", [EXPERTS, 512])
        pooled = st.sb("pooled", [P, B])
        lg, ex, pr, tmp, hot1, hot2, W = (st.sb(n, [P, 1, EXPERTS])
                                          for n in ("lg", "ex", "pr", "tmp", "hot1", "hot2", "W"))
        m, sm, top, g1, g2 = (st.sb(n, [P, 1]) for n in ("m", "sm", "top", "g1", "g2"))
        wT = st.sb("wT", [EXPERTS, P])
        ps = st.ps("ps", [P, 512])
        loaded, dve_step, lg_made, exp_done, w_done, w_turned, wx_made = (
            st.sem(n) for n in ("loaded", "dve_step", "lg_made", "exp_done", "w_done", "w_turned", "wx_made"))
        with nc.Block() as block:
            @block.sync
            def _(sp):
                sp.dma_start(gw[:, :], gate_d).then_inc(loaded, 16)
                sp.dma_start(spread[:, :], env.a.c_spread).then_inc(loaded, 16)

            @block.tensor
            def _(pe):
                pe.wait_ge(loaded, 32)
                pe.wait_ge(dve_step, 2)
                pe.matmul(ps[:, 0:EXPERTS], pooled[:, :], gw[:, :]).then_inc(lg_made, 1)
                pe.wait_ge(w_done, 1)
                pe.transpose(ps[0:EXPERTS, 0:P], W[:, 0, :], env.ident[:, :]).then_inc(w_turned, 1)
                pe.wait_ge(w_done, 3)
                for c in range(4):
                    last = pe.matmul(ps[:, c * P:(c + 1) * P], spread[:, c * P:(c + 1) * P], wT[:, :])
                last.then_inc(wx_made, 1)

            @block.scalar
            def _(act):
                act.wait_ge(dve_step, 5)
                act.activation(ex[:, :, :], lg[:, :, :], ACT.Exp).then_inc(exp_done, 1)

            @block.vector
            def _(dve):
                step = [0]

                def done(ins):
                    step[0] += 1
                    ins.then_inc(dve_step, 1)
                    dve.wait_ge(dve_step, step[0])

                done(dve.tensor_reduce(pooled[:, :], env.XNT[:, :].rearrange("p (b s) -> p b s", s=S), AX.X, ALU.add))
                done(dve.tensor_scalar(pooled[:, :], pooled[:, :], 1.0 / S, None, ALU.mult))
                dve.wait_ge(lg_made, 1)
                done(dve.tensor_copy(lg[:, 0, :], ps[:, 0:EXPERTS]))
                done(dve.tensor_reduce(m[:, :], lg[:, :, :], AX.X, ALU.max))
                done(dve.tensor_scalar(lg[:, 0, :], lg[:, 0, :], m[:, 0:1], None, ALU.subtract))
                dve.wait_ge(exp_done, 1)
                done(dve.tensor_reduce(sm[:, :], ex[:, :, :], AX.X, ALU.add))
                done(dve.reciprocal(sm[:, :], sm[:, :]))
                done(dve.tensor_scalar(pr[:, 0, :], ex[:, 0, :], sm[:, 0:1], None, ALU.mult))
                done(dve.tensor_reduce(g1[:, :], pr[:, :, :], AX.X, ALU.max))
                first_of_max(dve, done, env, pr, g1, tmp, top, hot1)
                done(dve.scalar_tensor_tensor(out=pr[:, 0, :], in0=hot1[:, 0, :], scalar=-2.0, in1=pr[:, 0, :],
                                              op0=ALU.mult, op1=ALU.add))
                done(dve.tensor_reduce(g2[:, :], pr[:, :, :], AX.X, ALU.max))
                first_of_max(dve, done, env, pr, g2, tmp, top, hot2)
                done(dve.scalar_tensor_tensor(out=sm[:, :], in0=g1[:, :], scalar=1e-8, in1=g2[:, :],
                                              op0=ALU.add, op1=ALU.add))
                done(dve.reciprocal(sm[:, :], sm[:, :]))
                done(dve.tensor_scalar(hot1[:, 0, :], hot1[:, 0, :], g1[:, 0:1], None, ALU.mult))
                done(dve.scalar_tensor_tensor(out=hot1[:, 0, :], in0=hot2[:, 0, :], scalar=g2[:, 0:1],
                                              in1=hot1[:, 0, :], op0=ALU.mult, op1=ALU.add))
                dve.tensor_scalar(W[:, 0, :], hot1[:, 0, :], sm[:, 0:1], None, ALU.mult).then_inc(w_done, 1)
                dve.wait_ge(w_turned, 1)
                dve.tensor_copy(wT[:, :], ps[0:EXPERTS, 0:P]).then_inc(w_done, 1)
                dve.wait_ge(w_done, 2)
                dve.tensor_copy(WT[:, :].rearrange("e (b s) -> e b s", s=S), bc(wT[:, :], 2, S)).then_inc(w_done, 1)
                dve.wait_ge(wx_made, 1)
                dve.tensor_copy(wx[:, :, :], ps[:, :].rearrange("p (c b) -> p c b", b=B))


def l3_ffn(nc, env, a):
    normalise(nc, env, "l3f_ln", env.X, dst_t=env.XNT)
    with stage(nc, "l3f") as st:
        WT = st.sb("WT", [EXPERTS, T])
        wx = st.sb("wx", [P, 4, B])
        pooled_gate(nc, env, "l3f_gate", a.L3_ffn_gate_w, WT, wx)
        w = Names(w1=a.L3_ffn_down_w, b1=a.L3_ffn_down_b, w2=a.L3_ffn_up_w, b2=a.L3_ffn_up_b)
        gelu_experts(nc, env, "l3f_exp", w, 1, 4, WT=WT, hidden_scale=wx)


def context_tail_sum(nc, env, title, csum):
    with stage(nc, title) as st:
        ctx = st.sb("ctx", [P, 2, 8, KEYS])
        landed, summed = st.pair("landed"), st.pair("summed")
        with nc.Block() as block:
            @block.gpsimd
            def _(pool):
                st.open(pool)

            @block.sync
            def _(sp):
                with sp.Fori(0, B // 16) as i:
                    for s in range(2):
                        sp.wait_ge(summed[s], before(i))
                        sp.dma_start(ctx[:, s].rearrange("p b k -> p (b k)"), env.a.ctx_t[
                            :, bass.ds((2 * i + s) * 8 * KEYS, 8 * KEYS)]).then_inc(landed[s], 16)

            @block.vector
            def _(dve):
                with dve.Fori(0, B // 16) as i:
                    for s in range(2):
                        dve.wait_ge(landed[s], 16 * i + 17)
                        dve.tensor_reduce(csum[:, bass.ds((2 * i + s) * 8, 8)], ctx[:, s, :, S:KEYS], AX.X, ALU.add
                                          ).then_inc(summed[s], 1)


def add_transposed(nc, env, title, src, res):
    with stage(nc, title) as st:
        stg = st.sb("stg", [P, 2, 512])
        pt = [st.ps(f"pt{s}", [P, 512]) for s in range(2)]
        staged, turned, added = st.pair("staged"), st.pair("turned"), st.pair("added")
        with nc.Block() as block:
            @block.gpsimd
            def _(pool):
                st.open(pool)

            @block.scalar
            def _(act):
                with act.Fori(0, GROUPS // 2) as i:
                    for s in range(2):
                        act.wait_ge(turned[s], before(i))
                        act.activation(stg[:, s, :], src[:, bass.ds((2 * i + s) * 512, 512)], ACT.Copy
                                       ).then_inc(staged[s], 1)

            @block.tensor
            def _(pe):
                with pe.Fori(0, GROUPS // 2) as i:
                    for s in range(2):
                        pe.wait_ge(staged[s], made(i))
                        pe.wait_ge(added[s], before(i))
                        for t in range(TG):
                            last = pe.transpose(pt[s][:, t * P:(t + 1) * P], stg[:, s, t * P:(t + 1) * P],
                                                env.ident[:, :])
                        last.then_inc(turned[s], 1)

            @block.vector
            def _(dve):
                with dve.Fori(0, GROUPS // 2) as i:
                    for s in range(2):
                        dve.wait_ge(turned[s], made(i))
                        x = res[:, bass.ds((2 * i + s) * TG, TG), :]
                        dve.tensor_tensor(x, x, pt[s][:, :].rearrange("p (t d) -> p t d", d=D), ALU.add
                                          ).then_inc(added[s], 1)


def l0_xattn(nc, env, a):
    with stage(nc, "l0x") as st:
        csum = st.sb("csum", [P, B])
        context_tail_sum(nc, env, "l0x_sum", csum)
        normalise(nc, env, "l0x_ln", env.X, dst_t=env.XNT)
        w = Names(wq=a.L0_xattn_Wq, wk=a.L0_xattn_Wk, wv=a.L0_xattn_Wv, wo=a.L0_xattn_Wo)
        block_attention(nc, env, "l0x_att", w, env.X, csum=csum)


def run_slots(eng, slot, units, first=-2, last=2):
    low, high = last, units + first
    high -= (high - low) % 2
    for n in range(first, low):
        slot(n, n % 2)
    with eng.Fori(0, (high - low) // 2) as i:
        slot(2 * i + low, low % 2)
        slot(2 * i + low + 1, (low + 1) % 2)
    for n in range(high, units + last):
        slot(n, n % 2)


def after(eng, sem, n):
    if not isinstance(n, int) or n >= 0:
        eng.wait_ge(sem, made(n))


def block_attention(nc, env, title, w, res, csum=None):
    cross = csum is not None
    units = TILES
    with stage(nc, title) as st:
        wq, wk, wv, wo = (st.sb(n, [P, D]) for n in ("wq", "wk", "wv", "wo"))
        own_group = st.sb("own_group", [P, 4])
        causal = st.sb("causal", [P, S])
        xs = st.sb("xs", [P, 2, BT, 4, S])
        qk = st.sb("qk", [P, 2, 2, P])
        qb, kb = st.sb("qb", [P, 2, BT, 4, S]), st.sb("kb", [P, 2, BT, 4, S])
        v = st.sb("v", [P, 2, BT, D])
        prob, probT = st.sb("prob", [P, 2, BT * 4, S]), st.sb("probT", [P, 2, BT, P])
        mx, sums, rs = (st.sb(n, [P, 2, BT * 4]) for n in ("mx", "sums", "rs"))
        own, oT = st.sb("own", [P, BT, 4, S]), st.sb("oT", [P, 2, P])
        loads = [(wq[:, :], w.wq), (wk[:, :], w.wk), (wv[:, :], w.wv), (wo[:, :], w.wo),
                 (own_group[:, :], env.a.c_m4q), (causal[:, :], env.a.c_causal_q01 if cross else env.a.c_causal_q_add)]
        if cross:
            kvs = st.sb("kvs", [P, 2, BT, S])
            cs = st.sb("cs", [P, 2, BT, 4])
            keep_i = st.sb("keep_i", [P, B, S], I32)
            keep, fill = st.sb("keep", [P, B, S]), st.sb("fill", [P, B, S])
            tail = st.sb("tail", [P, 2, BT * 4])
            vs, tailT = st.sb("vs", [16, 2, D]), st.sb("tailT", [16, 2, BT, P])
            group16, batch16 = st.sb("group16", [16, D]), st.sb("batch16", [16, BT])
            loads += [(keep_i[:, :, :], env.a.mask_pad[:, 0:S].unsqueeze(0).to_broadcast([P, B, S])),
                      (group16[:, :], env.a.c_group16), (batch16[:, :], env.a.c_batch16)]
        else:
            wq2, wk2 = st.sb("wq2", [P, D]), st.sb("wk2", [P, D])
            cos, sin = st.sb("cos", [P, 2, P]), st.sb("sin", [P, 2, P])
            t1, t2 = st.sb("t1", [P, 2, 2, P]), st.sb("t2", [P, 2, 2, P])
            loads += [(wq2[:, :], w.wq2), (wk2[:, :], w.wk2), (cos[:, :, :], w.cos), (sin[:, :, :], w.sin)]
        pA, pV, pT, pO, pX, pE = (st.ps(n, [P, 512]) for n in ("pA", "pV", "pT", "pO", "pX", "pE"))
        pS = [st.ps(f"pS{s}", [P, 512]) for s in range(2)]
        loaded, zeroed, keep_step = st.sem("loaded"), st.sem("zeroed"), st.sem("keep_step")
        landed = st.pair("landed")
        (xs_ready, qk_made, qk_read, qk_ready, kb_made, v_made, v_kept, s_made, score_step, m_made, shifted, p_made,
         sums_made, rs_made, p_scaled, t_made, t_kept, e_made, e_kept, o_made, own_made, ot_made, out_made, added, kept,
         cs_ready) = (
            st.loop_sem(n) for n in (
                "xs_ready", "qk_made", "qk_read", "qk_ready", "kb_made", "v_made", "v_kept", "s_made", "score_step",
                "m_made", "shifted", "p_made", "sums_made", "rs_made", "p_scaled", "t_made", "t_kept", "e_made",
                "e_kept", "o_made", "own_made", "ot_made", "out_made", "added",
                "kept", "cs_ready"))

        def inside(n):
            return not isinstance(n, int) or 0 <= n < units

        def landed_count(n, s):
            return 16 * ((n - s) // 2) + 17 if isinstance(n, int) else 8 * (n - s) + 17

        with nc.Block() as block:
            @block.gpsimd
            def _(pool):
                st.open(pool)
                pool.memset(v[:, :, :, :], 0.0).then_inc(zeroed, 1)
                pool.wait_ge(loaded, 16 * len(loads))

                def keys(n, s):
                    if cross:
                        pool.wait_ge(qk_ready, made(n))
                    else:
                        pool.wait_ge(qk_read, made(n))
                        after(pool, kb_made, n - 2)
                        pool.tensor_tensor(qk[:, s], t1[:, s], t2[:, s], ALU.add).then_inc(qk_ready, 1)
                        pool.wait_ge(qk_ready, made(n))
                    after(pool, s_made, n - 2)
                    q, k = (qk[:, s, u, :].rearrange("p (b t) -> p b t", t=S) for u in range(2))
                    pool.tensor_tensor(qb[:, s], bc(q, 2, 4), bc(bc(env.m4[:, :], 1, BT), 3, S), ALU.mult)
                    pool.tensor_tensor(kb[:, s], bc(k, 2, 4), bc(bc(own_group[:, :], 1, BT), 3, S), ALU.mult
                                       ).then_inc(kb_made, 1)

                def slot(n, s):
                    if inside(n + 2):
                        keys(n + 2, s)

                run_slots(pool, slot, units)

            @block.sync
            def _(sp):
                for dst, src in loads:
                    sp.dma_start(dst, src).then_inc(loaded, 16)
                if cross:
                    def load(n, s):
                        after(sp, v_made, n - 2)
                        after(sp, xs_ready, n - 2)
                        sp.dma_start(kvs[:, s], env.a.ctx_t.rearrange("d (b k) -> d b k", k=KEYS)[
                            :, bass.ds(n * BT, BT), 0:S]).then_inc(landed[s], 16)

                    load(0, 0)
                    load(1, 1)
                    with sp.Fori(0, units // 2 - 1) as i:
                        for s in range(2):
                            load(2 * i + s + 2, s)

            @block.tensor
            def _(pe):
                pe.wait_ge(loaded, 16 * len(loads))
                pe.wait_ge(st.opened, 1)

                def project(n, s):
                    after(pe, qk_ready if cross else qk_read, n - 1)
                    x = env.XNT[:, bass.ds(n * P, P)]
                    if cross:
                        pe.wait_ge(landed[s], landed_count(n, s))
                        kv = kvs[:, s].rearrange("p b k -> p (b k)")
                        pe.matmul(pA[:, 0:P], wq[:, :], x)
                        pe.matmul(pA[:, P:2 * P], wk[:, :], kv).then_inc(qk_made, 1)
                    else:
                        for u, wt in enumerate((wq, wk, wq2, wk2)):
                            last = pe.matmul(pA[:, u * P:(u + 1) * P], wt[:, :], x)
                        last.then_inc(qk_made, 1)
                    after(pe, v_kept, n - 1)
                    pe.wait_ge(xs_ready, made(n))
                    for b in range(BT):
                        last = pe.matmul(pV[:, b * D:(b + 1) * D], xs[:, s, b].rearrange("p j k -> p (j k)"),
                                         wv[:, :])
                    last.then_inc(v_made, 1)

                def scores(n, s):
                    pe.wait_ge(kb_made, made(n))
                    after(pe, shifted, n - 2)
                    for b in range(BT):
                        last = pe.matmul(pS[s][:, b * P:(b + 1) * P], qb[:, s, b].rearrange("p h q -> p (h q)"),
                                         kb[:, s, b].rearrange("p j k -> p (j k)"))
                    last.then_inc(s_made, 1)

                def turn(n, s):
                    pe.wait_ge(p_scaled, made(n))
                    after(pe, t_kept, n - 1)
                    for b in range(BT):
                        last = pe.transpose(pT[:, b * P:(b + 1) * P],
                                            prob[:, s, 4 * b:4 * b + 4, :].rearrange("p j k -> p (j k)"),
                                            env.ident[:, :])
                    last.then_inc(t_made, 1)
                    if cross:
                        after(pe, e_kept, n - 1)
                        pe.wait_ge(cs_ready, made(n))
                        pe.matmul(pE[0:16, 0:D], cs[:, s].rearrange("p b j -> p (b j)"), wv[:, :])
                        pe.transpose(pE[0:16, D:D + P], tail[:, s, :], env.ident[:, :]).then_inc(e_made, 1)

                def attend(n, s):
                    pe.wait_ge(t_kept, made(n))
                    pe.wait_ge(v_kept, made(n))
                    after(pe, own_made, n - 1)
                    if cross:
                        pe.wait_ge(e_kept, made(n))
                        pe.matmul(pO[:, :], vs[:, s, :], tailT[:, s].rearrange("p b q -> p (b q)"), start=True,
                                  stop=False)
                    for b in range(BT):
                        last = pe.matmul(pO[:, b * P:(b + 1) * P], v[:, s, b, :], probT[:, s, b, :],
                                         start=not cross, stop=not cross or b == BT - 1)
                    last.then_inc(o_made, 1)

                def output(n, s):
                    pe.wait_ge(ot_made, made(n))
                    after(pe, added, n - 1)
                    pe.matmul(pX[:, 0:D], oT[:, s, :], wo[:, :]).then_inc(out_made, 1)

                def slot(n, s):
                    if inside(n + 1):
                        scores(n + 1, 1 - s)
                    if inside(n):
                        turn(n, s)
                    if inside(n + 2):
                        project(n + 2, s)
                    if inside(n):
                        attend(n, s)
                    if inside(n - 1):
                        output(n - 1, 1 - s)

                run_slots(pe, slot, units)

            @block.scalar
            def _(act):
                act.wait_ge(zeroed, 1)
                act.wait_ge(st.opened, 1)

                def stage_tokens(n, s):
                    after(act, v_made, n - 2)
                    if cross:
                        act.wait_ge(landed[s], landed_count(n, s))
                        x = kvs[:, s]
                    else:
                        x = env.XNT[:, bass.ds(n * P, P)].rearrange("p (b t) -> p b t", t=S)
                    act.activation(xs[:, s], bc(x, 2, 4), ACT.Copy).then_inc(xs_ready, 1)

                def stage_tail(n, s):
                    after(act, e_made, n - 2)
                    act.activation(cs[:, s], bc(csum[:, bass.ds(n * BT, BT)], 2, 4), ACT.Copy).then_inc(cs_ready, 1)

                def keep_turned(n, s):
                    act.wait_ge(t_made, made(n))
                    after(act, o_made, n - 2)
                    act.activation(probT[:, s].rearrange("p b q -> p (b q)"), pT[:, :], ACT.Copy).then_inc(t_kept, 1)

                def exponentials(n, s):
                    act.wait_ge(shifted, made(n))
                    if cross:
                        after(act, e_made, n - 2)
                        act.activation(tail[:, s, :], mx[:, s, :], ACT.Exp, bias=env.neg[:, 0:1], scale=-1.0)
                    act.activation(prob[:, s], prob[:, s], ACT.Exp).then_inc(p_made, 1)

                def projections(n, s):
                    if cross:
                        act.wait_ge(qk_made, made(n))
                        after(act, kb_made, n - 2)
                        act.activation(qk[:, s, 0, :], pA[:, 0:P], ACT.Copy, scale=HD ** -0.5)
                        act.activation(qk[:, s, 1, :], pA[:, P:2 * P], ACT.Copy).then_inc(qk_ready, 1)

                def values(n, s):
                    act.wait_ge(v_made, made(n))
                    after(act, o_made, n - 2)
                    for j in range(4):
                        r = slice(32 * j, 32 * j + 32)
                        last = act.activation(v[r, s, :, r], pV[r, :].rearrange("p (b f) -> p b f", f=D)[:, :, r],
                                              ACT.Copy)
                    last.then_inc(v_kept, 1)

                def slot(n, s):
                    if inside(n + 2):
                        stage_tokens(n + 2, s)
                    if inside(n):
                        keep_turned(n, s)
                    if inside(n + 2):
                        projections(n + 2, s)
                    if inside(n + 1):
                        exponentials(n + 1, 1 - s)
                    if inside(n + 1) and cross:
                        stage_tail(n + 1, 1 - s)
                    if inside(n + 2):
                        values(n + 2, s)

                run_slots(act, slot, units)

            @block.vector
            def _(dve):
                dve.wait_ge(loaded, 16 * len(loads))
                dve.wait_ge(st.opened, 1)
                if cross:
                    dve.tensor_copy(keep[:, :, :], keep_i[:, :, :]).then_inc(keep_step, 1)
                    dve.wait_ge(keep_step, 1)
                    dve.tensor_scalar(keep[:, :, :], keep[:, :, :], 0.0, None, ALU.not_equal).then_inc(keep_step, 1)
                    dve.wait_ge(keep_step, 2)
                    dve.tensor_tensor(keep[:, :, :], keep[:, :, :], bc(causal[:, :], 1, B), ALU.mult
                                      ).then_inc(keep_step, 1)
                    dve.wait_ge(keep_step, 3)
                    dve.tensor_scalar(fill[:, :, :], keep[:, :, :], -NEG, NEG, ALU.mult, ALU.add
                                      ).then_inc(keep_step, 1)
                    dve.wait_ge(keep_step, 4)

                def scores(n, s):
                    dve.wait_ge(s_made, made(n))
                    sc = pS[s][:, :].rearrange("p (g k) -> p g k", k=S)
                    if cross:
                        sc4 = pS[s][:, :].rearrange("p (b j k) -> p b j k", j=4, k=S)
                        dve.tensor_tensor(sc4, sc4, bc(keep[:, bass.ds(n * BT, BT), :], 2, 4), ALU.mult
                                          ).then_inc(kept, 1)
                        dve.wait_ge(kept, made(n))
                        dve.tensor_tensor(sc4, sc4, bc(fill[:, bass.ds(n * BT, BT), :], 2, 4), ALU.add
                                          ).then_inc(score_step, 1)
                    else:
                        dve.tensor_tensor(sc, sc, bc(causal[:, :], 1, BT * 4), ALU.add).then_inc(score_step, 1)
                    dve.wait_ge(score_step, made(n))
                    after(dve, p_made, n - 2)
                    dve.tensor_reduce(mx[:, s, :], sc, AX.X, ALU.max).then_inc(m_made, 1)
                    if cross:
                        dve.wait_ge(m_made, 2 * n + 2)
                        dve.tensor_scalar(mx[:, s, :], mx[:, s, :], NEG, None, ALU.max).then_inc(m_made, 1)
                        dve.wait_ge(m_made, 2 * n + 3)
                    else:
                        dve.wait_ge(m_made, made(n))
                    after(dve, t_made, n - 2)
                    dve.tensor_tensor(prob[:, s], sc, bc(mx[:, s, :], 2, S), ALU.subtract).then_inc(shifted, 1)

                def scale(n, s):
                    dve.wait_ge(p_made, made(n))
                    dve.tensor_reduce(sums[:, s, :], prob[:, s], AX.X, ALU.add).then_inc(sums_made, 1)
                    if cross:
                        dve.wait_ge(sums_made, 2 * n + 2)
                        dve.scalar_tensor_tensor(out=sums[:, s, :], in0=tail[:, s, :], scalar=float(KEYS - S),
                                                 in1=sums[:, s, :], op0=ALU.mult, op1=ALU.add).then_inc(sums_made, 1)
                        dve.wait_ge(sums_made, 2 * n + 3)
                    else:
                        dve.wait_ge(sums_made, made(n))
                    dve.reciprocal(rs[:, s, :], sums[:, s, :]).then_inc(rs_made, 1)
                    dve.wait_ge(rs_made, made(n))
                    if cross:
                        dve.tensor_tensor(tail[:, s, :], tail[:, s, :], rs[:, s, :], ALU.mult)
                    dve.tensor_tensor(prob[:, s], prob[:, s], bc(rs[:, s, :], 2, S), ALU.mult).then_inc(p_scaled, 1)

                def rotate(n, s):
                    dve.wait_ge(qk_made, made(n))
                    after(dve, qk_ready, n - 2)
                    ab = lambda o: pA[:, o:o + 2 * P].rearrange("p (a t) -> p a t", t=P)
                    dve.tensor_tensor(t1[:, s], ab(0), cos[:, :, :], ALU.mult)
                    dve.tensor_tensor(t2[:, s], ab(2 * P), sin[:, :, :], ALU.mult).then_inc(qk_read, 1)

                def tails(n, s):
                    dve.wait_ge(e_made, made(n))
                    after(dve, o_made, n - 2)
                    dve.tensor_tensor(vs[:, s, :], pE[0:16, 0:D], group16[:, :], ALU.mult)
                    dve.tensor_tensor(tailT[:, s], bc(pE[0:16, D:D + P], 1, BT), bc(batch16[:, :], 2, P), ALU.mult
                                      ).then_inc(e_kept, 1)

                def own_head(n, s):
                    dve.wait_ge(o_made, made(n))
                    dve.tensor_tensor(own[:, :, :, :], pO[:, :].rearrange("p (b h q) -> p b h q", h=4, q=S),
                                      bc(bc(env.m4[:, :], 1, BT), 3, S), ALU.mult).then_inc(own_made, 1)
                    dve.wait_ge(own_made, made(n))
                    after(dve, out_made, n - 2)
                    dve.tensor_reduce(oT[:, s, :].rearrange("p (b q) -> p b q", q=S),
                                      own[:, :, :, :].rearrange("p b h q -> p b q h"), AX.X, ALU.add
                                      ).then_inc(ot_made, 1)

                def add(n):
                    dve.wait_ge(out_made, made(n))
                    x = res[:, n, :]
                    dve.tensor_tensor(x, x, pX[:, 0:D], ALU.add).then_inc(added, 1)

                def slot(n, s):
                    if inside(n + 1):
                        scores(n + 1, 1 - s)
                    if inside(n - 2):
                        add(n - 2)
                    if inside(n) and cross:
                        tails(n, s)
                    if inside(n - 1):
                        own_head(n - 1, 1 - s)
                    if inside(n + 2) and not cross:
                        rotate(n + 2, s)
                    if inside(n + 1):
                        scale(n + 1, 1 - s)

                run_slots(dve, slot, units, last=2)


def cosine_attention(nc, env, title, w, QA, KA):
    units = S
    with stage(nc, title) as st:
        wv, wo = st.sb("wv", [P, D]), st.sb("wo", [P, D])
        bv, bo, hs = st.sb("bv", [1, D]), st.sb("bo", [P, 1]), st.sb("hs", [P, 1])
        own_head = st.sb("own_head", [P, HEADS])
        xs, qT, v = (st.sb(n, [P, 2, P]) for n in ("xs", "qT", "v"))
        kb = st.sb("kb", [P, 2, HEADS, P])
        prob, probT = st.sb("prob", [P, 2, HEADS, P]), st.sb("probT", [P, 2, HEADS, P])
        nmx, sums, rs = (st.sb(n, [P, 2, HEADS]) for n in ("nmx", "sums", "rs"))
        os_, oT = st.sb("os", [P, 2, D]), st.sb("oT", [P, 2, P])
        loads = [(wv[:, :], w.wv), (wo[:, :], w.wo), (bv[:, :], w.bv), (bo[:, :], w.bo), (hs[:, :], w.hs),
                 (own_head[:, :], env.a.c_own_head)]
        pS = [st.ps(f"pS{j}", [P, 512]) for j in range(4)]
        pT = [st.ps(f"pT{j}", [P, 512]) for j in range(2)]
        pO, pM = st.ps("pO", [P, 512]), st.ps("pM", [P, 512])
        O, V, OT, OUT = pO[:, 0:P], pM[:, 0:P], pM[:, P:2 * P], pM[:, 2 * P:3 * P]
        loaded = st.sem("loaded")
        (xs_ready, kb_made, v_made, v_kept, s_made, m_made, p_made, o_made, rs_made, os_made, ot_made, ot_kept,
         out_made, finished) = (st.loop_sem(n) for n in (
             "xs_ready", "kb_made", "v_made", "v_kept", "s_made", "m_made", "p_made", "o_made", "rs_made", "os_made",
             "ot_made", "ot_kept", "out_made", "finished"))
        turned, kept = st.pair("turned"), st.pair("kept")

        def inside(n):
            return not isinstance(n, int) or 0 <= n < units

        def used_group(eng, sem, n):
            if not isinstance(n, int) or n >= 0:
                eng.wait_ge(sem, made(4 * n + 3))

        with nc.Block() as block:
            @block.gpsimd
            def _(pool):
                st.open(pool)
                pool.wait_ge(loaded, 16 * len(loads))

                def keys(n, s):
                    used_group(pool, s_made, n - 2)
                    pool.tensor_tensor(kb[:, s], bc(KA[:, bass.ds(n, P, step=S)], 1, HEADS),
                                       bc(own_head[:, :], 2, P), ALU.mult).then_inc(kb_made, 1)

                def slot(n, s):
                    if inside(n + 2):
                        keys(n + 2, s)

                run_slots(pool, slot, units, last=1)

            @block.sync
            def _(sp):
                for dst, src in loads:
                    sp.dma_start(dst, src).then_inc(loaded, 16)

            @block.tensor
            def _(pe):
                pe.wait_ge(loaded, 16 * len(loads))
                pe.wait_ge(st.opened, 1)

                def values(n, s):
                    pe.wait_ge(xs_ready, made(n))
                    after(pe, v_kept, n - 1)
                    after(pe, finished, n - 3)
                    pe.matmul(V, xs[:, s, :], wv[:, :], start=True, stop=False)
                    pe.matmul(V, env.ones[0:1, 0:P], bv[:, :], start=False, stop=True).then_inc(v_made, 1)

                def scores(n, s, j):
                    if j == 0:
                        pe.wait_ge(xs_ready, made(n))
                        pe.wait_ge(kb_made, made(n))
                    if not isinstance(n, int) or n:
                        pe.wait_ge(p_made, made(4 * n + j - 4))
                    pe.matmul(pS[j][:, :], qT[:, s, :], kb[:, s, 4 * j:4 * j + 4].rearrange("p h k -> p (h k)")
                              ).then_inc(s_made, 1)

                def turn(n, s, j):
                    pe.wait_ge(p_made, made(4 * n + j))
                    pe.wait_ge(kept[j % 2], before(2 * n + j // 2))
                    for h in range(4):
                        last = pe.transpose(pT[j % 2][:, h * P:(h + 1) * P], prob[:, s, 4 * j + h, :],
                                            env.ident[:, :])
                    last.then_inc(turned[j % 2], 1)

                def attend(n, s, j):
                    if j == 0:
                        pe.wait_ge(v_kept, made(n))
                        after(pe, os_made, n - 1)
                    pe.wait_ge(kept[j % 2], made(2 * n + j // 2))
                    for h in range(4 * j, 4 * j + 4):
                        last = pe.matmul(O[:, h * HD:(h + 1) * HD], probT[:, s, h, :], v[:, s, h * HD:(h + 1) * HD])
                    if j == 3:
                        last.then_inc(o_made, 1)

                def turn_output(n, s):
                    pe.wait_ge(os_made, made(n))
                    pe.wait_ge(v_kept, made(min(n + 2, units - 1) if isinstance(n, int) else n + 2))
                    after(pe, finished, n - 1)
                    pe.transpose(OT, os_[:, s, :], env.ident[:, :]).then_inc(ot_made, 1)

                def project(n, s):
                    pe.wait_ge(ot_kept, made(n))
                    pe.matmul(OUT, wo[:, :], oT[:, s, :]).then_inc(out_made, 1)

                def slot(n, s):
                    for j in range(4):
                        if inside(n):
                            turn(n, s, j)
                        if inside(n + 1):
                            scores(n + 1, 1 - s, j)
                        if j == 0 and inside(n - 1):
                            turn_output(n - 1, 1 - s)
                        if j >= 1 and inside(n):
                            attend(n, s, j - 1)
                        if j == 1 and inside(n - 1):
                            project(n - 1, 1 - s)
                        if j == 2 and inside(n + 2):
                            values(n + 2, s)
                    if inside(n):
                        attend(n, s, 3)

                run_slots(pe, slot, units, last=1)

            @block.scalar
            def _(act):
                act.wait_ge(loaded, 16 * len(loads))
                act.wait_ge(st.opened, 1)

                def tokens(n, s):
                    used_group(act, s_made, n - 2)
                    after(act, v_made, n - 2)
                    act.activation(qT[:, s, :], QA[:, bass.ds(n, P, step=S)], ACT.Copy)
                    act.activation(xs[:, s, :], env.XNT[:, bass.ds(n, P, step=S)], ACT.Copy).then_inc(xs_ready, 1)

                def values(n, s):
                    act.wait_ge(v_made, made(n))
                    after(act, o_made, n - 2)
                    act.activation(v[:, s, :], V, ACT.Copy).then_inc(v_kept, 1)

                def exponentials(n, s, j):
                    act.wait_ge(m_made, made(4 * n + j))
                    if j == 0 and (not isinstance(n, int) or n >= 2):
                        act.wait_ge(turned[1], made(2 * n - 3))
                        act.wait_ge(rs_made, made(n - 2))
                    for h in range(4):
                        u = 4 * j + h
                        last = act.activation(prob[:, s, u, :], pS[j][:, h * P:(h + 1) * P], ACT.Exp,
                                              bias=nmx[:, s, u:u + 1], accum_out=sums[:, s, u:u + 1])
                    last.then_inc(p_made, 1)

                def keep_turned(n, s, j):
                    act.wait_ge(turned[1], made(2 * n + j // 2))
                    act.activation(probT[:, s, 4 * j:4 * j + 4, :], pT[1][:, :].rearrange("p (h q) -> p h q", q=P),
                                   ACT.Copy).then_inc(kept[1], 1)

                def keep_output(n, s):
                    act.wait_ge(ot_made, made(n))
                    act.activation(oT[:, s, :], OT, ACT.Copy, scale=hs[:, 0:1]).then_inc(ot_kept, 1)

                def slot(n, s):
                    if inside(n + 2):
                        tokens(n + 2, s)
                    for j in range(4):
                        if j % 2 and inside(n):
                            keep_turned(n, s, j)
                        if inside(n + 1):
                            exponentials(n + 1, 1 - s, j)
                        if j == 0 and inside(n - 1):
                            keep_output(n - 1, 1 - s)
                    if inside(n + 2):
                        values(n + 2, s)

                run_slots(act, slot, units, last=1)

            @block.vector
            def _(dve):
                dve.wait_ge(loaded, 16 * len(loads))
                dve.wait_ge(st.opened, 1)

                def maxima(n, s, j):
                    dve.wait_ge(s_made, made(4 * n + j))
                    dve.tensor_reduce(nmx[:, s, 4 * j:4 * j + 4], pS[j][:, :].rearrange("p (h k) -> p h k", k=P),
                                      AX.X, ALU.max, negate=True).then_inc(m_made, 1)

                def keep_turned(n, s, j):
                    dve.wait_ge(turned[0], made(2 * n + j // 2))
                    dve.tensor_copy(probT[:, s, 4 * j:4 * j + 4, :], pT[0][:, :].rearrange("p (h q) -> p h q", q=P)
                                    ).then_inc(kept[0], 1)

                def factors(n, s):
                    dve.wait_ge(p_made, made(4 * n + 3))
                    dve.reciprocal(rs[:, s, :], sums[:, s, :]).then_inc(rs_made, 1)

                def scale(n, s):
                    dve.wait_ge(o_made, made(n))
                    dve.wait_ge(rs_made, made(n))
                    after(dve, ot_made, n - 2)
                    dve.tensor_tensor(os_[:, s, :].rearrange("p (h d) -> p h d", d=HD),
                                      O.rearrange("p (h d) -> p h d", d=HD), bc(rs[:, s, :], 2, HD), ALU.mult
                                      ).then_inc(os_made, 1)

                def finish(n):
                    dve.wait_ge(out_made, made(n))
                    dve.tensor_scalar(env.XNT[:, bass.ds(n, P, step=S)], OUT, bo[:, 0:1], None, ALU.add
                                      ).then_inc(finished, 1)

                def slot(n, s):
                    if inside(n - 1):
                        scale(n - 1, 1 - s)
                    for j in range(4):
                        if j % 2 == 0 and inside(n):
                            keep_turned(n, s, j)
                        if inside(n + 1):
                            maxima(n + 1, 1 - s, j)
                        if j == 1 and inside(n - 1):
                            finish(n - 1)
                    if inside(n):
                        factors(n, s)

                run_slots(dve, slot, units, last=1)


def head_projection(nc, env, title, mode, w_d, src, dst, units, width, ctx=False, bias_d=None, gain_d=None,
                    scale=1.0, logit_d=None):
    ln, l2 = mode == "ln", mode == "l2"
    with stage(nc, title) as st:
        w = st.sb("w", [P, D])
        cols = st.sb("cols", [P, 4])
        y = st.sb("y", [P, 2, width])
        y2 = st.sb("y2", [P, 2, width])
        sd = st.sb("sd", [P, 2, width])
        if ctx:
            xin = st.sb("xin", [P, 2, width])
        raw, centre = (st.sb("raw", [P, D]), st.sb("centre", [P, P])) if ln else (None, None)
        blk = st.sb("blk", [P, P])
        pY = [st.ps(f"pY{s}", [P, 512]) for s in range(2)]
        pV = [st.ps(f"pV{s}", [P, 512]) for s in range(2)]
        loaded, w_made, w_kept, logit = (st.sem(n) for n in ("loaded", "w_made", "w_kept", "logit"))
        landed, y_made, y_kept, sq_made, var_made, sd_made, rs_made, n_made, done = (
            st.pair(n) for n in ("landed", "y_made", "y_kept", "sq_made", "var_made", "sd_made", "rs_made", "n_made",
                                 "done"))
        loads = [(w[:, :], w_d)] if not ln else [(raw[:, :], w_d), (centre[:, :], env.a.c_centre)]
        loads += [(blk[:, :], env.a.c_head_mean if ln else env.a.c_head_sum)]
        if bias_d is not None:
            loads += [(cols[:, 0:1], bias_d)]
        if gain_d is not None:
            loads += [(cols[:, 1:2], gain_d)]
        if logit_d is not None:
            loads += [(cols[:, 2:3], logit_d)]
        with nc.Block() as block:
            @block.gpsimd
            def _(pool):
                st.open(pool)

            @block.sync
            def _(sp):
                for d, s_ in loads:
                    sp.dma_start(d, s_).then_inc(loaded, 16)
                if ctx:
                    with sp.Fori(0, units // 2) as i:
                        for s in range(2):
                            sp.wait_ge(y_made[s], before(i))
                            sp.dma_start(xin[:, s, :], src[:, bass.ds((2 * i + s) * width, width)]
                                         ).then_inc(landed[s], 16)

            @block.tensor
            def _(pe):
                pe.wait_ge(loaded, 16 * len(loads))
                if ln:
                    pe.matmul(pY[0][:, 0:D], raw[:, :], centre[:, :]).then_inc(w_made, 1)
                    pe.wait_ge(w_kept, 1)
                with pe.Fori(0, units // 2) as i:
                    for s in range(2):
                        if ctx:
                            pe.wait_ge(landed[s], 16 * i + 17)
                            x = xin[:, s, :]
                        else:
                            x = src[:, bass.ds((2 * i + s) * width, width)]
                        pe.wait_ge(y_kept[s], before(i))
                        pe.matmul(pY[s][:, 0:width], w[:, :], x).then_inc(y_made[s], 1)
                    for s in range(2):
                        if mode != "plain":
                            pe.wait_ge(sq_made[s], made(i))
                            pe.wait_ge(sd_made[s], before(i))
                            pe.matmul(pV[s][:, 0:width], blk[:, :], y2[:, s, :]).then_inc(var_made[s], 1)

            @block.scalar
            def _(act):
                act.wait_ge(loaded, 16 * len(loads))
                if ln:
                    act.wait_ge(w_made, 1)
                    act.activation(w[:, :], pY[0][:, 0:D], ACT.Copy).then_inc(w_kept, 1)
                if logit_d is not None:
                    act.wait_ge(logit, 1)
                    act.activation(cols[:, 3:4], cols[:, 2:3], ACT.Exp).then_inc(logit, 1)
                with act.Fori(0, units // 2) as i:
                    for s in range(2):
                        act.wait_ge(y_made[s], made(i))
                        if mode == "plain":
                            out = dst[:, bass.ds((2 * i + s) * width, width)]
                            if bias_d is None:
                                act.activation(out, pY[s][:, 0:width], ACT.Copy, scale=scale).then_inc(y_kept[s], 1)
                            elif scale == 1.0:
                                act.activation(out, pY[s][:, 0:width], ACT.Identity, bias=cols[:, 0:1]
                                               ).then_inc(y_kept[s], 1)
                            else:
                                act.activation(y[:, s, :], pY[s][:, 0:width], ACT.Identity, bias=cols[:, 0:1]
                                               ).then_inc(y_kept[s], 1)
                                act.wait_ge(y_kept[s], made(i))
                                act.activation(out, y[:, s, :], ACT.Copy, scale=scale).then_inc(done[s], 1)
                            continue
                        act.wait_ge(n_made[s], before(i))
                        if l2:
                            act.activation(y[:, s, :], pY[s][:, 0:width], ACT.Identity, bias=cols[:, 0:1]
                                           ).then_inc(y_kept[s], 1)
                        else:
                            act.activation(y[:, s, :], pY[s][:, 0:width], ACT.Copy).then_inc(y_kept[s], 1)
                        act.wait_ge(y_kept[s], made(i))
                        act.wait_ge(var_made[s], before(i))
                        act.activation(y2[:, s, :], y[:, s, :], ACT.Square).then_inc(sq_made[s], 1)
                    if mode != "plain":
                        for s in range(2):
                            act.wait_ge(var_made[s], made(i))
                            act.wait_ge(n_made[s], before(i))
                            if ln:
                                act.activation(sd[:, s, :], pV[s][:, 0:width], ACT.Sqrt, bias=env.eps[:, 0:1]
                                               ).then_inc(sd_made[s], 1)
                            else:
                                act.activation(sd[:, s, :], pV[s][:, 0:width], ACT.Sqrt).then_inc(sd_made[s], 1)

            @block.vector
            def _(dve):
                dve.wait_ge(loaded, 16 * len(loads))
                if logit_d is not None:
                    dve.tensor_scalar(cols[:, 2:3], cols[:, 2:3], float(np.log(100.0)), None, ALU.min
                                      ).then_inc(logit, 1)
                    dve.wait_ge(logit, 2)
                if mode == "plain":
                    return
                with dve.Fori(0, units // 2) as i:
                    for s in range(2):
                        out = dst[:, bass.ds((2 * i + s) * width, width)]
                        dve.wait_ge(sd_made[s], made(i))
                        if l2:
                            dve.tensor_scalar(sd[:, s, :], sd[:, s, :], 1e-12, None, ALU.max).then_inc(rs_made[s], 1)
                            dve.wait_ge(rs_made[s], 2 * i + 2)
                        dve.reciprocal(sd[:, s, :], sd[:, s, :]).then_inc(rs_made[s], 1)
                        dve.wait_ge(rs_made[s], 2 * i + 3 if l2 else made(i))
                        if ln:
                            dve.tensor_tensor(sd[:, s, :], y[:, s, :], sd[:, s, :], ALU.mult).then_inc(done[s], 1)
                            dve.wait_ge(done[s], made(i))
                            dve.tensor_scalar(out, sd[:, s, :], cols[:, 1:2], cols[:, 0:1], ALU.mult, ALU.add
                                              ).then_inc(n_made[s], 1)
                        elif logit_d is not None:
                            dve.scalar_tensor_tensor(out=out, in0=y[:, s, :], scalar=cols[:, 3:4], in1=sd[:, s, :],
                                                     op0=ALU.mult, op1=ALU.mult).then_inc(n_made[s], 1)
                        else:
                            dve.tensor_tensor(out, y[:, s, :], sd[:, s, :], ALU.mult).then_inc(n_made[s], 1)


def cross_attention(nc, env, title, w, QT, KA=None, masked=False):
    with stage(nc, title) as st:
        wk, wv = st.sb("wk", [P, D]), st.sb("wv", [P, D])
        cols = st.sb("cols", [P, 2])
        m4q, selq = st.sb("m4q", [P, 4]), st.sb("selq", [P, S])
        ctx = st.sb("ctx", [P, 2, KPAD])
        kT = st.sb("kT", [P, 2, KPAD])
        qb = st.sb("qb", [P, 2, HEADS, S])
        own_head16 = st.sb("own_head16", [P, HEADS])
        v = st.sb("v", [CH, 2, 3, D])
        prob = st.sb("prob", [P, 2, 4, KPAD])
        probT = st.sb("probT", [CH, 2, 4, 3 * P])
        nmx, sums, rs = (st.sb(n, [P, 2, 4]) for n in ("nmx", "sums", "rs"))
        rm = st.sb("rm", [P, 2, 4, 4])
        rx = st.sb("rx", [P, 2, D])
        own = st.sb("own", [P, 4, S])
        ou, on = st.sb("ou", [P, S]), st.sb("on", [P, 2, S])
        loads = [(wv[:, :], w.wv), (m4q[:, :], env.a.c_m4q), (selq[:, :], env.a.c_selq),
                 (own_head16[:, :], env.a.c_own_head)]
        if KA is None:
            loads += [(wk[:, :], w.wk), (cols[:, 0:1], w.bk), (cols[:, 1:2], w.bv)]
        if masked:
            mask_i, mask = st.sb("mask_i", [P, KEYS], I32), st.sb("mask", [P, KEYS])
            mask_b, ident_b = st.sb("mask_b", [P, KEYS], BF16), st.sb("ident_b", [P, P], BF16)
            loads += [(mask_i[:, :], w.mask)]
        pS = [st.ps(f"pS{j}", [P, 512]) for j in range(4)]
        pT = [st.ps(f"pT{j}", [P, 512]) for j in range(2)]
        pKV = st.ps("pKV", [P, 512])
        pO = st.ps("pO", [P, 512])
        O, R = pO[:, 0:P], pKV[:, 448:448 + S]
        loaded, mask_made, padded, rs_step = (st.sem(n) for n in ("loaded", "mask_made", "padded", "rs_step"))
        landed = st.pair("landed")
        (q_made, k_made, v_made, k_kept, v_kept, s_made, m_made, p_made, o_made, rs_made, rm_made, rx_made, own_made,
         ou_made, r_made, on_made, done) = (st.loop_sem(n) for n in (
             "q_made", "k_made", "v_made", "k_kept", "v_kept", "s_made", "m_made", "p_made", "o_made", "rs_made",
             "rm_made", "rx_made", "own_made", "ou_made", "r_made", "on_made", "done"))
        turned, kept = st.pair("turned"), st.pair("kept")

        def slots(eng, slot):
            slot(0, 0)
            with eng.Fori(0, (B - 4) // 2) as i:
                slot(2 * i + 1, 1)
                slot(2 * i + 2, 0)
            for n in range(B - 3, B):
                slot(n, n % 2)

        def inside(n, ahead=0):
            return not isinstance(n, int) or 0 <= n + ahead < B

        with nc.Block() as block:
            @block.gpsimd
            def _(pool):
                st.open(pool)
                pool.memset(ctx[:, :, KEYS:KPAD], 0.0)
                pool.memset(kT[:, :, KEYS:KPAD], 0.0)
                pool.memset(prob[:, :, :, KEYS:KPAD], 0.0).then_inc(padded, 1)
                pool.wait_ge(loaded, 16 * len(loads))

                def queries(n, s):
                    if not isinstance(n, int) or n >= 2:
                        pool.wait_ge(s_made, made(4 * n - 5))
                    pool.tensor_tensor(qb[:, s], bc(QT[:, bass.ds(n * S, S)], 1, HEADS), bc(own_head16[:, :], 2, S),
                                       ALU.mult).then_inc(q_made, 1)

                for n in range(2):
                    queries(n, n)
                with pool.Fori(0, B // 2 - 1) as i:
                    for s in range(2):
                        queries(2 * i + s + 2, s)

            @block.sync
            def _(sp):
                for d, s_ in loads:
                    sp.dma_start(d, s_).then_inc(loaded, 16)

                def load(n, s):
                    sp.dma_start(ctx[:, s, 0:KEYS], env.a.ctx_t[:, bass.ds(n * KEYS, KEYS)]).then_inc(landed[s], 16)

                load(0, 0)
                load(1, 1)
                with sp.Fori(0, B // 2 - 1) as i:
                    for s in range(2):
                        sp.wait_ge(v_made, made(2 * i + s))
                        load(2 * i + s + 2, s)

            @block.tensor
            def _(pe):
                pe.wait_ge(loaded, 16 * len(loads))
                pe.wait_ge(padded, 1)
                if masked:
                    pe.wait_ge(mask_made, 3)

                def landed_count(n, s):
                    return 16 * ((n - s) // 2) + 17 if isinstance(n, int) else 8 * (n - s) + 17

                def keys(n, s):
                    pe.wait_ge(landed[s], landed_count(n, s))
                    pe.wait_ge(v_kept, before(n))
                    if KA is None:
                        pe.matmul(pKV[:, 0:KEYS], wk[:, :], ctx[:, s, 0:KEYS]).then_inc(k_made, 1)

                def values(n, s):
                    if KA is None:
                        pe.wait_ge(k_kept, made(n))
                    if not isinstance(n, int) or n >= 3:
                        pe.wait_ge(on_made, made(n - 3))
                    for c in range(3):
                        last = pe.matmul(pKV[0:CH, c * D:(c + 1) * D], ctx[:, s, c * CH:(c + 1) * CH], wv[:, :])
                    last.then_inc(v_made, 1)

                def scores(n, s, j):
                    if j == 0:
                        pe.wait_ge(q_made, made(n))
                        pe.wait_ge(k_kept, made(n))
                    if not isinstance(n, int) or n:
                        pe.wait_ge(p_made, made(4 * n + j - 4))
                    last = pe.matmul(pS[j][:, 0:KEYS], qb[:, s, 4 * j:4 * j + 4].rearrange("p h q -> p (h q)"),
                              kT[:, s, 0:KEYS], start=True, stop=not masked)
                    if masked:
                        last = pe.matmul(pS[j][:, 0:KEYS], ident_b[:, :], mask_b[:, :], start=False, stop=True)
                    last.then_inc(s_made, 1)

                def turn(n, s, j):
                    pe.wait_ge(p_made, made(4 * n + j))
                    pe.wait_ge(kept[j % 2], before(2 * n + j // 2))
                    for c in range(3):
                        last = pe.transpose(pT[j % 2][0:CH, c * P:(c + 1) * P], prob[:, s, j, c * CH:(c + 1) * CH],
                                            env.ident[:, :])
                    last.then_inc(turned[j % 2], 1)

                def attend(n, s, j):
                    if j == 0:
                        pe.wait_ge(v_kept, made(n))
                        pe.wait_ge(own_made, before(n))
                    pe.wait_ge(kept[j % 2], made(2 * n + j // 2))
                    for c in range(3):
                        last = pe.matmul(O[j * 32:j * 32 + 32, :], v[:, s, c, j * 32:j * 32 + 32],
                                         probT[:, s, j, c * P:(c + 1) * P], start=c == 0, stop=c == 2)
                    if j == 3:
                        last.then_inc(o_made, 1)

                def normaliser(n, s):
                    pe.wait_ge(rx_made, made(n))
                    if inside(n, 3):
                        pe.wait_ge(k_kept, made(n + 3))
                    pe.wait_ge(v_kept, made(min(n + 2, B - 1) if isinstance(n, int) else n + 2))
                    pe.matmul(R, rx[:, s, :], selq[:, :]).then_inc(r_made, 1)

                for n in range(2):
                    keys(n, n)
                    values(n, n)
                for j in range(4):
                    scores(0, 0, j)

                def slot(n, s):
                    for j in range(4):
                        turn(n, s, j)
                        if inside(n, 1):
                            scores(n + 1, 1 - s, j)
                        if j == 0 and inside(n, 2):
                            keys(n + 2, s)
                        if j == 1 and inside(n, -1):
                            normaliser(n - 1, 1 - s)
                        if j >= 1:
                            attend(n, s, j - 1)
                        if j == 2 and inside(n, 2):
                            values(n + 2, s)
                    attend(n, s, 3)

                slots(pe, slot)
                normaliser(B - 1, 1)

            @block.scalar
            def _(act):
                act.wait_ge(loaded, 16 * len(loads))
                act.wait_ge(padded, 1)

                def keys(n, s):
                    if KA is not None:
                        if not isinstance(n, int) or n >= 2:
                            act.wait_ge(s_made, made(4 * n - 5))
                        act.activation(kT[:, s, 0:KEYS], KA[:, bass.ds(n * KEYS, KEYS)], ACT.Copy
                                       ).then_inc(k_kept, 1)
                    else:
                        act.wait_ge(k_made, made(n))
                        act.activation(kT[:, s, 0:KEYS], pKV[:, 0:KEYS], ACT.Identity, bias=cols[:, 0:1]
                                       ).then_inc(k_kept, 1)

                def values(n, s):
                    act.wait_ge(v_made, made(n))
                    if not isinstance(n, int) or n >= 2:
                        act.wait_ge(o_made, made(n - 2))
                    act.activation(v[:, s].rearrange("p c d -> p (c d)"), pKV[0:CH, 0:3 * D], ACT.Copy
                                   ).then_inc(v_kept, 1)

                def exponentials(n, s, j):
                    act.wait_ge(m_made, made(4 * n + j))
                    if j == 0 and (not isinstance(n, int) or n >= 2):
                        act.wait_ge(turned[1], made(2 * n - 3))
                        act.wait_ge(rs_made, made(n - 2))
                    act.activation(prob[:, s, j, 0:KEYS], pS[j][:, 0:KEYS], ACT.Exp, bias=nmx[:, s, j:j + 1],
                                   accum_out=sums[:, s, j:j + 1]).then_inc(p_made, 1)

                def keep_turned(n, s, j):
                    act.wait_ge(turned[1], made(2 * n + j // 2))
                    act.activation(probT[:, s, j, :], pT[1][0:CH, 0:3 * P], ACT.Copy).then_inc(kept[1], 1)

                def output(n, s):
                    act.wait_ge(on_made, made(n))
                    out = QT[:, bass.ds(n * S, S)]
                    if KA is None:
                        act.activation(out, on[:, s, :], ACT.Identity, bias=cols[:, 1:2]).then_inc(done, 1)
                    else:
                        act.activation(out, on[:, s, :], ACT.Copy).then_inc(done, 1)

                for n in range(2):
                    keys(n, n)
                    values(n, n)
                for j in range(4):
                    exponentials(0, 0, j)

                def slot(n, s):
                    for j in range(4):
                        if j % 2:
                            keep_turned(n, s, j)
                        if inside(n, 1):
                            exponentials(n + 1, 1 - s, j)
                        if j == 0 and inside(n, 2):
                            keys(n + 2, s)
                        if j == 1 and inside(n, -1):
                            output(n - 1, 1 - s)
                    if inside(n, 2):
                        values(n + 2, s)

                slots(act, slot)
                output(B - 1, 1)

            @block.vector
            def _(dve):
                dve.wait_ge(loaded, 16 * len(loads))
                dve.wait_ge(st.opened, 1)
                if masked:
                    dve.tensor_copy(mask[:, :], mask_i[:, :]).then_inc(mask_made, 1)
                    dve.wait_ge(mask_made, 1)
                    dve.tensor_scalar(mask[:, :], mask[:, :], 0.0, -BIG, ALU.is_equal, ALU.mult
                                      ).then_inc(mask_made, 1)
                    dve.wait_ge(mask_made, 2)
                    dve.tensor_copy(ident_b[:, :], env.ident[:, :])
                    dve.tensor_copy(mask_b[:, :], mask[:, :]).then_inc(mask_made, 1)

                def maxima(n, s, j):
                    dve.wait_ge(s_made, made(4 * n + j))
                    sc = pS[j][:, 0:KEYS]
                    dve.tensor_reduce(nmx[:, s, j:j + 1], sc, AX.X, ALU.max, negate=True).then_inc(m_made, 1)

                def keep_turned(n, s, j):
                    dve.wait_ge(turned[0], made(2 * n + j // 2))
                    dve.tensor_copy(probT[:, s, j, :], pT[0][0:CH, 0:3 * P]).then_inc(kept[0], 1)

                def factors(n, s):
                    dve.wait_ge(p_made, made(4 * n + 3))
                    dve.reciprocal(rs[:, s, :], sums[:, s, :]).then_inc(rs_made, 1)
                    dve.wait_ge(rs_made, made(n))
                    dve.tensor_tensor(rm[:, s], bc(rs[:, s, :], 2, 4), bc(m4q[:, :], 1, 4), ALU.mult
                                      ).then_inc(rm_made, 1)
                    dve.wait_ge(rm_made, made(n))
                    dve.tensor_copy(rx[:, s, :].rearrange("p (g d) -> p g d", d=HD),
                                    bc(rm[:, s].rearrange("p j h -> p (j h)"), 2, HD)).then_inc(rx_made, 1)

                def own_head(n, s):
                    dve.wait_ge(o_made, made(n))
                    dve.tensor_tensor(own[:, :, :], O.rearrange("p (h q) -> p h q", q=S), bc(env.m4[:, :], 2, S),
                                      ALU.mult).then_inc(own_made, 1)
                    dve.wait_ge(own_made, made(n))
                    dve.tensor_reduce(ou[:, :], own[:, :, :].rearrange("p h q -> p q h"), AX.X, ALU.add
                                      ).then_inc(ou_made, 1)

                def outputs(n, s):
                    dve.wait_ge(ou_made, made(n))
                    dve.wait_ge(r_made, made(n))
                    if not isinstance(n, int) or n >= 2:
                        dve.wait_ge(done, made(n - 2))
                    dve.tensor_tensor(on[:, s, :], R, ou[:, :], ALU.mult).then_inc(on_made, 1)

                for j in range(4):
                    maxima(0, 0, j)

                def slot(n, s):
                    for j in range(4):
                        if j % 2 == 0:
                            keep_turned(n, s, j)
                        if inside(n, 1):
                            maxima(n + 1, 1 - s, j)
                        if j == 0 and inside(n, -1):
                            own_head(n - 1, 1 - s)
                        if j == 1 and inside(n, -1):
                            outputs(n - 1, 1 - s)
                    factors(n, s)

                slots(dve, slot)
                own_head(B - 1, 1)
                outputs(B - 1, 1)


def project_out(nc, env, title, w_d, b_d, src, res):
    with stage(nc, title) as st:
        w, b = st.sb("w", [P, D]), st.sb("b", [1, D])
        stg = st.sb("stg", [P, 2, 512])
        py = [st.ps(f"py{s}", [P, 512]) for s in range(2)]
        loaded = st.sem("loaded")
        staged, y_made, added = st.pair("staged"), st.pair("y_made"), st.pair("added")
        with nc.Block() as block:
            @block.gpsimd
            def _(pool):
                st.open(pool)

            @block.sync
            def _(sp):
                sp.dma_start(w[:, :], w_d).then_inc(loaded, 16)
                sp.dma_start(b[:, :], b_d).then_inc(loaded, 16)

            @block.scalar
            def _(act):
                with act.Fori(0, GROUPS // 2) as i:
                    for s in range(2):
                        act.wait_ge(y_made[s], before(i))
                        act.activation(stg[:, s, :], src[:, bass.ds((2 * i + s) * 512, 512)], ACT.Copy
                                       ).then_inc(staged[s], 1)

            @block.tensor
            def _(pe):
                pe.wait_ge(loaded, 32)
                with pe.Fori(0, GROUPS // 2) as i:
                    for s in range(2):
                        pe.wait_ge(staged[s], made(i))
                        pe.wait_ge(added[s], before(i))
                        for t in range(TG):
                            o = py[s][:, t * D:(t + 1) * D]
                            pe.matmul(o, stg[:, s, t * P:(t + 1) * P], w[:, :], start=True, stop=False)
                            last = pe.matmul(o, env.ones[0:1, 0:P], b[:, :], start=False, stop=True)
                        last.then_inc(y_made[s], 1)

            @block.vector
            def _(dve):
                with dve.Fori(0, GROUPS // 2) as i:
                    for s in range(2):
                        dve.wait_ge(y_made[s], made(i))
                        x = res[:, bass.ds((2 * i + s) * TG, TG), :]
                        dve.tensor_tensor(x, x, py[s][:, :].rearrange("p (t d) -> p t d", d=D), ALU.add
                                          ).then_inc(added[s], 1)


def l1_xattn(nc, env, a):
    normalise(nc, env, "l1x_ln", env.X, dst_t=env.XNT)
    with stage(nc, "l1x") as st:
        KA = st.sb("KA", [P, B * KEYS])
        head_projection(nc, env, "l1x_q", "ln", a.L1_xattn_Wq, env.XNT, env.XNT, GROUPS, 512,
                        bias_d=a.L1_xattn_ln_b, gain_d=a.L1_xattn_ln_g)
        head_projection(nc, env, "l1x_k", "ln", a.L1_xattn_Wk, a.ctx_t, KA, B, KEYS, ctx=True,
                        bias_d=a.L1_xattn_ln_b, gain_d=a.L1_xattn_ln_g)
        w = Names(wv=a.L1_xattn_Wv)
        cross_attention(nc, env, "l1x_att", w, env.XNT, KA=KA)
    project_out(nc, env, "l1x_out", a.L1_xattn_Wp, a.L1_xattn_bp, env.XNT, env.X)


def l2_xattn(nc, env, a):
    normalise(nc, env, "l2x_ln", env.X, dst_t=env.XNT)
    head_projection(nc, env, "l2x_q", "plain", a.L2_xattn_Wq, env.XNT, env.XNT, GROUPS, 512,
                    bias_d=a.L2_xattn_bq, scale=HD ** -0.5)
    w = Names(wk=a.L2_xattn_Wk, bk=a.L2_xattn_bk, wv=a.L2_xattn_Wv, bv=a.L2_xattn_bv, mask=a.mask_if)
    cross_attention(nc, env, "l2x_att", w, env.XNT, masked=True)
    project_out(nc, env, "l2x_out", a.L2_xattn_Wo, a.L2_xattn_bo, env.XNT, env.X)


def l3_attn(nc, env, a):
    normalise(nc, env, "l3a_ln", env.X, dst_t=env.XNT)
    with stage(nc, "l3a") as st:
        QA, KA = st.sb("QA", [P, T]), st.sb("KA", [P, T])
        head_projection(nc, env, "l3a_q", "l2", a.L3_attn_wq, env.XNT, QA, GROUPS, 512, bias_d=a.L3_attn_bq,
                        logit_d=a.L3_attn_logit)
        head_projection(nc, env, "l3a_k", "l2", a.L3_attn_wk, env.XNT, KA, GROUPS, 512, bias_d=a.L3_attn_bk)
        w = Names(wv=a.L3_attn_wv, wo=a.L3_attn_out_w, bv=a.L3_attn_bv, bo=a.L3_attn_out_b,
                            hs=a.L3_attn_head)
        cosine_attention(nc, env, "l3a_att", w, QA, KA)
    add_transposed(nc, env, "l3a_add", env.XNT, env.X)


def multi_query_attention(nc, env, title, w, Y):
    NH, DH = 8, 64
    with stage(nc, title) as st:
        wq, wk, wv, wo = (st.sb(n, [P, k]) for n, k in (("wq", 512), ("wk", D), ("wv", DH), ("wo", 512)))
        off = st.sb("off", [P, P])
        xs = st.sb("xs", [P, 2, P])
        qT = st.sb("qT", [P, 2, 4, P])
        kT = st.sb("kT", [P, 2, P])
        v = st.sb("v", [P, 2, DH])
        prob, probT = st.sb("prob", [P, 2, NH, P]), st.sb("probT", [P, 2, NH, P])
        mx, nmx, sums, rs = (st.sb(n, [P, 2, NH]) for n in ("mx", "nmx", "sums", "rs"))
        os_ = st.sb("os", [P, 2, 4, 2, DH])
        oT = st.sb("oT", [P, 2, 4, P])
        pQ, pK, pO, pX = (st.ps(n, [P, 512]) for n in ("pQ", "pK", "pO", "pX"))
        pS = st.ps("pS", [P, 2, 4, P])
        pT = [st.ps(f"pT{r}", [P, 512]) for r in range(2)]
        loads = [(wq[:, :], w.wq), (wk[:, :], w.wk), (wv[:, :], w.wv), (wo[:, :], w.wo), (off[:, :], w.off)]
        loaded = st.sem("loaded")
        (xs_ready, qkv_made, qkv_kept, s_made, masked, m_made, nm_made, p_made, o_made, rs_made, o_kept, ot_made,
         ot_kept, out_made, finished, turned, kept) = (st.pair(n) for n in (
             "xs_ready", "qkv_made", "qkv_kept", "s_made", "masked", "m_made", "nm_made", "p_made", "o_made",
             "rs_made", "o_kept", "ot_made", "ot_kept", "out_made", "finished", "turned", "kept"))
        with nc.Block() as block:
            @block.gpsimd
            def _(pool):
                st.open(pool)

            @block.sync
            def _(sp):
                for d, s_ in loads:
                    sp.dma_start(d, s_).then_inc(loaded, 16)

            @block.scalar
            def _(act):
                with act.Fori(0, TILES // 2) as i:
                    for s in range(2):
                        act.wait_ge(qkv_made[s], before(i))
                        act.activation(xs[:, s, :], env.XNT[:, bass.ds((2 * i + s) * P, P)], ACT.Copy
                                       ).then_inc(xs_ready[s], 1)
                    for s in range(2):
                        act.wait_ge(qkv_made[s], made(i))
                        act.wait_ge(o_made[s], before(i))
                        act.activation(qT[:, s].rearrange("p c t -> p (c t)"), pQ[:, :], ACT.Copy, scale=DH ** -0.5)
                        act.activation(kT[:, s, :], pK[:, 0:P], ACT.Copy)
                        act.activation(v[:, s, :], pK[:, P:P + DH], ACT.Copy).then_inc(qkv_kept[s], 1)
                    for s in range(2):
                        act.wait_ge(nm_made[s], made(i))
                        act.wait_ge(o_kept[s], before(i))
                        for u in range(NH):
                            e = act.activation(prob[:, s, u, :], pS[:, u // 4, u % 4, :], ACT.Exp,
                                               bias=nmx[:, s, u:u + 1], accum_out=sums[:, s, u:u + 1])
                            if u % 4 == 3:
                                e.then_inc(p_made[s], 1)
                    for s in range(2):
                        act.wait_ge(turned[1], made(2 * i + s))
                        act.activation(probT[:, s, 4:8, :], pT[1][:, :].rearrange("p (h q) -> p h q", q=P), ACT.Copy
                                       ).then_inc(kept[1], 1)
                    for s in range(2):
                        act.wait_ge(ot_made[s], made(i))
                        act.activation(oT[:, s].rearrange("p c t -> p (c t)"), pQ[:, :], ACT.Copy
                                       ).then_inc(ot_kept[s], 1)

            @block.tensor
            def _(pe):
                pe.wait_ge(loaded, 16 * len(loads))
                with pe.Fori(0, TILES // 2) as i:
                    for s in range(2):
                        pe.wait_ge(xs_ready[s], made(i))
                        pe.wait_ge(*((qkv_kept[0], made(i)) if s else (ot_kept[1], before(i))))
                        for c in range(4):
                            pe.matmul(pQ[:, c * P:(c + 1) * P], wq[:, c * P:(c + 1) * P], xs[:, s, :])
                        pe.matmul(pK[:, 0:P], wk[:, :], xs[:, s, :])
                        pe.matmul(pK[:, P:P + DH], xs[:, s, :], wv[:, :]).then_inc(qkv_made[s], 1)
                    for s in range(2):
                        pe.wait_ge(qkv_kept[s], made(i))
                        sem, value = previous(p_made, s, i)
                        pe.wait_ge(sem, 2 * value - 1)
                        for h in range(NH):
                            r = slice(DH * (h % 2), DH * (h % 2) + DH)
                            last = pe.matmul(pS[:, h % 2, h // 2, :], qT[r, s, h // 2, :], kT[r, s, :])
                        last.then_inc(s_made[s], 1)
                    for s in range(2):
                        n = 2 * i + s
                        for r in range(2):
                            pe.wait_ge(p_made[s], 2 * i + r + 2)
                            pe.wait_ge(kept[r], before(n))
                            for u in range(4):
                                last = pe.transpose(pT[r][:, u * P:(u + 1) * P], prob[:, s, 4 * r + u, :],
                                                    env.ident[:, :])
                            last.then_inc(turned[r], 1)
                        pe.wait_ge(*previous(o_kept, s, i))
                        for r in range(2):
                            pe.wait_ge(kept[r], made(n))
                            for u in range(4):
                                h = 2 * u + r
                                last = pe.matmul(pO[:, h * DH:(h + 1) * DH], probT[:, s, 4 * r + u, :], v[:, s, :])
                        last.then_inc(o_made[s], 1)
                    for s in range(2):
                        pe.wait_ge(o_kept[s], made(i))
                        pe.wait_ge(*((ot_kept[0], made(i)) if s else (qkv_kept[1], made(i))))
                        for c in range(4):
                            last = pe.transpose(pQ[:, c * P:(c + 1) * P],
                                                os_[:, s, c].rearrange("p r d -> p (r d)"), env.ident[:, :])
                        last.then_inc(ot_made[s], 1)
                        pe.wait_ge(ot_kept[s], made(i))
                        pe.wait_ge(*previous(finished, s, i))
                        for c in range(4):
                            last = pe.matmul(pX[:, 0:D], oT[:, s, c, :], wo[:, c * D:(c + 1) * D], start=c == 0,
                                             stop=c == 3)
                        last.then_inc(out_made[s], 1)

            @block.vector
            def _(dve):
                dve.wait_ge(loaded, 16 * len(loads))
                with dve.Fori(0, TILES // 2) as i:
                    for s in range(2):
                        dve.wait_ge(s_made[s], made(i))
                        sc = pS[:, :, :, :].rearrange("p r h k -> p (r h) k")
                        dve.tensor_tensor(sc, sc, bc(off[:, :], 1, NH), ALU.add).then_inc(masked[s], 1)
                        dve.wait_ge(masked[s], made(i))
                        dve.tensor_reduce(mx[:, s, :], sc, AX.X, ALU.max).then_inc(m_made[s], 1)
                        dve.wait_ge(m_made[s], made(i))
                        dve.tensor_scalar(nmx[:, s, :], mx[:, s, :], -1.0, None, ALU.mult).then_inc(nm_made[s], 1)
                    for s in range(2):
                        dve.wait_ge(turned[0], made(2 * i + s))
                        dve.tensor_copy(probT[:, s, 0:4, :], pT[0][:, :].rearrange("p (h q) -> p h q", q=P)
                                        ).then_inc(kept[0], 1)
                        dve.wait_ge(p_made[s], 2 * i + 3)
                        dve.reciprocal(rs[:, s, :], sums[:, s, :]).then_inc(rs_made[s], 1)
                        dve.wait_ge(rs_made[s], made(i))
                        dve.wait_ge(o_made[s], made(i))
                        o = pO[:, :].rearrange("p (c r d) -> p c r d", r=2, d=DH)
                        for r in range(2):
                            last = dve.tensor_tensor(os_[:, s, :, r, :], o[:, :, r, :],
                                                     bc(rs[:, s, 4 * r:4 * r + 4], 2, DH), ALU.mult)
                        last.then_inc(o_kept[s], 1)
                    for s in range(2):
                        dve.wait_ge(out_made[s], made(i))
                        dve.tensor_copy(Y[:, 2 * i + s, :], pX[:, 0:D]).then_inc(finished[s], 1)


def l0_attn(nc, env, a):
    with stage(nc, "l0a") as st:
        Y, YN = st.sb("Y", [P, TILES, D]), st.sb("YN", [P, TILES, D])
        ln = st.sb("ln", [P, 2])
        gain, shift = st.sb("gain", [P, D]), st.sb("shift", [P, D])
        landed, step = st.sem("landed"), st.sem("step")
        with nc.Block() as block:
            @block.sync
            def _(sp):
                sp.dma_start(ln[:, :], a.L0_attn_ln).then_inc(landed, 16)
                sp.dma_start(gain[:, :], a.L0_attn_out_norm_w.to_broadcast([P, D])).then_inc(landed, 16)
                sp.dma_start(shift[:, :], a.L0_attn_out_norm_b.to_broadcast([P, D])).then_inc(landed, 16)
                sp.wait_ge(landed, 48)
        normalise(nc, env, "l0a_ln0", env.X, dst=YN)
        normalise(nc, env, "l0a_ln1", YN, dst_t=env.XNT, gain=ln[:, 0:1], shift=ln[:, 1:2])
        w = Names(wq=a.L0_attn_Wq, wk=a.L0_attn_wk2, wv=a.L0_attn_wv, wo=a.L0_attn_Wo, off=a.c_other_batch)
        multi_query_attention(nc, env, "l0a_att", w, Y)
        normalise(nc, env, "l0a_ln2", Y, dst=YN)
        with nc.Block() as block:
            @block.vector
            def _(dve):
                dve.tensor_tensor(YN[:, :, :], YN[:, :, :], bc(gain[:, :], 1, TILES), ALU.mult)
                dve.tensor_tensor(env.X[:, :, :], env.X[:, :, :], bc(shift[:, :], 1, TILES), ALU.add
                                  ).then_inc(step, 1)
                dve.wait_ge(step, 1)
                dve.tensor_tensor(env.X[:, :, :], env.X[:, :, :], YN[:, :, :], ALU.add)


def selective_scan(nc, env, title, a):
    NC, NS = 2, 16
    BG = 512 // S
    with stage(nc, title) as st:
        w_in = st.sb("w_in", [P, 4 * P])
        w_dt_raw, w_bc = st.sb("w_dt_raw", [P, NC, P]), st.sb("w_bc", [P, NC, 96])
        w_out = st.sb("w_out", [P, NC, D])
        conv_w, cols, A = st.sb("conv_w", [P, NC, 4]), st.sb("cols", [P, NC, 4]), st.sb("A", [P, NC, NS])
        sel_f, sel = st.sb("sel_f", [96, 2 * NS]), st.sb("sel", [96, 2 * NS, P], BF16)
        xi, acc, th, xc, sz = (st.sb(n, [P, NC, 512]) for n in ("xi", "acc", "th", "xc", "sz"))
        ab, lg, dl, dx = (st.sb(n, [P, NC, 512]) for n in ("ab", "lg", "dl", "dx"))
        r1, stk = st.sb("r1", [96, 512]), st.sb("stk", [96, 512], BF16)
        dA, dbu, hh, hc = (st.sb(n, [P, NC, 512]) for n in ("dA", "dbu", "hh", "hc"))
        pX = [st.ps(f"pX{c}", [P, 512]) for c in range(2)]
        pZ = [st.ps(f"pZ{c}", [P, 512]) for c in range(2)]
        pBn = [st.ps(f"pBn{c}", [P, 512]) for c in range(2)]
        pCn = [st.ps(f"pCn{c}", [P, 512]) for c in range(2)]
        loads = [(w_in[:, :], a.L2_attn_W_in), (w_dt_raw[:, :, :], a.L2_attn_wx0.rearrange("p (c m) -> p c m", c=NC)),
                 (w_bc[:, :, :], a.L2_attn_wbc.rearrange("p (c m) -> p c m", c=NC)),
                 (w_out[:, :, :], a.L2_attn_W_out.rearrange("p (c m) -> p c m", c=NC)),
                 (conv_w[:, :, :], a.L2_attn_conv_w.rearrange("p (c m) -> p c m", c=NC)),
                 (cols[:, :, :], a.L2_attn_cols.rearrange("p (c m) -> p c m", c=NC)),
                 (A[:, :, :], a.L2_attn_A_log.rearrange("p (c m) -> p c m", c=NC)),
                 (sel_f[:, 0:2 * NS], env.a.c_pick)]
        loaded, prep = st.sem("loaded"), st.sem("prep")
        xz_made, xi_kept, z_act, conv, xc_act, xc_made, sz_made, dbc_made, dl_abs, dl_log, dl_made, split, stk_made = (
            st.loop_sem(n) for n in ("xz_made", "xi_kept", "z_act", "conv", "xc_act", "xc_made", "sz_made",
                                     "dbc_made", "dl_abs", "dl_log", "dl_made", "split", "stk_made"))
        bc_made, da_made, dbu_made, h_made, hc_made, y_added, y_made, y_step, y_ready, out_made, added = (
            st.loop_sem(n) for n in ("bc_made", "da_made", "dbu_made", "h_made", "hc_made", "y_added", "y_made",
                                     "y_step", "y_ready", "out_made", "added"))
        xc_act2, sz_half, dstep = (st.loop_sem(n) for n in ("xc_act2", "sz_half", "dstep"))
        CB, WDT, BDT, DP = range(4)
        by_batch = lambda ap: ap.rearrange("p (b t) -> p b t", t=S)
        with nc.Block() as block:
            @block.gpsimd
            def _(pool):
                st.open(pool)

            @block.sync
            def _(sp):
                for d, s_ in loads:
                    sp.dma_start(d, s_).then_inc(loaded, 16)

            @block.tensor
            def _(pe):
                pe.wait_ge(st.opened, 1)
                pe.wait_ge(loaded, 16 * len(loads))
                pe.wait_ge(prep, 3)
                with pe.Fori(0, GROUPS) as g:
                    pe.wait_ge(added, before(g))
                    x = env.XNT[:, bass.ds(g * 512, 512)]
                    for c in range(NC):
                        pe.matmul(pX[c][:, :], w_in[:, c * P:(c + 1) * P], x)
                        last = pe.matmul(pZ[c][:, :], w_in[:, (2 + c) * P:(3 + c) * P], x)
                    last.then_inc(xz_made, 1)
                    pe.wait_ge(xc_made, made(2 * g + 1))
                    for c in range(NC):
                        pe.matmul(pX[0][:, :], w_dt_raw[:, c, :], xc[:, c, :], start=c == 0, stop=c == 1)
                    for c in range(NC):
                        last = pe.matmul(pX[1][0:96, :], w_bc[:, c, :], xc[:, c, :], start=c == 0, stop=c == 1)
                    last.then_inc(dbc_made, 1)
                    pe.wait_ge(stk_made, made(g))
                    pe.wait_ge(sz_made, made(2 * g + 1))
                    for n in range(NS + 1):
                        if n < NS:
                            pe.wait_ge(hc_made, before(g * NS * NC + max(n - 1, 0) * NC))
                            pe.matmul(pBn[n % 2][:, :], sel[:, n, :], stk[:, :])
                            pe.matmul(pCn[n % 2][:, :], sel[:, NS + n, :], stk[:, :]).then_inc(bc_made, 1)
                        if n >= 1:
                            for c in range(NC):
                                k = (n - 1) * NC + c
                                pe.wait_ge(hc_made, made(g * NS * NC + k))
                                last = pe.matmul(pZ[c][:, :], env.ident[:, :], hc[:, c, :], start=n == 1,
                                                 stop=n == NS).then_inc(y_added, 1)
                    pe.wait_ge(y_ready, made(g))
                    for t in range(TG):
                        for c in range(NC):
                            last = pe.matmul(pX[0][:, t * D:(t + 1) * D], dx[:, c, t * P:(t + 1) * P],
                                             w_out[:, c, :], start=c == 0, stop=c == 1)
                    last.then_inc(out_made, 1)

            @block.scalar
            def _(act):
                act.wait_ge(st.opened, 1)
                act.wait_ge(loaded, 16 * len(loads))
                act.activation(A[:, :, :], A[:, :, :], ACT.Exp).then_inc(prep, 1)
                act.wait_ge(prep, 3)
                with act.Fori(0, GROUPS) as g:
                    act.wait_ge(xz_made, made(g))
                    for c in range(NC):
                        act.activation(xi[:, c, :], pX[c][:, :], ACT.Copy).then_inc(xi_kept, 1)
                    for c in range(NC):
                        act.activation(sz[:, c, :], pZ[c][:, :], ACT.Tanh, scale=0.5).then_inc(z_act, 1)
                    for c in range(NC):
                        act.wait_ge(conv, 5 * (2 * g + c) + 6)
                        act.activation(th[:, c, :], acc[:, c, :], ACT.Tanh, scale=0.5).then_inc(xc_act, 1)
                    act.wait_ge(dbc_made, made(g))
                    for c in range(NC):
                        act.activation(ab[:, c, :], pX[0][:, :], ACT.Abs, scale=cols[:, c, WDT:WDT + 1],
                                       bias=cols[:, c, BDT:BDT + 1]).then_inc(dl_abs, 1)
                        act.wait_ge(dl_abs, 4 * g + 2 * c + 2)
                        act.activation(ab[:, c, :], ab[:, c, :], ACT.Exp, scale=-1.0).then_inc(dl_abs, 1)
                    act.wait_ge(dl_abs, 4 * g + 5)
                    for c in range(NC):
                        act.activation(lg[:, c, :], ab[:, c, :], ACT.Ln, bias=env.ones[:, 0:1]).then_inc(dl_log, 1)
                    act.wait_ge(dl_made, made(g))
                    for n in range(NS):
                        for c in range(NC):
                            k = n * NC + c
                            act.wait_ge(h_made, before(g * NS * NC + max(k - 1, 0)))
                            act.activation(dA[:, c, :], dl[:, c, :], ACT.Exp, scale=A[:, c, n:n + 1]
                                           ).then_inc(da_made, 1)

            @block.vector
            def _(dve):
                dve.wait_ge(st.opened, 1)
                dve.wait_ge(loaded, 16 * len(loads))
                dve.tensor_copy(sel[:, :, :], bc(sel_f[:, 0:2 * NS], 2, P)).then_inc(prep, 1)
                dve.wait_ge(prep, 2)
                dve.tensor_scalar(A[:, :, :], A[:, :, :], -1.0, None, ALU.mult).then_inc(prep, 1)
                with dve.Fori(0, GROUPS) as g:
                    for c in range(NC):
                        dve.wait_ge(xi_kept, made(2 * g + c))
                        dve.tensor_scalar(acc[:, c, :], xi[:, c, :], conv_w[:, c, 3:4], cols[:, c, CB:CB + 1],
                                          ALU.mult, ALU.add).then_inc(conv, 1)
                        for s in range(1, 4):
                            dve.wait_ge(conv, 5 * (2 * g + c) + 1 + s)
                            dve.scalar_tensor_tensor(
                                out=by_batch(acc[:, c, :])[:, :, s:S], in0=by_batch(xi[:, c, :])[:, :, 0:S - s],
                                scalar=conv_w[:, c, 3 - s:4 - s], in1=by_batch(acc[:, c, :])[:, :, s:S],
                                op0=ALU.mult, op1=ALU.add).then_inc(conv, 1)
                        dve.wait_ge(conv, 5 * (2 * g + c) + 5)
                        dve.sem_inc(conv, 1)
                    for c in range(NC):
                        dve.wait_ge(xc_act, made(2 * g + c))
                        dve.tensor_scalar(th[:, c, :], th[:, c, :], 0.5, 0.5, ALU.mult, ALU.add).then_inc(xc_act2, 1)
                        dve.wait_ge(xc_act2, made(2 * g + c))
                        dve.tensor_tensor(xc[:, c, :], acc[:, c, :], th[:, c, :], ALU.mult).then_inc(xc_made, 1)
                    for c in range(NC):
                        dve.wait_ge(z_act, made(2 * g + 1))
                        dve.tensor_scalar(sz[:, c, :], sz[:, c, :], 0.5, 0.5, ALU.mult, ALU.add).then_inc(sz_half, 1)
                        dve.wait_ge(sz_half, made(2 * g + c))
                        dve.tensor_tensor(sz[:, c, :], pZ[c][:, :], sz[:, c, :], ALU.mult).then_inc(sz_made, 1)
                    dve.wait_ge(dbc_made, made(g))
                    src = pX[1]
                    for r, parts in ((0, 1), (32, 2), (64, 3)):
                        rows = slice(r, r + 32)
                        dve.tensor_copy(stk[rows, :], src[rows, :]).then_inc(split, 1)
                        base = 9 * g + {0: 0, 32: 1, 64: 4}[r]
                        for q in range(1, parts):
                            dve.wait_ge(split, base + 2 * (q - 1) + 2)
                            if q == 1:
                                dve.tensor_tensor(r1[rows, :], src[rows, :], stk[rows, :], ALU.subtract
                                                  ).then_inc(split, 1)
                            else:
                                dve.tensor_tensor(r1[rows, :], r1[rows, :], stk[rows, :], ALU.subtract
                                                  ).then_inc(split, 1)
                            dve.wait_ge(split, base + 2 * (q - 1) + 3)
                            dve.tensor_copy(stk[rows, :], r1[rows, :]).then_inc(split, 1)
                    dve.wait_ge(split, 9 * g + 10)
                    dve.sem_inc(stk_made, 1)
                    dve.wait_ge(dl_log, made(2 * g + 1))
                    for c in range(NC):
                        dve.tensor_scalar(dl[:, c, :], pX[0][:, :], cols[:, c, WDT:WDT + 1], cols[:, c, BDT:BDT + 1],
                                          ALU.mult, ALU.add).then_inc(dstep, 1)
                    for c in range(NC):
                        dve.wait_ge(dstep, 8 * g + c + 2)
                        dve.tensor_scalar(dl[:, c, :], dl[:, c, :], 0.0, None, ALU.max).then_inc(dstep, 1)
                    for c in range(NC):
                        dve.wait_ge(dstep, 8 * g + c + 4)
                        dve.tensor_tensor(dl[:, c, :], dl[:, c, :], lg[:, c, :], ALU.add).then_inc(dstep, 1)
                    for c in range(NC):
                        dve.wait_ge(dstep, 8 * g + c + 6)
                        dve.tensor_tensor(dx[:, c, :], dl[:, c, :], xc[:, c, :], ALU.mult).then_inc(dstep, 1)
                    dve.wait_ge(dstep, 8 * g + 9)
                    dve.memset(dl[:, :, :].rearrange("p c (b t) -> p (c b) t", t=S)[:, :, 0:1], BIG
                               ).then_inc(dl_made, 1)
                    for n in range(NS):
                        dve.wait_ge(bc_made, made(g * NS + n))
                        for c in range(NC):
                            k = g * NS * NC + n * NC + c
                            dve.tensor_tensor(dbu[:, c, :], dx[:, c, :], pBn[n % 2][:, :], ALU.mult
                                              ).then_inc(dbu_made, 1)
                        for c in range(NC):
                            k = g * NS * NC + n * NC + c
                            dve.wait_ge(dbu_made, made(k))
                            dve.wait_ge(da_made, made(k))
                            dve.tensor_tensor_scan(hh[:, c, :], dA[:, c, :], dbu[:, c, :], 0.0, ALU.mult, ALU.add
                                                   ).then_inc(h_made, 1)
                        for c in range(NC):
                            k = g * NS * NC + n * NC + c
                            dve.wait_ge(h_made, made(k))
                            dve.wait_ge(y_added, before(g * NS * NC + max(n * NC + c - 1, 0)))
                            dve.tensor_tensor(hc[:, c, :], hh[:, c, :], pCn[n % 2][:, :], ALU.mult
                                              ).then_inc(hc_made, 1)
                    for c in range(NC):
                        dve.wait_ge(y_added, made((g + 1) * NS * NC - 2 + c))
                        dve.scalar_tensor_tensor(out=xc[:, c, :], in0=xc[:, c, :], scalar=cols[:, c, DP:DP + 1],
                                                 in1=pZ[c][:, :], op0=ALU.mult, op1=ALU.add).then_inc(y_step, 1)
                    for c in range(NC):
                        dve.wait_ge(y_step, made(2 * g + c))
                        last = dve.tensor_tensor(dx[:, c, :], xc[:, c, :], sz[:, c, :], ALU.mult)
                    last.then_inc(y_ready, 1)
                    dve.wait_ge(out_made, made(g))
                    x = env.X[:, bass.ds(g * TG, TG), :]
                    dve.tensor_tensor(x, x, pX[0][:, :].rearrange("p (t d) -> p t d", d=D), ALU.add
                                      ).then_inc(added, 1)


def l2_attn(nc, env, a):
    normalise(nc, env, "l2a_ln", env.X, dst_t=env.XNT)
    selective_scan(nc, env, "l2a", a)


def two_way_cross(nc, env, title, a, QC, QP, KC):
    SUB = 2 * S
    SC = D ** -0.5
    with stage(nc, title) as st:
        wqs, wvs, wvc, wg = st.sb("wqs", [P, D]), st.sb("wvs", [P, D]), st.sb("wvc", [P, D]), st.sb("wg", [P, 2 * D])
        cols = st.sb("cols", [P, 5])
        interp, m4q, m2 = st.sb("interp", [P, S]), st.sb("m4q", [P, 4]), st.sb("m2", [P, 2, 4])
        xs, qc, qp, kc = (st.sb(n, [P, 2, P]) for n in ("xs", "qc", "qp", "kc"))
        ctx = st.sb("ctx", [P, 2, BT, KEYS])
        ctn = st.sb("ctn", [CH, 2, BT, 3, D])
        sub = st.sb("sub", [P, 2, BT * SUB])
        qs = st.sb("qs", [P, 2, BT * SUB])
        v = st.sb("v", [P, 2, D])
        qbk = st.sb("qbk", [P, 2, 1])
        p1 = st.sb("p1", [P, 2, KPAD])
        p1T = st.sb("p1T", [CH, 2, 3, P])
        m1, n1, s1, r1 = (st.sb(n, [P, 2, 1]) for n in ("m1", "n1", "s1", "r1"))
        p2 = st.sb("p2", [P, 2, 2, S])
        mx2, nmx2, sm2, rs2 = (st.sb(n, [P, 2, 2]) for n in ("mx2", "nmx2", "sm2", "rs2"))
        rm2 = st.sb("rm2", [P, 2, 2, 4])
        p2m = st.sb("p2m", [P, 2, 2, 4, S])
        pib = st.sb("pib", [P, 2, 4, S])
        cn, cT, c2s, s2c, gt, o = (st.sb(n, [P, 2, P]) for n in ("cn", "cT", "c2s", "s2c", "gt", "o"))
        pA, pS, pS2, pT, pC, pX, pG = (st.ps(n, [P, 512]) for n in ("pA", "pS", "pS2", "pT", "pC", "pX", "pG"))
        BQS, BKS, BVS, BVC, BG_ = range(5)
        loads = [(wqs[:, :], a.L3_xattn_Wq_s), (wvs[:, :], a.L3_xattn_Wv_s), (wvc[:, :], a.L3_xattn_Wv_c),
                 (wg[:, :], a.L3_xattn_Wg), (cols[:, :], a.L3_xattn_cols), (interp[:, :], a.c_interp),
                 (m4q[:, :], a.c_m4q), (m2[:, :, :], a.c_pair.rearrange("p (a b) -> p a b", a=2))]
        loaded, prep = st.sem("loaded"), st.sem("prep")
        names = ("landed", "tokens", "proj", "q_kept", "kept", "s_made", "shifted", "m_made", "n_made", "p_made",
                 "s2_made", "m2_made", "n2_made", "p2_made", "turned", "t_kept", "c_made", "r_made", "c_kept",
                 "ct_made", "ct_kept", "c2s_made", "c2s_kept", "r2_made", "rm_made", "p2m_made", "pi_made", "pib_made",
                 "s2c_made", "s2c_kept", "g_made", "g_kept", "mix", "o_made", "finished")
        q = Names(**{n: st.pair(n) for n in names})
        with nc.Block() as block:
            @block.gpsimd
            def _(pool):
                st.open(pool)
                pool.memset(ctn[:, :, :, 2, :], 0.0)
                pool.memset(p1[:, :, KEYS:KPAD], 0.0).then_inc(prep, 1)

            @block.sync
            def _(sp):
                for d, s_ in loads:
                    sp.dma_start(d, s_).then_inc(loaded, 16)
                sp.wait_ge(prep, 1)
                with sp.Fori(0, TILES // 2) as i:
                    for s in range(2):
                        n = 2 * i + s
                        sp.wait_ge(q.c_made[s], before(i))
                        sp.dma_start(ctx[:, s].rearrange("p b k -> p (b k)"),
                                     a.ctx_t[:, bass.ds(n * BT * KEYS, BT * KEYS)]).then_inc(q.landed[s], 16)
                        sp.dma_start(sub[:, s, :], a.ctx_sub[:, bass.ds(n * BT * SUB, BT * SUB)]
                                     ).then_inc(q.landed[s], 16)
                        rows = a.ctx_n[bass.ds(n * BT, BT)]
                        for c, k in ((0, CH), (1, CH), (2, KEYS - 2 * CH)):
                            sp.dma_start(ctn[0:k, s, :, c, :],
                                         rows[:, c * CH:c * CH + k, :].rearrange("b k d -> k b d")
                                         ).then_inc(q.landed[s], 16)

            @block.scalar
            def _(act):
                act.wait_ge(loaded, 16 * len(loads))
                act.wait_ge(prep, 2)
                with act.Fori(0, TILES // 2) as i:
                    for s in range(2):
                        n = 2 * i + s
                        act.wait_ge(q.s2_made[s], before(i))
                        act.activation(xs[:, s, :], env.XNT[:, bass.ds(n * P, P)], ACT.Copy)
                        act.activation(qc[:, s, :], QC[:, bass.ds(n * P, P)], ACT.Copy)
                        act.activation(qp[:, s, :], QP[:, bass.ds(n * P, P)], ACT.Copy)
                        act.activation(kc[:, s, :], KC[:, bass.ds(n * P, P)], ACT.Copy).then_inc(q.tokens[s], 1)
                    for s in range(2):
                        act.wait_ge(q.proj[s], made(i))
                        act.activation(qs[:, s, :], pA[:, 0:BT * SUB], ACT.Identity, bias=cols[:, BQS:BQS + 1]
                                       ).then_inc(q.q_kept[s], 1)
                        act.wait_ge(q.finished[s], before(i))
                        act.activation(qbk[:, s, :], pA[:, 256:257], ACT.Copy, scale=SC)
                        act.activation(v[:, s, :], pA[:, 260:260 + D], ACT.Copy).then_inc(q.kept[s], 1)
                    for s in range(2):
                        act.wait_ge(q.n_made[s], made(i))
                        act.activation(p1[:, s, 0:KEYS], pS[:, 0:KEYS], ACT.Exp, bias=n1[:, s, :],
                                       accum_out=s1[:, s, :]).then_inc(q.p_made[s], 1)
                        act.wait_ge(q.n2_made[s], made(i))
                        for r in range(2):
                            last = act.activation(p2[:, s, r, :], pS2[:, r * S:(r + 1) * S], ACT.Exp, scale=SC,
                                                  bias=nmx2[:, s, r:r + 1], accum_out=sm2[:, s, r:r + 1])
                        last.then_inc(q.p2_made[s], 1)
                    for s in range(2):
                        act.wait_ge(q.turned[s], made(i))
                        act.activation(p1T[:, s].rearrange("p c q -> p (c q)"), pT[0:CH, 0:3 * P], ACT.Copy
                                       ).then_inc(q.t_kept[s], 1)
                    for s in range(2):
                        act.wait_ge(q.ct_made[s], made(i))
                        act.activation(cT[:, s, :], pC[:, P:2 * P], ACT.Copy).then_inc(q.ct_kept[s], 1)
                        act.wait_ge(q.c2s_made[s], made(i))
                        act.activation(c2s[:, s, :], pX[:, 0:P], ACT.Identity, bias=cols[:, BVS:BVS + 1]
                                       ).then_inc(q.c2s_kept[s], 1)
                        act.wait_ge(q.s2c_made[s], made(i))
                        act.activation(s2c[:, s, :], pX[:, P:2 * P], ACT.Identity, bias=cols[:, BVC:BVC + 1]
                                       ).then_inc(q.s2c_kept[s], 1)
                    for s in range(2):
                        act.wait_ge(q.g_made[s], made(i))
                        act.activation(gt[:, s, :], pG[:, 0:P], ACT.Tanh, scale=0.5, bias=cols[:, BG_:BG_ + 1]
                                       ).then_inc(q.g_kept[s], 1)

            @block.tensor
            def _(pe):
                pe.wait_ge(loaded, 16 * len(loads))
                with pe.Fori(0, TILES // 2) as i:
                    for s in range(2):
                        pe.wait_ge(q.tokens[s], made(i))
                        pe.wait_ge(q.landed[s], 80 * i + 81)
                        pe.wait_ge(*previous(q.kept, s, i))
                        pe.matmul(pA[:, 0:BT * SUB], wqs[:, :], sub[:, s, :])
                        pe.matmul(pA[:, 256:257], qc[:, s, :], cols[:, BKS:BKS + 1])
                        pe.matmul(pA[:, 260:260 + D], xs[:, s, :], wvc[:, :]).then_inc(q.proj[s], 1)
                    for s in range(2):
                        pe.wait_ge(*previous(q.p_made, s, i))
                        for b in range(BT):
                            last = pe.matmul(pS[b * S:(b + 1) * S, 0:KEYS], qp[:, s, b * S:(b + 1) * S],
                                             ctx[:, s, b, :])
                        last.then_inc(q.s_made[s], 1)
                        pe.wait_ge(q.q_kept[s], made(i))
                        pe.wait_ge(*previous(q.p2_made, s, i))
                        if not s:
                            pe.wait_ge(q.pib_made[1], before(i))
                        for b in range(BT):
                            h = (b % 2) * SUB
                            last = pe.matmul(pS2[h:h + SUB, (b // 2) * S:(b // 2 + 1) * S],
                                             qs[:, s, b * SUB:(b + 1) * SUB], kc[:, s, b * S:(b + 1) * S])
                        last.then_inc(q.s2_made[s], 1)
                    for s in range(2):
                        pe.wait_ge(q.p_made[s], made(i))
                        pe.wait_ge(*previous(q.t_kept, s, i))
                        for c in range(3):
                            last = pe.transpose(pT[0:CH, c * P:(c + 1) * P], p1[:, s, c * CH:(c + 1) * CH],
                                                env.ident[:, :])
                        last.then_inc(q.turned[s], 1)
                        pe.wait_ge(q.t_kept[s], made(i))
                        pe.wait_ge(*((q.c_kept[0], made(i)) if s else (q.ct_kept[1], before(i))))
                        for b in range(BT):
                            for c in range(3):
                                last = pe.matmul(pC[b * S:(b + 1) * S, 0:D], p1T[:, s, c, b * S:(b + 1) * S],
                                                 ctn[:, s, b, c, :], start=c == 0, stop=c == 2)
                        last.then_inc(q.c_made[s], 1)
                    for s in range(2):
                        pe.wait_ge(q.p2m_made[s], made(i))
                        pe.wait_ge(*((q.pib_made[0], made(i)) if s else (q.p2_made[1], made(i))))
                        for r in range(2):
                            last = pe.matmul(pS2[:, 64:64 + S], p2m[:, s, r].rearrange("p b k -> p (b k)"),
                                             interp[:, :], start=r == 0, stop=r == 1)
                        last.then_inc(q.pi_made[s], 1)
                    for s in range(2):
                        pe.wait_ge(q.c_kept[s], made(i))
                        pe.wait_ge(*((q.ct_kept[0], made(i)) if s else (q.c_kept[1], made(i))))
                        pe.transpose(pC[:, P:2 * P], cn[:, s, :], env.ident[:, :]).then_inc(q.ct_made[s], 1)
                        pe.wait_ge(q.ct_kept[s], made(i))
                        pe.wait_ge(*previous(q.s2c_kept, s, i))
                        pe.matmul(pX[:, 0:P], wvs[:, :], cT[:, s, :]).then_inc(q.c2s_made[s], 1)
                        pe.wait_ge(q.pib_made[s], made(i))
                        pe.wait_ge(q.kept[s], made(i))
                        pe.wait_ge(q.c2s_kept[s], made(i))
                        pe.matmul(pX[:, P:2 * P], v[:, s, :], pib[:, s].rearrange("p b k -> p (b k)")
                                  ).then_inc(q.s2c_made[s], 1)
                    for s in range(2):
                        pe.wait_ge(q.s2c_kept[s], made(i))
                        pe.wait_ge(*((q.g_kept[0], made(i)) if s else (q.finished[1], before(i))))
                        pe.matmul(pG[:, 0:P], wg[:, 0:D], c2s[:, s, :], start=True, stop=False)
                        pe.matmul(pG[:, 0:P], wg[:, D:2 * D], s2c[:, s, :], start=False, stop=True
                                  ).then_inc(q.g_made[s], 1)
                    for s in range(2):
                        pe.wait_ge(q.mix[s], 4 * i + 5)
                        pe.wait_ge(*((q.finished[0], made(i)) if s else (q.g_kept[1], made(i))))
                        pe.transpose(pG[:, P:2 * P], o[:, s, :], env.ident[:, :]).then_inc(q.o_made[s], 1)

            @block.vector
            def _(dve):
                dve.wait_ge(loaded, 16 * len(loads))
                dve.wait_ge(prep, 1)
                dve.tensor_scalar(cols[:, BG_:BG_ + 1], cols[:, BG_:BG_ + 1], 0.5, None, ALU.mult).then_inc(prep, 1)
                with dve.Fori(0, TILES // 2) as i:
                    for s in range(2):
                        dve.wait_ge(q.s_made[s], made(i))
                        dve.wait_ge(q.kept[s], made(i))
                        dve.tensor_scalar(pS[:, 0:KEYS], pS[:, 0:KEYS], qbk[:, s, :], None, ALU.add
                                          ).then_inc(q.shifted[s], 1)
                        dve.wait_ge(q.shifted[s], made(i))
                        dve.tensor_reduce(m1[:, s, :], pS[:, 0:KEYS], AX.X, ALU.max).then_inc(q.m_made[s], 1)
                        dve.wait_ge(q.m_made[s], made(i))
                        dve.tensor_scalar(n1[:, s, :], m1[:, s, :], -1.0, None, ALU.mult).then_inc(q.n_made[s], 1)
                        dve.wait_ge(q.s2_made[s], made(i))
                        dve.tensor_reduce(mx2[:, s, :], pS2[:, 0:2 * S].rearrange("p (r k) -> p r k", k=S), AX.X,
                                          ALU.max).then_inc(q.m2_made[s], 1)
                        dve.wait_ge(q.m2_made[s], made(i))
                        dve.tensor_scalar(nmx2[:, s, :], mx2[:, s, :], -SC, None, ALU.mult).then_inc(q.n2_made[s], 1)
                    for s in range(2):
                        dve.wait_ge(q.p2_made[s], made(i))
                        dve.reciprocal(r1[:, s, :], s1[:, s, :])
                        dve.reciprocal(rs2[:, s, :], sm2[:, s, :]).then_inc(q.r2_made[s], 1)
                        dve.wait_ge(q.r2_made[s], made(i))
                        dve.tensor_tensor(rm2[:, s], m2[:, :, :], bc(rs2[:, s, :], 2, 4), ALU.mult
                                          ).then_inc(q.rm_made[s], 1)
                        dve.wait_ge(q.rm_made[s], made(i))
                        dve.tensor_tensor(p2m[:, s], bc(p2[:, s], 2, 4), bc(rm2[:, s], 3, S), ALU.mult
                                          ).then_inc(q.p2m_made[s], 1)
                    for s in range(2):
                        dve.wait_ge(q.c_made[s], made(i))
                        dve.tensor_scalar(cn[:, s, :], pC[:, 0:D], r1[:, s, :], None, ALU.mult).then_inc(q.c_kept[s], 1)
                    for s in range(2):
                        dve.wait_ge(q.pi_made[s], made(i))
                        dve.tensor_tensor(pib[:, s], bc(pS2[:, 64:64 + S], 1, 4), bc(m4q[:, :], 2, S), ALU.mult
                                          ).then_inc(q.pib_made[s], 1)
                    for s in range(2):
                        dve.wait_ge(q.g_kept[s], made(i))
                        dve.tensor_scalar(gt[:, s, :], gt[:, s, :], 0.5, 0.5, ALU.mult, ALU.add).then_inc(q.mix[s], 1)
                        dve.tensor_tensor(c2s[:, s, :], c2s[:, s, :], s2c[:, s, :], ALU.subtract).then_inc(q.mix[s], 1)
                        dve.wait_ge(q.mix[s], 4 * i + 3)
                        dve.tensor_tensor(o[:, s, :], c2s[:, s, :], gt[:, s, :], ALU.mult).then_inc(q.mix[s], 1)
                        dve.wait_ge(q.mix[s], 4 * i + 4)
                        dve.tensor_tensor(o[:, s, :], o[:, s, :], s2c[:, s, :], ALU.add).then_inc(q.mix[s], 1)
                    for s in range(2):
                        dve.wait_ge(q.o_made[s], made(i))
                        x = env.X[:, 2 * i + s, :]
                        dve.tensor_tensor(x, x, pG[:, P:2 * P], ALU.add).then_inc(q.finished[s], 1)


def l3_xattn(nc, env, a):
    normalise(nc, env, "l3x_ln", env.X, dst_t=env.XNT)
    with stage(nc, "l3x") as st:
        QC, QP, KC = (st.sb(n, [P, T]) for n in ("QC", "QP", "KC"))
        head_projection(nc, env, "l3x_q", "plain", a.L3_xattn_Wq_c, env.XNT, QC, GROUPS, 512,
                        bias_d=a.L3_xattn_bq_c)
        head_projection(nc, env, "l3x_p", "plain", a.L3_xattn_Wk_s, QC, QP, GROUPS, 512, scale=D ** -0.5)
        head_projection(nc, env, "l3x_k", "plain", a.L3_xattn_Wk_c, env.XNT, KC, GROUPS, 512,
                        bias_d=a.L3_xattn_bk_c)
        two_way_cross(nc, env, "l3x_att", a, QC, QP, KC)


def layouts(v):
    o = {}
    o["x"] = v["x"].reshape(T, D)
    row = lambda n: v[n].reshape(1, -1)
    col = lambda n: v[n].reshape(-1, 1)
    for n in ("L0_ffn_router_w",):
        o[n] = v[n]
    o["L0_ffn_router_b"] = row("L0_ffn_router_b")
    o["L0_ffn_expert_w"] = v["L0_ffn_expert_w"].transpose(1, 0, 2).reshape(D, EXPERTS * D)
    o["L0_ffn_expert_b"] = v["L0_ffn_expert_b"]
    o["ctx_t"] = v["ctx_1024"].transpose(2, 0, 1).reshape(D, B * KEYS)
    o["mask_pad"] = v["mask_BxS2_if1"]
    for n in ("Wq", "Wk", "Wv", "Wo"):
        o["L0_xattn_" + n] = v["L0_xattn_" + n].T
    o["L1_xattn_Wq"], o["L1_xattn_Wk"] = v["L1_xattn_Wq"], v["L1_xattn_Wk"]
    o["L1_xattn_Wv"], o["L1_xattn_Wp"] = v["L1_xattn_Wv"].T, v["L1_xattn_Wp"].T
    o["L1_xattn_bp"] = row("L1_xattn_bp")
    for n in ("L1_xattn_ln_g", "L1_xattn_ln_b"):
        o[n] = np.tile(v[n], HEADS).reshape(D, 1)
    for n in ("Wq", "Wk", "Wv", "Wo"):
        o["L2_xattn_" + n] = v["L2_xattn_" + n].T
    for n in ("bq", "bk", "bv"):
        o["L2_xattn_" + n] = col("L2_xattn_" + n)
    o["L2_xattn_bo"] = row("L2_xattn_bo")
    o["mask_if"] = np.tile(v["mask_1x1xSxS2_ik0"][0, 0], (BT, 1))
    w, b = v["L3_attn_in_proj_weight"], v["L3_attn_in_proj_bias"]
    for n, k in enumerate("qkv"):
        o["L3_attn_w" + k] = w[n * D:(n + 1) * D].T
        o["L3_attn_b" + k] = b[n * D:(n + 1) * D].reshape((1, D) if k == "v" else (D, 1))
    o["L3_attn_logit"] = np.repeat(v["L3_attn_logit_scale"].reshape(HEADS, 1), HD, axis=0)
    o["L3_attn_head"] = np.repeat(v["L3_attn_head_scale"].reshape(HEADS, 1), HD, axis=0)
    o["L3_attn_out_w"], o["L3_attn_out_b"] = v["L3_attn_out_w"].T, col("L3_attn_out_b")
    wqkv = v["L1_attn_Wqkv"]
    swap = np.arange(D) ^ 1
    for n, k in enumerate("qkv"):
        o["L1_attn_w" + k] = wqkv[:, n * D:(n + 1) * D]
    o["L1_attn_wq2"], o["L1_attn_wk2"] = o["L1_attn_wq"][:, swap], o["L1_attn_wk"][:, swap]
    o["L1_attn_Wo"] = v["L1_attn_Wo"]
    o["L1_attn_ln"] = np.stack([v["L1_attn_" + n] for n in ("ln1_g", "ln1_b", "ln2_g", "ln2_b")], axis=1)
    def mlp(w1, b1, w2):
        w1, b1, w2 = (x if x.ndim == 1 + k else x[None] for x, k in ((w1, 2), (b1, 1), (w2, 2)))
        e, _, h = w1.shape
        return (w1.transpose(1, 0, 2).reshape(D, e * h), b1.reshape(e * h // P, P).T,
                w2.reshape(e, h // P, P, D).transpose(2, 0, 1, 3).reshape(P, e * h // P * D))
    o["L1_attn_W1"], o["L1_attn_b1"], o["L1_attn_W2"] = mlp(v["L1_attn_W1"], v["L1_attn_b1"], v["L1_attn_W2"])
    o["L1_attn_b2"] = row("L1_attn_b2")
    o["L1_ffn_Wr"], o["L1_ffn_br"], o["L1_ffn_b2"] = v["L1_ffn_Wr"], row("L1_ffn_br"), v["L1_ffn_b2"]
    o["L1_ffn_W1"], o["L1_ffn_b1"], o["L1_ffn_W2"] = mlp(v["L1_ffn_W1"], v["L1_ffn_b1"], v["L1_ffn_W2"])
    o["L2_ffn_norm_weight"] = col("L2_ffn_norm_weight")
    o["L2_ffn_router_w"], o["L2_ffn_router_b"] = v["L2_ffn_router_w"].T, row("L2_ffn_router_b")
    o["L2_ffn_fc1_w"], o["L2_ffn_fc1_b"], o["L2_ffn_fc2_w"] = mlp(
        v["L2_ffn_fc1_w"].transpose(0, 2, 1), v["L2_ffn_fc1_b"], v["L2_ffn_fc2_w"].transpose(0, 2, 1))
    o["L2_ffn_fc2_b"] = v["L2_ffn_fc2_b"]
    o["L3_ffn_gate_w"] = v["L3_ffn_gate_w"].T
    o["L3_ffn_down_w"], o["L3_ffn_down_b"], o["L3_ffn_up_w"] = mlp(
        v["L3_ffn_down_w"].reshape(512, D).T, v["L3_ffn_down_b"].reshape(512),
        v["L3_ffn_up_w"].transpose(0, 2, 1).reshape(512, D))
    o["L3_ffn_up_b"] = v["L3_ffn_up_b"]
    o["bits"] = np.tile((1 << np.arange(29, -1, -1)).astype(np.int32), (P, 1))
    o["L0_attn_Wq"] = v["L0_attn_Wq"]
    wkv = v["L0_attn_Wkv"]
    o["L0_attn_wk2"], o["L0_attn_wv"] = np.concatenate([wkv[:, :64], wkv[:, :64]], axis=1), wkv[:, 64:]
    o["L0_attn_Wo"] = v["L0_attn_Wo"].reshape(4, P, D).transpose(1, 0, 2).reshape(P, 4 * D)
    o["L0_attn_ln"] = np.stack([v["L0_attn_norm_w"], v["L0_attn_norm_b"]], axis=1)
    o["L0_attn_out_norm_w"], o["L0_attn_out_norm_b"] = row("L0_attn_out_norm_w"), row("L0_attn_out_norm_b")
    o["L2_attn_W_in"] = v["L2_attn_W_in"]
    chunked = lambda m: m.reshape(2, P, -1).transpose(1, 0, 2).reshape(P, -1)
    wx = v["L2_attn_W_xproj"]
    o["L2_attn_wx0"] = chunked(np.repeat(wx[:, 0:1], P, axis=1))
    o["L2_attn_wbc"] = chunked(np.concatenate([wx[:, 1:33]] * 3, axis=1))
    o["L2_attn_W_out"] = chunked(v["L2_attn_W_out"])
    o["L2_attn_conv_w"] = chunked(v["L2_attn_conv_w"][:, 0, :])
    o["L2_attn_cols"] = chunked(np.stack([v["L2_attn_" + n] for n in ("conv_b", "w_dt", "b_dt", "D_param")], axis=1))
    o["L2_attn_A_log"] = chunked(v["L2_attn_A_log"])
    for n in ("Wq_c", "Wk_c", "Wq_s", "Wv_s", "Wv_c"):
        o["L3_xattn_" + n] = v["L3_xattn_" + n].T
    o["L3_xattn_Wk_s"] = v["L3_xattn_Wk_s"]
    o["L3_xattn_bq_c"], o["L3_xattn_bk_c"] = col("L3_xattn_bq_c"), col("L3_xattn_bk_c")
    o["L3_xattn_Wg"] = v["L3_xattn_Wg"].reshape(D, 2, D).transpose(2, 1, 0).reshape(D, 2 * D)
    o["L3_xattn_cols"] = np.stack([v["L3_xattn_" + n] for n in ("bq_s", "bk_s", "bv_s", "bv_c", "bg")], axis=1)
    o["ctx_n"] = v["ctx_1024"]
    lo, hi, _ = interpolation()
    o["ctx_sub"] = v["ctx_1024"][:, np.concatenate([lo, hi])].transpose(2, 0, 1).reshape(D, B * 2 * S)
    return o


def interpolation():
    pos = (np.arange(S, dtype=np.float32) + np.float32(0.5)) * np.float32(KEYS / S) - np.float32(0.5)
    pos = np.clip(pos, 0.0, KEYS - 1)
    lo = np.floor(pos).astype(np.int32)
    return lo, np.minimum(lo + 1, KEYS - 1), pos - lo


def more_constants(c):
    tok = np.arange(P)
    same = tok[:, None] // S == tok[None, :] // S
    causal = same & (tok[:, None] % S >= tok[None, :] % S)
    c["causal01"] = causal
    c["other_batch"] = np.where(same, 0.0, -BIG)
    c["m4"] = np.equal.outer(tok % 32 // HD, np.arange(4))
    c["m4q"] = np.equal.outer(tok // S, np.arange(4))
    c["selq"] = np.equal.outer(tok % S, np.arange(S))
    head = np.equal.outer(tok // HD, tok // HD)
    c["head_sum"] = head
    c["head_mean"] = head / HD
    c["centre"] = np.eye(P) - head / HD
    c["eps"] = np.full((P, 1), EPS)
    c["causal_add"] = np.where(causal, 0.0, -BIG)
    freq = 10000.0 ** (-(np.arange(0, HD, 2, dtype=np.float32) / np.float32(HD)))
    theta = np.arange(S, dtype=np.float32)[None, :] * freq[tok % HD // 2][:, None].astype(np.float32)
    theta = theta[:, tok % S]
    sign = np.where(tok % 2 == 0, -1.0, 1.0)[:, None]
    c["rope_cos"] = np.concatenate([np.cos(theta) * HD ** -0.5, np.cos(theta)], axis=1)
    c["rope_sin"] = np.concatenate([np.sin(theta) * sign * HD ** -0.5, np.sin(theta) * sign], axis=1)
    chunk = P // EXPERTS
    expert_of = tok // chunk
    c["same_expert"] = np.equal.outer(expert_of, expert_of)
    c["lower_chunk"] = c["same_expert"] & (tok[:, None] < tok[None, :])
    c["spread"] = np.equal.outer(np.arange(EXPERTS), np.arange(512) // 64)
    c["pick"] = np.equal.outer(np.arange(96) % 32, np.arange(32))
    weight = interpolation()[2]
    both = np.concatenate([np.diag(1 - weight), np.diag(weight)])
    c["interp"] = np.tile(both, (2, 1))
    c["pair"] = np.concatenate([np.equal.outer(tok // (2 * S) + 2 * r, np.arange(BT)) for r in range(2)], axis=1)
    c["causal_q01"] = tok[:, None] % S >= np.arange(S)[None, :]
    c["causal_q_add"] = np.where(c["causal_q01"], 0.0, -BIG)
    c["group16"] = np.equal.outer(np.arange(16) % 4, tok // S)
    c["batch16"] = np.equal.outer(np.arange(16) // 4, np.arange(BT))
    c["own_head"] = np.equal.outer(tok // HD, np.arange(HEADS))
    c["neg"] = np.full((P, 1), NEG)


def build(nc, a, out):
    with ExitStack() as ctx:
        def sb(name, shape, dt=F32):
            return ctx.enter_context(nc.sbuf_tensor(name, shape, dt))

        env = Names(
            X=sb("X", [P, TILES, D]),
            XNT=sb("XNT", [P, T]),
            ident=sb("ident", [P, P]),
            ones=sb("ones", [P, 512]),
            countdown=sb("countdown", [P, EXPERTS]),
            m4=sb("m4", [P, 4]),
            neg=sb("neg", [P, 1]),
            eps=sb("eps", [P, 1]),
            a=a,
        )
        with stage(nc, "load") as st:
            loaded = st.sem("loaded")
            with nc.Block() as block:
                @block.sync
                def _(sp):
                    sp.dma_start(env.X[:, :, :], a.x.rearrange("(i p) d -> p i d", p=P)).then_inc(loaded, 16)
                    for name in ("ident", "ones", "countdown", "m4", "neg", "eps"):
                        sp.dma_start(env[name][:, :], a["c_" + name]).then_inc(loaded, 16)
                    sp.wait_ge(loaded, 112)
        for layer in LAYERS:
            layer(nc, env, a)
        with stage(nc, "store") as st:
            stored = st.sem("stored")
            with nc.Block() as block:
                @block.sync
                def _(sp):
                    sp.dma_start(out.rearrange("(i p) d -> p i d", p=P), env.X[:, :, :]).then_inc(stored, 16)
                    sp.wait_ge(stored, 16)


LAYERS = [l0_xattn, l0_attn, l0_ffn, l1_xattn, l1_attn, l1_ffn, l2_xattn, l2_attn, l2_ffn, l3_xattn, l3_attn, l3_ffn]


def constants():
    c = {}
    c["ident"] = np.eye(P)
    c["ones"] = np.ones((P, 512))
    c["countdown"] = np.tile(EXPERTS - np.arange(EXPERTS), (P, 1))
    more_constants(c)
    return {"c_" + n: np.ascontiguousarray(v, dtype=np.float32) for n, v in c.items()}


def kernel(**inputs):
    import concourse.bacc as bacc
    from concourse.bass_utils import run_bass_kernel_spmd as run

    arrays = {n: np.ascontiguousarray(v) for n, v in layouts({n: np.asarray(v) for n, v in inputs.items()}).items()}
    arrays.update(constants())
    nc = bacc.Bacc("TRN2", target_bir_lowering=False, num_devices=1)
    a = Names(**{n: nc.dram_tensor(n, v.shape, mybir.dt.from_np(v.dtype), kind="ExternalInput").ap()
                           for n, v in arrays.items()})
    out = nc.dram_tensor("out", (T, D), F32, kind="ExternalOutput").ap()
    build(nc, a, out)
    r = run(nc, [arrays], core_ids=[0])
    return r.results[0]["out"].reshape(B, S, D)
```

```python
from contextlib import ExitStack, contextmanager

import numpy as np
import concourse.bass as bass
from concourse import mybir

P = 128
B, S, D = 128, 32, 128
T = B * S
TILES = T // P
BT = P // S
GROUPS = T // 512
TG = 512 // P
KEYS = 257
CH = 86
KPAD = 3 * CH
HEADS, HD = 16, 8
EXPERTS = 8
CAP = T // EXPERTS
BIG = 1.0e30
NEG = -1.0e9
EPS = 1e-5

F32 = mybir.dt.float32
BF16 = mybir.dt.bfloat16
I32 = mybir.dt.int32
ALU = mybir.AluOpType
ACT = mybir.ActivationFunctionType
AX = mybir.AxisListType


def made(n):
    return n + 2


def before(n):
    return n + 1


def previous(sems, s, i):
    return (sems[0], made(i)) if s else (sems[1], before(i))


class Names(dict):

    __getattr__ = dict.__getitem__


@contextmanager
def stage(nc, title):
    with ExitStack() as ctx:
        sems, primed = [], []
        opened = ctx.enter_context(nc.semaphore(f"{title}_opened"))
        sems.append(opened)

        def sem(name):
            sems.append(ctx.enter_context(nc.semaphore(f"{title}_{name}")))
            return sems[-1]

        def loop_sem(name):
            primed.append(sem(name))
            return primed[-1]

        yield Names(
            sb=lambda name, shape, dt=F32: ctx.enter_context(nc.sbuf_tensor(f"{title}_{name}", shape, dt)),
            ps=lambda name, shape, dt=F32: ctx.enter_context(nc.psum_tensor(f"{title}_{name}", shape, dt)),
            sem=sem,
            loop_sem=loop_sem,
            pair=lambda name: [loop_sem(f"{name}_a"), loop_sem(f"{name}_b")],
            open=lambda pool: [pool.sem_inc(s, 1) for s in primed + [opened]],
            opened=opened,
        )
        with nc.Block() as block:
            @block.gpsimd
            def _(pool):
                for s in sems:
                    pool.sem_clear(s)


def bc(ap, axis, n):
    a = ap.unsqueeze(axis)
    shape = list(a.shape)
    shape[axis] = n
    return a.to_broadcast(shape)


def normalise(nc, env, title, src, dst_t=None, dst=None, gain=None, shift=None, rms=False):
    with stage(nc, title) as st:
        mean, var = st.sb("mean", [P, TILES]), st.sb("var", [P, TILES])
        xc = src if rms else st.sb("xc", [P, TILES, D])
        sq = st.sb("sq", [P, TILES, D])
        std = st.sb("std", [P, TILES])
        rstd = st.sb("rstd", [P, TILES])
        stg = st.sb("stg", [P, 2, TG, D])
        pst = [st.ps(f"pst{s}", [P, 512]) for s in range(2)]
        mean_step, centred, squared, summed, var_done = (
            st.sem(n) for n in ("mean_step", "centred", "squared", "summed", "var_done"))
        quarters = [slice(c * TILES // 4, (c + 1) * TILES // 4) for c in range(4)]
        std_done, rstd_done = st.sem("std_done"), st.sem("rstd_done")
        norm_done, turned, copied, kept = st.pair("norm_done"), st.pair("turned"), st.pair("copied"), st.pair("kept")

        with nc.Block() as block:
            @block.gpsimd
            def _(pool):
                st.open(pool)

            @block.vector
            def _(dve):
                if not rms:
                    for c, r in enumerate(quarters):
                        dve.tensor_reduce(mean[:, r], src[:, r, :], AX.X, ALU.add).then_inc(mean_step, 1)
                        dve.wait_ge(mean_step, 2 * c + 1)
                        dve.tensor_scalar(mean[:, r], mean[:, r], 1.0 / D, None, ALU.mult).then_inc(mean_step, 1)
                        dve.wait_ge(mean_step, 2 * c + 2)
                        dve.tensor_tensor(xc[:, r, :], src[:, r, :], bc(mean[:, r], 2, D), ALU.subtract
                                          ).then_inc(centred, 1)
                for c, r in enumerate(quarters):
                    dve.wait_ge(squared, c + 1)
                    dve.tensor_reduce(var[:, r], sq[:, r, :], AX.X, ALU.add).then_inc(summed, 1)
                dve.wait_ge(summed, 4)
                dve.tensor_scalar(var[:, :], var[:, :], 1.0 / D, EPS, ALU.mult, ALU.add).then_inc(var_done, 1)
                dve.wait_ge(std_done, 1)
                dve.reciprocal(rstd[:, :], std[:, :]).then_inc(rstd_done, 1)
                dve.wait_ge(rstd_done, 1)
                with dve.Fori(0, GROUPS // 2) as i:
                    for s in range(2):
                        if dst_t is not None:
                            dve.wait_ge(turned[s], before(i))
                        if dst is not None:
                            dve.wait_ge(kept[s], before(i))
                        g = bass.ds((2 * i + s) * TG, TG)
                        dve.tensor_tensor(stg[:, s], xc[:, g, :], bc(rstd[:, g], 2, D), ALU.mult
                                          ).then_inc(norm_done[s], 1)

            @block.tensor
            def _(pe):
                if dst_t is None:
                    return
                with pe.Fori(0, GROUPS // 2) as i:
                    for s in range(2):
                        pe.wait_ge(norm_done[s], made(i))
                        pe.wait_ge(copied[s], before(i))
                        for t in range(TG):
                            last = pe.transpose(pst[s][:, t * P:(t + 1) * P], stg[:, s, t, :], env.ident[:, :])
                        last.then_inc(turned[s], 1)

            @block.scalar
            def _(act):
                for c, r in enumerate(quarters):
                    if not rms:
                        act.wait_ge(centred, c + 1)
                    act.activation(sq[:, r, :], xc[:, r, :], ACT.Square).then_inc(squared, 1)
                act.wait_ge(var_done, 1)
                act.activation(std[:, :], var[:, :], ACT.Sqrt).then_inc(std_done, 1)
                with act.Fori(0, GROUPS // 2) as i:
                    for s in range(2):
                        g = 2 * i + s
                        if dst is not None:
                            act.wait_ge(norm_done[s], made(i))
                            act.activation(dst[:, bass.ds(g * TG, TG), :], stg[:, s], ACT.Copy).then_inc(kept[s], 1)
                        if dst_t is not None:
                            act.wait_ge(turned[s], made(i))
                            out = dst_t[:, bass.ds(g * 512, 512)]
                            if gain is not None and shift is not None:
                                act.activation(out, pst[s][:, :], ACT.Identity, bias=shift, scale=gain
                                               ).then_inc(copied[s], 1)
                            elif gain is not None:
                                act.activation(out, pst[s][:, :], ACT.Copy, scale=gain).then_inc(copied[s], 1)
                            else:
                                act.activation(out, pst[s][:, :], ACT.Copy).then_inc(copied[s], 1)


def route(nc, env, title, names, W, WT, kind):
    rw_d, rb_d = names
    with stage(nc, title) as st:
        rw = st.sb("rw", [P, EXPERTS])
        rb = st.sb("rb", [1, EXPERTS])
        xs = st.sb("xs", [P, 2, 512])
        LG = st.sb("LG", [P, TILES, EXPERTS])
        m = st.sb("m", [P, TILES])
        l0 = st.sb("l0", [P, TILES, EXPERTS])
        pr = st.sb("pr", [P, TILES, EXPERTS])
        sm = st.sb("sm", [P, TILES])
        rs = st.sb("rs", [P, TILES])
        pl = [st.ps(f"pl{s}", [P, 512]) for s in range(2)]
        loaded, xs_ready, logits, kept = st.sem("loaded"), st.pair("xs_ready"), st.pair("logits"), st.pair("kept")
        dve_step, exp_done, w_ready, w_turned, w_kept = (st.sem(n) for n in
                                                         ("dve_step", "exp_done", "w_ready", "w_turned", "w_kept"))
        with nc.Block() as block:
            @block.gpsimd
            def _(pool):
                st.open(pool)

            @block.sync
            def _(sp):
                sp.dma_start(rw[:, :], rw_d).then_inc(loaded, 16)
                sp.dma_start(rb[:, :], rb_d).then_inc(loaded, 16)

            @block.scalar
            def _(act):
                with act.Fori(0, GROUPS // 2) as i:
                    for s in range(2):
                        act.wait_ge(logits[s], before(i))
                        act.activation(xs[:, s, :], env.XNT[:, bass.ds((2 * i + s) * 512, 512)], ACT.Copy
                                       ).then_inc(xs_ready[s], 1)
                if kind != "one":
                    act.wait_ge(dve_step, 2)
                    act.activation(l0[:, :, :], l0[:, :, :], ACT.Exp).then_inc(exp_done, 1)
                for g in range(GROUPS):
                    act.wait_ge(w_turned, g + 1)
                    act.activation(WT[:, g * 512:(g + 1) * 512], pl[g % 2][0:EXPERTS, :], ACT.Copy).then_inc(w_kept, 1)

            @block.tensor
            def _(pe):
                pe.wait_ge(loaded, 32)
                with pe.Fori(0, GROUPS // 2) as i:
                    for s in range(2):
                        pe.wait_ge(xs_ready[s], made(i))
                        pe.wait_ge(kept[s], before(i))
                        for t in range(TG):
                            o = pl[s][:, t * EXPERTS:(t + 1) * EXPERTS]
                            pe.matmul(o, xs[:, s, t * P:(t + 1) * P], rw[:, :], start=True, stop=False)
                            last = pe.matmul(o, env.ones[0:1, 0:P], rb[:, :], start=False, stop=True)
                        last.then_inc(logits[s], 1)
                pe.wait_ge(w_ready, 1)
                for g in range(GROUPS):
                    if g >= 2:
                        pe.wait_ge(w_kept, g - 1)
                    for t in range(TG):
                        last = pe.transpose(pl[g % 2][0:EXPERTS, t * P:(t + 1) * P], W[:, g * TG + t, :],
                                            env.ident[:, :])
                    last.then_inc(w_turned, 1)

            @block.vector
            def _(dve):
                with dve.Fori(0, GROUPS // 2) as i:
                    for s in range(2):
                        dve.wait_ge(logits[s], made(i))
                        dve.tensor_copy(LG[:, bass.ds((2 * i + s) * TG, TG), :],
                                        pl[s][:, 0:TG * EXPERTS].rearrange("p (t e) -> p t e", e=EXPERTS)
                                        ).then_inc(kept[s], 1)
                dve.wait_ge(kept[0], before(GROUPS // 2))
                dve.wait_ge(kept[1], before(GROUPS // 2))
                step = [0]

                def done(ins):
                    step[0] += 1
                    ins.then_inc(dve_step, 1)
                    dve.wait_ge(dve_step, step[0])

                done(dve.tensor_reduce(m[:, :], LG[:, :, :], AX.X, ALU.max))
                if kind != "one":
                    done(dve.tensor_tensor(l0[:, :, :], LG[:, :, :], bc(m[:, :], 2, EXPERTS), ALU.subtract))
                    dve.wait_ge(exp_done, 1)
                    done(dve.tensor_reduce(sm[:, :], l0[:, :, :], AX.X, ALU.add))
                    done(dve.reciprocal(rs[:, :], sm[:, :]))
                    done(dve.tensor_tensor(pr[:, :, :], l0[:, :, :], bc(rs[:, :], 2, EXPERTS), ALU.mult))
                    done(dve.tensor_reduce(m[:, :], pr[:, :, :], AX.X, ALU.max))
                    src = pr
                else:
                    src = LG
                if kind == "choice":
                    done(dve.tensor_copy(W[:, :, :], pr[:, :, :]))
                else:
                    first_of_max(dve, done, env, src, m, l0, rs, W)
                if kind == "max":
                    done(dve.tensor_tensor(W[:, :, :], W[:, :, :], bc(m[:, :], 2, EXPERTS), ALU.mult))
                dve.wait_ge(dve_step, step[0])
                dve.sem_inc(w_ready, 1)


def first_of_max(dve, done, env, src, m, tmp, top, hot):
    n = src.shape[1]
    done(dve.tensor_tensor(tmp[:, 0:n, :], src[:, 0:n, :], bc(m[:, 0:n], 2, EXPERTS), ALU.is_equal))
    done(dve.tensor_tensor(tmp[:, 0:n, :], tmp[:, 0:n, :], bc(env.countdown[:, :], 1, n), ALU.mult))
    done(dve.tensor_reduce(top[:, 0:n], tmp[:, 0:n, :], AX.X, ALU.max))
    done(dve.tensor_tensor(hot[:, 0:n, :], tmp[:, 0:n, :], bc(top[:, 0:n], 2, EXPERTS), ALU.is_equal))


def linear_experts(nc, env, title, w_d, b_d, W, WT):
    with stage(nc, title) as st:
        we = st.sb("we", [P, EXPERTS * D])
        be = st.sb("be", [EXPERTS, D])
        xs = st.sb("xs", [P, 2, P])
        ws = st.sb("ws", [EXPERTS, 2, P])
        py = [st.ps(f"py{s}", [P, EXPERTS * D]) for s in range(2)]
        pb = [st.ps(f"pb{s}", [P, 512]) for s in range(2)]
        loaded = st.sem("loaded")
        staged, y_ready, y_used, added = st.pair("staged"), st.pair("y_ready"), st.pair("y_used"), st.sem("added")
        with nc.Block() as block:
            @block.gpsimd
            def _(pool):
                st.open(pool)

            @block.sync
            def _(sp):
                sp.dma_start(we[:, :], w_d).then_inc(loaded, 16)
                sp.dma_start(be[:, :], b_d).then_inc(loaded, 16)

            @block.scalar
            def _(act):
                with act.Fori(0, TILES // 2) as i:
                    for s in range(2):
                        n = 2 * i + s
                        act.wait_ge(y_ready[s], before(i))
                        act.activation(xs[:, s, :], env.XNT[:, bass.ds(n * P, P)], ACT.Copy)
                        act.activation(ws[:, s, :], WT[:, bass.ds(n * P, P)], ACT.Copy).then_inc(staged[s], 1)

            @block.tensor
            def _(pe):
                pe.wait_ge(loaded, 32)
                with pe.Fori(0, TILES // 2) as i:
                    for s in range(2):
                        pe.wait_ge(staged[s], made(i))
                        pe.wait_ge(y_used[s], before(i))
                        for h in range(2):
                            pe.matmul(py[s][:, h * 512:(h + 1) * 512], xs[:, s, :], we[:, h * 512:(h + 1) * 512])
                        pe.matmul(pb[s][:, 0:D], ws[:, s, :], be[:, :]).then_inc(y_ready[s], 1)

            @block.vector
            def _(dve):
                with dve.Fori(0, TILES // 2) as i:
                    for s in range(2):
                        n = 2 * i + s
                        dve.wait_ge(y_ready[s], made(i))
                        x = env.X[:, n, :]
                        dve.tensor_tensor(x, x, pb[s][:, 0:D], ALU.add).then_inc(added, 1)
                        for e in range(EXPERTS):
                            dve.wait_ge(added, n * (EXPERTS + 1) + e + 1)
                            dve.scalar_tensor_tensor(out=x, in0=py[s][:, e * D:(e + 1) * D],
                                                     scalar=W[:, n, e:e + 1], in1=x,
                                                     op0=ALU.mult, op1=ALU.add).then_inc(added, 1)
                        dve.wait_ge(added, (n + 1) * (EXPERTS + 1))
                        dve.sem_inc(y_used[s], 1)


def l0_ffn(nc, env, a):
    normalise(nc, env, "l0f_ln", env.X, dst_t=env.XNT)
    with stage(nc, "l0f") as st:
        W = st.sb("W", [P, TILES, EXPERTS])
        WT = st.sb("WT", [EXPERTS, T])
        route(nc, env, "l0f_route", (a.L0_ffn_router_w, a.L0_ffn_router_b), W, WT, "max")
        linear_experts(nc, env, "l0f_exp", a.L0_ffn_expert_w, a.L0_ffn_expert_b, W, WT)


def gelu_experts(nc, env, title, w, experts, chunks, W=None, WT=None, hidden_scale=None, extra=None):
    EC = experts * chunks
    with stage(nc, title) as st:
        w1, w2 = st.sb("w1", [P, EC * P]), st.sb("w2", [P, EC * D])
        b1 = st.sb("b1", [P, EC])
        b2 = st.sb("b2", [EXPERTS if WT is not None else 1, D])
        hid = st.sb("hid", [P, 2, chunks, 512])
        if WT is not None:
            ws = st.sb("ws", [EXPERTS, 512])
        if hidden_scale is not None:
            raw = st.sb("raw", [P, 4, 512])
        pH = [st.ps(f"pH{j}", [P, 512]) for j in range(4)]
        pY = [st.ps(f"pY{j}", [P, 512]) for j in range(2)]
        pB = st.ps("pB", [P, 512])
        loaded = st.sem("loaded")
        h_made, h_kept, h_ready, y_made, y_used, staged, b_made, b_used = (
            st.loop_sem(n) for n in ("h_made", "h_kept", "h_ready", "y_made", "y_used", "staged", "b_made", "b_used"))
        scaled = hidden_scale is not None
        ready = h_ready if scaled else h_kept
        with nc.Block() as block:
            @block.gpsimd
            def _(pool):
                st.open(pool)

            @block.sync
            def _(sp):
                for d, s_ in ((w1[:, :], w.w1), (b1[:, :], w.b1), (w2[:, :], w.w2), (b2[:, :], w.b2)):
                    sp.dma_start(d, s_).then_inc(loaded, 16)

            @block.tensor
            def _(pe):
                pe.wait_ge(loaded, 64)
                with pe.Fori(0, GROUPS) as g:
                    if WT is not None:
                        pe.wait_ge(staged, made(g))
                    pe.wait_ge(b_used, before(g))
                    for t in range(TG):
                        rows = ws[:, t * P:(t + 1) * P] if WT is not None else env.ones[0:1, 0:P]
                        last = pe.matmul(pB[:, t * D:(t + 1) * D], rows, b2[:, :])
                    last.then_inc(b_made, 1)
                    for e in range(experts + 1):
                        if e < experts:
                            for c in range(chunks):
                                k = e * chunks + c
                                pe.wait_ge(h_kept, before(g * EC + max(k - 3, 0)))
                                pe.matmul(pH[k % 4][:, :], w1[:, k * P:(k + 1) * P],
                                          env.XNT[:, bass.ds(g * 512, 512)]).then_inc(h_made, 1)
                        if e >= 1:
                            y = e - 1
                            pe.wait_ge(ready, made(g * EC + y * chunks + chunks - 1))
                            pe.wait_ge(y_used, before(g * experts + max(y - 1, 0)))
                            for t in range(TG):
                                for c in range(chunks):
                                    k = y * chunks + c
                                    last = pe.matmul(pY[y % 2][:, t * D:(t + 1) * D],
                                                     hid[:, y % 2, c, t * P:(t + 1) * P],
                                                     w2[:, k * D:(k + 1) * D], start=c == 0, stop=c == chunks - 1)
                            last.then_inc(y_made, 1)

            @block.scalar
            def _(act):
                act.wait_ge(loaded, 64)
                with act.Fori(0, GROUPS) as g:
                    if WT is not None:
                        act.wait_ge(b_made, before(g))
                        act.activation(ws[:, :], WT[:, bass.ds(g * 512, 512)], ACT.Copy).then_inc(staged, 1)
                    for k in range(EC):
                        e, c = divmod(k, chunks)
                        act.wait_ge(h_made, made(g * EC + k))
                        if scaled:
                            act.wait_ge(h_ready, before(g * EC))
                            out = raw[:, k % 4, :]
                        else:
                            act.wait_ge(y_made, before(g * experts + max(e - 1, 0)))
                            out = hid[:, e % 2, c, :]
                        act.activation(out, pH[k % 4][:, :], ACT.Gelu, bias=b1[:, k:k + 1]).then_inc(h_kept, 1)

            @block.vector
            def _(dve):
                with dve.Fori(0, GROUPS) as g:
                    xg = env.X[:, bass.ds(g * TG, TG), :]
                    tok = lambda ap: ap.rearrange("p (t d) -> p t d", d=D)
                    dve.wait_ge(b_made, made(g))
                    dve.tensor_tensor(xg, xg, tok(pB[:, :]), ALU.add).then_inc(b_used, 1)
                    dve.wait_ge(b_used, made(g))
                    if scaled:
                        dve.wait_ge(y_made, before(g * experts))
                        for c in range(chunks):
                            dve.wait_ge(h_kept, made(g * EC + c))
                            dve.tensor_tensor(hid[:, 0, c, :].rearrange("p (b s) -> p b s", s=S),
                                              raw[:, c % 4, :].rearrange("p (b s) -> p b s", s=S),
                                              bc(hidden_scale[:, c, bass.ds(g * 16, 16)], 2, S), ALU.mult
                                              ).then_inc(h_ready, 1)
                    for e in range(experts):
                        dve.wait_ge(y_made, made(g * experts + e))
                        dve.wait_ge(y_used, before(g * experts + e))
                        if W is None:
                            last = dve.tensor_tensor(xg, xg, tok(pY[e % 2][:, :]), ALU.add)
                        else:
                            for t in range(TG):
                                x = env.X[:, g * TG + t, :]
                                last = dve.scalar_tensor_tensor(
                                    out=x, in0=pY[e % 2][:, t * D:(t + 1) * D], scalar=W[:, g * TG + t, e:e + 1],
                                    in1=x, op0=ALU.mult, op1=ALU.add)
                        last.then_inc(y_used, 1)
                if extra is not None:
                    dve.wait_ge(y_used, before(GROUPS * experts))
                    dve.tensor_tensor(env.X[:, :, :], env.X[:, :, :], extra[:, :, :], ALU.add)


def weights_by_token(nc, env, title, W, WT, normalised):
    with stage(nc, title) as st:
        sm = st.sb("sm", [P, TILES])
        pw = st.ps("pw", [P, 512])
        turned, kept = st.sem("turned"), st.sem("kept")
        with nc.Block() as block:
            @block.tensor
            def _(pe):
                for n in range(TILES):
                    last = pe.transpose(pw[:, n * EXPERTS:(n + 1) * EXPERTS], WT[:, n * P:(n + 1) * P],
                                        env.ident[0:EXPERTS, 0:EXPERTS])
                last.then_inc(turned, 1)

            @block.vector
            def _(dve):
                dve.wait_ge(turned, 1)
                dve.tensor_copy(W[:, :, :], pw[:, 0:TILES * EXPERTS].rearrange("p (n e) -> p n e", e=EXPERTS)
                                ).then_inc(kept, 1)
                if normalised:
                    dve.wait_ge(kept, 1)
                    dve.tensor_reduce(sm[:, :], W[:, :, :], AX.X, ALU.add).then_inc(kept, 1)
                    dve.wait_ge(kept, 2)
                    dve.tensor_scalar(sm[:, :], sm[:, :], 1e-9, None, ALU.max).then_inc(kept, 1)
                    dve.wait_ge(kept, 3)
                    dve.reciprocal(sm[:, :], sm[:, :]).then_inc(kept, 1)
                    dve.wait_ge(kept, 4)
                    dve.tensor_tensor(W[:, :, :], W[:, :, :], bc(sm[:, :], 2, EXPERTS), ALU.mult)


def weights_by_expert(nc, env, title, W, WT):
    with stage(nc, title) as st:
        pw = [st.ps(f"pw{j}", [EXPERTS, 512]) for j in range(2)]
        turned, kept = st.sem("turned"), st.sem("kept")
        with nc.Block() as block:
            @block.tensor
            def _(pe):
                for g in range(GROUPS):
                    if g >= 2:
                        pe.wait_ge(kept, g - 1)
                    for t in range(TG):
                        last = pe.transpose(pw[g % 2][:, t * P:(t + 1) * P], W[:, g * TG + t, :], env.ident[:, :])
                    last.then_inc(turned, 1)

            @block.scalar
            def _(act):
                for g in range(GROUPS):
                    act.wait_ge(turned, g + 1)
                    act.activation(WT[:, g * 512:(g + 1) * 512], pw[g % 2][:, :], ACT.Copy).then_inc(kept, 1)


def choose_tokens(nc, env, title, WT):
    C = P // EXPERTS
    W_ = T // C
    BITS = 30
    scratch = nc.dram_tensor(f"{title}_scratch", (EXPERTS, T), F32).ap()
    scratch2 = nc.dram_tensor(f"{title}_scratch2", (EXPERTS, T), F32).ap()
    rows = lambda s: s.rearrange("e (c t) -> (e c) t", c=C)
    with stage(nc, title) as st:
        pc, gt, rank = (st.sb(n, [P, W_]) for n in ("pc", "gt", "rank"))
        ones, eq = st.sb("ones", [P, W_]), st.sb("eq", [P, W_])
        same, lower = st.sb("same", [P, P]), st.sb("lower", [P, P])
        bits = st.sb("bits", [P, BITS], I32)
        thr, cand, keep, cnt, need = (st.sb(n, [P, 1]) for n in ("thr", "cand", "keep", "cnt", "need"))
        ps = st.ps("ps", [P, 512])
        moved, landed, written = st.sem("moved"), st.sem("landed"), st.sem("written")
        step, counted, summed = st.loop_sem("step"), st.loop_sem("counted"), st.loop_sem("summed")
        ready, zeroed = st.sem("ready"), st.sem("zeroed")
        with nc.Block() as block:
            @block.gpsimd
            def _(pool):
                st.open(pool)

            @block.sync
            def _(sp):
                sp.dma_start(scratch, WT[:, :]).then_inc(moved, 16)
                sp.wait_ge(moved, 16)
                sp.dma_start(pc[:, :], rows(scratch)).then_inc(landed, 16)
                sp.dma_start(same[:, :], env.a.c_same_expert).then_inc(landed, 16)
                sp.dma_start(lower[:, :], env.a.c_lower_chunk).then_inc(landed, 16)
                sp.dma_start(bits[:, :], env.a.bits).then_inc(landed, 16)
                sp.wait_ge(ready, 1)
                sp.dma_start(rows(scratch2), pc[:, :]).then_inc(written, 16)
                sp.wait_ge(written, 16)
                sp.dma_start(WT[:, :], scratch2).then_inc(written, 16)
                sp.wait_ge(written, 32)

            @block.tensor
            def _(pe):
                pe.wait_ge(st.opened, 1)
                pe.wait_ge(landed, 64)
                with pe.Fori(0, BITS) as k:
                    pe.wait_ge(counted, made(k))
                    pe.matmul(ps[:, 0:1], same[:, :], cnt[:, :]).then_inc(summed, 1)
                pe.wait_ge(counted, made(BITS))
                pe.matmul(ps[:, 0:1], same[:, :], cnt[:, :]).then_inc(summed, 1)
                pe.wait_ge(counted, made(BITS + 1))
                pe.matmul(ps[:, 0:1], lower[:, :], cnt[:, :]).then_inc(summed, 1)

            @block.vector
            def _(dve):
                dve.wait_ge(st.opened, 1)
                dve.memset(thr[:, :], 0.0)
                dve.memset(ones[:, :], 1.0).then_inc(zeroed, 1)
                dve.wait_ge(zeroed, 1)
                dve.wait_ge(landed, 64)
                with dve.Fori(0, BITS) as k:
                    dve.wait_ge(step, 4 * k + 1)
                    dve.tensor_tensor(cand[:, :].bitcast(I32), thr[:, :].bitcast(I32), bits[:, bass.ds(k, 1)],
                                      ALU.bitwise_or).then_inc(step, 1)
                    dve.wait_ge(step, 4 * k + 2)
                    dve.tensor_scalar(gt[:, :], pc[:, :], cand[:, 0:1], None, ALU.is_ge).then_inc(step, 1)
                    dve.wait_ge(step, 4 * k + 3)
                    dve.tensor_reduce(cnt[:, :], gt[:, :], AX.X, ALU.add).then_inc(counted, 1)
                    dve.wait_ge(summed, made(k))
                    dve.tensor_scalar(keep[:, :], ps[:, 0:1], float(CAP), None, ALU.is_ge).then_inc(step, 1)
                    dve.wait_ge(step, 4 * k + 4)
                    dve.scalar_tensor_tensor(out=thr[:, :], in0=cand[:, :], scalar=keep[:, 0:1], in1=thr[:, :],
                                             op0=ALU.mult, op1=ALU.max).then_inc(step, 1)
                dve.wait_ge(step, 4 * BITS + 1)
                dve.tensor_scalar(gt[:, :], pc[:, :], thr[:, 0:1], None, ALU.is_gt).then_inc(step, 1)
                dve.wait_ge(step, 4 * BITS + 2)
                dve.tensor_reduce(cnt[:, :], gt[:, :], AX.X, ALU.add).then_inc(counted, 1)
                dve.wait_ge(summed, made(BITS))
                dve.tensor_scalar(need[:, :], ps[:, 0:1], -1.0, float(CAP), ALU.mult, ALU.add).then_inc(step, 1)
                dve.wait_ge(step, 4 * BITS + 3)
                dve.tensor_scalar(eq[:, :], pc[:, :], thr[:, 0:1], None, ALU.is_equal).then_inc(step, 1)
                dve.wait_ge(step, 4 * BITS + 4)
                dve.tensor_tensor_scan(rank[:, :], ones[:, :], eq[:, :], 0.0, ALU.mult, ALU.add).then_inc(step, 1)
                dve.wait_ge(step, 4 * BITS + 5)
                dve.tensor_copy(cnt[:, :], rank[:, W_ - 1:W_]).then_inc(counted, 1)
                dve.wait_ge(summed, made(BITS + 1))
                dve.tensor_scalar(rank[:, :], rank[:, :], ps[:, 0:1], None, ALU.add).then_inc(step, 1)
                dve.wait_ge(step, 4 * BITS + 6)
                dve.tensor_scalar(rank[:, :], rank[:, :], need[:, 0:1], None, ALU.is_le).then_inc(step, 1)
                dve.wait_ge(step, 4 * BITS + 7)
                dve.tensor_tensor(rank[:, :], rank[:, :], eq[:, :], ALU.mult).then_inc(step, 1)
                dve.wait_ge(step, 4 * BITS + 8)
                dve.tensor_tensor(rank[:, :], rank[:, :], gt[:, :], ALU.add).then_inc(step, 1)
                dve.wait_ge(step, 4 * BITS + 9)
                dve.tensor_tensor(pc[:, :], pc[:, :], rank[:, :], ALU.mult).then_inc(ready, 1)


def l1_attn(nc, env, a):
    with stage(nc, "l1a") as st:
        XN = st.sb("XN", [P, TILES, D])
        ln = st.sb("ln", [P, 4])
        landed = st.sem("landed")
        with nc.Block() as block:
            @block.sync
            def _(sp):
                sp.dma_start(ln[:, :], a.L1_attn_ln).then_inc(landed, 16)
                sp.wait_ge(landed, 16)
        normalise(nc, env, "l1a_ln0", env.X, dst=XN)
        normalise(nc, env, "l1a_ln1", XN, dst_t=env.XNT, gain=ln[:, 0:1], shift=ln[:, 1:2])
        w = Names(wq=a.L1_attn_wq, wk=a.L1_attn_wk, wv=a.L1_attn_wv, wo=a.L1_attn_Wo, wq2=a.L1_attn_wq2,
                            wk2=a.L1_attn_wk2, cos=a.c_rope_cos.rearrange("p (a t) -> p a t", a=2),
                            sin=a.c_rope_sin.rearrange("p (a t) -> p a t", a=2))
        block_attention(nc, env, "l1a_att", w, XN)
        normalise(nc, env, "l1a_ln2", XN, dst_t=env.XNT, gain=ln[:, 2:3], shift=ln[:, 3:4])
        w = Names(w1=a.L1_attn_W1, b1=a.L1_attn_b1, w2=a.L1_attn_W2, b2=a.L1_attn_b2)
        gelu_experts(nc, env, "l1a_mlp", w, 1, 4, extra=XN)


def l1_ffn(nc, env, a):
    normalise(nc, env, "l1f_ln", env.X, dst_t=env.XNT)
    with stage(nc, "l1f") as st:
        W = st.sb("W", [P, TILES, EXPERTS])
        WT = st.sb("WT", [EXPERTS, T])
        route(nc, env, "l1f_route", (a.L1_ffn_Wr, a.L1_ffn_br), W, WT, "one")
        w = Names(w1=a.L1_ffn_W1, b1=a.L1_ffn_b1, w2=a.L1_ffn_W2, b2=a.L1_ffn_b2)
        gelu_experts(nc, env, "l1f_exp", w, EXPERTS, 3, W=W, WT=WT)


def l2_ffn(nc, env, a):
    with stage(nc, "l2f") as st:
        W = st.sb("W", [P, TILES, EXPERTS])
        WT = st.sb("WT", [EXPERTS, T])
        with stage(nc, "l2f_norm") as st2:
            XN = st2.sb("XN", [P, TILES, D])
            gain = st2.sb("gain", [P, 1])
            landed = st2.sem("landed")
            with nc.Block() as block:
                @block.sync
                def _(sp):
                    sp.dma_start(gain[:, :], a.L2_ffn_norm_weight).then_inc(landed, 16)
                    sp.wait_ge(landed, 16)
            normalise(nc, env, "l2f_ln", env.X, dst=XN)
            normalise(nc, env, "l2f_rms", XN, dst_t=env.XNT, gain=gain[:, 0:1], rms=True)
        route(nc, env, "l2f_route", (a.L2_ffn_router_w, a.L2_ffn_router_b), W, WT, "choice")
        choose_tokens(nc, env, "l2f_choose", WT)
        weights_by_token(nc, env, "l2f_byt", W, WT, normalised=True)
        weights_by_expert(nc, env, "l2f_bye", W, WT)
        w = Names(w1=a.L2_ffn_fc1_w, b1=a.L2_ffn_fc1_b, w2=a.L2_ffn_fc2_w, b2=a.L2_ffn_fc2_b)
        gelu_experts(nc, env, "l2f_exp", w, EXPERTS, 4, W=W, WT=WT)


def pooled_gate(nc, env, title, gate_d, WT, wx):
    with stage(nc, title) as st:
        gw, spread = st.sb("gw", [P, EXPERTS]), st.sb("spread", [EXPERTS, 512])
        pooled = st.sb("pooled", [P, B])
        lg, ex, pr, tmp, hot1, hot2, W = (st.sb(n, [P, 1, EXPERTS])
                                          for n in ("lg", "ex", "pr", "tmp", "hot1", "hot2", "W"))
        m, sm, top, g1, g2 = (st.sb(n, [P, 1]) for n in ("m", "sm", "top", "g1", "g2"))
        wT = st.sb("wT", [EXPERTS, P])
        ps = st.ps("ps", [P, 512])
        loaded, dve_step, lg_made, exp_done, w_done, w_turned, wx_made = (
            st.sem(n) for n in ("loaded", "dve_step", "lg_made", "exp_done", "w_done", "w_turned", "wx_made"))
        with nc.Block() as block:
            @block.sync
            def _(sp):
                sp.dma_start(gw[:, :], gate_d).then_inc(loaded, 16)
                sp.dma_start(spread[:, :], env.a.c_spread).then_inc(loaded, 16)

            @block.tensor
            def _(pe):
                pe.wait_ge(loaded, 32)
                pe.wait_ge(dve_step, 2)
                pe.matmul(ps[:, 0:EXPERTS], pooled[:, :], gw[:, :]).then_inc(lg_made, 1)
                pe.wait_ge(w_done, 1)
                pe.transpose(ps[0:EXPERTS, 0:P], W[:, 0, :], env.ident[:, :]).then_inc(w_turned, 1)
                pe.wait_ge(w_done, 3)
                for c in range(4):
                    last = pe.matmul(ps[:, c * P:(c + 1) * P], spread[:, c * P:(c + 1) * P], wT[:, :])
                last.then_inc(wx_made, 1)

            @block.scalar
            def _(act):
                act.wait_ge(dve_step, 5)
                act.activation(ex[:, :, :], lg[:, :, :], ACT.Exp).then_inc(exp_done, 1)

            @block.vector
            def _(dve):
                step = [0]

                def done(ins):
                    step[0] += 1
                    ins.then_inc(dve_step, 1)
                    dve.wait_ge(dve_step, step[0])

                done(dve.tensor_reduce(pooled[:, :], env.XNT[:, :].rearrange("p (b s) -> p b s", s=S), AX.X, ALU.add))
                done(dve.tensor_scalar(pooled[:, :], pooled[:, :], 1.0 / S, None, ALU.mult))
                dve.wait_ge(lg_made, 1)
                done(dve.tensor_copy(lg[:, 0, :], ps[:, 0:EXPERTS]))
                done(dve.tensor_reduce(m[:, :], lg[:, :, :], AX.X, ALU.max))
                done(dve.tensor_scalar(lg[:, 0, :], lg[:, 0, :], m[:, 0:1], None, ALU.subtract))
                dve.wait_ge(exp_done, 1)
                done(dve.tensor_reduce(sm[:, :], ex[:, :, :], AX.X, ALU.add))
                done(dve.reciprocal(sm[:, :], sm[:, :]))
                done(dve.tensor_scalar(pr[:, 0, :], ex[:, 0, :], sm[:, 0:1], None, ALU.mult))
                done(dve.tensor_reduce(g1[:, :], pr[:, :, :], AX.X, ALU.max))
                first_of_max(dve, done, env, pr, g1, tmp, top, hot1)
                done(dve.scalar_tensor_tensor(out=pr[:, 0, :], in0=hot1[:, 0, :], scalar=-2.0, in1=pr[:, 0, :],
                                              op0=ALU.mult, op1=ALU.add))
                done(dve.tensor_reduce(g2[:, :], pr[:, :, :], AX.X, ALU.max))
                first_of_max(dve, done, env, pr, g2, tmp, top, hot2)
                done(dve.scalar_tensor_tensor(out=sm[:, :], in0=g1[:, :], scalar=1e-8, in1=g2[:, :],
                                              op0=ALU.add, op1=ALU.add))
                done(dve.reciprocal(sm[:, :], sm[:, :]))
                done(dve.tensor_scalar(hot1[:, 0, :], hot1[:, 0, :], g1[:, 0:1], None, ALU.mult))
                done(dve.scalar_tensor_tensor(out=hot1[:, 0, :], in0=hot2[:, 0, :], scalar=g2[:, 0:1],
                                              in1=hot1[:, 0, :], op0=ALU.mult, op1=ALU.add))
                dve.tensor_scalar(W[:, 0, :], hot1[:, 0, :], sm[:, 0:1], None, ALU.mult).then_inc(w_done, 1)
                dve.wait_ge(w_turned, 1)
                dve.tensor_copy(wT[:, :], ps[0:EXPERTS, 0:P]).then_inc(w_done, 1)
                dve.wait_ge(w_done, 2)
                dve.tensor_copy(WT[:, :].rearrange("e (b s) -> e b s", s=S), bc(wT[:, :], 2, S)).then_inc(w_done, 1)
                dve.wait_ge(wx_made, 1)
                dve.tensor_copy(wx[:, :, :], ps[:, :].rearrange("p (c b) -> p c b", b=B))


def l3_ffn(nc, env, a):
    normalise(nc, env, "l3f_ln", env.X, dst_t=env.XNT)
    with stage(nc, "l3f") as st:
        WT = st.sb("WT", [EXPERTS, T])
        wx = st.sb("wx", [P, 4, B])
        pooled_gate(nc, env, "l3f_gate", a.L3_ffn_gate_w, WT, wx)
        w = Names(w1=a.L3_ffn_down_w, b1=a.L3_ffn_down_b, w2=a.L3_ffn_up_w, b2=a.L3_ffn_up_b)
        gelu_experts(nc, env, "l3f_exp", w, 1, 4, WT=WT, hidden_scale=wx)


def context_tail_sum(nc, env, title, csum):
    with stage(nc, title) as st:
        ctx = st.sb("ctx", [P, 2, 8, KEYS])
        landed, summed = st.pair("landed"), st.pair("summed")
        with nc.Block() as block:
            @block.gpsimd
            def _(pool):
                st.open(pool)

            @block.sync
            def _(sp):
                with sp.Fori(0, B // 16) as i:
                    for s in range(2):
                        sp.wait_ge(summed[s], before(i))
                        sp.dma_start(ctx[:, s].rearrange("p b k -> p (b k)"), env.a.ctx_t[
                            :, bass.ds((2 * i + s) * 8 * KEYS, 8 * KEYS)]).then_inc(landed[s], 16)

            @block.vector
            def _(dve):
                with dve.Fori(0, B // 16) as i:
                    for s in range(2):
                        dve.wait_ge(landed[s], 16 * i + 17)
                        dve.tensor_reduce(csum[:, bass.ds((2 * i + s) * 8, 8)], ctx[:, s, :, S:KEYS], AX.X, ALU.add
                                          ).then_inc(summed[s], 1)


def add_transposed(nc, env, title, src, res):
    with stage(nc, title) as st:
        stg = st.sb("stg", [P, 2, 512])
        pt = [st.ps(f"pt{s}", [P, 512]) for s in range(2)]
        staged, turned, added = st.pair("staged"), st.pair("turned"), st.pair("added")
        with nc.Block() as block:
            @block.gpsimd
            def _(pool):
                st.open(pool)

            @block.scalar
            def _(act):
                with act.Fori(0, GROUPS // 2) as i:
                    for s in range(2):
                        act.wait_ge(turned[s], before(i))
                        act.activation(stg[:, s, :], src[:, bass.ds((2 * i + s) * 512, 512)], ACT.Copy
                                       ).then_inc(staged[s], 1)

            @block.tensor
            def _(pe):
                with pe.Fori(0, GROUPS // 2) as i:
                    for s in range(2):
                        pe.wait_ge(staged[s], made(i))
                        pe.wait_ge(added[s], before(i))
                        for t in range(TG):
                            last = pe.transpose(pt[s][:, t * P:(t + 1) * P], stg[:, s, t * P:(t + 1) * P],
                                                env.ident[:, :])
                        last.then_inc(turned[s], 1)

            @block.vector
            def _(dve):
                with dve.Fori(0, GROUPS // 2) as i:
                    for s in range(2):
                        dve.wait_ge(turned[s], made(i))
                        x = res[:, bass.ds((2 * i + s) * TG, TG), :]
                        dve.tensor_tensor(x, x, pt[s][:, :].rearrange("p (t d) -> p t d", d=D), ALU.add
                                          ).then_inc(added[s], 1)


def l0_xattn(nc, env, a):
    with stage(nc, "l0x") as st:
        csum = st.sb("csum", [P, B])
        context_tail_sum(nc, env, "l0x_sum", csum)
        normalise(nc, env, "l0x_ln", env.X, dst_t=env.XNT)
        w = Names(wq=a.L0_xattn_Wq, wk=a.L0_xattn_Wk, wv=a.L0_xattn_Wv, wo=a.L0_xattn_Wo)
        block_attention(nc, env, "l0x_att", w, env.X, csum=csum)


def run_slots(eng, slot, units, first=-2, last=2):
    low, high = last, units + first
    high -= (high - low) % 2
    for n in range(first, low):
        slot(n, n % 2)
    if high > low:
        with eng.Fori(0, (high - low) // 2) as i:
            slot(2 * i + low, low % 2)
            slot(2 * i + low + 1, (low + 1) % 2)
    for n in range(high, units + last):
        slot(n, n % 2)


def after(eng, sem, n):
    if not isinstance(n, int) or n >= 0:
        eng.wait_ge(sem, made(n))


def block_attention(nc, env, title, w, res, csum=None):
    cross = csum is not None
    units = TILES
    with stage(nc, title) as st:
        wq, wk, wv, wo = (st.sb(n, [P, D]) for n in ("wq", "wk", "wv", "wo"))
        own_group = st.sb("own_group", [P, 4])
        causal = st.sb("causal", [P, S])
        xs = st.sb("xs", [P, 2, BT, 4, S])
        qk = st.sb("qk", [P, 2, 2, P])
        qb, kb = st.sb("qb", [P, 2, BT, 4, S]), st.sb("kb", [P, 2, BT, 4, S])
        v = st.sb("v", [P, 2, BT, D])
        prob, probT = st.sb("prob", [P, 2, BT * 4, S]), st.sb("probT", [P, 2, BT, P])
        mx, sums, rs = (st.sb(n, [P, 2, BT * 4]) for n in ("mx", "sums", "rs"))
        own, oT = st.sb("own", [P, BT, 4, S]), st.sb("oT", [P, 2, P])
        loads = [(wq[:, :], w.wq), (wk[:, :], w.wk), (wv[:, :], w.wv), (wo[:, :], w.wo),
                 (own_group[:, :], env.a.c_m4q), (causal[:, :], env.a.c_causal_q01 if cross else env.a.c_causal_q_add)]
        if cross:
            kvs = st.sb("kvs", [P, 2, BT, S])
            cs = st.sb("cs", [P, 2, BT, 4])
            keep_i = st.sb("keep_i", [P, B, S], I32)
            keep, fill = st.sb("keep", [P, B, S]), st.sb("fill", [P, B, S])
            tail = st.sb("tail", [P, 2, BT * 4])
            vs, tailT = st.sb("vs", [16, 2, D]), st.sb("tailT", [16, 2, BT, P])
            group16, batch16 = st.sb("group16", [16, D]), st.sb("batch16", [16, BT])
            loads += [(keep_i[:, :, :], env.a.mask_pad[:, 0:S].unsqueeze(0).to_broadcast([P, B, S])),
                      (group16[:, :], env.a.c_group16), (batch16[:, :], env.a.c_batch16)]
        else:
            wq2, wk2 = st.sb("wq2", [P, D]), st.sb("wk2", [P, D])
            cos, sin = st.sb("cos", [P, 2, P]), st.sb("sin", [P, 2, P])
            t1, t2 = st.sb("t1", [P, 2, 2, P]), st.sb("t2", [P, 2, 2, P])
            loads += [(wq2[:, :], w.wq2), (wk2[:, :], w.wk2), (cos[:, :, :], w.cos), (sin[:, :, :], w.sin)]
        pA, pV, pT, pO, pX, pE = (st.ps(n, [P, 512]) for n in ("pA", "pV", "pT", "pO", "pX", "pE"))
        pS = [st.ps(f"pS{s}", [P, 512]) for s in range(2)]
        loaded, zeroed, keep_step = st.sem("loaded"), st.sem("zeroed"), st.sem("keep_step")
        landed = st.pair("landed")
        (xs_ready, qk_made, qk_read, qk_ready, kb_made, v_made, v_kept, s_made, score_step, m_made, shifted, p_made,
         sums_made, rs_made, p_scaled, t_made, t_kept, e_made, e_kept, o_made, own_made, ot_made, out_made, added, kept,
         cs_ready) = (
            st.loop_sem(n) for n in (
                "xs_ready", "qk_made", "qk_read", "qk_ready", "kb_made", "v_made", "v_kept", "s_made", "score_step",
                "m_made", "shifted", "p_made", "sums_made", "rs_made", "p_scaled", "t_made", "t_kept", "e_made",
                "e_kept", "o_made", "own_made", "ot_made", "out_made", "added",
                "kept", "cs_ready"))

        def inside(n):
            return not isinstance(n, int) or 0 <= n < units

        def landed_count(n, s):
            return 16 * ((n - s) // 2) + 17 if isinstance(n, int) else 8 * (n - s) + 17

        with nc.Block() as block:
            @block.gpsimd
            def _(pool):
                st.open(pool)
                pool.memset(v[:, :, :, :], 0.0).then_inc(zeroed, 1)
                pool.wait_ge(loaded, 16 * len(loads))

                def keys(n, s):
                    if cross:
                        pool.wait_ge(qk_ready, made(n))
                    else:
                        pool.wait_ge(qk_read, made(n))
                        after(pool, kb_made, n - 2)
                        pool.tensor_tensor(qk[:, s], t1[:, s], t2[:, s], ALU.add).then_inc(qk_ready, 1)
                        pool.wait_ge(qk_ready, made(n))
                    after(pool, s_made, n - 2)
                    q, k = (qk[:, s, u, :].rearrange("p (b t) -> p b t", t=S) for u in range(2))
                    pool.tensor_tensor(qb[:, s], bc(q, 2, 4), bc(bc(env.m4[:, :], 1, BT), 3, S), ALU.mult)
                    pool.tensor_tensor(kb[:, s], bc(k, 2, 4), bc(bc(own_group[:, :], 1, BT), 3, S), ALU.mult
                                       ).then_inc(kb_made, 1)

                def slot(n, s):
                    if inside(n + 3):
                        keys(n + 3, 1 - s)

                run_slots(pool, slot, units, first=-3)

            @block.sync
            def _(sp):
                for dst, src in loads:
                    sp.dma_start(dst, src).then_inc(loaded, 16)
                if cross:
                    def load(n, s):
                        after(sp, qk_made, n - 2)
                        after(sp, xs_ready, n - 2)
                        sp.dma_start(kvs[:, s], env.a.ctx_t.rearrange("d (b k) -> d b k", k=KEYS)[
                            :, bass.ds(n * BT, BT), 0:S]).then_inc(landed[s], 16)

                    load(0, 0)
                    load(1, 1)
                    with sp.Fori(0, units // 2 - 1) as i:
                        for s in range(2):
                            load(2 * i + s + 2, s)

            @block.tensor
            def _(pe):
                pe.wait_ge(loaded, 16 * len(loads))
                pe.wait_ge(st.opened, 1)

                def project(n, s):
                    after(pe, qk_ready if cross else qk_read, n - 1)
                    x = env.XNT[:, bass.ds(n * P, P)]
                    if cross:
                        pe.wait_ge(landed[s], landed_count(n, s))
                        kv = kvs[:, s].rearrange("p b k -> p (b k)")
                        pe.matmul(pA[:, 0:P], wq[:, :], x)
                        pe.matmul(pA[:, P:2 * P], wk[:, :], kv).then_inc(qk_made, 1)
                    else:
                        for u, wt in enumerate((wq, wk, wq2, wk2)):
                            last = pe.matmul(pA[:, u * P:(u + 1) * P], wt[:, :], x)
                        last.then_inc(qk_made, 1)

                def project_values(n, s):
                    after(pe, v_kept, n - 1)
                    pe.wait_ge(xs_ready, made(n))
                    for b in range(BT):
                        last = pe.matmul(pV[:, b * D:(b + 1) * D], xs[:, s, b].rearrange("p j k -> p (j k)"),
                                         wv[:, :])
                    last.then_inc(v_made, 1)

                def scores(n, s):
                    pe.wait_ge(kb_made, made(n))
                    after(pe, shifted, n - 2)
                    for b in range(BT):
                        last = pe.matmul(pS[s][:, b * P:(b + 1) * P], qb[:, s, b].rearrange("p h q -> p (h q)"),
                                         kb[:, s, b].rearrange("p j k -> p (j k)"))
                    last.then_inc(s_made, 1)

                def turn(n, s):
                    pe.wait_ge(p_scaled, made(n))
                    after(pe, t_kept, n - 1)
                    for b in range(BT):
                        last = pe.transpose(pT[:, b * P:(b + 1) * P],
                                            prob[:, s, 4 * b:4 * b + 4, :].rearrange("p j k -> p (j k)"),
                                            env.ident[:, :])
                    last.then_inc(t_made, 1)
                    if cross:
                        after(pe, e_kept, n - 1)
                        pe.wait_ge(cs_ready, made(n))
                        pe.matmul(pE[0:16, 0:D], cs[:, s].rearrange("p b j -> p (b j)"), wv[:, :])
                        pe.transpose(pE[0:16, D:D + P], tail[:, s, :], env.ident[:, :]).then_inc(e_made, 1)

                def attend(n, s):
                    pe.wait_ge(t_kept, made(n))
                    pe.wait_ge(v_kept, made(n))
                    after(pe, own_made, n - 1)
                    if cross:
                        pe.wait_ge(e_kept, made(n))
                        pe.matmul(pO[:, :], vs[:, s, :], tailT[:, s].rearrange("p b q -> p (b q)"), start=True,
                                  stop=False)
                    for b in range(BT):
                        last = pe.matmul(pO[:, b * P:(b + 1) * P], v[:, s, b, :], probT[:, s, b, :],
                                         start=not cross, stop=not cross or b == BT - 1)
                    last.then_inc(o_made, 1)

                def output(n, s):
                    pe.wait_ge(ot_made, made(n))
                    after(pe, added, n - 1)
                    pe.matmul(pX[:, 0:D], oT[:, s, :], wo[:, :]).then_inc(out_made, 1)

                def slot(n, s):
                    if inside(n + 1):
                        scores(n + 1, 1 - s)
                    if inside(n):
                        turn(n, s)
                    if inside(n + 3):
                        project(n + 3, 1 - s)
                    if inside(n + 2):
                        project_values(n + 2, s)
                    if inside(n):
                        attend(n, s)
                    if inside(n - 1):
                        output(n - 1, 1 - s)

                run_slots(pe, slot, units, first=-3)

            @block.scalar
            def _(act):
                act.wait_ge(zeroed, 1)
                act.wait_ge(st.opened, 1)

                def stage_tokens(n, s):
                    after(act, v_made, n - 2)
                    if cross:
                        act.wait_ge(landed[s], landed_count(n, s))
                        x = kvs[:, s]
                    else:
                        x = env.XNT[:, bass.ds(n * P, P)].rearrange("p (b t) -> p b t", t=S)
                    act.activation(xs[:, s], bc(x, 2, 4), ACT.Copy).then_inc(xs_ready, 1)

                def stage_tail(n, s):
                    after(act, e_made, n - 2)
                    act.activation(cs[:, s], bc(csum[:, bass.ds(n * BT, BT)], 2, 4), ACT.Copy).then_inc(cs_ready, 1)

                def keep_turned(n, s):
                    act.wait_ge(t_made, made(n))
                    after(act, o_made, n - 2)
                    act.activation(probT[:, s].rearrange("p b q -> p (b q)"), pT[:, :], ACT.Copy).then_inc(t_kept, 1)

                def exponentials(n, s):
                    act.wait_ge(shifted, made(n))
                    if cross:
                        after(act, e_made, n - 2)
                        act.activation(tail[:, s, :], mx[:, s, :], ACT.Exp, bias=env.neg[:, 0:1], scale=-1.0)
                    act.activation(prob[:, s], prob[:, s], ACT.Exp).then_inc(p_made, 1)

                def projections(n, s):
                    if cross:
                        act.wait_ge(qk_made, made(n))
                        after(act, kb_made, n - 2)
                        act.activation(qk[:, s, 0, :], pA[:, 0:P], ACT.Copy, scale=HD ** -0.5)
                        act.activation(qk[:, s, 1, :], pA[:, P:2 * P], ACT.Copy).then_inc(qk_ready, 1)

                def values(n, s):
                    act.wait_ge(v_made, made(n))
                    after(act, o_made, n - 2)
                    for j in range(4):
                        r = slice(32 * j, 32 * j + 32)
                        last = act.activation(v[r, s, :, r], pV[r, :].rearrange("p (b f) -> p b f", f=D)[:, :, r],
                                              ACT.Copy)
                    last.then_inc(v_kept, 1)

                def slot(n, s):
                    if inside(n + 2):
                        stage_tokens(n + 2, s)
                    if inside(n):
                        keep_turned(n, s)
                    if inside(n + 3):
                        projections(n + 3, 1 - s)
                    if inside(n + 1):
                        exponentials(n + 1, 1 - s)
                    if inside(n + 1) and cross:
                        stage_tail(n + 1, 1 - s)
                    if inside(n + 2):
                        values(n + 2, s)

                run_slots(act, slot, units, first=-3)

            @block.vector
            def _(dve):
                dve.wait_ge(loaded, 16 * len(loads))
                dve.wait_ge(st.opened, 1)
                if cross:
                    dve.tensor_copy(keep[:, :, :], keep_i[:, :, :]).then_inc(keep_step, 1)
                    dve.wait_ge(keep_step, 1)
                    dve.tensor_scalar(keep[:, :, :], keep[:, :, :], 0.0, None, ALU.not_equal).then_inc(keep_step, 1)
                    dve.wait_ge(keep_step, 2)
                    dve.tensor_tensor(keep[:, :, :], keep[:, :, :], bc(causal[:, :], 1, B), ALU.mult
                                      ).then_inc(keep_step, 1)
                    dve.wait_ge(keep_step, 3)
                    dve.tensor_scalar(fill[:, :, :], keep[:, :, :], -NEG, NEG, ALU.mult, ALU.add
                                      ).then_inc(keep_step, 1)
                    dve.wait_ge(keep_step, 4)

                def scores(n, s):
                    dve.wait_ge(s_made, made(n))
                    sc = pS[s][:, :].rearrange("p (g k) -> p g k", k=S)
                    if cross:
                        sc4 = pS[s][:, :].rearrange("p (b j k) -> p b j k", j=4, k=S)
                        dve.tensor_tensor(sc4, sc4, bc(keep[:, bass.ds(n * BT, BT), :], 2, 4), ALU.mult
                                          ).then_inc(kept, 1)
                        dve.wait_ge(kept, made(n))
                        dve.tensor_tensor(sc4, sc4, bc(fill[:, bass.ds(n * BT, BT), :], 2, 4), ALU.add
                                          ).then_inc(score_step, 1)
                    else:
                        dve.tensor_tensor(sc, sc, bc(causal[:, :], 1, BT * 4), ALU.add).then_inc(score_step, 1)
                    dve.wait_ge(score_step, made(n))
                    after(dve, p_made, n - 2)
                    dve.tensor_reduce(mx[:, s, :], sc, AX.X, ALU.max).then_inc(m_made, 1)
                    if cross:
                        dve.wait_ge(m_made, 2 * n + 2)
                        dve.tensor_scalar(mx[:, s, :], mx[:, s, :], NEG, None, ALU.max).then_inc(m_made, 1)
                        dve.wait_ge(m_made, 2 * n + 3)
                    else:
                        dve.wait_ge(m_made, made(n))
                    after(dve, t_made, n - 2)
                    dve.tensor_tensor(prob[:, s], sc, bc(mx[:, s, :], 2, S), ALU.subtract).then_inc(shifted, 1)

                def scale(n, s):
                    dve.wait_ge(p_made, made(n))
                    dve.tensor_reduce(sums[:, s, :], prob[:, s], AX.X, ALU.add).then_inc(sums_made, 1)
                    if cross:
                        dve.wait_ge(sums_made, 2 * n + 2)
                        dve.scalar_tensor_tensor(out=sums[:, s, :], in0=tail[:, s, :], scalar=float(KEYS - S),
                                                 in1=sums[:, s, :], op0=ALU.mult, op1=ALU.add).then_inc(sums_made, 1)
                        dve.wait_ge(sums_made, 2 * n + 3)
                    else:
                        dve.wait_ge(sums_made, made(n))
                    dve.reciprocal(rs[:, s, :], sums[:, s, :]).then_inc(rs_made, 1)
                    dve.wait_ge(rs_made, made(n))
                    if cross:
                        dve.tensor_tensor(tail[:, s, :], tail[:, s, :], rs[:, s, :], ALU.mult)
                    dve.tensor_tensor(prob[:, s], prob[:, s], bc(rs[:, s, :], 2, S), ALU.mult).then_inc(p_scaled, 1)

                def rotate(n, s):
                    dve.wait_ge(qk_made, made(n))
                    after(dve, qk_ready, n - 2)
                    ab = lambda o: pA[:, o:o + 2 * P].rearrange("p (a t) -> p a t", t=P)
                    dve.tensor_tensor(t1[:, s], ab(0), cos[:, :, :], ALU.mult)
                    dve.tensor_tensor(t2[:, s], ab(2 * P), sin[:, :, :], ALU.mult).then_inc(qk_read, 1)

                def tails(n, s):
                    dve.wait_ge(e_made, made(n))
                    after(dve, o_made, n - 2)
                    dve.tensor_tensor(vs[:, s, :], pE[0:16, 0:D], group16[:, :], ALU.mult)
                    dve.tensor_tensor(tailT[:, s], bc(pE[0:16, D:D + P], 1, BT), bc(batch16[:, :], 2, P), ALU.mult
                                      ).then_inc(e_kept, 1)

                def own_head(n, s):
                    dve.wait_ge(o_made, made(n))
                    dve.tensor_tensor(own[:, :, :, :], pO[:, :].rearrange("p (b h q) -> p b h q", h=4, q=S),
                                      bc(bc(env.m4[:, :], 1, BT), 3, S), ALU.mult).then_inc(own_made, 1)
                    dve.wait_ge(own_made, made(n))
                    after(dve, out_made, n - 2)
                    dve.tensor_reduce(oT[:, s, :].rearrange("p (b q) -> p b q", q=S),
                                      own[:, :, :, :].rearrange("p b h q -> p b q h"), AX.X, ALU.add
                                      ).then_inc(ot_made, 1)

                def add(n):
                    dve.wait_ge(out_made, made(n))
                    x = res[:, n, :]
                    dve.tensor_tensor(x, x, pX[:, 0:D], ALU.add).then_inc(added, 1)

                def slot(n, s):
                    if inside(n + 1):
                        scores(n + 1, 1 - s)
                    if inside(n - 2):
                        add(n - 2)
                    if inside(n) and cross:
                        tails(n, s)
                    if inside(n - 1):
                        own_head(n - 1, 1 - s)
                    if inside(n + 3) and not cross:
                        rotate(n + 3, 1 - s)
                    if inside(n + 1):
                        scale(n + 1, 1 - s)

                run_slots(dve, slot, units, first=-3)


def cosine_attention(nc, env, title, w, QA, KA):
    units = S
    with stage(nc, title) as st:
        wv, wo = st.sb("wv", [P, D]), st.sb("wo", [P, D])
        bv, bo, hs = st.sb("bv", [1, D]), st.sb("bo", [P, 1]), st.sb("hs", [P, 1])
        own_head = st.sb("own_head", [P, HEADS])
        xs, qT, v = (st.sb(n, [P, 2, P]) for n in ("xs", "qT", "v"))
        kb = st.sb("kb", [P, 2, HEADS, P])
        prob, probT = st.sb("prob", [P, 2, HEADS, P]), st.sb("probT", [P, 2, HEADS, P])
        nmx, sums, rs = (st.sb(n, [P, 2, HEADS]) for n in ("nmx", "sums", "rs"))
        os_, oT = st.sb("os", [P, 2, D]), st.sb("oT", [P, 2, P])
        loads = [(wv[:, :], w.wv), (wo[:, :], w.wo), (bv[:, :], w.bv), (bo[:, :], w.bo), (hs[:, :], w.hs),
                 (own_head[:, :], env.a.c_own_head)]
        pS = [st.ps(f"pS{j}", [P, 512]) for j in range(4)]
        pT = [st.ps(f"pT{j}", [P, 512]) for j in range(2)]
        pO, pM = st.ps("pO", [P, 512]), st.ps("pM", [P, 512])
        O, V, OT, OUT = pO[:, 0:P], pM[:, 0:P], pM[:, P:2 * P], pM[:, 2 * P:3 * P]
        loaded = st.sem("loaded")
        (xs_ready, kb_made, v_made, v_kept, s_made, m_made, p_made, o_made, rs_made, os_made, ot_made, ot_kept,
         out_made, finished) = (st.loop_sem(n) for n in (
             "xs_ready", "kb_made", "v_made", "v_kept", "s_made", "m_made", "p_made", "o_made", "rs_made", "os_made",
             "ot_made", "ot_kept", "out_made", "finished"))
        turned, kept = st.pair("turned"), st.pair("kept")

        def inside(n):
            return not isinstance(n, int) or 0 <= n < units

        def used_group(eng, sem, n):
            if not isinstance(n, int) or n >= 0:
                eng.wait_ge(sem, made(4 * n + 3))

        with nc.Block() as block:
            @block.gpsimd
            def _(pool):
                st.open(pool)
                pool.wait_ge(loaded, 16 * len(loads))

                def keys(n, s):
                    used_group(pool, s_made, n - 2)
                    pool.tensor_tensor(kb[:, s], bc(KA[:, bass.ds(n, P, step=S)], 1, HEADS),
                                       bc(own_head[:, :], 2, P), ALU.mult).then_inc(kb_made, 1)

                def slot(n, s):
                    if inside(n + 2):
                        keys(n + 2, s)

                run_slots(pool, slot, units, last=1)

            @block.sync
            def _(sp):
                for dst, src in loads:
                    sp.dma_start(dst, src).then_inc(loaded, 16)

            @block.tensor
            def _(pe):
                pe.wait_ge(loaded, 16 * len(loads))
                pe.wait_ge(st.opened, 1)

                def values(n, s):
                    pe.wait_ge(xs_ready, made(n))
                    after(pe, v_kept, n - 1)
                    after(pe, finished, n - 3)
                    pe.matmul(V, xs[:, s, :], wv[:, :], start=True, stop=False)
                    pe.matmul(V, env.ones[0:1, 0:P], bv[:, :], start=False, stop=True).then_inc(v_made, 1)

                def scores(n, s, j):
                    if j == 0:
                        pe.wait_ge(xs_ready, made(n))
                        pe.wait_ge(kb_made, made(n))
                    if not isinstance(n, int) or n:
                        pe.wait_ge(p_made, made(4 * n + j - 4))
                    pe.matmul(pS[j][:, :], qT[:, s, :], kb[:, s, 4 * j:4 * j + 4].rearrange("p h k -> p (h k)")
                              ).then_inc(s_made, 1)

                def turn(n, s, j):
                    pe.wait_ge(p_made, made(4 * n + j))
                    pe.wait_ge(kept[j % 2], before(2 * n + j // 2))
                    for h in range(4):
                        last = pe.transpose(pT[j % 2][:, h * P:(h + 1) * P], prob[:, s, 4 * j + h, :],
                                            env.ident[:, :])
                    last.then_inc(turned[j % 2], 1)

                def attend(n, s, j):
                    if j == 0:
                        pe.wait_ge(v_kept, made(n))
                        after(pe, os_made, n - 1)
                    pe.wait_ge(kept[j % 2], made(2 * n + j // 2))
                    for h in range(4 * j, 4 * j + 4):
                        last = pe.matmul(O[:, h * HD:(h + 1) * HD], probT[:, s, h, :], v[:, s, h * HD:(h + 1) * HD])
                    if j == 3:
                        last.then_inc(o_made, 1)

                def turn_output(n, s):
                    pe.wait_ge(os_made, made(n))
                    pe.wait_ge(v_kept, made(min(n + 2, units - 1) if isinstance(n, int) else n + 2))
                    after(pe, finished, n - 1)
                    pe.transpose(OT, os_[:, s, :], env.ident[:, :]).then_inc(ot_made, 1)

                def project(n, s):
                    pe.wait_ge(ot_kept, made(n))
                    pe.matmul(OUT, wo[:, :], oT[:, s, :]).then_inc(out_made, 1)

                def slot(n, s):
                    for j in range(4):
                        if inside(n + 1):
                            scores(n + 1, 1 - s, j)
                        if inside(n):
                            turn(n, s, j)
                        if j == 0 and inside(n - 1):
                            turn_output(n - 1, 1 - s)
                        if j >= 1 and inside(n):
                            attend(n, s, j - 1)
                        if j == 1 and inside(n - 1):
                            project(n - 1, 1 - s)
                        if j == 2 and inside(n + 2):
                            values(n + 2, s)
                    if inside(n):
                        attend(n, s, 3)

                run_slots(pe, slot, units, last=1)

            @block.scalar
            def _(act):
                act.wait_ge(loaded, 16 * len(loads))
                act.wait_ge(st.opened, 1)

                def tokens(n, s):
                    used_group(act, s_made, n - 2)
                    after(act, v_made, n - 2)
                    act.activation(qT[:, s, :], QA[:, bass.ds(n, P, step=S)], ACT.Copy)
                    act.activation(xs[:, s, :], env.XNT[:, bass.ds(n, P, step=S)], ACT.Copy).then_inc(xs_ready, 1)

                def values(n, s):
                    act.wait_ge(v_made, made(n))
                    after(act, o_made, n - 2)
                    act.activation(v[:, s, :], V, ACT.Copy).then_inc(v_kept, 1)

                def exponentials(n, s, j):
                    act.wait_ge(m_made, made(4 * n + j))
                    if j == 0 and (not isinstance(n, int) or n >= 2):
                        act.wait_ge(turned[1], made(2 * n - 3))
                        act.wait_ge(rs_made, made(n - 2))
                    for h in range(4):
                        u = 4 * j + h
                        last = act.activation(prob[:, s, u, :], pS[j][:, h * P:(h + 1) * P], ACT.Exp,
                                              bias=nmx[:, s, u:u + 1], accum_out=sums[:, s, u:u + 1])
                    last.then_inc(p_made, 1)

                def keep_turned(n, s, j):
                    act.wait_ge(turned[1], made(2 * n + j // 2))
                    act.activation(probT[:, s, 4 * j:4 * j + 4, :], pT[1][:, :].rearrange("p (h q) -> p h q", q=P),
                                   ACT.Copy).then_inc(kept[1], 1)

                def keep_output(n, s):
                    act.wait_ge(ot_made, made(n))
                    act.activation(oT[:, s, :], OT, ACT.Copy, scale=hs[:, 0:1]).then_inc(ot_kept, 1)

                def slot(n, s):
                    if inside(n + 2):
                        tokens(n + 2, s)
                    for j in range(4):
                        if j == 3 and inside(n):
                            keep_turned(n, s, j)
                        if inside(n + 1):
                            exponentials(n + 1, 1 - s, j)
                        if j == 0 and inside(n - 1):
                            keep_output(n - 1, 1 - s)
                    if inside(n + 2):
                        values(n + 2, s)

                run_slots(act, slot, units, last=1)

            @block.vector
            def _(dve):
                dve.wait_ge(loaded, 16 * len(loads))
                dve.wait_ge(st.opened, 1)

                def maxima(n, s, j):
                    dve.wait_ge(s_made, made(4 * n + j))
                    dve.tensor_reduce(nmx[:, s, 4 * j:4 * j + 4], pS[j][:, :].rearrange("p (h k) -> p h k", k=P),
                                      AX.X, ALU.max, negate=True).then_inc(m_made, 1)

                def keep_turned(n, s, j):
                    dve.wait_ge(turned[j % 2], made(2 * n + j // 2))
                    dve.tensor_copy(probT[:, s, 4 * j:4 * j + 4, :],
                                    pT[j % 2][:, :].rearrange("p (h q) -> p h q", q=P)).then_inc(kept[j % 2], 1)

                def factors(n, s):
                    dve.wait_ge(p_made, made(4 * n + 3))
                    dve.reciprocal(rs[:, s, :], sums[:, s, :]).then_inc(rs_made, 1)

                def scale(n, s):
                    dve.wait_ge(o_made, made(n))
                    dve.wait_ge(rs_made, made(n))
                    after(dve, ot_made, n - 2)
                    dve.tensor_tensor(os_[:, s, :].rearrange("p (h d) -> p h d", d=HD),
                                      O.rearrange("p (h d) -> p h d", d=HD), bc(rs[:, s, :], 2, HD), ALU.mult
                                      ).then_inc(os_made, 1)

                def finish(n):
                    dve.wait_ge(out_made, made(n))
                    dve.tensor_scalar(env.XNT[:, bass.ds(n, P, step=S)], OUT, bo[:, 0:1], None, ALU.add
                                      ).then_inc(finished, 1)

                def slot(n, s):
                    if inside(n - 1):
                        scale(n - 1, 1 - s)
                    for j in range(4):
                        if inside(n + 1):
                            maxima(n + 1, 1 - s, j)
                        if j < 3 and inside(n):
                            keep_turned(n, s, j)
                        if j == 1 and inside(n - 1):
                            finish(n - 1)
                    if inside(n):
                        factors(n, s)

                run_slots(dve, slot, units, last=1)


def plain_projection(nc, env, title, w_d, src, dst, bias_d=None, scale=1.0):
    with stage(nc, title) as st:
        w, bias = st.sb("w", [P, D]), st.sb("bias", [P, 1])
        y = st.sb("y", [P, 2, 512])
        pY = [st.ps(f"pY{s}", [P, 512]) for s in range(2)]
        loaded = st.sem("loaded")
        y_made, y_kept, done = st.pair("y_made"), st.pair("y_kept"), st.pair("done")
        loads = [(w[:, :], w_d)] + ([(bias[:, :], bias_d)] if bias_d is not None else [])
        with nc.Block() as block:
            @block.gpsimd
            def _(pool):
                st.open(pool)

            @block.sync
            def _(sp):
                for d, s_ in loads:
                    sp.dma_start(d, s_).then_inc(loaded, 16)

            @block.tensor
            def _(pe):
                pe.wait_ge(loaded, 16 * len(loads))
                with pe.Fori(0, GROUPS // 2) as i:
                    for s in range(2):
                        pe.wait_ge(y_kept[s], before(i))
                        pe.matmul(pY[s][:, :], w[:, :], src[:, bass.ds((2 * i + s) * 512, 512)]
                                  ).then_inc(y_made[s], 1)

            @block.scalar
            def _(act):
                act.wait_ge(loaded, 16 * len(loads))
                with act.Fori(0, GROUPS // 2) as i:
                    for s in range(2):
                        out = dst[:, bass.ds((2 * i + s) * 512, 512)]
                        act.wait_ge(y_made[s], made(i))
                        if bias_d is None:
                            act.activation(out, pY[s][:, :], ACT.Copy, scale=scale).then_inc(y_kept[s], 1)
                            continue
                        if scale == 1.0:
                            act.activation(out, pY[s][:, :], ACT.Identity, bias=bias[:, 0:1]).then_inc(y_kept[s], 1)
                            continue
                        act.activation(y[:, s, :], pY[s][:, :], ACT.Identity, bias=bias[:, 0:1]
                                       ).then_inc(y_kept[s], 1)
                        act.wait_ge(y_kept[s], made(i))
                        act.activation(out, y[:, s, :], ACT.Copy, scale=scale).then_inc(done[s], 1)


def head_projection(nc, env, title, mode, w_d, src, dst, pieces, width, ctx=False, bias_d=None, gain_d=None,
                    logit_d=None):
    ln = mode == "ln"
    units = pieces // 4
    with stage(nc, title) as st:
        w = st.sb("w", [P, D])
        cols = st.sb("cols", [P, 4])
        y = st.sb("y", [P, 2, 4, width])
        y2 = st.sb("y2", [P, 4, width])
        sd = st.sb("sd", [P, width])
        gather, spread = st.sb("gather", [P, 4, P]), st.sb("spread", [P, 4, P])
        if ctx:
            xin = st.sb("xin", [P, 2, 4, width])
        raw, centre = (st.sb("raw", [P, D]), st.sb("centre", [P, P])) if ln else (None, None)
        pY = [st.ps(f"pY{u}", [P, 512]) for u in range(4)]
        pV = st.ps("pV", [P, 512])
        pR = [st.ps(f"pR{r}", [P, 512]) for r in range(2)]
        loaded, w_made, w_kept, logit = (st.sem(n) for n in ("loaded", "w_made", "w_kept", "logit"))
        landed = st.pair("landed")
        (y_made, y_kept, sq_made, var_made, sd_made, sd_step, rs_made, r_made, r_used, done) = (
            st.loop_sem(n) for n in ("y_made", "y_kept", "sq_made", "var_made", "sd_made", "sd_step", "rs_made",
                                     "r_made", "r_used", "done"))
        loads = [(w[:, :], w_d)] if not ln else [(raw[:, :], w_d), (centre[:, :], env.a.c_centre)]
        loads += [(gather[:, :, :], (env.a.c_gather_mean if ln else env.a.c_gather_sum).rearrange(
            "p (u r) -> p u r", u=4)), (spread[:, :, :], env.a.c_spread_heads.rearrange("p (u f) -> p u f", u=4))]
        if bias_d is not None:
            loads += [(cols[:, 0:1], bias_d)]
        if gain_d is not None:
            loads += [(cols[:, 1:2], gain_d)]
        if logit_d is not None:
            loads += [(cols[:, 2:3], logit_d)]

        def inside(n):
            return not isinstance(n, int) or 0 <= n < units

        def after_pieces(eng, sem, n, u=3):
            if not isinstance(n, int) or n >= 0:
                eng.wait_ge(sem, made(4 * n + u))

        with nc.Block() as block:
            @block.gpsimd
            def _(pool):
                st.open(pool)

            @block.sync
            def _(sp):
                for d, s_ in loads:
                    sp.dma_start(d, s_).then_inc(loaded, 16)
                if ctx:
                    def load(n, s):
                        sp.dma_start(xin[:, s].rearrange("p u t -> p (u t)"),
                                     src[:, bass.ds(n * 4 * width, 4 * width)]).then_inc(landed[s], 16)

                    load(0, 0)
                    load(1, 1)
                    with sp.Fori(0, units // 2 - 1) as i:
                        for s in range(2):
                            sp.wait_ge(y_made, made(4 * (2 * i + s) + 3))
                            load(2 * i + s + 2, s)

            @block.tensor
            def _(pe):
                pe.wait_ge(loaded, 16 * len(loads))
                pe.wait_ge(st.opened, 1)
                if ln:
                    pe.matmul(pY[0][:, 0:D], raw[:, :], centre[:, :]).then_inc(w_made, 1)
                    pe.wait_ge(w_kept, 1)

                def project(n, s):
                    if ctx:
                        pe.wait_ge(landed[s], 16 * ((n - s) // 2) + 17 if isinstance(n, int) else 8 * (n - s) + 17)
                    for u in range(4):
                        x = xin[:, s, u, :] if ctx else src[:, bass.ds((4 * n + u) * width, width)]
                        after_pieces(pe, y_kept, n - 1, u)
                        pe.matmul(pY[u][:, 0:width], w[:, :], x).then_inc(y_made, 1)

                def variances(n):
                    after(pe, sd_made, n - 1)
                    for u in range(4):
                        pe.wait_ge(sq_made, made(4 * n + u))
                        last = pe.matmul(pV[:, 0:width], gather[:, u, :], y2[:, u, :], start=u == 0, stop=u == 3)
                    last.then_inc(var_made, 1)

                def factors(n):
                    pe.wait_ge(rs_made, made(n))
                    for u in range(4):
                        if u >= 2:
                            pe.wait_ge(r_used, made(4 * n + u - 2))
                        else:
                            after_pieces(pe, r_used, n - 1, u + 2)
                        pe.matmul(pR[u % 2][:, 0:width], spread[:, u, :], sd[:, :]).then_inc(r_made, 1)

                def slot(n, s):
                    if inside(n):
                        variances(n)
                    if inside(n + 1):
                        project(n + 1, 1 - s)
                    if inside(n):
                        factors(n)

                run_slots(pe, slot, units, first=-1, last=0)

            @block.scalar
            def _(act):
                act.wait_ge(loaded, 16 * len(loads))
                act.wait_ge(st.opened, 1)
                if ln:
                    act.wait_ge(w_made, 1)
                    act.activation(w[:, :], pY[0][:, 0:D], ACT.Copy).then_inc(w_kept, 1)
                if logit_d is not None:
                    act.wait_ge(logit, 1)
                    act.activation(cols[:, 3:4], cols[:, 2:3], ACT.Exp).then_inc(logit, 1)

                def projected(n, s):
                    for u in range(4):
                        act.wait_ge(y_made, made(4 * n + u))
                        if u == 0:
                            after_pieces(act, done if ln else r_used, n - 2)
                        if ln:
                            act.activation(y[:, s, u, :], pY[u][:, 0:width], ACT.Copy).then_inc(y_kept, 1)
                        else:
                            act.activation(y[:, s, u, :], pY[u][:, 0:width], ACT.Identity, bias=cols[:, 0:1]
                                           ).then_inc(y_kept, 1)
                        act.wait_ge(y_kept, made(4 * n + u))
                        after(act, var_made, n - 1)
                        act.activation(y2[:, u, :], y[:, s, u, :], ACT.Square).then_inc(sq_made, 1)

                def roots(n):
                    act.wait_ge(var_made, made(n))
                    after_pieces(act, r_made, n - 1)
                    if ln:
                        act.activation(sd[:, :], pV[:, 0:width], ACT.Sqrt, bias=env.eps[:, 0:1]).then_inc(sd_made, 1)
                    else:
                        act.activation(sd[:, :], pV[:, 0:width], ACT.Sqrt).then_inc(sd_made, 1)

                def finish(n, s):
                    for u in range(4):
                        act.wait_ge(r_used, made(4 * n + u))
                        act.activation(dst[:, bass.ds((4 * n + u) * width, width)], y[:, s, u, :], ACT.Identity,
                                       scale=cols[:, 1:2], bias=cols[:, 0:1]).then_inc(done, 1)

                def slot(n, s):
                    if inside(n):
                        roots(n)
                    if inside(n + 1):
                        projected(n + 1, 1 - s)
                    if ln and inside(n):
                        finish(n, s)

                run_slots(act, slot, units, first=-1, last=0)

            @block.vector
            def _(dve):
                dve.wait_ge(loaded, 16 * len(loads))
                dve.wait_ge(st.opened, 1)
                if logit_d is not None:
                    dve.tensor_scalar(cols[:, 2:3], cols[:, 2:3], float(np.log(100.0)), None, ALU.min
                                      ).then_inc(logit, 1)
                    dve.wait_ge(logit, 2)

                def slot(n, s):
                    if not inside(n):
                        return
                    dve.wait_ge(sd_made, made(n))
                    if not ln:
                        dve.tensor_scalar(sd[:, :], sd[:, :], 1e-12, None, ALU.max).then_inc(sd_step, 1)
                        dve.wait_ge(sd_step, made(n))
                    dve.reciprocal(sd[:, :], sd[:, :]).then_inc(rs_made, 1)
                    for u in range(4):
                        dve.wait_ge(r_made, made(4 * n + u))
                        yu, ru, out = y[:, s, u, :], pR[u % 2][:, 0:width], dst[:, bass.ds((4 * n + u) * width, width)]
                        if ln:
                            dve.tensor_tensor(yu, yu, ru, ALU.mult).then_inc(r_used, 1)
                        elif logit_d is not None:
                            dve.scalar_tensor_tensor(out=out, in0=yu, scalar=cols[:, 3:4], in1=ru, op0=ALU.mult,
                                                     op1=ALU.mult).then_inc(r_used, 1)
                        else:
                            dve.tensor_tensor(out, yu, ru, ALU.mult).then_inc(r_used, 1)

                run_slots(dve, slot, units, first=-1, last=0)


def cross_attention(nc, env, title, w, QT, KA=None, masked=False):
    with stage(nc, title) as st:
        wk, wv = st.sb("wk", [P, D]), st.sb("wv", [P, D])
        cols = st.sb("cols", [P, 2])
        m4q, selq = st.sb("m4q", [P, 4]), st.sb("selq", [P, S])
        ctx = st.sb("ctx", [P, 2, KPAD])
        kT = st.sb("kT", [P, 2, KPAD])
        qb = st.sb("qb", [P, 2, HEADS, S])
        own_head16 = st.sb("own_head16", [P, HEADS])
        v = st.sb("v", [CH, 2, 3, D])
        prob = st.sb("prob", [P, 2, 4, KPAD])
        probT = st.sb("probT", [CH, 2, 4, 3 * P])
        nmx, sums, rs = (st.sb(n, [P, 2, 4]) for n in ("nmx", "sums", "rs"))
        rm = st.sb("rm", [P, 2, 4, 4])
        rx = st.sb("rx", [P, 2, D])
        own = st.sb("own", [P, 4, S])
        ou, on = st.sb("ou", [P, S]), st.sb("on", [P, 2, S])
        loads = [(wv[:, :], w.wv), (m4q[:, :], env.a.c_m4q), (selq[:, :], env.a.c_selq),
                 (own_head16[:, :], env.a.c_own_head)]
        if KA is None:
            loads += [(wk[:, :], w.wk), (cols[:, 0:1], w.bk), (cols[:, 1:2], w.bv)]
        if masked:
            mask_i, mask = st.sb("mask_i", [P, KEYS], I32), st.sb("mask", [P, KEYS])
            mask_b, ident_b = st.sb("mask_b", [P, KEYS], BF16), st.sb("ident_b", [P, P], BF16)
            loads += [(mask_i[:, :], w.mask)]
        pS = [st.ps(f"pS{j}", [P, 512]) for j in range(4)]
        pT = [st.ps(f"pT{j}", [P, 512]) for j in range(2)]
        pKV = st.ps("pKV", [P, 512])
        pO = st.ps("pO", [P, 512])
        O, R = pO[:, 0:P], pKV[:, 448:448 + S]
        loaded, mask_made, padded = (st.sem(n) for n in ("loaded", "mask_made", "padded"))
        landed = st.pair("landed")
        (q_made, k_made, v_made, k_kept, v_kept, s_made, m_made, p_made, o_made, rs_made, rm_made, rx_made, own_made,
         ou_made, r_made, on_made, done) = (st.loop_sem(n) for n in (
             "q_made", "k_made", "v_made", "k_kept", "v_kept", "s_made", "m_made", "p_made", "o_made", "rs_made",
             "rm_made", "rx_made", "own_made", "ou_made", "r_made", "on_made", "done"))
        turned, kept = st.pair("turned"), st.pair("kept")

        def slots(eng, slot):
            slot(0, 0)
            with eng.Fori(0, (B - 4) // 2) as i:
                slot(2 * i + 1, 1)
                slot(2 * i + 2, 0)
            for n in range(B - 3, B):
                slot(n, n % 2)

        def inside(n, ahead=0):
            return not isinstance(n, int) or 0 <= n + ahead < B

        with nc.Block() as block:
            @block.gpsimd
            def _(pool):
                st.open(pool)
                pool.memset(ctx[:, :, KEYS:KPAD], 0.0)
                pool.memset(kT[:, :, KEYS:KPAD], 0.0)
                pool.memset(prob[:, :, :, KEYS:KPAD], 0.0).then_inc(padded, 1)
                pool.wait_ge(loaded, 16 * len(loads))

                def queries(n, s):
                    if not isinstance(n, int) or n >= 2:
                        pool.wait_ge(s_made, made(4 * n - 5))
                    pool.tensor_tensor(qb[:, s], bc(QT[:, bass.ds(n * S, S)], 1, HEADS), bc(own_head16[:, :], 2, S),
                                       ALU.mult).then_inc(q_made, 1)

                for n in range(2):
                    queries(n, n)
                with pool.Fori(0, B // 2 - 1) as i:
                    for s in range(2):
                        queries(2 * i + s + 2, s)

            @block.sync
            def _(sp):
                for d, s_ in loads:
                    sp.dma_start(d, s_).then_inc(loaded, 16)

                def load(n, s):
                    sp.dma_start(ctx[:, s, 0:KEYS], env.a.ctx_t[:, bass.ds(n * KEYS, KEYS)]).then_inc(landed[s], 16)

                load(0, 0)
                load(1, 1)
                with sp.Fori(0, B // 2 - 1) as i:
                    for s in range(2):
                        sp.wait_ge(v_made, made(2 * i + s))
                        load(2 * i + s + 2, s)

            @block.tensor
            def _(pe):
                pe.wait_ge(loaded, 16 * len(loads))
                pe.wait_ge(padded, 1)
                if masked:
                    pe.wait_ge(mask_made, 3)

                def landed_count(n, s):
                    return 16 * ((n - s) // 2) + 17 if isinstance(n, int) else 8 * (n - s) + 17

                def keys(n, s):
                    pe.wait_ge(landed[s], landed_count(n, s))
                    pe.wait_ge(v_kept, before(n))
                    if KA is None:
                        pe.matmul(pKV[:, 0:KEYS], wk[:, :], ctx[:, s, 0:KEYS]).then_inc(k_made, 1)

                def values(n, s):
                    if KA is None:
                        pe.wait_ge(k_kept, made(n))
                    if not isinstance(n, int) or n >= 3:
                        pe.wait_ge(on_made, made(n - 3))
                    for c in range(3):
                        last = pe.matmul(pKV[0:CH, c * D:(c + 1) * D], ctx[:, s, c * CH:(c + 1) * CH], wv[:, :])
                    last.then_inc(v_made, 1)

                def scores(n, s, j):
                    if j == 0:
                        pe.wait_ge(q_made, made(n))
                        pe.wait_ge(k_kept, made(n))
                    if not isinstance(n, int) or n:
                        pe.wait_ge(p_made, made(4 * n + j - 4))
                    last = pe.matmul(pS[j][:, 0:KEYS], qb[:, s, 4 * j:4 * j + 4].rearrange("p h q -> p (h q)"),
                              kT[:, s, 0:KEYS], start=True, stop=not masked)
                    if masked:
                        last = pe.matmul(pS[j][:, 0:KEYS], ident_b[:, :], mask_b[:, :], start=False, stop=True)
                    last.then_inc(s_made, 1)

                def turn(n, s, j):
                    pe.wait_ge(p_made, made(4 * n + j))
                    pe.wait_ge(kept[j % 2], before(2 * n + j // 2))
                    for c in range(3):
                        last = pe.transpose(pT[j % 2][0:CH, c * P:(c + 1) * P], prob[:, s, j, c * CH:(c + 1) * CH],
                                            env.ident[:, :])
                    last.then_inc(turned[j % 2], 1)

                def attend(n, s, j):
                    if j == 0:
                        pe.wait_ge(v_kept, made(n))
                        pe.wait_ge(own_made, before(n))
                    pe.wait_ge(kept[j % 2], made(2 * n + j // 2))
                    for c in range(3):
                        last = pe.matmul(O[j * 32:j * 32 + 32, :], v[:, s, c, j * 32:j * 32 + 32],
                                         probT[:, s, j, c * P:(c + 1) * P], start=c == 0, stop=c == 2)
                    if j == 3:
                        last.then_inc(o_made, 1)

                def normaliser(n, s):
                    pe.wait_ge(rx_made, made(n))
                    if inside(n, 3):
                        pe.wait_ge(k_kept, made(n + 3))
                    pe.wait_ge(v_kept, made(min(n + 2, B - 1) if isinstance(n, int) else n + 2))
                    pe.matmul(R, rx[:, s, :], selq[:, :]).then_inc(r_made, 1)

                for n in range(2):
                    keys(n, n)
                    values(n, n)
                for j in range(4):
                    scores(0, 0, j)

                def slot(n, s):
                    for j in range(4):
                        turn(n, s, j)
                        if inside(n, 1):
                            scores(n + 1, 1 - s, j)
                        if j == 0 and inside(n, 2):
                            keys(n + 2, s)
                        if j == 1 and inside(n, -1):
                            normaliser(n - 1, 1 - s)
                        if j >= 1:
                            attend(n, s, j - 1)
                        if j == 2 and inside(n, 2):
                            values(n + 2, s)
                    attend(n, s, 3)

                slots(pe, slot)
                normaliser(B - 1, 1)

            @block.scalar
            def _(act):
                act.wait_ge(loaded, 16 * len(loads))
                act.wait_ge(padded, 1)

                def keys(n, s):
                    if KA is not None:
                        if not isinstance(n, int) or n >= 2:
                            act.wait_ge(s_made, made(4 * n - 5))
                        act.activation(kT[:, s, 0:KEYS], KA[:, bass.ds(n * KEYS, KEYS)], ACT.Copy
                                       ).then_inc(k_kept, 1)
                    else:
                        act.wait_ge(k_made, made(n))
                        act.activation(kT[:, s, 0:KEYS], pKV[:, 0:KEYS], ACT.Identity, bias=cols[:, 0:1]
                                       ).then_inc(k_kept, 1)

                def values(n, s):
                    act.wait_ge(v_made, made(n))
                    if not isinstance(n, int) or n >= 2:
                        act.wait_ge(o_made, made(n - 2))
                    act.activation(v[:, s].rearrange("p c d -> p (c d)"), pKV[0:CH, 0:3 * D], ACT.Copy
                                   ).then_inc(v_kept, 1)

                def exponentials(n, s, j):
                    act.wait_ge(m_made, made(4 * n + j))
                    if j == 0 and (not isinstance(n, int) or n >= 2):
                        act.wait_ge(turned[1], made(2 * n - 3))
                        act.wait_ge(rs_made, made(n - 2))
                    act.activation(prob[:, s, j, 0:KEYS], pS[j][:, 0:KEYS], ACT.Exp, bias=nmx[:, s, j:j + 1],
                                   accum_out=sums[:, s, j:j + 1]).then_inc(p_made, 1)

                def keep_turned(n, s, j):
                    act.wait_ge(turned[1], made(2 * n + j // 2))
                    act.activation(probT[:, s, j, :], pT[1][0:CH, 0:3 * P], ACT.Copy).then_inc(kept[1], 1)

                def output(n, s):
                    act.wait_ge(on_made, made(n))
                    out = QT[:, bass.ds(n * S, S)]
                    if KA is None:
                        act.activation(out, on[:, s, :], ACT.Identity, bias=cols[:, 1:2]).then_inc(done, 1)
                    else:
                        act.activation(out, on[:, s, :], ACT.Copy).then_inc(done, 1)

                for n in range(2):
                    keys(n, n)
                    values(n, n)
                for j in range(4):
                    exponentials(0, 0, j)

                def slot(n, s):
                    for j in range(4):
                        if j % 2:
                            keep_turned(n, s, j)
                        if inside(n, 1):
                            exponentials(n + 1, 1 - s, j)
                        if j == 0 and inside(n, 2):
                            keys(n + 2, s)
                        if j == 1 and inside(n, -1):
                            output(n - 1, 1 - s)
                    if inside(n, 2):
                        values(n + 2, s)

                slots(act, slot)
                output(B - 1, 1)

            @block.vector
            def _(dve):
                dve.wait_ge(loaded, 16 * len(loads))
                dve.wait_ge(st.opened, 1)
                if masked:
                    dve.tensor_copy(mask[:, :], mask_i[:, :]).then_inc(mask_made, 1)
                    dve.wait_ge(mask_made, 1)
                    dve.tensor_scalar(mask[:, :], mask[:, :], 0.0, -BIG, ALU.is_equal, ALU.mult
                                      ).then_inc(mask_made, 1)
                    dve.wait_ge(mask_made, 2)
                    dve.tensor_copy(ident_b[:, :], env.ident[:, :])
                    dve.tensor_copy(mask_b[:, :], mask[:, :]).then_inc(mask_made, 1)

                def maxima(n, s, j):
                    dve.wait_ge(s_made, made(4 * n + j))
                    sc = pS[j][:, 0:KEYS]
                    dve.tensor_reduce(nmx[:, s, j:j + 1], sc, AX.X, ALU.max, negate=True).then_inc(m_made, 1)

                def keep_turned(n, s, j):
                    dve.wait_ge(turned[0], made(2 * n + j // 2))
                    dve.tensor_copy(probT[:, s, j, :], pT[0][0:CH, 0:3 * P]).then_inc(kept[0], 1)

                def factors(n, s):
                    dve.wait_ge(p_made, made(4 * n + 3))
                    dve.reciprocal(rs[:, s, :], sums[:, s, :]).then_inc(rs_made, 1)
                    dve.wait_ge(rs_made, made(n))
                    dve.tensor_tensor(rm[:, s], bc(rs[:, s, :], 2, 4), bc(m4q[:, :], 1, 4), ALU.mult
                                      ).then_inc(rm_made, 1)
                    dve.wait_ge(rm_made, made(n))
                    dve.tensor_copy(rx[:, s, :].rearrange("p (g d) -> p g d", d=HD),
                                    bc(rm[:, s].rearrange("p j h -> p (j h)"), 2, HD)).then_inc(rx_made, 1)

                def own_head(n, s):
                    dve.wait_ge(o_made, made(n))
                    dve.tensor_tensor(own[:, :, :], O.rearrange("p (h q) -> p h q", q=S), bc(env.m4[:, :], 2, S),
                                      ALU.mult).then_inc(own_made, 1)
                    dve.wait_ge(own_made, made(n))
                    dve.tensor_reduce(ou[:, :], own[:, :, :].rearrange("p h q -> p q h"), AX.X, ALU.add
                                      ).then_inc(ou_made, 1)

                def outputs(n, s):
                    dve.wait_ge(ou_made, made(n))
                    dve.wait_ge(r_made, made(n))
                    if not isinstance(n, int) or n >= 2:
                        dve.wait_ge(done, made(n - 2))
                    dve.tensor_tensor(on[:, s, :], R, ou[:, :], ALU.mult).then_inc(on_made, 1)

                for j in range(4):
                    maxima(0, 0, j)

                def slot(n, s):
                    for j in range(4):
                        if j % 2 == 0:
                            keep_turned(n, s, j)
                        if inside(n, 1):
                            maxima(n + 1, 1 - s, j)
                        if j == 0 and inside(n, -1):
                            own_head(n - 1, 1 - s)
                        if j == 1 and inside(n, -1):
                            outputs(n - 1, 1 - s)
                    factors(n, s)

                slots(dve, slot)
                own_head(B - 1, 1)
                outputs(B - 1, 1)


def project_out(nc, env, title, w_d, b_d, src, res):
    with stage(nc, title) as st:
        w, b = st.sb("w", [P, D]), st.sb("b", [1, D])
        stg = st.sb("stg", [P, 2, 512])
        py = [st.ps(f"py{s}", [P, 512]) for s in range(2)]
        loaded = st.sem("loaded")
        staged, y_made, added = st.pair("staged"), st.pair("y_made"), st.pair("added")
        with nc.Block() as block:
            @block.gpsimd
            def _(pool):
                st.open(pool)

            @block.sync
            def _(sp):
                sp.dma_start(w[:, :], w_d).then_inc(loaded, 16)
                sp.dma_start(b[:, :], b_d).then_inc(loaded, 16)

            @block.scalar
            def _(act):
                with act.Fori(0, GROUPS // 2) as i:
                    for s in range(2):
                        act.wait_ge(y_made[s], before(i))
                        act.activation(stg[:, s, :], src[:, bass.ds((2 * i + s) * 512, 512)], ACT.Copy
                                       ).then_inc(staged[s], 1)

            @block.tensor
            def _(pe):
                pe.wait_ge(loaded, 32)
                with pe.Fori(0, GROUPS // 2) as i:
                    for s in range(2):
                        pe.wait_ge(staged[s], made(i))
                        pe.wait_ge(added[s], before(i))
                        for t in range(TG):
                            o = py[s][:, t * D:(t + 1) * D]
                            pe.matmul(o, stg[:, s, t * P:(t + 1) * P], w[:, :], start=True, stop=False)
                            last = pe.matmul(o, env.ones[0:1, 0:P], b[:, :], start=False, stop=True)
                        last.then_inc(y_made[s], 1)

            @block.vector
            def _(dve):
                with dve.Fori(0, GROUPS // 2) as i:
                    for s in range(2):
                        dve.wait_ge(y_made[s], made(i))
                        x = res[:, bass.ds((2 * i + s) * TG, TG), :]
                        dve.tensor_tensor(x, x, py[s][:, :].rearrange("p (t d) -> p t d", d=D), ALU.add
                                          ).then_inc(added[s], 1)


def l1_xattn(nc, env, a):
    normalise(nc, env, "l1x_ln", env.X, dst_t=env.XNT)
    head_projection(nc, env, "l1x_q", "ln", a.L1_xattn_Wq, env.XNT, env.XNT, GROUPS, 512,
                    bias_d=a.L1_xattn_ln_b, gain_d=a.L1_xattn_ln_g)
    with stage(nc, "l1x") as st:
        KA = st.sb("KA", [P, B * KEYS])
        head_projection(nc, env, "l1x_k", "ln", a.L1_xattn_Wk, a.ctx_t, KA, B, KEYS, ctx=True,
                        bias_d=a.L1_xattn_ln_b, gain_d=a.L1_xattn_ln_g)
        w = Names(wv=a.L1_xattn_Wv)
        cross_attention(nc, env, "l1x_att", w, env.XNT, KA=KA)
    project_out(nc, env, "l1x_out", a.L1_xattn_Wp, a.L1_xattn_bp, env.XNT, env.X)


def l2_xattn(nc, env, a):
    normalise(nc, env, "l2x_ln", env.X, dst_t=env.XNT)
    plain_projection(nc, env, "l2x_q", a.L2_xattn_Wq, env.XNT, env.XNT, bias_d=a.L2_xattn_bq, scale=HD ** -0.5)
    w = Names(wk=a.L2_xattn_Wk, bk=a.L2_xattn_bk, wv=a.L2_xattn_Wv, bv=a.L2_xattn_bv, mask=a.mask_if)
    cross_attention(nc, env, "l2x_att", w, env.XNT, masked=True)
    project_out(nc, env, "l2x_out", a.L2_xattn_Wo, a.L2_xattn_bo, env.XNT, env.X)


def l3_attn(nc, env, a):
    normalise(nc, env, "l3a_ln", env.X, dst_t=env.XNT)
    with stage(nc, "l3a") as st:
        QA, KA = st.sb("QA", [P, T]), st.sb("KA", [P, T])
        head_projection(nc, env, "l3a_q", "l2", a.L3_attn_wq, env.XNT, QA, GROUPS, 512, bias_d=a.L3_attn_bq,
                        logit_d=a.L3_attn_logit)
        head_projection(nc, env, "l3a_k", "l2", a.L3_attn_wk, env.XNT, KA, GROUPS, 512, bias_d=a.L3_attn_bk)
        w = Names(wv=a.L3_attn_wv, wo=a.L3_attn_out_w, bv=a.L3_attn_bv, bo=a.L3_attn_out_b,
                            hs=a.L3_attn_head)
        cosine_attention(nc, env, "l3a_att", w, QA, KA)
    add_transposed(nc, env, "l3a_add", env.XNT, env.X)


def multi_query_attention(nc, env, title, w, Y):
    NC, DH, units = 4, 64, TILES
    with stage(nc, title) as st:
        wq, wk, wv, wo = (st.sb(n, [P, k]) for n, k in (("wq", 512), ("wk", D), ("wv", 2 * DH), ("wo", 512)))
        half, parity = st.sb("half", [P, 2]), st.sb("parity", [P, 2])
        xs = st.sb("xs", [P, 2, BT, 2, S])
        qT = st.sb("qT", [P, 2, BT, NC, S])
        kb = st.sb("kb", [P, 2, BT, 2, S])
        v = st.sb("v", [P, 2, 2, 2, DH])
        prob, probT = st.sb("prob", [P, 2, BT * 2, S]), st.sb("probT", [P, 2, 2, P])
        mx, sums, rs = (st.sb(n, [P, 2, BT * 2]) for n in ("mx", "sums", "rs"))
        oT = st.sb("oT", [P, 2, NC, BT, S])
        pQ, pK, pT, pX = (st.ps(n, [P, 512]) for n in ("pQ", "pK", "pT", "pX"))
        pO = [st.ps(f"pO{r}", [P, 512]) for r in range(2)]
        pS = [st.ps(f"pS{s}", [P, 512]) for s in range(2)]
        loads = [(wq[:, :], w.wq), (wk[:, :], w.wk), (wv[:, 0:DH], w.wv), (wv[:, DH:2 * DH], w.wv), (wo[:, :], w.wo),
                 (half[:, :], env.a.c_half), (parity[:, :], env.a.c_parity)]
        loaded = st.sem("loaded")
        (xs_ready, qkv_made, q_kept, kv_kept, s_made, m_made, shifted, p_made, sums_made, rs_made, p_scaled, t_made,
         t_kept, o_made, o_kept, out_made, finished) = (st.loop_sem(n) for n in (
             "xs_ready", "qkv_made", "q_kept", "kv_kept", "s_made", "m_made", "shifted", "p_made", "sums_made",
             "rs_made", "p_scaled", "t_made", "t_kept", "o_made", "o_kept", "out_made", "finished"))

        def inside(n):
            return not isinstance(n, int) or 0 <= n < units

        def after_both(eng, sem, n):
            if not isinstance(n, int) or n >= 0:
                eng.wait_ge(sem, 2 * n + 3)

        with nc.Block() as block:
            @block.gpsimd
            def _(pool):
                st.open(pool)

            @block.sync
            def _(sp):
                for d, s_ in loads:
                    sp.dma_start(d, s_).then_inc(loaded, 16)

            @block.tensor
            def _(pe):
                pe.wait_ge(loaded, 16 * len(loads))
                pe.wait_ge(st.opened, 1)

                def project(n, s):
                    after(pe, q_kept, n - 1)
                    after(pe, kv_kept, n - 1)
                    x = env.XNT[:, bass.ds(n * P, P)]
                    for c in range(NC):
                        pe.matmul(pQ[:, c * P:(c + 1) * P], wq[:, c * P:(c + 1) * P], x)
                    pe.matmul(pK[:, 0:P], wk[:, :], x)
                    pe.wait_ge(xs_ready, made(n))
                    for u in range(2):
                        last = pe.matmul(pK[:, (u + 1) * P:(u + 2) * P],
                                         xs[:, s, 2 * u:2 * u + 2].rearrange("p b r k -> p (b r k)"), wv[:, :])
                    last.then_inc(qkv_made, 1)

                def scores(n, s):
                    pe.wait_ge(q_kept, made(n))
                    pe.wait_ge(kv_kept, made(n))
                    after(pe, shifted, n - 2)
                    for b in range(BT):
                        last = pe.matmul(pS[s][:, b * 2 * S:(b + 1) * 2 * S], qT[:, s, b].rearrange("p c q -> p (c q)"),
                                         kb[:, s, b].rearrange("p r k -> p (r k)"))
                    last.then_inc(s_made, 1)

                def turn(n, s):
                    pe.wait_ge(p_scaled, made(n))
                    after(pe, t_kept, n - 1)
                    for u in range(2):
                        last = pe.transpose(pT[:, u * P:(u + 1) * P],
                                            prob[:, s, 4 * u:4 * u + 4, :].rearrange("p g k -> p (g k)"),
                                            env.ident[:, :])
                    last.then_inc(t_made, 1)

                def attend(n, s):
                    pe.wait_ge(t_kept, made(n))
                    pe.wait_ge(kv_kept, made(n))
                    after_both(pe, o_kept, n - 1)
                    for b in range(BT):
                        r = slice(DH * (b % 2), DH * (b % 2) + DH)
                        last = pe.matmul(pO[b % 2][:, b // 2 * P:(b // 2 + 1) * P], v[r, s, b // 2].rearrange("p r d -> p (r d)"),
                                         probT[r, s, b // 2, :])
                        if b >= 2:
                            last.then_inc(o_made, 1)

                def output(n, s):
                    after_both(pe, o_kept, n)
                    after(pe, finished, n - 1)
                    for c in range(NC):
                        last = pe.matmul(pX[:, 0:D], oT[:, s, c].rearrange("p b q -> p (b q)"),
                                         wo[:, c * D:(c + 1) * D], start=c == 0, stop=c == NC - 1)
                    last.then_inc(out_made, 1)

                def slot(n, s):
                    if inside(n + 1):
                        scores(n + 1, 1 - s)
                    if inside(n):
                        turn(n, s)
                    if inside(n + 2):
                        project(n + 2, s)
                    if inside(n):
                        attend(n, s)
                    if inside(n - 1):
                        output(n - 1, 1 - s)

                run_slots(pe, slot, units)

            @block.scalar
            def _(act):
                act.wait_ge(st.opened, 1)

                def tokens(n, s):
                    after(act, qkv_made, n - 2)
                    x = env.XNT[:, bass.ds(n * P, P)].rearrange("p (b t) -> p b t", t=S)
                    act.activation(xs[:, s], bc(x, 2, 2), ACT.Copy).then_inc(xs_ready, 1)

                def queries(n, s):
                    act.wait_ge(qkv_made, made(n))
                    after(act, s_made, n - 2)
                    act.activation(qT[:, s], pQ[:, :].rearrange("p (c b q) -> p b c q", b=BT, q=S), ACT.Copy,
                                   scale=DH ** -0.5).then_inc(q_kept, 1)

                def keep_turned(n, s):
                    act.wait_ge(t_made, made(n))
                    after_both(act, o_made, n - 2)
                    act.activation(probT[:, s].rearrange("p u q -> p (u q)"), pT[:, 0:2 * P], ACT.Copy
                                   ).then_inc(t_kept, 1)

                def exponentials(n, s):
                    act.wait_ge(shifted, made(n))
                    act.activation(prob[:, s], prob[:, s], ACT.Exp).then_inc(p_made, 1)

                def keep_output(n, s):
                    after_both(act, o_made, n)
                    after(act, out_made, n - 2)
                    for r in range(2):
                        act.activation(oT[:, s, :, r::2, :],
                                       pO[r][:, 0:2 * P].rearrange("p (u c q) -> p c u q", c=NC, q=S), ACT.Copy
                                       ).then_inc(o_kept, 1)

                def slot(n, s):
                    if inside(n + 2):
                        tokens(n + 2, s)
                    if inside(n - 1):
                        keep_output(n - 1, 1 - s)
                    if inside(n):
                        keep_turned(n, s)
                    if inside(n + 1):
                        exponentials(n + 1, 1 - s)
                    if inside(n + 2):
                        queries(n + 2, s)

                run_slots(act, slot, units)

            @block.vector
            def _(dve):
                dve.wait_ge(loaded, 16 * len(loads))
                dve.wait_ge(st.opened, 1)

                def keys_values(n, s):
                    dve.wait_ge(qkv_made, made(n))
                    after(dve, s_made, n - 2)
                    dve.tensor_tensor(kb[:, s], bc(pK[:, 0:P].rearrange("p (b k) -> p b k", k=S), 2, 2),
                                      bc(bc(half[:, :], 1, BT), 3, S), ALU.mult)
                    after_both(dve, o_made, n - 2)
                    dve.tensor_tensor(v[:, s], pK[:, P:3 * P].rearrange("p (u r d) -> p u r d", r=2, d=DH),
                                      bc(bc(parity[:, :], 1, 2), 3, DH), ALU.mult).then_inc(kv_kept, 1)

                def scores(n, s):
                    dve.wait_ge(s_made, made(n))
                    sc = pS[s][:, 0:BT * 2 * S].rearrange("p (g k) -> p g k", k=S)
                    dve.tensor_reduce(mx[:, s, :], sc, AX.X, ALU.max).then_inc(m_made, 1)
                    dve.wait_ge(m_made, made(n))
                    after(dve, t_made, n - 2)
                    dve.tensor_tensor(prob[:, s], sc, bc(mx[:, s, :], 2, S), ALU.subtract).then_inc(shifted, 1)

                def scale(n, s):
                    dve.wait_ge(p_made, made(n))
                    dve.tensor_reduce(sums[:, s, :], prob[:, s], AX.X, ALU.add).then_inc(sums_made, 1)
                    dve.wait_ge(sums_made, made(n))
                    dve.reciprocal(rs[:, s, :], sums[:, s, :]).then_inc(rs_made, 1)
                    dve.wait_ge(rs_made, made(n))
                    dve.tensor_tensor(prob[:, s], prob[:, s], bc(rs[:, s, :], 2, S), ALU.mult).then_inc(p_scaled, 1)

                def finish(n):
                    dve.wait_ge(out_made, made(n))
                    dve.tensor_copy(Y[:, n, :], pX[:, 0:D]).then_inc(finished, 1)

                def slot(n, s):
                    if inside(n + 1):
                        scores(n + 1, 1 - s)
                    if inside(n - 2):
                        finish(n - 2)
                    if inside(n + 2):
                        keys_values(n + 2, s)
                    if inside(n + 1):
                        scale(n + 1, 1 - s)

                run_slots(dve, slot, units)


def l0_attn(nc, env, a):
    with stage(nc, "l0a") as st:
        Y, YN = st.sb("Y", [P, TILES, D]), st.sb("YN", [P, TILES, D])
        ln = st.sb("ln", [P, 2])
        gain, shift = st.sb("gain", [P, D]), st.sb("shift", [P, D])
        landed, step = st.sem("landed"), st.sem("step")
        with nc.Block() as block:
            @block.sync
            def _(sp):
                sp.dma_start(ln[:, :], a.L0_attn_ln).then_inc(landed, 16)
                sp.dma_start(gain[:, :], a.L0_attn_out_norm_w.to_broadcast([P, D])).then_inc(landed, 16)
                sp.dma_start(shift[:, :], a.L0_attn_out_norm_b.to_broadcast([P, D])).then_inc(landed, 16)
                sp.wait_ge(landed, 48)
        normalise(nc, env, "l0a_ln0", env.X, dst=YN)
        normalise(nc, env, "l0a_ln1", YN, dst_t=env.XNT, gain=ln[:, 0:1], shift=ln[:, 1:2])
        w = Names(wq=a.L0_attn_Wq, wk=a.L0_attn_wk2, wv=a.L0_attn_wv, wo=a.L0_attn_Wo)
        multi_query_attention(nc, env, "l0a_att", w, Y)
        normalise(nc, env, "l0a_ln2", Y, dst=YN)
        with nc.Block() as block:
            @block.vector
            def _(dve):
                dve.tensor_tensor(YN[:, :, :], YN[:, :, :], bc(gain[:, :], 1, TILES), ALU.mult)
                dve.tensor_tensor(env.X[:, :, :], env.X[:, :, :], bc(shift[:, :], 1, TILES), ALU.add
                                  ).then_inc(step, 1)
                dve.wait_ge(step, 1)
                dve.tensor_tensor(env.X[:, :, :], env.X[:, :, :], YN[:, :, :], ALU.add)


def selective_scan(nc, env, title, a):
    NC, NS = 2, 16
    BG = 512 // S
    with stage(nc, title) as st:
        w_in = st.sb("w_in", [P, 4 * P])
        w_dt_raw, w_bc = st.sb("w_dt_raw", [P, NC, P]), st.sb("w_bc", [P, NC, 96])
        w_out = st.sb("w_out", [P, NC, D])
        conv_w, cols, A = st.sb("conv_w", [P, NC, 4]), st.sb("cols", [P, NC, 4]), st.sb("A", [P, NC, NS])
        sel_f, sel = st.sb("sel_f", [96, 2 * NS]), st.sb("sel", [96, 2 * NS, P], BF16)
        xi, acc, th, xc, sz = (st.sb(n, [P, NC, 512]) for n in ("xi", "acc", "th", "xc", "sz"))
        ab, lg, dl, dx = (st.sb(n, [P, NC, 512]) for n in ("ab", "lg", "dl", "dx"))
        r1, stk = st.sb("r1", [96, 512]), st.sb("stk", [96, 512], BF16)
        dA, dbu, hh, hc = (st.sb(n, [P, NC, 512]) for n in ("dA", "dbu", "hh", "hc"))
        pX = [st.ps(f"pX{c}", [P, 512]) for c in range(2)]
        pZ = [st.ps(f"pZ{c}", [P, 512]) for c in range(2)]
        bn = st.sb("bn", [P, 2, 512])
        pBn = [st.ps(f"pBn{c}", [P, 512]) for c in range(2)]
        pCn = [st.ps(f"pCn{c}", [P, 512]) for c in range(2)]
        loads = [(w_in[:, :], a.L2_attn_W_in), (w_dt_raw[:, :, :], a.L2_attn_wx0.rearrange("p (c m) -> p c m", c=NC)),
                 (w_bc[:, :, :], a.L2_attn_wbc.rearrange("p (c m) -> p c m", c=NC)),
                 (w_out[:, :, :], a.L2_attn_W_out.rearrange("p (c m) -> p c m", c=NC)),
                 (conv_w[:, :, :], a.L2_attn_conv_w.rearrange("p (c m) -> p c m", c=NC)),
                 (cols[:, :, :], a.L2_attn_cols.rearrange("p (c m) -> p c m", c=NC)),
                 (A[:, :, :], a.L2_attn_A_log.rearrange("p (c m) -> p c m", c=NC)),
                 (sel_f[:, 0:2 * NS], env.a.c_pick)]
        loaded, prep = st.sem("loaded"), st.sem("prep")
        xz_made, xi_kept, z_act, conv, xc_act, xc_made, sz_made, db_made, dl_abs, dl_log, dl_made, split, stk_made = (
            st.loop_sem(n) for n in ("xz_made", "xi_kept", "z_act", "conv", "xc_act", "xc_made", "sz_made",
                                     "db_made", "dl_abs", "dl_log", "dl_made", "split", "stk_made"))
        b_made, da_made, dbu_made, h_made, hc_made, y_added, y_step, y_ready, out_made, added = (
            st.loop_sem(n) for n in ("b_made", "da_made", "dbu_made", "h_made", "hc_made", "y_added",
                                     "y_step", "y_ready", "out_made", "added"))
        xc_act2, sz_half, dstep, b_kept, c_made = (st.loop_sem(n) for n in ("xc_act2", "sz_half", "dstep", "b_kept",
                                                                       "c_made"))
        CB, WDT, BDT, DP = range(4)
        by_batch = lambda ap: ap.rearrange("p (b t) -> p b t", t=S)
        with nc.Block() as block:
            @block.gpsimd
            def _(pool):
                st.open(pool)
                with pool.Fori(0, GROUPS) as g:
                    pool.wait_ge(dl_made, made(g))
                    for n in range(NS):
                        pool.wait_ge(b_kept, made(g * NS + n))
                        for c in range(NC):
                            pool.wait_ge(h_made, before(g * NS * NC + max(n * NC + c - 1, 0)))
                            pool.tensor_tensor(dbu[:, c, :], dx[:, c, :], bn[:, n % 2, :], ALU.mult
                                               ).then_inc(dbu_made, 1)

            @block.sync
            def _(sp):
                for d, s_ in loads:
                    sp.dma_start(d, s_).then_inc(loaded, 16)

            @block.tensor
            def _(pe):
                pe.wait_ge(st.opened, 1)
                pe.wait_ge(loaded, 16 * len(loads))
                pe.wait_ge(prep, 3)
                with pe.Fori(0, GROUPS) as g:
                    pe.wait_ge(added, before(g))
                    x = env.XNT[:, bass.ds(g * 512, 512)]
                    for c in range(NC):
                        pe.matmul(pX[c][:, :], w_in[:, c * P:(c + 1) * P], x)
                        last = pe.matmul(pZ[c][:, :], w_in[:, (2 + c) * P:(3 + c) * P], x)
                    last.then_inc(xz_made, 1)
                    pe.wait_ge(xc_made, made(2 * g + 1))
                    for c in range(NC):
                        pe.matmul(pX[0][:, :], w_dt_raw[:, c, :], xc[:, c, :], start=c == 0, stop=c == 1)
                    for c in range(NC):
                        last = pe.matmul(pX[1][0:96, :], w_bc[:, c, :], xc[:, c, :], start=c == 0, stop=c == 1)
                    last.then_inc(db_made, 1)
                    pe.wait_ge(stk_made, made(g))
                    pe.wait_ge(sz_made, made(2 * g + 1))
                    for n in range(-2, NS):
                        if n + 2 < NS:
                            pe.wait_ge(b_kept, before(g * NS + max(n + 1, 0)))
                            pe.matmul(pBn[n % 2][:, :], sel[:, n + 2, :], stk[:, :]).then_inc(b_made, 1)
                        if 0 <= n + 1 < NS:
                            pe.wait_ge(hc_made, before(g * NS * NC + max(n, 0) * NC))
                            pe.matmul(pCn[(n + 1) % 2][:, :], sel[:, NS + n + 1, :], stk[:, :]).then_inc(c_made, 1)
                        for c in range(NC if n >= 0 else 0):
                            pe.wait_ge(hc_made, made(g * NS * NC + n * NC + c))
                            last = pe.matmul(pZ[c][:, :], env.ident[:, :], hc[:, c, :], start=n == 0,
                                             stop=n == NS - 1).then_inc(y_added, 1)
                    pe.wait_ge(y_ready, made(g))
                    for t in range(TG):
                        for c in range(NC):
                            last = pe.matmul(pX[0][:, t * D:(t + 1) * D], dx[:, c, t * P:(t + 1) * P],
                                             w_out[:, c, :], start=c == 0, stop=c == 1)
                    last.then_inc(out_made, 1)

            @block.scalar
            def _(act):
                act.wait_ge(st.opened, 1)
                act.wait_ge(loaded, 16 * len(loads))
                act.activation(A[:, :, :], A[:, :, :], ACT.Exp).then_inc(prep, 1)
                act.wait_ge(prep, 3)
                with act.Fori(0, GROUPS) as g:
                    act.wait_ge(xz_made, made(g))
                    for c in range(NC):
                        act.activation(xi[:, c, :], pX[c][:, :], ACT.Copy).then_inc(xi_kept, 1)
                    for c in range(NC):
                        act.activation(sz[:, c, :], pZ[c][:, :], ACT.Tanh, scale=0.5).then_inc(z_act, 1)
                    for c in range(NC):
                        act.wait_ge(conv, 5 * (2 * g + c) + 6)
                        act.activation(th[:, c, :], acc[:, c, :], ACT.Tanh, scale=0.5).then_inc(xc_act, 1)
                    act.wait_ge(db_made, made(g))
                    for c in range(NC):
                        act.activation(ab[:, c, :], pX[0][:, :], ACT.Abs, scale=cols[:, c, WDT:WDT + 1],
                                       bias=cols[:, c, BDT:BDT + 1]).then_inc(dl_abs, 1)
                        act.wait_ge(dl_abs, 4 * g + 2 * c + 2)
                        act.activation(ab[:, c, :], ab[:, c, :], ACT.Exp, scale=-1.0).then_inc(dl_abs, 1)
                    act.wait_ge(dl_abs, 4 * g + 5)
                    for c in range(NC):
                        act.activation(lg[:, c, :], ab[:, c, :], ACT.Ln, bias=env.ones[:, 0:1]).then_inc(dl_log, 1)
                    act.wait_ge(dl_made, made(g))
                    for n in range(NS):
                        act.wait_ge(b_made, made(g * NS + n))
                        act.wait_ge(dbu_made, before(g * NS * NC + max(n - 1, 0) * NC))
                        act.activation(bn[:, n % 2, :], pBn[n % 2][:, :], ACT.Copy).then_inc(b_kept, 1)
                        for c in range(NC):
                            k = n * NC + c
                            act.wait_ge(h_made, before(g * NS * NC + max(k - 1, 0)))
                            act.activation(dA[:, c, :], dl[:, c, :], ACT.Exp, scale=A[:, c, n:n + 1]
                                           ).then_inc(da_made, 1)

            @block.vector
            def _(dve):
                dve.wait_ge(st.opened, 1)
                dve.wait_ge(loaded, 16 * len(loads))
                dve.tensor_copy(sel[:, :, :], bc(sel_f[:, 0:2 * NS], 2, P)).then_inc(prep, 1)
                dve.wait_ge(prep, 2)
                dve.tensor_scalar(A[:, :, :], A[:, :, :], -1.0, None, ALU.mult).then_inc(prep, 1)
                with dve.Fori(0, GROUPS) as g:
                    for c in range(NC):
                        dve.wait_ge(xi_kept, made(2 * g + c))
                        dve.tensor_scalar(acc[:, c, :], xi[:, c, :], conv_w[:, c, 3:4], cols[:, c, CB:CB + 1],
                                          ALU.mult, ALU.add).then_inc(conv, 1)
                        for s in range(1, 4):
                            dve.wait_ge(conv, 5 * (2 * g + c) + 1 + s)
                            dve.scalar_tensor_tensor(
                                out=by_batch(acc[:, c, :])[:, :, s:S], in0=by_batch(xi[:, c, :])[:, :, 0:S - s],
                                scalar=conv_w[:, c, 3 - s:4 - s], in1=by_batch(acc[:, c, :])[:, :, s:S],
                                op0=ALU.mult, op1=ALU.add).then_inc(conv, 1)
                        dve.wait_ge(conv, 5 * (2 * g + c) + 5)
                        dve.sem_inc(conv, 1)
                    for c in range(NC):
                        dve.wait_ge(xc_act, made(2 * g + c))
                        dve.tensor_scalar(th[:, c, :], th[:, c, :], 0.5, 0.5, ALU.mult, ALU.add).then_inc(xc_act2, 1)
                        dve.wait_ge(xc_act2, made(2 * g + c))
                        dve.tensor_tensor(xc[:, c, :], acc[:, c, :], th[:, c, :], ALU.mult).then_inc(xc_made, 1)
                    for c in range(NC):
                        dve.wait_ge(z_act, made(2 * g + 1))
                        dve.tensor_scalar(sz[:, c, :], sz[:, c, :], 0.5, 0.5, ALU.mult, ALU.add).then_inc(sz_half, 1)
                        dve.wait_ge(sz_half, made(2 * g + c))
                        dve.tensor_tensor(sz[:, c, :], pZ[c][:, :], sz[:, c, :], ALU.mult).then_inc(sz_made, 1)
                    dve.wait_ge(db_made, made(g))
                    src = pX[1]
                    for r, parts in ((0, 1), (32, 2), (64, 3)):
                        rows = slice(r, r + 32)
                        dve.tensor_copy(stk[rows, :], src[rows, :]).then_inc(split, 1)
                        base = 9 * g + {0: 0, 32: 1, 64: 4}[r]
                        for q in range(1, parts):
                            dve.wait_ge(split, base + 2 * (q - 1) + 2)
                            if q == 1:
                                dve.tensor_tensor(r1[rows, :], src[rows, :], stk[rows, :], ALU.subtract
                                                  ).then_inc(split, 1)
                            else:
                                dve.tensor_tensor(r1[rows, :], r1[rows, :], stk[rows, :], ALU.subtract
                                                  ).then_inc(split, 1)
                            dve.wait_ge(split, base + 2 * (q - 1) + 3)
                            dve.tensor_copy(stk[rows, :], r1[rows, :]).then_inc(split, 1)
                    dve.wait_ge(split, 9 * g + 10)
                    dve.sem_inc(stk_made, 1)
                    dve.wait_ge(dl_log, made(2 * g + 1))
                    for c in range(NC):
                        dve.tensor_scalar(dl[:, c, :], pX[0][:, :], cols[:, c, WDT:WDT + 1], cols[:, c, BDT:BDT + 1],
                                          ALU.mult, ALU.add).then_inc(dstep, 1)
                    for c in range(NC):
                        dve.wait_ge(dstep, 8 * g + c + 2)
                        dve.tensor_scalar(dl[:, c, :], dl[:, c, :], 0.0, None, ALU.max).then_inc(dstep, 1)
                    for c in range(NC):
                        dve.wait_ge(dstep, 8 * g + c + 4)
                        dve.tensor_tensor(dl[:, c, :], dl[:, c, :], lg[:, c, :], ALU.add).then_inc(dstep, 1)
                    for c in range(NC):
                        dve.wait_ge(dstep, 8 * g + c + 6)
                        dve.tensor_tensor(dx[:, c, :], dl[:, c, :], xc[:, c, :], ALU.mult).then_inc(dstep, 1)
                    dve.wait_ge(dstep, 8 * g + 9)
                    dve.memset(dl[:, :, :].rearrange("p c (b t) -> p (c b) t", t=S)[:, :, 0:1], BIG
                               ).then_inc(dl_made, 1)
                    for n in range(NS):
                        for c in range(NC):
                            k = g * NS * NC + n * NC + c
                            dve.wait_ge(hc_made, before(g * NS * NC + max(n * NC + c - 1, 0)))
                            dve.wait_ge(dbu_made, made(k))
                            dve.wait_ge(da_made, made(k))
                            dve.tensor_tensor_scan(hh[:, c, :], dA[:, c, :], dbu[:, c, :], 0.0, ALU.mult, ALU.add
                                                   ).then_inc(h_made, 1)
                        for c in range(NC):
                            k = g * NS * NC + n * NC + c
                            dve.wait_ge(h_made, made(k))
                            dve.wait_ge(c_made, made(g * NS + n))
                            dve.wait_ge(y_added, before(g * NS * NC + max(n * NC + c - 1, 0)))
                            dve.tensor_tensor(hc[:, c, :], hh[:, c, :], pCn[n % 2][:, :], ALU.mult
                                              ).then_inc(hc_made, 1)
                    for c in range(NC):
                        dve.wait_ge(y_added, made((g + 1) * NS * NC - 2 + c))
                        dve.scalar_tensor_tensor(out=xc[:, c, :], in0=xc[:, c, :], scalar=cols[:, c, DP:DP + 1],
                                                 in1=pZ[c][:, :], op0=ALU.mult, op1=ALU.add).then_inc(y_step, 1)
                    for c in range(NC):
                        dve.wait_ge(y_step, made(2 * g + c))
                        last = dve.tensor_tensor(dx[:, c, :], xc[:, c, :], sz[:, c, :], ALU.mult)
                    last.then_inc(y_ready, 1)
                    dve.wait_ge(out_made, made(g))
                    x = env.X[:, bass.ds(g * TG, TG), :]
                    dve.tensor_tensor(x, x, pX[0][:, :].rearrange("p (t d) -> p t d", d=D), ALU.add
                                      ).then_inc(added, 1)


def l2_attn(nc, env, a):
    normalise(nc, env, "l2a_ln", env.X, dst_t=env.XNT)
    selective_scan(nc, env, "l2a", a)


def two_way_cross(nc, env, title, a, QC, QP, KC):
    SUB = 2 * S
    SC = D ** -0.5
    with stage(nc, title) as st:
        wqs, wvs, wvc, wg = st.sb("wqs", [P, D]), st.sb("wvs", [P, D]), st.sb("wvc", [P, D]), st.sb("wg", [P, 2 * D])
        cols = st.sb("cols", [P, 5])
        interp, m4q, m2 = st.sb("interp", [P, S]), st.sb("m4q", [P, 4]), st.sb("m2", [P, 2, 4])
        xs, qc, qp, kc = (st.sb(n, [P, 2, P]) for n in ("xs", "qc", "qp", "kc"))
        ctx = st.sb("ctx", [P, 2, BT, KEYS])
        ctn = st.sb("ctn", [CH, 2, BT, 3, D])
        sub = st.sb("sub", [P, 2, BT * SUB])
        qs = st.sb("qs", [P, 2, BT * SUB])
        v = st.sb("v", [P, 2, D])
        qbk = st.sb("qbk", [P, 2, 1])
        p1 = st.sb("p1", [P, 2, KPAD])
        p1T = st.sb("p1T", [CH, 2, 3, P])
        m1, n1, s1, r1 = (st.sb(n, [P, 2, 1]) for n in ("m1", "n1", "s1", "r1"))
        p2 = st.sb("p2", [P, 2, 2, S])
        mx2, nmx2, sm2, rs2 = (st.sb(n, [P, 2, 2]) for n in ("mx2", "nmx2", "sm2", "rs2"))
        rm2 = st.sb("rm2", [P, 2, 2, 4])
        p2m = st.sb("p2m", [P, 2, 2, 4, S])
        pib = st.sb("pib", [P, 2, 4, S])
        cn, cT, c2s, s2c, gt, o = (st.sb(n, [P, 2, P]) for n in ("cn", "cT", "c2s", "s2c", "gt", "o"))
        pA, pS, pS2, pT, pC, pX, pG = (st.ps(n, [P, 512]) for n in ("pA", "pS", "pS2", "pT", "pC", "pX", "pG"))
        BQS, BKS, BVS, BVC, BG_ = range(5)
        loads = [(wqs[:, :], a.L3_xattn_Wq_s), (wvs[:, :], a.L3_xattn_Wv_s), (wvc[:, :], a.L3_xattn_Wv_c),
                 (wg[:, :], a.L3_xattn_Wg), (cols[:, :], a.L3_xattn_cols), (interp[:, :], a.c_interp),
                 (m4q[:, :], a.c_m4q), (m2[:, :, :], a.c_pair.rearrange("p (a b) -> p a b", a=2))]
        loaded, prep = st.sem("loaded"), st.sem("prep")
        names = ("landed", "tokens", "proj", "q_kept", "kept", "s_made", "shifted", "m_made", "n_made", "p_made",
                 "s2_made", "m2_made", "n2_made", "p2_made", "turned", "t_kept", "c_made", "r_made", "c_kept",
                 "ct_made", "ct_kept", "c2s_made", "c2s_kept", "r2_made", "rm_made", "p2m_made", "pi_made", "pib_made",
                 "s2c_made", "s2c_kept", "g_made", "g_kept", "mix", "o_made", "finished")
        q = Names(**{n: st.pair(n) for n in names})
        with nc.Block() as block:
            @block.gpsimd
            def _(pool):
                st.open(pool)
                pool.memset(ctn[:, :, :, 2, :], 0.0)
                pool.memset(p1[:, :, KEYS:KPAD], 0.0).then_inc(prep, 1)

            @block.sync
            def _(sp):
                for d, s_ in loads:
                    sp.dma_start(d, s_).then_inc(loaded, 16)
                sp.wait_ge(prep, 1)
                with sp.Fori(0, TILES // 2) as i:
                    for s in range(2):
                        n = 2 * i + s
                        sp.wait_ge(q.c_made[s], before(i))
                        sp.dma_start(ctx[:, s].rearrange("p b k -> p (b k)"),
                                     a.ctx_t[:, bass.ds(n * BT * KEYS, BT * KEYS)]).then_inc(q.landed[s], 16)
                        sp.dma_start(sub[:, s, :], a.ctx_sub[:, bass.ds(n * BT * SUB, BT * SUB)]
                                     ).then_inc(q.landed[s], 16)
                        rows = a.ctx_n[bass.ds(n * BT, BT)]
                        for c, k in ((0, CH), (1, CH), (2, KEYS - 2 * CH)):
                            sp.dma_start(ctn[0:k, s, :, c, :],
                                         rows[:, c * CH:c * CH + k, :].rearrange("b k d -> k b d")
                                         ).then_inc(q.landed[s], 16)

            @block.scalar
            def _(act):
                act.wait_ge(loaded, 16 * len(loads))
                act.wait_ge(prep, 2)
                with act.Fori(0, TILES // 2) as i:
                    for s in range(2):
                        n = 2 * i + s
                        act.wait_ge(q.s2_made[s], before(i))
                        act.activation(xs[:, s, :], env.XNT[:, bass.ds(n * P, P)], ACT.Copy)
                        act.activation(qc[:, s, :], QC[:, bass.ds(n * P, P)], ACT.Copy)
                        act.activation(qp[:, s, :], QP[:, bass.ds(n * P, P)], ACT.Copy)
                        act.activation(kc[:, s, :], KC[:, bass.ds(n * P, P)], ACT.Copy).then_inc(q.tokens[s], 1)
                    for s in range(2):
                        act.wait_ge(q.proj[s], made(i))
                        act.activation(qs[:, s, :], pA[:, 0:BT * SUB], ACT.Identity, bias=cols[:, BQS:BQS + 1]
                                       ).then_inc(q.q_kept[s], 1)
                        act.wait_ge(q.finished[s], before(i))
                        act.activation(qbk[:, s, :], pA[:, 256:257], ACT.Copy, scale=SC)
                        act.activation(v[:, s, :], pA[:, 260:260 + D], ACT.Copy).then_inc(q.kept[s], 1)
                    for s in range(2):
                        act.wait_ge(q.n_made[s], made(i))
                        act.activation(p1[:, s, 0:KEYS], pS[:, 0:KEYS], ACT.Exp, bias=n1[:, s, :],
                                       accum_out=s1[:, s, :]).then_inc(q.p_made[s], 1)
                        act.wait_ge(q.n2_made[s], made(i))
                        for r in range(2):
                            last = act.activation(p2[:, s, r, :], pS2[:, r * S:(r + 1) * S], ACT.Exp, scale=SC,
                                                  bias=nmx2[:, s, r:r + 1], accum_out=sm2[:, s, r:r + 1])
                        last.then_inc(q.p2_made[s], 1)
                    for s in range(2):
                        act.wait_ge(q.turned[s], made(i))
                        act.activation(p1T[:, s].rearrange("p c q -> p (c q)"), pT[0:CH, 0:3 * P], ACT.Copy
                                       ).then_inc(q.t_kept[s], 1)
                    for s in range(2):
                        act.wait_ge(q.ct_made[s], made(i))
                        act.activation(cT[:, s, :], pC[:, P:2 * P], ACT.Copy).then_inc(q.ct_kept[s], 1)
                        act.wait_ge(q.c2s_made[s], made(i))
                        act.activation(c2s[:, s, :], pX[:, 0:P], ACT.Identity, bias=cols[:, BVS:BVS + 1]
                                       ).then_inc(q.c2s_kept[s], 1)
                        act.wait_ge(q.s2c_made[s], made(i))
                        act.activation(s2c[:, s, :], pX[:, P:2 * P], ACT.Identity, bias=cols[:, BVC:BVC + 1]
                                       ).then_inc(q.s2c_kept[s], 1)
                    for s in range(2):
                        act.wait_ge(q.g_made[s], made(i))
                        act.activation(gt[:, s, :], pG[:, 0:P], ACT.Tanh, scale=0.5, bias=cols[:, BG_:BG_ + 1]
                                       ).then_inc(q.g_kept[s], 1)

            @block.tensor
            def _(pe):
                pe.wait_ge(loaded, 16 * len(loads))
                with pe.Fori(0, TILES // 2) as i:
                    for s in range(2):
                        pe.wait_ge(q.tokens[s], made(i))
                        pe.wait_ge(q.landed[s], 80 * i + 81)
                        pe.wait_ge(*previous(q.kept, s, i))
                        pe.matmul(pA[:, 0:BT * SUB], wqs[:, :], sub[:, s, :])
                        pe.matmul(pA[:, 256:257], qc[:, s, :], cols[:, BKS:BKS + 1])
                        pe.matmul(pA[:, 260:260 + D], xs[:, s, :], wvc[:, :]).then_inc(q.proj[s], 1)
                    for s in range(2):
                        pe.wait_ge(*previous(q.p_made, s, i))
                        for b in range(BT):
                            last = pe.matmul(pS[b * S:(b + 1) * S, 0:KEYS], qp[:, s, b * S:(b + 1) * S],
                                             ctx[:, s, b, :])
                        last.then_inc(q.s_made[s], 1)
                        pe.wait_ge(q.q_kept[s], made(i))
                        pe.wait_ge(*previous(q.p2_made, s, i))
                        if not s:
                            pe.wait_ge(q.pib_made[1], before(i))
                        for b in range(BT):
                            h = (b % 2) * SUB
                            last = pe.matmul(pS2[h:h + SUB, (b // 2) * S:(b // 2 + 1) * S],
                                             qs[:, s, b * SUB:(b + 1) * SUB], kc[:, s, b * S:(b + 1) * S])
                        last.then_inc(q.s2_made[s], 1)
                    for s in range(2):
                        pe.wait_ge(q.p_made[s], made(i))
                        pe.wait_ge(*previous(q.t_kept, s, i))
                        for c in range(3):
                            last = pe.transpose(pT[0:CH, c * P:(c + 1) * P], p1[:, s, c * CH:(c + 1) * CH],
                                                env.ident[:, :])
                        last.then_inc(q.turned[s], 1)
                        pe.wait_ge(q.t_kept[s], made(i))
                        pe.wait_ge(*((q.c_kept[0], made(i)) if s else (q.ct_kept[1], before(i))))
                        for b in range(BT):
                            for c in range(3):
                                last = pe.matmul(pC[b * S:(b + 1) * S, 0:D], p1T[:, s, c, b * S:(b + 1) * S],
                                                 ctn[:, s, b, c, :], start=c == 0, stop=c == 2)
                        last.then_inc(q.c_made[s], 1)
                    for s in range(2):
                        pe.wait_ge(q.p2m_made[s], made(i))
                        pe.wait_ge(*((q.pib_made[0], made(i)) if s else (q.p2_made[1], made(i))))
                        for r in range(2):
                            last = pe.matmul(pS2[:, 64:64 + S], p2m[:, s, r].rearrange("p b k -> p (b k)"),
                                             interp[:, :], start=r == 0, stop=r == 1)
                        last.then_inc(q.pi_made[s], 1)
                    for s in range(2):
                        pe.wait_ge(q.c_kept[s], made(i))
                        pe.wait_ge(*((q.ct_kept[0], made(i)) if s else (q.c_kept[1], made(i))))
                        pe.transpose(pC[:, P:2 * P], cn[:, s, :], env.ident[:, :]).then_inc(q.ct_made[s], 1)
                        pe.wait_ge(q.ct_kept[s], made(i))
                        pe.wait_ge(*previous(q.s2c_kept, s, i))
                        pe.matmul(pX[:, 0:P], wvs[:, :], cT[:, s, :]).then_inc(q.c2s_made[s], 1)
                        pe.wait_ge(q.pib_made[s], made(i))
                        pe.wait_ge(q.kept[s], made(i))
                        pe.wait_ge(q.c2s_kept[s], made(i))
                        pe.matmul(pX[:, P:2 * P], v[:, s, :], pib[:, s].rearrange("p b k -> p (b k)")
                                  ).then_inc(q.s2c_made[s], 1)
                    for s in range(2):
                        pe.wait_ge(q.s2c_kept[s], made(i))
                        pe.wait_ge(*((q.g_kept[0], made(i)) if s else (q.finished[1], before(i))))
                        pe.matmul(pG[:, 0:P], wg[:, 0:D], c2s[:, s, :], start=True, stop=False)
                        pe.matmul(pG[:, 0:P], wg[:, D:2 * D], s2c[:, s, :], start=False, stop=True
                                  ).then_inc(q.g_made[s], 1)
                    for s in range(2):
                        pe.wait_ge(q.mix[s], 4 * i + 5)
                        pe.wait_ge(*((q.finished[0], made(i)) if s else (q.g_kept[1], made(i))))
                        pe.transpose(pG[:, P:2 * P], o[:, s, :], env.ident[:, :]).then_inc(q.o_made[s], 1)

            @block.vector
            def _(dve):
                dve.wait_ge(loaded, 16 * len(loads))
                dve.wait_ge(prep, 1)
                dve.tensor_scalar(cols[:, BG_:BG_ + 1], cols[:, BG_:BG_ + 1], 0.5, None, ALU.mult).then_inc(prep, 1)
                with dve.Fori(0, TILES // 2) as i:
                    for s in range(2):
                        dve.wait_ge(q.s_made[s], made(i))
                        dve.wait_ge(q.kept[s], made(i))
                        dve.tensor_scalar(pS[:, 0:KEYS], pS[:, 0:KEYS], qbk[:, s, :], None, ALU.add
                                          ).then_inc(q.shifted[s], 1)
                        dve.wait_ge(q.shifted[s], made(i))
                        dve.tensor_reduce(m1[:, s, :], pS[:, 0:KEYS], AX.X, ALU.max).then_inc(q.m_made[s], 1)
                        dve.wait_ge(q.m_made[s], made(i))
                        dve.tensor_scalar(n1[:, s, :], m1[:, s, :], -1.0, None, ALU.mult).then_inc(q.n_made[s], 1)
                        dve.wait_ge(q.s2_made[s], made(i))
                        dve.tensor_reduce(mx2[:, s, :], pS2[:, 0:2 * S].rearrange("p (r k) -> p r k", k=S), AX.X,
                                          ALU.max).then_inc(q.m2_made[s], 1)
                        dve.wait_ge(q.m2_made[s], made(i))
                        dve.tensor_scalar(nmx2[:, s, :], mx2[:, s, :], -SC, None, ALU.mult).then_inc(q.n2_made[s], 1)
                    for s in range(2):
                        dve.wait_ge(q.p2_made[s], made(i))
                        dve.reciprocal(r1[:, s, :], s1[:, s, :])
                        dve.reciprocal(rs2[:, s, :], sm2[:, s, :]).then_inc(q.r2_made[s], 1)
                        dve.wait_ge(q.r2_made[s], made(i))
                        dve.tensor_tensor(rm2[:, s], m2[:, :, :], bc(rs2[:, s, :], 2, 4), ALU.mult
                                          ).then_inc(q.rm_made[s], 1)
                        dve.wait_ge(q.rm_made[s], made(i))
                        dve.tensor_tensor(p2m[:, s], bc(p2[:, s], 2, 4), bc(rm2[:, s], 3, S), ALU.mult
                                          ).then_inc(q.p2m_made[s], 1)
                    for s in range(2):
                        dve.wait_ge(q.c_made[s], made(i))
                        dve.tensor_scalar(cn[:, s, :], pC[:, 0:D], r1[:, s, :], None, ALU.mult).then_inc(q.c_kept[s], 1)
                    for s in range(2):
                        dve.wait_ge(q.pi_made[s], made(i))
                        dve.tensor_tensor(pib[:, s], bc(pS2[:, 64:64 + S], 1, 4), bc(m4q[:, :], 2, S), ALU.mult
                                          ).then_inc(q.pib_made[s], 1)
                    for s in range(2):
                        dve.wait_ge(q.g_kept[s], made(i))
                        dve.tensor_scalar(gt[:, s, :], gt[:, s, :], 0.5, 0.5, ALU.mult, ALU.add).then_inc(q.mix[s], 1)
                        dve.tensor_tensor(c2s[:, s, :], c2s[:, s, :], s2c[:, s, :], ALU.subtract).then_inc(q.mix[s], 1)
                        dve.wait_ge(q.mix[s], 4 * i + 3)
                        dve.tensor_tensor(o[:, s, :], c2s[:, s, :], gt[:, s, :], ALU.mult).then_inc(q.mix[s], 1)
                        dve.wait_ge(q.mix[s], 4 * i + 4)
                        dve.tensor_tensor(o[:, s, :], o[:, s, :], s2c[:, s, :], ALU.add).then_inc(q.mix[s], 1)
                    for s in range(2):
                        dve.wait_ge(q.o_made[s], made(i))
                        x = env.X[:, 2 * i + s, :]
                        dve.tensor_tensor(x, x, pG[:, P:2 * P], ALU.add).then_inc(q.finished[s], 1)


def l3_xattn(nc, env, a):
    normalise(nc, env, "l3x_ln", env.X, dst_t=env.XNT)
    with stage(nc, "l3x") as st:
        QC, QP, KC = (st.sb(n, [P, T]) for n in ("QC", "QP", "KC"))
        plain_projection(nc, env, "l3x_q", a.L3_xattn_Wq_c, env.XNT, QC,
                        bias_d=a.L3_xattn_bq_c)
        plain_projection(nc, env, "l3x_p", a.L3_xattn_Wk_s, QC, QP, scale=D ** -0.5)
        plain_projection(nc, env, "l3x_k", a.L3_xattn_Wk_c, env.XNT, KC,
                        bias_d=a.L3_xattn_bk_c)
        two_way_cross(nc, env, "l3x_att", a, QC, QP, KC)


def layouts(v):
    o = {}
    o["x"] = v["x"].reshape(T, D)
    row = lambda n: v[n].reshape(1, -1)
    col = lambda n: v[n].reshape(-1, 1)
    for n in ("L0_ffn_router_w",):
        o[n] = v[n]
    o["L0_ffn_router_b"] = row("L0_ffn_router_b")
    o["L0_ffn_expert_w"] = v["L0_ffn_expert_w"].transpose(1, 0, 2).reshape(D, EXPERTS * D)
    o["L0_ffn_expert_b"] = v["L0_ffn_expert_b"]
    o["ctx_t"] = v["ctx_1024"].transpose(2, 0, 1).reshape(D, B * KEYS)
    o["mask_pad"] = v["mask_BxS2_if1"]
    for n in ("Wq", "Wk", "Wv", "Wo"):
        o["L0_xattn_" + n] = v["L0_xattn_" + n].T
    o["L1_xattn_Wq"], o["L1_xattn_Wk"] = v["L1_xattn_Wq"], v["L1_xattn_Wk"]
    o["L1_xattn_Wv"], o["L1_xattn_Wp"] = v["L1_xattn_Wv"].T, v["L1_xattn_Wp"].T
    o["L1_xattn_bp"] = row("L1_xattn_bp")
    for n in ("L1_xattn_ln_g", "L1_xattn_ln_b"):
        o[n] = np.tile(v[n], HEADS).reshape(D, 1)
    for n in ("Wq", "Wk", "Wv", "Wo"):
        o["L2_xattn_" + n] = v["L2_xattn_" + n].T
    for n in ("bq", "bk", "bv"):
        o["L2_xattn_" + n] = col("L2_xattn_" + n)
    o["L2_xattn_bo"] = row("L2_xattn_bo")
    o["mask_if"] = np.tile(v["mask_1x1xSxS2_ik0"][0, 0], (BT, 1))
    w, b = v["L3_attn_in_proj_weight"], v["L3_attn_in_proj_bias"]
    for n, k in enumerate("qkv"):
        o["L3_attn_w" + k] = w[n * D:(n + 1) * D].T
        o["L3_attn_b" + k] = b[n * D:(n + 1) * D].reshape((1, D) if k == "v" else (D, 1))
    o["L3_attn_logit"] = np.repeat(v["L3_attn_logit_scale"].reshape(HEADS, 1), HD, axis=0)
    o["L3_attn_head"] = np.repeat(v["L3_attn_head_scale"].reshape(HEADS, 1), HD, axis=0)
    o["L3_attn_out_w"], o["L3_attn_out_b"] = v["L3_attn_out_w"].T, col("L3_attn_out_b")
    wqkv = v["L1_attn_Wqkv"]
    swap = np.arange(D) ^ 1
    for n, k in enumerate("qkv"):
        o["L1_attn_w" + k] = wqkv[:, n * D:(n + 1) * D]
    o["L1_attn_wq2"], o["L1_attn_wk2"] = o["L1_attn_wq"][:, swap], o["L1_attn_wk"][:, swap]
    o["L1_attn_Wo"] = v["L1_attn_Wo"]
    o["L1_attn_ln"] = np.stack([v["L1_attn_" + n] for n in ("ln1_g", "ln1_b", "ln2_g", "ln2_b")], axis=1)
    def mlp(w1, b1, w2):
        w1, b1, w2 = (x if x.ndim == 1 + k else x[None] for x, k in ((w1, 2), (b1, 1), (w2, 2)))
        e, _, h = w1.shape
        return (w1.transpose(1, 0, 2).reshape(D, e * h), b1.reshape(e * h // P, P).T,
                w2.reshape(e, h // P, P, D).transpose(2, 0, 1, 3).reshape(P, e * h // P * D))
    o["L1_attn_W1"], o["L1_attn_b1"], o["L1_attn_W2"] = mlp(v["L1_attn_W1"], v["L1_attn_b1"], v["L1_attn_W2"])
    o["L1_attn_b2"] = row("L1_attn_b2")
    o["L1_ffn_Wr"], o["L1_ffn_br"], o["L1_ffn_b2"] = v["L1_ffn_Wr"], row("L1_ffn_br"), v["L1_ffn_b2"]
    o["L1_ffn_W1"], o["L1_ffn_b1"], o["L1_ffn_W2"] = mlp(v["L1_ffn_W1"], v["L1_ffn_b1"], v["L1_ffn_W2"])
    o["L2_ffn_norm_weight"] = col("L2_ffn_norm_weight")
    o["L2_ffn_router_w"], o["L2_ffn_router_b"] = v["L2_ffn_router_w"].T, row("L2_ffn_router_b")
    o["L2_ffn_fc1_w"], o["L2_ffn_fc1_b"], o["L2_ffn_fc2_w"] = mlp(
        v["L2_ffn_fc1_w"].transpose(0, 2, 1), v["L2_ffn_fc1_b"], v["L2_ffn_fc2_w"].transpose(0, 2, 1))
    o["L2_ffn_fc2_b"] = v["L2_ffn_fc2_b"]
    o["L3_ffn_gate_w"] = v["L3_ffn_gate_w"].T
    o["L3_ffn_down_w"], o["L3_ffn_down_b"], o["L3_ffn_up_w"] = mlp(
        v["L3_ffn_down_w"].reshape(512, D).T, v["L3_ffn_down_b"].reshape(512),
        v["L3_ffn_up_w"].transpose(0, 2, 1).reshape(512, D))
    o["L3_ffn_up_b"] = v["L3_ffn_up_b"]
    o["bits"] = np.tile((1 << np.arange(29, -1, -1)).astype(np.int32), (P, 1))
    o["L0_attn_Wq"] = v["L0_attn_Wq"]
    wkv = v["L0_attn_Wkv"]
    o["L0_attn_wk2"], o["L0_attn_wv"] = np.concatenate([wkv[:, :64], wkv[:, :64]], axis=1), wkv[:, 64:]
    o["L0_attn_Wo"] = v["L0_attn_Wo"].reshape(4, P, D).transpose(1, 0, 2).reshape(P, 4 * D)
    o["L0_attn_ln"] = np.stack([v["L0_attn_norm_w"], v["L0_attn_norm_b"]], axis=1)
    o["L0_attn_out_norm_w"], o["L0_attn_out_norm_b"] = row("L0_attn_out_norm_w"), row("L0_attn_out_norm_b")
    o["L2_attn_W_in"] = v["L2_attn_W_in"]
    chunked = lambda m: m.reshape(2, P, -1).transpose(1, 0, 2).reshape(P, -1)
    wx = v["L2_attn_W_xproj"]
    o["L2_attn_wx0"] = chunked(np.repeat(wx[:, 0:1], P, axis=1))
    o["L2_attn_wbc"] = chunked(np.concatenate([wx[:, 1:33]] * 3, axis=1))
    o["L2_attn_W_out"] = chunked(v["L2_attn_W_out"])
    o["L2_attn_conv_w"] = chunked(v["L2_attn_conv_w"][:, 0, :])
    o["L2_attn_cols"] = chunked(np.stack([v["L2_attn_" + n] for n in ("conv_b", "w_dt", "b_dt", "D_param")], axis=1))
    o["L2_attn_A_log"] = chunked(v["L2_attn_A_log"])
    for n in ("Wq_c", "Wk_c", "Wq_s", "Wv_s", "Wv_c"):
        o["L3_xattn_" + n] = v["L3_xattn_" + n].T
    o["L3_xattn_Wk_s"] = v["L3_xattn_Wk_s"]
    o["L3_xattn_bq_c"], o["L3_xattn_bk_c"] = col("L3_xattn_bq_c"), col("L3_xattn_bk_c")
    o["L3_xattn_Wg"] = v["L3_xattn_Wg"].reshape(D, 2, D).transpose(2, 1, 0).reshape(D, 2 * D)
    o["L3_xattn_cols"] = np.stack([v["L3_xattn_" + n] for n in ("bq_s", "bk_s", "bv_s", "bv_c", "bg")], axis=1)
    o["ctx_n"] = v["ctx_1024"]
    lo, hi, _ = interpolation()
    o["ctx_sub"] = v["ctx_1024"][:, np.concatenate([lo, hi])].transpose(2, 0, 1).reshape(D, B * 2 * S)
    return o


def interpolation():
    pos = (np.arange(S, dtype=np.float32) + np.float32(0.5)) * np.float32(KEYS / S) - np.float32(0.5)
    pos = np.clip(pos, 0.0, KEYS - 1)
    lo = np.floor(pos).astype(np.int32)
    return lo, np.minimum(lo + 1, KEYS - 1), pos - lo


def more_constants(c):
    tok = np.arange(P)
    c["m4"] = np.equal.outer(tok % 32 // HD, np.arange(4))
    c["m4q"] = np.equal.outer(tok // S, np.arange(4))
    c["selq"] = np.equal.outer(tok % S, np.arange(S))
    head = np.equal.outer(tok // HD, tok // HD)
    c["centre"] = np.eye(P) - head / HD
    c["eps"] = np.full((P, 1), EPS)
    freq = 10000.0 ** (-(np.arange(0, HD, 2, dtype=np.float32) / np.float32(HD)))
    theta = np.arange(S, dtype=np.float32)[None, :] * freq[tok % HD // 2][:, None].astype(np.float32)
    theta = theta[:, tok % S]
    sign = np.where(tok % 2 == 0, -1.0, 1.0)[:, None]
    c["rope_cos"] = np.concatenate([np.cos(theta) * HD ** -0.5, np.cos(theta)], axis=1)
    c["rope_sin"] = np.concatenate([np.sin(theta) * sign * HD ** -0.5, np.sin(theta) * sign], axis=1)
    chunk = P // EXPERTS
    expert_of = tok // chunk
    c["same_expert"] = np.equal.outer(expert_of, expert_of)
    c["lower_chunk"] = c["same_expert"] & (tok[:, None] < tok[None, :])
    c["spread"] = np.equal.outer(np.arange(EXPERTS), np.arange(512) // 64)
    c["pick"] = np.equal.outer(np.arange(96) % 32, np.arange(32))
    weight = interpolation()[2]
    both = np.concatenate([np.diag(1 - weight), np.diag(weight)])
    c["interp"] = np.tile(both, (2, 1))
    c["pair"] = np.concatenate([np.equal.outer(tok // (2 * S) + 2 * r, np.arange(BT)) for r in range(2)], axis=1)
    c["causal_q01"] = tok[:, None] % S >= np.arange(S)[None, :]
    c["causal_q_add"] = np.where(c["causal_q01"], 0.0, -BIG)
    c["group16"] = np.equal.outer(np.arange(16) % 4, tok // S)
    c["batch16"] = np.equal.outer(np.arange(16) // 4, np.arange(BT))
    c["own_head"] = np.equal.outer(tok // HD, np.arange(HEADS))
    c["half"] = np.equal.outer(tok // (P // 2), np.arange(2))
    c["parity"] = np.equal.outer(tok // S % 2, np.arange(2))
    rows = np.concatenate([np.equal.outer(tok // HD + 32 * u, tok) for u in range(4)], axis=1)
    c["gather_sum"], c["gather_mean"] = rows, rows / HD
    c["spread_heads"] = np.concatenate([np.equal.outer(tok, tok // HD + 32 * u) for u in range(4)], axis=1)
    c["neg"] = np.full((P, 1), NEG)


def build(nc, a, out):
    with ExitStack() as ctx:
        def sb(name, shape, dt=F32):
            return ctx.enter_context(nc.sbuf_tensor(name, shape, dt))

        env = Names(
            X=sb("X", [P, TILES, D]),
            XNT=sb("XNT", [P, T]),
            ident=sb("ident", [P, P]),
            ones=sb("ones", [P, 512]),
            countdown=sb("countdown", [P, EXPERTS]),
            m4=sb("m4", [P, 4]),
            neg=sb("neg", [P, 1]),
            eps=sb("eps", [P, 1]),
            a=a,
        )
        with stage(nc, "load") as st:
            loaded = st.sem("loaded")
            with nc.Block() as block:
                @block.sync
                def _(sp):
                    sp.dma_start(env.X[:, :, :], a.x.rearrange("(i p) d -> p i d", p=P)).then_inc(loaded, 16)
                    for name in ("ident", "ones", "countdown", "m4", "neg", "eps"):
                        sp.dma_start(env[name][:, :], a["c_" + name]).then_inc(loaded, 16)
                    sp.wait_ge(loaded, 112)
        for layer in LAYERS:
            layer(nc, env, a)
        with stage(nc, "store") as st:
            stored = st.sem("stored")
            with nc.Block() as block:
                @block.sync
                def _(sp):
                    sp.dma_start(out.rearrange("(i p) d -> p i d", p=P), env.X[:, :, :]).then_inc(stored, 16)
                    sp.wait_ge(stored, 16)


LAYERS = [l0_xattn, l0_attn, l0_ffn, l1_xattn, l1_attn, l1_ffn, l2_xattn, l2_attn, l2_ffn, l3_xattn, l3_attn, l3_ffn]


def constants():
    c = {}
    c["ident"] = np.eye(P)
    c["ones"] = np.ones((P, 512))
    c["countdown"] = np.tile(EXPERTS - np.arange(EXPERTS), (P, 1))
    more_constants(c)
    return {"c_" + n: np.ascontiguousarray(v, dtype=np.float32) for n, v in c.items()}


def kernel(**inputs):
    import concourse.bacc as bacc
    from concourse.bass_utils import run_bass_kernel_spmd as run

    arrays = {n: np.ascontiguousarray(v) for n, v in layouts({n: np.asarray(v) for n, v in inputs.items()}).items()}
    arrays.update(constants())
    nc = bacc.Bacc("TRN2", target_bir_lowering=False, num_devices=1)
    a = Names(**{n: nc.dram_tensor(n, v.shape, mybir.dt.from_np(v.dtype), kind="ExternalInput").ap()
                           for n, v in arrays.items()})
    out = nc.dram_tensor("out", (T, D), F32, kind="ExternalOutput").ap()
    build(nc, a, out)
    r = run(nc, [arrays], core_ids=[0])
    return r.results[0]["out"].reshape(B, S, D)
```
